# Optimizing a Trainium2 kernel written in Bass

```python
import numpy as np
import jax
import jax.numpy as jnp

def _softmax(x, axis=-1):
    return jax.nn.softmax(x, axis=axis)

def _gelu(x):
    return jax.nn.gelu(x, approximate=True)

def _silu(x):
    return jax.nn.silu(x)

def _sigmoid(x):
    return jax.nn.sigmoid(x)

def _layernorm(x, axis=-1, eps=1e-05):
    m = jnp.mean(x, axis=axis, keepdims=True)
    v = jnp.var(x, axis=axis, keepdims=True)
    return (x - m) / jnp.sqrt(v + eps)

def _scatter_add(tgt, idx, src, axis=0):
    return tgt.at[idx].add(src)

def _segment_sum(src, seg, n):
    return jax.ops.segment_sum(src, seg, n)
kernel_name = 'mk_seq_preln_d4_jaxref_r8_fb8ea1'

def setup_inputs(seed: int=0):
    np.random.seed(seed)
    _w = jnp.asarray

    def _L0_attn_setup():
        import jax, jax.numpy as jnp
        import numpy as np
        B, S, D, H = (2, 256, 128, 16)
        HD = D // H
        key = jax.random.key(seed)
        ks = jax.random.split(key, 5)
        scale = 1.0 / np.sqrt(D)
        x = jax.random.normal(ks[0], (B, S, D), dtype=jnp.float32)
        W_Q = jax.random.uniform(ks[1], (D, D), jnp.float32, -scale, scale)
        W_K = jax.random.uniform(ks[2], (D, D), jnp.float32, -scale, scale)
        W_V = jax.random.uniform(ks[3], (D, D), jnp.float32, -scale, scale)
        W_O = jax.random.uniform(ks[4], (D, D), jnp.float32, -scale, scale)
        return {'x': x, 'W_Q': W_Q, 'W_K': W_K, 'W_V': W_V, 'W_O': W_O}
    _L0_attn_in = _L0_attn_setup()

    def _L0_ffn_setup():
        import jax, jax.numpy as jnp
        import numpy as np
        EXPERT_NUM = 8
        CAPACITY = 100
        key = jax.random.key(seed)
        k1, k2, k3 = jax.random.split(key, 3)
        B, S, H, E = (8, 256, 128, EXPERT_NUM)
        x = jax.random.normal(k1, (B, S, H), dtype=jnp.float32)
        w_gate = jax.random.normal(k2, (H, E), dtype=jnp.float32) * 0.02
        w_expert = jax.random.normal(k3, (H, H), dtype=jnp.float32) * 0.02
        b_expert = jnp.zeros((H,), dtype=jnp.float32)
        return {'x': x, 'w_gate': w_gate, 'w_expert': w_expert, 'b_expert': b_expert}
    _L0_ffn_in = _L0_ffn_setup()

    def _L1_attn_setup():
        import jax, jax.numpy as jnp
        import numpy as np
        from jax import lax
        B, T, HID = (4, 128, 128)
        H, DK, DV = (8, 128, 128)
        KCONV = 4
        EPS = 1e-06
        KEY_DIM = H * DK
        VAL_DIM = H * DV
        CONV_DIM = 2 * KEY_DIM + VAL_DIM
        key = jax.random.key(seed)
        ks = jax.random.split(key, 11)
        s = 0.02
        return {'hidden_states': jax.random.normal(ks[0], (B, T, HID), jnp.float32), 'qkv_w': jax.random.normal(ks[1], (CONV_DIM, HID), jnp.float32) * s, 'z_w': jax.random.normal(ks[2], (VAL_DIM, HID), jnp.float32) * s, 'b_w': jax.random.normal(ks[3], (H, HID), jnp.float32) * s, 'a_w': jax.random.normal(ks[4], (H, HID), jnp.float32) * s, 'conv_w': jax.random.normal(ks[5], (CONV_DIM, 1, KCONV), jnp.float32) * 0.2, 'dt_bias': jnp.ones((H,), jnp.float32), 'A_log': jnp.log(jax.random.uniform(ks[6], (H,), jnp.float32, 0.001, 16.0)), 'norm_w': jnp.ones((DV,), jnp.float32), 'out_w': jax.random.normal(ks[7], (HID, VAL_DIM), jnp.float32) * s}
    _L1_attn_in = _L1_attn_setup()

    def _L1_ffn_setup():
        import jax, jax.numpy as jnp
        import numpy as np
        DIM = 128
        DEPTH = 6
        HEADS = 16
        DIM_HEAD = 64
        WINDOW = 32
        INNER = HEADS * DIM_HEAD
        DIM_INNER = int(DIM * 4 * 2 / 3)
        QK_SCALE = 8.0

        def shift_tokens(t):
            a, s = jnp.split(t, 2, -1)
            s = jnp.pad(s, ((0, 0), (1, 0), (0, 0)))[:, :-1]
            return jnp.concatenate([a, s], -1)

        def l2norm(t):
            return t / jnp.maximum(jnp.linalg.norm(t, axis=-1, keepdims=True), 1e-12)

        def rotate_half(x):
            x1, x2 = jnp.split(x, 2, -1)
            return jnp.concatenate([-x2, x1], -1)

        def rotary_tables(n):
            half = jnp.arange(0, DIM_HEAD, 2, dtype=jnp.float32)
            inv_freq = 1.0 / 10000.0 ** (half / DIM_HEAD)
            t = jnp.arange(n, dtype=jnp.float32)
            freqs = t[:, None] * inv_freq[None, :]
            freqs = jnp.concatenate([freqs, freqs], -1)
            base_scale = (half + 0.4 * DIM_HEAD) / (1.4 * DIM_HEAD)
            power = (t - n // 2) / (WINDOW // 2)
            scale = base_scale[None, :] ** power[:, None]
            scale = jnp.concatenate([scale, scale], -1)
            return (freqs, scale)

        def local_attention(q, k, v):
            b, h, n, d = q.shape
            w = WINDOW
            nw = n // w
            bq = q.reshape(b, h, nw, w, d)
            bk = k.reshape(b, h, nw, w, d)
            bv = v.reshape(b, h, nw, w, d)

            def look(t):
                p = jnp.pad(t, ((0, 0), (0, 0), (1, 0), (0, 0), (0, 0)))
                return jnp.concatenate([p[:, :, :nw], p[:, :, 1:]], axis=3)
            bk2, bv2 = (look(bk), look(bv))
            seq = jnp.arange(n).reshape(nw, w)
            seq_p = jnp.pad(seq, ((1, 0), (0, 0)), constant_values=-1)
            jt = jnp.concatenate([seq_p[:nw], seq_p[1:]], axis=1)
            it = seq[:, :, None]
            jb = jt[:, None, :]
            mask = (it < jb) | (it > jb + w) | (jb == -1)
            sim = jnp.einsum('bhwie,bhwje->bhwij', bq, bk2) * QK_SCALE
            sim = jnp.where(mask, -jnp.finfo(sim.dtype).max, sim)
            attn = jax.nn.softmax(sim, -1)
            out = jnp.einsum('bhwij,bhwje->bhwie', attn, bv2)
            return out.reshape(b, h, n, d)

        def attn_layer(x, Wqkv, qs, ksc, Wo):
            b, n, _ = x.shape
            qkv = x @ Wqkv
            q, k, v = jnp.split(qkv, 3, -1)
            sh = lambda t: t.reshape(b, n, HEADS, DIM_HEAD).transpose(0, 2, 1, 3)
            q, k, v = (sh(q), sh(k), sh(v))
            q = l2norm(q) * qs
            k = l2norm(k) * ksc
            freqs, scale = rotary_tables(n)
            cos, sin = (jnp.cos(freqs), jnp.sin(freqs))
            q = q * cos * scale + rotate_half(q) * sin * scale
            inv = 1.0 / scale
            k = k * cos * inv + rotate_half(k) * sin * inv
            out = local_attention(q, k, v)
            out = out.transpose(0, 2, 1, 3).reshape(b, n, INNER)
            return out @ Wo

        def ffn_layer(x, g, bln, W1, b1, W2, b2):
            mu = x.mean(-1, keepdims=True)
            var = ((x - mu) ** 2).mean(-1, keepdims=True)
            xn = (x - mu) / jnp.sqrt(var + 1e-05) * g + bln
            hg = xn @ W1 + b1
            a, gate = jnp.split(hg, 2, -1)
            return a * jax.nn.gelu(gate, approximate=False) @ W2 + b2
        key = jax.random.key(seed)
        ks = jax.random.split(key, 8)
        B, N = (2, 256)
        init = lambda k, shape: jax.random.normal(k, shape, jnp.float32) * 0.02
        return {'x': jax.random.normal(ks[0], (B, N, DIM), jnp.float32), 'Wqkv': init(ks[1], (DEPTH, DIM, 3 * INNER)), 'q_scale': jnp.ones((DEPTH, DIM_HEAD), jnp.float32), 'k_scale': jnp.ones((DEPTH, DIM_HEAD), jnp.float32), 'Wo': init(ks[2], (DEPTH, INNER, DIM)), 'ln_g': jnp.ones((DEPTH, DIM), jnp.float32), 'ln_b': jnp.zeros((DEPTH, DIM), jnp.float32), 'W1': init(ks[3], (DEPTH, DIM, 2 * DIM_INNER)), 'b1': jnp.zeros((DEPTH, 2 * DIM_INNER), jnp.float32), 'W2': init(ks[4], (DEPTH, DIM_INNER, DIM)), 'b2': jnp.zeros((DEPTH, DIM), jnp.float32)}
    _L1_ffn_in = _L1_ffn_setup()

    def _L2_attn_setup():
        import jax, jax.numpy as jnp
        import numpy as np
        EPS = 1e-08
        key = jax.random.key(seed)
        x = jax.random.normal(key, (32, 200, 128), dtype=jnp.float32)
        return {'x': x}
    _L2_attn_in = _L2_attn_setup()

    def _L2_ffn_setup():
        import jax, jax.numpy as jnp
        import numpy as np
        B, S, H = (1, 128, 128)
        E, I = (8, 256)
        JITTER_EPS = 0.01

        def _sparse_mixer_top2(scores, jitter_eps):
            vals, idx = jax.lax.top_k(scores, 2)
            neg_inf = jnp.array(-jnp.inf, scores.dtype)
            t1 = vals[:, :1]
            f1 = jnp.maximum(jnp.abs(scores), t1)
            m1 = (t1 - scores) / f1 > 2 * jitter_eps
            p1 = jax.nn.softmax(jnp.where(m1, neg_inf, scores), axis=-1)
            mult1 = jnp.take_along_axis(p1, idx[:, :1], axis=-1)
            t2 = vals[:, 1:2]
            f2 = jnp.maximum(jnp.abs(scores), t2)
            m2 = (t2 - scores) / f2 > 2 * jitter_eps
            rows = jnp.arange(scores.shape[0])[:, None]
            s2 = scores.at[rows, idx[:, :1]].set(neg_inf)
            p2 = jax.nn.softmax(jnp.where(m2, neg_inf, s2), axis=-1)
            mult2 = jnp.take_along_axis(p2, idx[:, 1:2], axis=-1)
            return (jnp.concatenate([mult1, mult2], axis=-1), idx)
        key = jax.random.key(seed)
        ks = jax.random.split(key, 5)
        s_h = 1.0 / np.sqrt(H)
        s_i = 1.0 / np.sqrt(I)
        return {'hidden_states': jax.random.normal(ks[0], (B, S, H), jnp.float32), 'gate_w': jax.random.normal(ks[1], (E, H), jnp.float32) * s_h, 'w1': jax.random.normal(ks[2], (E, I, H), jnp.float32) * s_h, 'w2': jax.random.normal(ks[3], (E, H, I), jnp.float32) * s_i, 'w3': jax.random.normal(ks[4], (E, I, H), jnp.float32) * s_h}
    _L2_ffn_in = _L2_ffn_setup()

    def _L3_attn_setup():
        import jax, jax.numpy as jnp
        import numpy as np
        CHUNK = 32
        FLOOR = 0.01
        EPS_MIX = 1e-05
        EPS_NORM = 1e-05

        def l2norm(x):
            return x / jnp.sqrt(jnp.sum(x * x, -1, keepdims=True) + 1e-12)

        def dw_causal_conv(x, w):
            K = w.shape[-1]
            L = x.shape[1]
            xp = jnp.pad(x, ((0, 0), (K - 1, 0), (0, 0)))
            y = jnp.zeros_like(x)
            for t in range(K):
                y = y + xp[:, t:t + L, :] * w[:, t]
            return y

        def delta_rule_chunkwise(q, k, v, beta):
            b, h, L, dk = q.shape
            dv = v.shape[-1]
            c = CHUNK
            n = L // c
            q = l2norm(q)
            k = l2norm(k)
            v = v * beta[..., None]
            kb = k * beta[..., None]
            rs = lambda x: x.reshape(b, h, n, c, -1)
            qc, kc, vc, kbc = (rs(q), rs(k), rs(v), rs(kb))
            T = -jnp.einsum('bhnid,bhnjd->bhnij', kbc, kc)
            tri_strict = jnp.tril(jnp.ones((c, c), bool), -1)
            T = jnp.where(tri_strict, T, 0.0)
            for i in range(1, c):
                T = T.at[..., i, :i].add(jnp.einsum('bhnj,bhnji->bhni', T[..., i, :], T[..., :, :i]))
            T = T + jnp.eye(c, dtype=T.dtype)
            u = jnp.einsum('bhnij,bhnjd->bhnid', T, vc)
            w = jnp.einsum('bhnij,bhnjd->bhnid', T, kbc)
            mask_incl = jnp.tril(jnp.ones((c, c), bool), 0)

            def step(S, inp):
                qi, ki, ui, wi = inp
                attn = jnp.einsum('bhid,bhjd->bhij', qi, ki)
                attn = jnp.where(mask_incl, attn, 0.0)
                u_i = ui - jnp.einsum('bhik,bhkd->bhid', wi, S)
                o_i = jnp.einsum('bhik,bhkd->bhid', qi, S) + jnp.einsum('bhij,bhjd->bhid', attn, u_i)
                S = S + jnp.einsum('bhci,bhcd->bhid', ki, u_i)
                return (S, o_i)
            S0 = jnp.zeros((b, h, dk, dv), q.dtype)
            xs = tuple((jnp.moveaxis(a, 2, 0) for a in (qc, kc, u, w)))
            S, o = jax.lax.scan(step, S0, xs)
            o = jnp.moveaxis(o, 0, 2).reshape(b, h, L, dv)
            return (o, S)
        key = jax.random.key(seed)
        B, L, D, H = (4, 512, 128, 4)
        dh = D // H
        ks = jax.random.split(key, 20)
        s = 1.0 / np.sqrt(D)
        inp = {'hidden_states': jax.random.normal(ks[0], (B, L, D), jnp.float32), 'Wq': jax.random.normal(ks[1], (D, D), jnp.float32) * s, 'Wk': jax.random.normal(ks[2], (D, D), jnp.float32) * s, 'Wv': jax.random.normal(ks[3], (D, D), jnp.float32) * s, 'Wb': jax.random.normal(ks[4], (D, H), jnp.float32) * s, 'conv_q_w': jax.random.normal(ks[5], (D, 4), jnp.float32) * 0.5, 'conv_k_w': jax.random.normal(ks[6], (D, 4), jnp.float32) * 0.5, 'conv_v_w': jax.random.normal(ks[7], (D, 4), jnp.float32) * 0.5, 'local_w': (jax.random.normal(ks[8], (H * dh, 7), jnp.float32) / np.sqrt(7.0)).at[:, -1].add(1.0), 'mid_w': (jax.random.normal(ks[9], (H * dh, 25), jnp.float32) / np.sqrt(25.0)).at[:, -1].add(1.0), 'r_w1': jax.random.normal(ks[10], (D + 14 * H, 2 * (D + 14 * H)), jnp.float32) / np.sqrt(D + 14 * H), 'r_b1': jnp.zeros((2 * (D + 14 * H),), jnp.float32), 'r_w2': jax.random.normal(ks[11], (2 * (D + 14 * H), H * 4), jnp.float32) / np.sqrt(2.0 * (D + 14 * H)), 'r_b2': jnp.zeros((H, 4), jnp.float32).at[:, 2:].set(0.7).reshape(-1), 'mix_w': jnp.ones((H, dh), jnp.float32), 'onorm_w': jnp.ones((dh,), jnp.float32), 'Wo': jax.random.normal(ks[12], (D, D), jnp.float32) * s}
        return inp
    _L3_attn_in = _L3_attn_setup()

    def _L3_ffn_setup():
        import jax, jax.numpy as jnp
        import numpy as np
        B, S, D, E = (2, 256, 128, 8)
        key = jax.random.key(seed)
        ks = jax.random.split(key, 5)
        x = jax.random.normal(ks[0], (B, S, D), dtype=jnp.float32)
        router_w = jax.random.normal(ks[1], (E, D), dtype=jnp.float32) * 0.02
        router_b = jnp.zeros((E,), dtype=jnp.float32)
        expert_w = jax.random.normal(ks[2], (E, D, D), dtype=jnp.float32) * 0.02
        expert_b = jnp.zeros((E, D), dtype=jnp.float32)
        return {'x': x, 'router_w': router_w, 'router_b': router_b, 'expert_w': expert_w, 'expert_b': expert_b}
    _L3_ffn_in = _L3_ffn_setup()
    _d = {'L0_attn_x': _L0_attn_in['x'], 'L0_attn_W_Q': _L0_attn_in['W_Q'], 'L0_attn_W_K': _L0_attn_in['W_K'], 'L0_attn_W_V': _L0_attn_in['W_V'], 'L0_attn_W_O': _L0_attn_in['W_O'], 'L0_ffn_w_gate': _L0_ffn_in['w_gate'], 'L0_ffn_w_expert': _L0_ffn_in['w_expert'], 'L0_ffn_b_expert': _L0_ffn_in['b_expert'], 'L1_attn_qkv_w': _L1_attn_in['qkv_w'], 'L1_attn_z_w': _L1_attn_in['z_w'], 'L1_attn_b_w': _L1_attn_in['b_w'], 'L1_attn_a_w': _L1_attn_in['a_w'], 'L1_attn_conv_w': _L1_attn_in['conv_w'], 'L1_attn_dt_bias': _L1_attn_in['dt_bias'], 'L1_attn_A_log': _L1_attn_in['A_log'], 'L1_attn_norm_w': _L1_attn_in['norm_w'], 'L1_attn_out_w': _L1_attn_in['out_w'], 'L1_ffn_Wqkv': _L1_ffn_in['Wqkv'], 'L1_ffn_q_scale': _L1_ffn_in['q_scale'], 'L1_ffn_k_scale': _L1_ffn_in['k_scale'], 'L1_ffn_Wo': _L1_ffn_in['Wo'], 'L1_ffn_ln_g': _L1_ffn_in['ln_g'], 'L1_ffn_ln_b': _L1_ffn_in['ln_b'], 'L1_ffn_W1': _L1_ffn_in['W1'], 'L1_ffn_b1': _L1_ffn_in['b1'], 'L1_ffn_W2': _L1_ffn_in['W2'], 'L1_ffn_b2': _L1_ffn_in['b2'], 'L2_ffn_gate_w': _L2_ffn_in['gate_w'], 'L2_ffn_w1': _L2_ffn_in['w1'], 'L2_ffn_w2': _L2_ffn_in['w2'], 'L2_ffn_w3': _L2_ffn_in['w3'], 'L3_attn_Wq': _L3_attn_in['Wq'], 'L3_attn_Wk': _L3_attn_in['Wk'], 'L3_attn_Wv': _L3_attn_in['Wv'], 'L3_attn_Wb': _L3_attn_in['Wb'], 'L3_attn_conv_q_w': _L3_attn_in['conv_q_w'], 'L3_attn_conv_k_w': _L3_attn_in['conv_k_w'], 'L3_attn_conv_v_w': _L3_attn_in['conv_v_w'], 'L3_attn_local_w': _L3_attn_in['local_w'], 'L3_attn_mid_w': _L3_attn_in['mid_w'], 'L3_attn_r_w1': _L3_attn_in['r_w1'], 'L3_attn_r_b1': _L3_attn_in['r_b1'], 'L3_attn_r_w2': _L3_attn_in['r_w2'], 'L3_attn_r_b2': _L3_attn_in['r_b2'], 'L3_attn_mix_w': _L3_attn_in['mix_w'], 'L3_attn_onorm_w': _L3_attn_in['onorm_w'], 'L3_attn_Wo': _L3_attn_in['Wo'], 'L3_ffn_router_w': _L3_ffn_in['router_w'], 'L3_ffn_router_b': _L3_ffn_in['router_b'], 'L3_ffn_expert_w': _L3_ffn_in['expert_w'], 'L3_ffn_expert_b': _L3_ffn_in['expert_b']}
    _x0 = _d['L0_attn_x']
    _d['L0_attn_x'] = jax.random.normal(jax.random.fold_in(jax.random.key(seed), 1), (4, 1024, 128), dtype=_x0.dtype)
    del _x0
    return _d

def reference(L0_attn_x, L0_attn_W_Q, L0_attn_W_K, L0_attn_W_V, L0_attn_W_O, L0_ffn_w_gate, L0_ffn_w_expert, L0_ffn_b_expert, L1_attn_qkv_w, L1_attn_z_w, L1_attn_b_w, L1_attn_a_w, L1_attn_conv_w, L1_attn_dt_bias, L1_attn_A_log, L1_attn_norm_w, L1_attn_out_w, L1_ffn_Wqkv, L1_ffn_q_scale, L1_ffn_k_scale, L1_ffn_Wo, L1_ffn_ln_g, L1_ffn_ln_b, L1_ffn_W1, L1_ffn_b1, L1_ffn_W2, L1_ffn_b2, L2_ffn_gate_w, L2_ffn_w1, L2_ffn_w2, L2_ffn_w3, L3_attn_Wq, L3_attn_Wk, L3_attn_Wv, L3_attn_Wb, L3_attn_conv_q_w, L3_attn_conv_k_w, L3_attn_conv_v_w, L3_attn_local_w, L3_attn_mid_w, L3_attn_r_w1, L3_attn_r_b1, L3_attn_r_w2, L3_attn_r_b2, L3_attn_mix_w, L3_attn_onorm_w, L3_attn_Wo, L3_ffn_router_w, L3_ffn_router_b, L3_ffn_expert_w, L3_ffn_expert_b):

    def _L0_attn_ref(x, W_Q, W_K, W_V, W_O):
        import jax, jax.numpy as jnp
        import numpy as np
        B, S, D, H = (2, 256, 128, 16)
        HD = D // H
        b, s, d = x.shape
        Q = (x @ W_Q.T).reshape(b, s, H, HD).transpose(0, 2, 1, 3)
        K = (x @ W_K.T).reshape(b, s, H, HD).transpose(0, 2, 1, 3)
        V = (x @ W_V.T).reshape(b, s, H, HD).transpose(0, 2, 1, 3)
        attn = jnp.einsum('bhqd,bhkd->bhqk', Q, K) / jnp.sqrt(jnp.float32(HD))
        slopes = 1.0 / (2.0 ** 8) ** ((jnp.arange(H, dtype=jnp.float32) + 1) / H)
        pos = jnp.arange(s)
        rel = jnp.minimum(pos[None, :] - pos[:, None], 0).astype(jnp.float32)
        bias = slopes[:, None, None] * rel[None, :, :]
        causal = pos[None, :] <= pos[:, None]
        attn = jnp.where(causal[None, None], attn + bias[None], -jnp.inf)
        attn = jax.nn.softmax(attn, axis=-1)
        out = jnp.einsum('bhqk,bhkd->bhqd', attn, V)
        out = out.transpose(0, 2, 1, 3).reshape(b, s, d)
        return out @ W_O.T

    def _L0_ffn_ref(x, w_gate, w_expert, b_expert):
        import jax, jax.numpy as jnp
        import numpy as np
        EXPERT_NUM = 8
        CAPACITY = 100
        B, S, H = x.shape
        E, C = (EXPERT_NUM, CAPACITY)
        hs = x.reshape(-1, H)
        logits = hs @ w_gate
        probs = jax.nn.softmax(logits, axis=1)
        best = jnp.argmax(probs, axis=1)
        mask = jax.nn.one_hot(best, E, dtype=jnp.int32)
        gate = jnp.sum(probs * mask.astype(probs.dtype), axis=1)
        locations = jnp.cumsum(mask, axis=0) - 1
        mask = mask * (locations < C).astype(jnp.int32)
        loc_sum = jnp.sum(locations * mask, axis=1)
        new_gates = gate[:, None] * mask.astype(probs.dtype)
        loc_oh = jax.nn.one_hot(loc_sum, C, dtype=probs.dtype)
        combine = new_gates[:, :, None] * loc_oh[:, None, :]
        dispatch = (combine != 0).astype(hs.dtype)
        dispatched = jnp.einsum('tec,th->ech', dispatch, hs).reshape(E * C, H)
        expert_out = dispatched @ w_expert + b_expert
        combined = combine.reshape(-1, E * C) @ expert_out
        return combined.reshape(B, S, H)

    def _L1_attn_ref(hidden_states, qkv_w, z_w, b_w, a_w, conv_w, dt_bias, A_log, norm_w, out_w):
        import jax, jax.numpy as jnp
        import numpy as np
        from jax import lax
        B, T, HID = (4, 128, 128)
        H, DK, DV = (8, 128, 128)
        KCONV = 4
        EPS = 1e-06
        KEY_DIM = H * DK
        VAL_DIM = H * DV
        CONV_DIM = 2 * KEY_DIM + VAL_DIM
        b_, t_, _ = hidden_states.shape
        mixed = jnp.einsum('bth,ch->btc', hidden_states, qkv_w)
        x = mixed.transpose(0, 2, 1)
        x = lax.conv_general_dilated(x, conv_w, window_strides=(1,), padding=[(KCONV - 1, 0)], feature_group_count=CONV_DIM, dimension_numbers=('NCH', 'OIH', 'NCH'))
        mixed = x.transpose(0, 2, 1)
        z = jnp.einsum('bth,vh->btv', hidden_states, z_w).reshape(b_, t_, H, DV)
        bb = jnp.einsum('bth,nh->btn', hidden_states, b_w)
        aa = jnp.einsum('bth,nh->btn', hidden_states, a_w)
        q, k, v = jnp.split(mixed, 3, axis=-1)
        q = q.reshape(b_, t_, H, DK)
        k = k.reshape(b_, t_, H, DK)
        v = v.reshape(b_, t_, H, DV)
        beta = jax.nn.sigmoid(bb)
        g = -jnp.exp(A_log) * jax.nn.softplus(aa + dt_bias)
        alpha = jnp.exp(g)

        def step(S, inp):
            q_t, k_t, v_t, beta_t, alpha_t = inp
            S = S * alpha_t[..., None, None]
            kv = jnp.einsum('bhk,bhkv->bhv', k_t, S)
            S = S + jnp.einsum('bhk,bhv->bhkv', k_t, (v_t - kv) * beta_t[..., None])
            o_t = jnp.einsum('bhk,bhkv->bhv', q_t, S)
            return (S, o_t)
        qt = q.transpose(1, 0, 2, 3)
        kt = k.transpose(1, 0, 2, 3)
        vt = v.transpose(1, 0, 2, 3)
        bt = beta.transpose(1, 0, 2)
        at = alpha.transpose(1, 0, 2)
        S0 = jnp.zeros((b_, H, DK, DV), hidden_states.dtype)
        _, o = lax.scan(step, S0, (qt, kt, vt, bt, at))
        o = o.transpose(1, 0, 2, 3)
        var = jnp.mean(jnp.square(o), axis=-1, keepdims=True)
        o = o * lax.rsqrt(var + EPS) * norm_w
        o = o * (z * jax.nn.sigmoid(z))
        out = jnp.einsum('btv,hv->bth', o.reshape(b_, t_, VAL_DIM), out_w)
        return out

    def _L1_ffn_ref(x, Wqkv, q_scale, k_scale, Wo, ln_g, ln_b, W1, b1, W2, b2):
        import jax, jax.numpy as jnp
        import numpy as np
        DIM = 128
        DEPTH = 6
        HEADS = 16
        DIM_HEAD = 64
        WINDOW = 32
        INNER = HEADS * DIM_HEAD
        DIM_INNER = int(DIM * 4 * 2 / 3)
        QK_SCALE = 8.0

        def shift_tokens(t):
            a, s = jnp.split(t, 2, -1)
            s = jnp.pad(s, ((0, 0), (1, 0), (0, 0)))[:, :-1]
            return jnp.concatenate([a, s], -1)

        def l2norm(t):
            return t / jnp.maximum(jnp.linalg.norm(t, axis=-1, keepdims=True), 1e-12)

        def rotate_half(x):
            x1, x2 = jnp.split(x, 2, -1)
            return jnp.concatenate([-x2, x1], -1)

        def rotary_tables(n):
            half = jnp.arange(0, DIM_HEAD, 2, dtype=jnp.float32)
            inv_freq = 1.0 / 10000.0 ** (half / DIM_HEAD)
            t = jnp.arange(n, dtype=jnp.float32)
            freqs = t[:, None] * inv_freq[None, :]
            freqs = jnp.concatenate([freqs, freqs], -1)
            base_scale = (half + 0.4 * DIM_HEAD) / (1.4 * DIM_HEAD)
            power = (t - n // 2) / (WINDOW // 2)
            scale = base_scale[None, :] ** power[:, None]
            scale = jnp.concatenate([scale, scale], -1)
            return (freqs, scale)

        def local_attention(q, k, v):
            b, h, n, d = q.shape
            w = WINDOW
            nw = n // w
            bq = q.reshape(b, h, nw, w, d)
            bk = k.reshape(b, h, nw, w, d)
            bv = v.reshape(b, h, nw, w, d)

            def look(t):
                p = jnp.pad(t, ((0, 0), (0, 0), (1, 0), (0, 0), (0, 0)))
                return jnp.concatenate([p[:, :, :nw], p[:, :, 1:]], axis=3)
            bk2, bv2 = (look(bk), look(bv))
            seq = jnp.arange(n).reshape(nw, w)
            seq_p = jnp.pad(seq, ((1, 0), (0, 0)), constant_values=-1)
            jt = jnp.concatenate([seq_p[:nw], seq_p[1:]], axis=1)
            it = seq[:, :, None]
            jb = jt[:, None, :]
            mask = (it < jb) | (it > jb + w) | (jb == -1)
            sim = jnp.einsum('bhwie,bhwje->bhwij', bq, bk2) * QK_SCALE
            sim = jnp.where(mask, -jnp.finfo(sim.dtype).max, sim)
            attn = jax.nn.softmax(sim, -1)
            out = jnp.einsum('bhwij,bhwje->bhwie', attn, bv2)
            return out.reshape(b, h, n, d)

        def attn_layer(x, Wqkv, qs, ksc, Wo):
            b, n, _ = x.shape
            qkv = x @ Wqkv
            q, k, v = jnp.split(qkv, 3, -1)
            sh = lambda t: t.reshape(b, n, HEADS, DIM_HEAD).transpose(0, 2, 1, 3)
            q, k, v = (sh(q), sh(k), sh(v))
            q = l2norm(q) * qs
            k = l2norm(k) * ksc
            freqs, scale = rotary_tables(n)
            cos, sin = (jnp.cos(freqs), jnp.sin(freqs))
            q = q * cos * scale + rotate_half(q) * sin * scale
            inv = 1.0 / scale
            k = k * cos * inv + rotate_half(k) * sin * inv
            out = local_attention(q, k, v)
            out = out.transpose(0, 2, 1, 3).reshape(b, n, INNER)
            return out @ Wo

        def ffn_layer(x, g, bln, W1, b1, W2, b2):
            mu = x.mean(-1, keepdims=True)
            var = ((x - mu) ** 2).mean(-1, keepdims=True)
            xn = (x - mu) / jnp.sqrt(var + 1e-05) * g + bln
            hg = xn @ W1 + b1
            a, gate = jnp.split(hg, 2, -1)
            return a * jax.nn.gelu(gate, approximate=False) @ W2 + b2
        for i in range(DEPTH):
            x = attn_layer(shift_tokens(x), Wqkv[i], q_scale[i], k_scale[i], Wo[i]) + x
            x = ffn_layer(shift_tokens(x), ln_g[i], ln_b[i], W1[i], b1[i], W2[i], b2[i]) + x
        return x

    def _L2_attn_ref(x):
        import jax, jax.numpy as jnp
        import numpy as np
        EPS = 1e-08
        norms = jnp.linalg.norm(x, axis=-1)
        dots = jnp.einsum('bil,bjl->bij', x, x)
        sim = dots / jnp.maximum(norms[:, :, None] * norms[:, None, :], EPS)
        atten = jax.nn.softmax(sim, axis=-1)
        out = jnp.einsum('bij,bjl->bil', atten, x) + x
        return out

    def _L2_ffn_ref(hidden_states, gate_w, w1, w2, w3):
        import jax, jax.numpy as jnp
        import numpy as np
        B, S, H = (1, 128, 128)
        E, I = (8, 256)
        JITTER_EPS = 0.01

        def _sparse_mixer_top2(scores, jitter_eps):
            vals, idx = jax.lax.top_k(scores, 2)
            neg_inf = jnp.array(-jnp.inf, scores.dtype)
            t1 = vals[:, :1]
            f1 = jnp.maximum(jnp.abs(scores), t1)
            m1 = (t1 - scores) / f1 > 2 * jitter_eps
            p1 = jax.nn.softmax(jnp.where(m1, neg_inf, scores), axis=-1)
            mult1 = jnp.take_along_axis(p1, idx[:, :1], axis=-1)
            t2 = vals[:, 1:2]
            f2 = jnp.maximum(jnp.abs(scores), t2)
            m2 = (t2 - scores) / f2 > 2 * jitter_eps
            rows = jnp.arange(scores.shape[0])[:, None]
            s2 = scores.at[rows, idx[:, :1]].set(neg_inf)
            p2 = jax.nn.softmax(jnp.where(m2, neg_inf, s2), axis=-1)
            mult2 = jnp.take_along_axis(p2, idx[:, 1:2], axis=-1)
            return (jnp.concatenate([mult1, mult2], axis=-1), idx)
        b, s, h = hidden_states.shape
        x = hidden_states.reshape(-1, h)
        T = x.shape[0]
        logits = x @ gate_w.T
        mult, sel = _sparse_mixer_top2(logits, JITTER_EPS)
        rows = jnp.arange(T)[:, None]
        dense_w = jnp.zeros((T, E), x.dtype).at[rows, sel].set(mult)
        h1 = jnp.einsum('th,eih->eti', x, w1)
        h3 = jnp.einsum('th,eih->eti', x, w3)
        act = jax.nn.silu(h1) * h3
        y = jnp.einsum('eti,ehi->eth', act, w2)
        out = jnp.einsum('eth,te->th', y, dense_w)
        return out.reshape(b, s, h)

    def _L3_attn_ref(hidden_states, Wq, Wk, Wv, Wb, conv_q_w, conv_k_w, conv_v_w, local_w, mid_w, r_w1, r_b1, r_w2, r_b2, mix_w, onorm_w, Wo):
        import jax, jax.numpy as jnp
        import numpy as np
        CHUNK = 32
        FLOOR = 0.01
        EPS_MIX = 1e-05
        EPS_NORM = 1e-05

        def l2norm(x):
            return x / jnp.sqrt(jnp.sum(x * x, -1, keepdims=True) + 1e-12)

        def dw_causal_conv(x, w):
            K = w.shape[-1]
            L = x.shape[1]
            xp = jnp.pad(x, ((0, 0), (K - 1, 0), (0, 0)))
            y = jnp.zeros_like(x)
            for t in range(K):
                y = y + xp[:, t:t + L, :] * w[:, t]
            return y

        def delta_rule_chunkwise(q, k, v, beta):
            b, h, L, dk = q.shape
            dv = v.shape[-1]
            c = CHUNK
            n = L // c
            q = l2norm(q)
            k = l2norm(k)
            v = v * beta[..., None]
            kb = k * beta[..., None]
            rs = lambda x: x.reshape(b, h, n, c, -1)
            qc, kc, vc, kbc = (rs(q), rs(k), rs(v), rs(kb))
            T = -jnp.einsum('bhnid,bhnjd->bhnij', kbc, kc)
            tri_strict = jnp.tril(jnp.ones((c, c), bool), -1)
            T = jnp.where(tri_strict, T, 0.0)
            for i in range(1, c):
                T = T.at[..., i, :i].add(jnp.einsum('bhnj,bhnji->bhni', T[..., i, :], T[..., :, :i]))
            T = T + jnp.eye(c, dtype=T.dtype)
            u = jnp.einsum('bhnij,bhnjd->bhnid', T, vc)
            w = jnp.einsum('bhnij,bhnjd->bhnid', T, kbc)
            mask_incl = jnp.tril(jnp.ones((c, c), bool), 0)

            def step(S, inp):
                qi, ki, ui, wi = inp
                attn = jnp.einsum('bhid,bhjd->bhij', qi, ki)
                attn = jnp.where(mask_incl, attn, 0.0)
                u_i = ui - jnp.einsum('bhik,bhkd->bhid', wi, S)
                o_i = jnp.einsum('bhik,bhkd->bhid', qi, S) + jnp.einsum('bhij,bhjd->bhid', attn, u_i)
                S = S + jnp.einsum('bhci,bhcd->bhid', ki, u_i)
                return (S, o_i)
            S0 = jnp.zeros((b, h, dk, dv), q.dtype)
            xs = tuple((jnp.moveaxis(a, 2, 0) for a in (qc, kc, u, w)))
            S, o = jax.lax.scan(step, S0, xs)
            o = jnp.moveaxis(o, 0, 2).reshape(b, h, L, dv)
            return (o, S)
        B, L, D = hidden_states.shape
        H = mix_w.shape[0]
        dh = mix_w.shape[1]
        q = jax.nn.silu(dw_causal_conv(hidden_states @ Wq, conv_q_w))
        k = jax.nn.silu(dw_causal_conv(hidden_states @ Wk, conv_k_w))
        v = jax.nn.silu(dw_causal_conv(hidden_states @ Wv, conv_v_w))
        q4 = q.reshape(B, L, H, dh)
        k4 = k.reshape(B, L, H, dh)
        v4 = v.reshape(B, L, H, dh)
        beta = jax.nn.sigmoid(hidden_states @ Wb)
        delta_out, _ = delta_rule_chunkwise(jnp.transpose(q4, (0, 2, 1, 3)), jnp.transpose(k4, (0, 2, 1, 3)), jnp.transpose(v4, (0, 2, 1, 3)), jnp.transpose(beta, (0, 2, 1)))
        delta_out = jnp.transpose(delta_out, (0, 2, 1, 3))
        v_direct = v4
        vflat = v4.reshape(B, L, H * dh)
        local_out = dw_causal_conv(vflat, local_w).reshape(B, L, H, dh)
        mid_out = dw_causal_conv(vflat, mid_w).reshape(B, L, H, dh)
        outs = [local_out, mid_out, delta_out, v_direct]
        feats = []
        for o_ in outs:
            feats.append(o_.mean(-1))
            feats.append(jnp.var(o_, -1, ddof=1))
        for i in range(4):
            for j in range(i + 1, 4):
                feats.append((outs[i] * outs[j]).mean(-1))
        router_feat = jnp.concatenate([hidden_states] + feats, axis=-1)
        h1 = jax.nn.silu(router_feat @ r_w1 + r_b1)
        logits = (h1 @ r_w2 + r_b2).reshape(B, L, H, 4)
        p = jax.nn.softmax(logits, -1)
        p = p * (1.0 - 4.0 * FLOOR) + FLOOR
        mixed = sum((p[..., i:i + 1] * outs[i] for i in range(4)))
        rms = jnp.sqrt(jnp.mean(mixed * mixed, -1, keepdims=True) + EPS_MIX)
        mixed = mixed / rms * mix_w
        rms2 = jnp.sqrt(jnp.mean(mixed * mixed, -1, keepdims=True) + EPS_NORM)
        o_n = mixed / rms2 * onorm_w
        return o_n.reshape(B, L, H * dh) @ Wo

    def _L3_ffn_ref(x, router_w, router_b, expert_w, expert_b):
        import jax, jax.numpy as jnp
        import numpy as np
        B, S, D, E = (2, 256, 128, 8)
        logits = jnp.einsum('bsd,ed->bse', x, router_w) + router_b
        probs = jax.nn.softmax(logits, axis=-1)
        weights = jnp.max(probs, axis=-1)
        top1 = jnp.argmax(probs, axis=-1)
        y_all = jnp.einsum('bsd,eod->bseo', x, expert_w) + expert_b
        y = jnp.take_along_axis(y_all, top1[:, :, None, None], axis=2)[:, :, 0, :]
        out = y * weights[:, :, None]
        return out
    x = L0_attn_x
    x = x + _L0_attn_ref(_layernorm(x, axis=-1), L0_attn_W_Q, L0_attn_W_K, L0_attn_W_V, L0_attn_W_O)
    x = x + _L0_ffn_ref(_layernorm(x, axis=-1), L0_ffn_w_gate, L0_ffn_w_expert, L0_ffn_b_expert)
    x = x + _L1_attn_ref(_layernorm(x, axis=-1), L1_attn_qkv_w, L1_attn_z_w, L1_attn_b_w, L1_attn_a_w, L1_attn_conv_w, L1_attn_dt_bias, L1_attn_A_log, L1_attn_norm_w, L1_attn_out_w)
    x = x + _L1_ffn_ref(_layernorm(x, axis=-1), L1_ffn_Wqkv, L1_ffn_q_scale, L1_ffn_k_scale, L1_ffn_Wo, L1_ffn_ln_g, L1_ffn_ln_b, L1_ffn_W1, L1_ffn_b1, L1_ffn_W2, L1_ffn_b2)
    x = x + _L2_attn_ref(_layernorm(x, axis=-1))
    x = x + _L2_ffn_ref(_layernorm(x, axis=-1), L2_ffn_gate_w, L2_ffn_w1, L2_ffn_w2, L2_ffn_w3)
    x = x + _L3_attn_ref(_layernorm(x, axis=-1), L3_attn_Wq, L3_attn_Wk, L3_attn_Wv, L3_attn_Wb, L3_attn_conv_q_w, L3_attn_conv_k_w, L3_attn_conv_v_w, L3_attn_local_w, L3_attn_mid_w, L3_attn_r_w1, L3_attn_r_b1, L3_attn_r_w2, L3_attn_r_b2, L3_attn_mix_w, L3_attn_onorm_w, L3_attn_Wo)
    x = x + _L3_ffn_ref(_layernorm(x, axis=-1), L3_ffn_router_w, L3_ffn_router_b, L3_ffn_expert_w, L3_ffn_expert_b)
    return x

_drawn_inputs = setup_inputs


def setup_inputs(seed=0):
    import zlib

    import numpy as np

    out = dict(_drawn_inputs(seed))
    spreads = {'L0_ffn_b_expert': (0.0, 0.42),
     'L1_attn_dt_bias': (1.0, 0.6),
     'L1_attn_norm_w': (1.0, 0.2),
     'L1_ffn_q_scale': (1.0, 0.6),
     'L1_ffn_k_scale': (1.0, 0.6),
     'L1_ffn_ln_g': (1.0, 0.6),
     'L1_ffn_ln_b': (0.0, 0.585),
     'L1_ffn_b1': (0.0, 0.274),
     'L1_ffn_b2': (0.0, 0.1),
     'L3_attn_r_b1': (0.0, 0.8),
     'L3_attn_mix_w': (1.0, 0.2),
     'L3_attn_onorm_w': (1.0, 0.2),
     'L3_ffn_router_b': (0.0, 0.8),
     'L3_ffn_expert_b': (0.0, 0.8)}
    factors = {'L0_ffn_w_gate': 5.573,
     'L1_attn_b_w': 6.808,
     'L1_attn_a_w': 8.0,
     'L1_attn_A_log': 6.114,
     'L3_ffn_router_w': 4.64,
     'L3_ffn_expert_w': 4.653}
    for name, (base, spread) in spreads.items():
        noise = np.random.default_rng([zlib.crc32(name.encode()), seed]).standard_normal(out[name].shape)
        drawn = base * np.exp(spread * noise) if base else spread * noise
        out[name] = jnp.asarray(drawn.astype(out[name].dtype))
    for name, factor in factors.items():
        out[name] = (out[name] * factor).astype(out[name].dtype)
    return out
```

```python
from contextlib import ExitStack

import numpy as np

import concourse.bass as bass
from concourse import mybir

F32 = mybir.dt.float32
U32 = mybir.dt.uint32
ACT = mybir.ActivationFunctionType
ALU = mybir.AluOpType
AX = mybir.AxisListType
ds = bass.ds

P = 128
BATCH = 4
BLOCKS = 8
TILES = BATCH * BLOCKS
SEQ = BLOCKS * P
G = 4
LN_EPS = 1e-5
NEG = -1e30


class Stage:

    def __init__(self, nc, name):
        self.nc, self.name, self.ctx = nc, name, ExitStack()

    def __enter__(self):
        self.ctx.__enter__()
        return self

    def __exit__(self, *exc):
        return self.ctx.__exit__(*exc)

    def sb(self, name, shape, dt=F32):
        return self.ctx.enter_context(self.nc.sbuf_tensor(f"{self.name}_{name}", shape, dt))

    def ps(self, name, shape=(P, 512)):
        return self.ctx.enter_context(self.nc.psum_tensor(f"{self.name}_{name}", list(shape), F32))

    def sems(self, names):
        made = {n: self.ctx.enter_context(self.nc.semaphore(f"{self.name}_{n}")) for n in names.split()}
        nums = sorted(sem.num for sem in made.values())
        starts = [n for n in nums if n - 1 not in nums]
        ends = [n + 1 for n in nums if n + 1 not in nums]
        self.ranges = [range(a, b) for a, b in zip(starts, ends)]
        return made

    def end_step(self):
        for r in self.ranges:
            self.nc.gpsimd.sem_clear(r)
        self.nc.all_engine_barrier(sem_only=True)


class Constants:

    def __init__(self, table):
        self.all = table
        (self.ident, self.ones, self.upto, self.after, self.strict, self.neg_upper,
         self.head_blocks) = (table[:, k * P:(k + 1) * P] for k in range(len(SQUARES)))
        self.count8 = table[:, len(SQUARES) * P:]


class Chain:

    def __init__(self, engine, sem):
        self.engine, self.sem, self.n = engine, sem, 0

    def __call__(self, ins):
        self.n += 1
        ins.then_inc(self.sem, 1)
        self.engine.wait_ge(self.sem, self.n)


def tile(X, i):
    return X[:, ds(i, 1), :].rearrange("p a d -> p (a d)")


def flat(ap):
    return ap.rearrange("p a d -> p (a d)")


def spread(ap, n):
    return ap.unsqueeze(2).broadcast_to([ap.shape[0], ap.shape[1], n])


def load_stage(nc, X, x, consts, c):
    with Stage(nc, "load") as st:
        s = st.sems("loaded")
        with nc.Block(no_gpsimd_drain=True) as block:
            @block.sync
            def _(sp):
                sp.dma_start(X[:], x.rearrange("b (t p) d -> p (b t) d", p=P)).then_inc(s["loaded"], 16)
                sp.dma_start(c.all[:], consts).then_inc(s["loaded"], 16)
                sp.wait_ge(s["loaded"], 32)
        st.end_step()


def layernorm_stage(nc, X, XN, XNT, c):
    with Stage(nc, f"ln{nc.next_id()}") as st:
        stats = st.sb("stats", [P, G, 6])
        mv = st.sb("mv", [P, G, 2])
        var = st.sb("var", [P, G])
        std = st.sb("std", [P, G])
        rstd = st.sb("rstd", [P, G])
        xs = st.sb("xs", [P, G, P])
        turned = st.ps("turned")
        s = st.sems("var_ready std_ready xs_ready turned_ready xnt_done xn_done chain")
        with nc.Fori(0, TILES // G) as i:
            with nc.Block(no_gpsimd_drain=True) as block:
                @block.vector
                def _(v):
                    step = Chain(v, s["chain"])
                    for j in range(G):
                        last = v.bn_stats(stats[:, j, :], tile(X, i * G + j))
                    step(last)
                    for j in range(G):
                        last = v.bn_aggr(mv[:, j, :], stats[:, j, :])
                    step(last)
                    v.tensor_scalar(var[:], mv[:, :, 1], LN_EPS, None, ALU.add).then_inc(s["var_ready"], 1)
                    v.wait_ge(s["std_ready"], 1)
                    step(v.reciprocal(rstd[:], std[:]))
                    for j in range(G):
                        last = v.tensor_scalar(xs[:, j, :], tile(X, i * G + j), mv[:, j, 0:1], rstd[:, j:j + 1],
                                               ALU.subtract, ALU.mult)
                    last.then_inc(s["xs_ready"], 1)

                @block.scalar
                def _(a):
                    a.wait_ge(s["var_ready"], 1)
                    a.activation(std[:], var[:], ACT.Sqrt).then_inc(s["std_ready"], 1)
                    a.wait_ge(s["turned_ready"], 1)
                    a.activation(XNT[:, ds(i * G * P, G * P)], turned[:], ACT.Copy).then_inc(s["xnt_done"], 1)
                    a.wait_ge(s["xnt_done"], 1)

                @block.tensor
                def _(pe):
                    pe.wait_ge(s["xs_ready"], 1)
                    for j in range(G):
                        last = pe.transpose(turned[:, j * P:(j + 1) * P], xs[:, j, :], c.ident)
                    last.then_inc(s["turned_ready"], 1)

                @block.gpsimd
                def _(g):
                    g.wait_ge(s["xs_ready"], 1)
                    g.tensor_copy(XN[:, ds(i * G, G), :], xs[:]).then_inc(s["xn_done"], 1)
                    g.wait_ge(s["xn_done"], 1)
            st.end_step()


def load_turned(nc, name, pairs, c):
    with Stage(nc, name) as st:
        raw = st.sb("raw", [P, len(pairs), P])
        turned = st.ps("turned", (P, 4, 512))
        s = st.sems("loaded turned_ready copied")
        with nc.Block(no_gpsimd_drain=True) as block:
            @block.sync
            def _(sp):
                for n, (dst, src) in enumerate(pairs):
                    a, b = src.shape
                    sp.dma_start(raw[0:a, n, 0:b], src).then_inc(s["loaded"], 16)

            @block.tensor
            def _(pe):
                pe.wait_ge(s["loaded"], 16 * len(pairs))
                for n, (dst, src) in enumerate(pairs):
                    a, b = src.shape
                    if n >= 4:
                        pe.wait_ge(s["copied"], n - 3)
                    pe.transpose(turned[0:b, n % 4, 0:a], raw[0:a, n, 0:b], c.ident[0:a, 0:a]).then_inc(s["turned_ready"], 1)

            @block.vector
            def _(v):
                for n, (dst, src) in enumerate(pairs):
                    a, b = src.shape
                    v.wait_ge(s["turned_ready"], n + 1)
                    v.tensor_copy(dst, turned[0:b, n % 4, 0:a]).then_inc(s["copied"], 1)
                v.wait_ge(s["copied"], len(pairs))
        st.end_step()


HEADS0 = 16
HD0 = P // HEADS0
AUG = HD0 + 1


def l0_attention_stage(nc, X, XNT, c, W_Q, W_K, W_V, W_O, alibi_rows, key_pos):
    with Stage(nc, "a0") as outer:
        WQT, WKT, WVT, WOT = (outer.sb(n, [P, P]) for n in ("WQT", "WKT", "WVT", "WOT"))
        load_turned(nc, "a0w", [(WQT[:], W_Q), (WKT[:], W_K), (WVT[:], W_V), (WOT[:], W_O)], c)
        slope_rows = outer.sb("slope_rows", [1, HEADS0, AUG])
        unit_row = outer.sb("unit_row", [1, AUG])
        pos = outer.sb("pos", [1, SEQ])
        ones = outer.sb("ones", [1, SEQ])
        V = outer.sb("V", [P, BLOCKS, P])
        O = outer.sb("O", [P, BLOCKS, P])
        xs = outer.sb("xs", [P, SEQ])
        wq = outer.sb("wq", [P, AUG])
        wk = outer.sb("wk", [P, AUG])
        with Stage(nc, "a0c") as st:
            s = st.sems("loaded")
            with nc.Block(no_gpsimd_drain=True) as block:
                @block.sync
                def _(sp):
                    sp.dma_start(slope_rows[:], alibi_rows[0:1, 0:HEADS0, :]).then_inc(s["loaded"], 16)
                    sp.dma_start(unit_row[:], alibi_rows[0:1, HEADS0, :]).then_inc(s["loaded"], 16)
                    sp.dma_start(pos[:], key_pos).then_inc(s["loaded"], 16)
                    sp.wait_ge(s["loaded"], 48)

                @block.vector
                def _(v):
                    v.memset(ones[:], 1.0)
                    v.memset(wq[:], 0.0)
                    v.memset(wk[:], 0.0)
            st.end_step()

        with nc.Fori(0, BATCH) as b:
            with Stage(nc, "a0v") as st:
                pv = st.ps("pv", (P, 2, 512))
                s = st.sems("xs_ready values copied")
                with nc.Block(no_gpsimd_drain=True) as block:
                    @block.scalar
                    def _(a):
                        a.activation(xs[:], XNT[:, ds(b * SEQ, SEQ)], ACT.Copy).then_inc(s["xs_ready"], 1)

                    @block.tensor
                    def _(pe):
                        pe.wait_ge(s["xs_ready"], 1)
                        for t in range(BLOCKS):
                            last = pe.matmul(pv[:, t // 4, (t % 4) * P:(t % 4 + 1) * P], xs[:, t * P:(t + 1) * P],
                                             WVT[:], start=True, stop=True)
                        last.then_inc(s["values"], 1)

                    @block.vector
                    def _(v):
                        v.wait_ge(s["values"], 1)
                        v.tensor_copy(flat(V[:]), flat(pv[:])).then_inc(s["copied"], 1)
                        v.wait_ge(s["copied"], 1)
                st.end_step()

            with Stage(nc, "a0h") as st:
                slope = st.sb("slope", [1, AUG])
                QA = st.sb("QA", [AUG, SEQ])
                KA = st.sb("KA", [AUG, SEQ])
                probs = st.sb("probs", [P, 2, SEQ])
                probsT = st.sb("probsT", [P, 2, SEQ])
                negmax = st.sb("negmax", [P, BLOCKS])
                total = st.sb("total", [P, BLOCKS])
                rtotal = st.sb("rtotal", [P, BLOCKS])
                scores = st.ps("scores", (P, 2, 2 * 512))
                turned = st.ps("turned", (P, 2 * 512))
                mix = st.ps("mix", (P, BLOCKS, HD0))
                s = st.sems("weights q_proj k_proj q_done k_done scores_ready max_ready probs_ready "
                            "turned_ready probsT_v probsT_a mixed out_done chain")
                with nc.Fori(0, HEADS0) as h:
                    with nc.Block(no_gpsimd_drain=True) as block:
                        @block.vector
                        def _(v):
                            v.tensor_copy(slope[:], slope_rows[0:1, ds(h, 1), :].rearrange("p a d -> p (a d)"))
                            v.tensor_scalar(wq[:, 0:HD0], WQT[:, ds(h * HD0, HD0)], HD0 ** -0.5, None, ALU.mult)
                            v.tensor_copy(wk[:, 0:HD0], WKT[:, ds(h * HD0, HD0)]).then_inc(s["weights"], 1)
                            v.wait_ge(s["q_proj"], 1)
                            v.tensor_copy(QA[:], scores[0:AUG, 0, :]).then_inc(s["q_done"], 1)

                            def row_max(t):
                                v.wait_ge(s["scores_ready"], t + 1)
                                v.tensor_reduce(negmax[:, t:t + 1], scores[:, t % 2, 0:(t + 1) * P], AX.X, ALU.max,
                                                negate=True).then_inc(s["max_ready"], 1)

                            row_max(0)
                            for t in range(BLOCKS):
                                if t + 1 < BLOCKS:
                                    row_max(t + 1)
                                n = min(512, (t + 1) * P)
                                v.wait_ge(s["turned_ready"], t + 1)
                                if t >= 2:
                                    v.wait_ge(s["mixed"], t - 1)
                                v.tensor_copy(probsT[:, t % 2, 0:n], turned[:, 0:n]).then_inc(s["probsT_v"], 1)
                            v.wait_ge(s["probs_ready"], BLOCKS)
                            v.reciprocal(rtotal[:], total[:]).then_inc(s["chain"], 1)
                            v.wait_ge(s["chain"], 1)
                            v.wait_ge(s["mixed"], BLOCKS)
                            v.tensor_tensor(O[:, :, ds(h * HD0, HD0)], mix[:], spread(rtotal[:], HD0),
                                            ALU.mult).then_inc(s["out_done"], 1)
                            v.wait_ge(s["out_done"], 1)

                        @block.scalar
                        def _(a):
                            a.wait_ge(s["k_proj"], 1)
                            a.activation(KA[:], scores[0:AUG, 1, :], ACT.Copy).then_inc(s["k_done"], 1)

                            def exps(t):
                                a.wait_ge(s["max_ready"], t + 1)
                                if t >= 2:
                                    a.wait_ge(s["turned_ready"], t - 1)
                                a.activation(probs[:, t % 2, 0:(t + 1) * P], scores[:, t % 2, 0:(t + 1) * P], ACT.Exp,
                                             bias=negmax[:, t:t + 1],
                                             accum_out=total[:, t:t + 1]).then_inc(s["probs_ready"], 1)

                            exps(0)
                            for t in range(BLOCKS):
                                if t + 1 < BLOCKS:
                                    exps(t + 1)
                                n = (t + 1) * P
                                if n > 512:
                                    a.wait_ge(s["turned_ready"], t + 1)
                                    a.wait_ge(s["mixed"], t - 1)
                                    a.activation(probsT[:, t % 2, 512:n], turned[:, 512:n],
                                                 ACT.Copy).then_inc(s["probsT_a"], 1)

                        @block.tensor
                        def _(pe):
                            pe.wait_ge(s["weights"], 1)
                            for w, extra, src, half, done in ((wq, unit_row, ones, 0, s["q_proj"]),
                                                              (wk, slope, pos, 1, s["k_proj"])):
                                for k in range(2):
                                    o = scores[0:AUG, half, k * 512:(k + 1) * 512]
                                    pe.matmul(o, w[:], xs[:, k * 512:(k + 1) * 512], start=True, stop=False)
                                    last = pe.matmul(o, extra[:], src[:, k * 512:(k + 1) * 512], start=False, stop=True)
                                last.then_inc(done, 1)

                            def score(t):
                                if t >= 2:
                                    pe.wait_ge(s["probs_ready"], t - 1)
                                n = (t + 1) * P
                                for k0 in range(0, n, 512):
                                    k1 = min(n, k0 + 512)
                                    diag = k1 == n
                                    last = pe.matmul(scores[:, t % 2, k0:k1], QA[:, t * P:(t + 1) * P], KA[:, k0:k1],
                                                     start=True, stop=not diag)
                                    if diag:
                                        last = pe.matmul(scores[:, t % 2, n - P:n], c.ident, c.neg_upper,
                                                         start=False, stop=True)
                                last.then_inc(s["scores_ready"], 1)

                            pe.wait_ge(s["q_done"], 1)
                            pe.wait_ge(s["k_done"], 1)
                            score(0)
                            for t in range(BLOCKS):
                                if t + 1 < BLOCKS:
                                    score(t + 1)
                                pe.wait_ge(s["probs_ready"], t + 1)
                                if t >= 1:
                                    pe.wait_ge(s["probsT_v"], t)
                                if t > 4:
                                    pe.wait_ge(s["probsT_a"], t - 4)
                                for k in range(t + 1):
                                    last = pe.transpose(turned[:, k * P:(k + 1) * P],
                                                        probs[:, t % 2, k * P:(k + 1) * P], c.ident)
                                last.then_inc(s["turned_ready"], 1)
                                pe.wait_ge(s["probsT_v"], t + 1)
                                if t >= 4:
                                    pe.wait_ge(s["probsT_a"], t - 3)
                                for k in range(t + 1):
                                    last = pe.matmul(mix[:, t, :], probsT[:, t % 2, k * P:(k + 1) * P],
                                                     V[:, k, ds(h * HD0, HD0)], start=(k == 0), stop=(k == t))
                                last.then_inc(s["mixed"], 1)
                    st.end_step()

            with Stage(nc, "a0o") as st:
                OT = st.sb("OT", [P, SEQ])
                turned = st.ps("turned", (P, 2 * 512))
                out = st.ps("out", (P, BLOCKS, P))
                s = st.sems("turned_ready copied out_ready added")
                with nc.Block(no_gpsimd_drain=True) as block:
                    @block.tensor
                    def _(pe):
                        for t in range(BLOCKS):
                            last = pe.transpose(turned[:, t * P:(t + 1) * P], O[:, t, :], c.ident)
                        last.then_inc(s["turned_ready"], 1)
                        pe.wait_ge(s["copied"], 1)
                        for t in range(BLOCKS):
                            last = pe.matmul(out[:, t, :], OT[:, t * P:(t + 1) * P], WOT[:], start=True, stop=True)
                        last.then_inc(s["out_ready"], 1)

                    @block.scalar
                    def _(a):
                        a.wait_ge(s["turned_ready"], 1)
                        a.activation(OT[:], turned[:], ACT.Copy).then_inc(s["copied"], 1)

                    @block.vector
                    def _(v):
                        v.wait_ge(s["out_ready"], 1)
                        v.tensor_tensor(X[:, ds(b * BLOCKS, BLOCKS), :], out[:], X[:, ds(b * BLOCKS, BLOCKS), :],
                                        ALU.add).then_inc(s["added"], 1)
                        v.wait_ge(s["added"], 1)
                st.end_step()


EXPERTS = 8
CAPACITY = 100


def l0_ffn_stage(nc, X, XNT, c, w_gate, w_expert, b_expert):
    with Stage(nc, "f0") as outer:
        wg = outer.sb("wg", [P, EXPERTS])
        we = outer.sb("we", [P, P])
        bias = outer.sb("bias", [1, P])
        seen = outer.sb("seen", [P, EXPERTS])
        with Stage(nc, "f0w") as st:
            s = st.sems("loaded")
            with nc.Block(no_gpsimd_drain=True) as block:
                @block.sync
                def _(sp):
                    sp.dma_start(wg[:], w_gate).then_inc(s["loaded"], 16)
                    sp.dma_start(we[:], w_expert).then_inc(s["loaded"], 16)
                    sp.dma_start(bias[:], b_expert.rearrange("(a d) -> a d", a=1)).then_inc(s["loaded"], 16)
                    sp.wait_ge(s["loaded"], 48)

                @block.vector
                def _(v):
                    v.memset(seen[:], 0.0)
            st.end_step()
        with Stage(nc, "f0s") as st:
            xs = st.sb("xs", [P, G * P])
            lg = st.sb("lg", [P, G, EXPERTS])
            top = st.sb("top", [P, G, 8])
            at = st.sb("at", [P, G, 8], U32)
            atf = st.sb("atf", [P, G, 8])
            choice = st.sb("choice", [P, G, EXPERTS])
            ex = st.sb("ex", [P, G, EXPERTS])
            kept = st.sb("kept", [P, G, EXPERTS])
            total, gate, keep = (st.sb(n, [P, G]) for n in ("total", "gate", "keep"))
            add = st.sb("add", [P, EXPERTS])
            logits = st.ps("logits", (P, G, EXPERTS))
            place = st.ps("place", (P, G, EXPERTS))
            y = st.ps("y", (P, G, P))
            s = st.sems("xs_ready logits_ready y_ready chosen shifted exps place_ready added chain")
            with nc.Fori(0, TILES // G) as i:
                with nc.Block(no_gpsimd_drain=True) as block:
                    @block.scalar
                    def _(a):
                        a.activation(xs[:], XNT[:, ds(i * G * P, G * P)], ACT.Copy).then_inc(s["xs_ready"], 1)
                        a.wait_ge(s["shifted"], 1)
                        a.activation(ex[:], ex[:], ACT.Exp).then_inc(s["exps"], 1)

                    @block.tensor
                    def _(pe):
                        pe.wait_ge(s["xs_ready"], 1)
                        for j in range(G):
                            last = pe.matmul(logits[:, j, :], xs[:, j * P:(j + 1) * P], wg[:], start=True, stop=True)
                        last.then_inc(s["logits_ready"], 1)
                        for j in range(G):
                            pe.matmul(y[:, j, :], xs[:, j * P:(j + 1) * P], we[:], start=True, stop=False)
                            last = pe.matmul(y[:, j, :], c.ones[0:1, :], bias[:], start=False, stop=True)
                        last.then_inc(s["y_ready"], 1)
                        pe.wait_ge(s["chosen"], 1)
                        for j in range(G):
                            pe.matmul(place[:, j, :], c.upto, choice[:, j, :], start=True, stop=False)
                            for k in range(j):
                                pe.matmul(place[:, j, :], c.ones, choice[:, k, :], start=False, stop=False)
                            last = pe.matmul(place[:, j, :], c.ones, seen[:], start=False, stop=True)
                        last.then_inc(s["place_ready"], 1)

                    @block.vector
                    def _(v):
                        step = Chain(v, s["chain"])
                        v.wait_ge(s["logits_ready"], 1)
                        step(v.tensor_copy(lg[:], logits[:]))
                        for j in range(G):
                            last = v.max(top[:, j, :], lg[:, j, :])
                        step(last)
                        v.tensor_tensor(ex[:], lg[:], top[:, :, 0:1].broadcast_to([P, G, EXPERTS]),
                                        ALU.subtract).then_inc(s["shifted"], 1)
                        for j in range(G):
                            last = v.max_index(at[:, j, :], top[:, j, :], lg[:, j, :])
                        step(last)
                        step(v.tensor_copy(atf[:], at[:]))
                        for j in range(G):
                            last = v.tensor_scalar(choice[:, j, :], c.count8, atf[:, j, 0:1], None, ALU.is_equal)
                        last.then_inc(s["chosen"], 1)
                        v.wait_ge(s["exps"], 1)
                        step(v.tensor_reduce(total[:], ex[:], AX.X, ALU.add))
                        step(v.reciprocal(gate[:], total[:]))
                        v.wait_ge(s["place_ready"], 1)
                        step(v.scalar_tensor_tensor(out=kept[:], in0=place[:], scalar=float(CAPACITY), in1=choice[:],
                                                    op0=ALU.is_le, op1=ALU.mult))
                        v.tensor_reduce(keep[:], kept[:], AX.X, ALU.add)
                        step(v.tensor_reduce(add[:], choice[:].rearrange("p j e -> p e j"), AX.X, ALU.add))
                        v.tensor_tensor(seen[:], seen[:], add[:], ALU.add)
                        step(v.tensor_tensor(gate[:], gate[:], keep[:], ALU.mult))
                        v.wait_ge(s["y_ready"], 1)
                        for j in range(G):
                            last = v.scalar_tensor_tensor(out=tile(X, i * G + j), in0=y[:, j, :],
                                                          scalar=gate[:, j:j + 1], in1=tile(X, i * G + j),
                                                          op0=ALU.mult, op1=ALU.add)
                        last.then_inc(s["added"], 1)
                        v.wait_ge(s["added"], 1)
                st.end_step()


HEADS1 = 8
TAPS = 4
RMS_EPS = 1e-6
LEVELS = [1, 2, 4, 8, 16, 32, 64]


def l1_gates_stage(nc, XNT, c, a_b_wT, dt_row, alog_row, g_all, beta_all):
    H = HEADS1
    with Stage(nc, "g1") as outer:
        rate = outer.sb("rate", [P, 1, H])
        with Stage(nc, "g1r") as st:
            pr = st.ps("pr", (P, H))
            s = st.sems("row_ready exp_ready done")
            with nc.Block(no_gpsimd_drain=True) as block:
                @block.tensor
                def _(pe):
                    pe.matmul(pr[:], c.ones[0:1, :], alog_row, start=True, stop=True).then_inc(s["row_ready"], 1)

                @block.scalar
                def _(a):
                    a.wait_ge(s["row_ready"], 1)
                    a.activation(rate[:, 0, :], pr[:], ACT.Exp).then_inc(s["exp_ready"], 1)

                @block.vector
                def _(v):
                    v.wait_ge(s["exp_ready"], 1)
                    v.tensor_scalar(rate[:], rate[:], -1.0, None, ALU.mult).then_inc(s["done"], 1)
                    v.wait_ge(s["done"], 1)
            st.end_step()
        with Stage(nc, "g1s") as st:
            xs = st.sb("xs", [P, G * P])
            th, mag, relu = (st.sb(n, [P, G, H]) for n in ("th", "mag", "relu"))
            pa = st.ps("pa", (P, G, H))
            pb = st.ps("pb", (P, G, H))
            s = st.sems("xs_ready a_ready b_ready th_ready mag_ready soft_ready done chain act_chain")
            with nc.Fori(0, TILES // G) as i:
                with nc.Block(no_gpsimd_drain=True) as block:
                    @block.scalar
                    def _(a):
                        a.activation(xs[:], XNT[:, ds(i * G * P, G * P)], ACT.Copy).then_inc(s["xs_ready"], 1)
                        step = Chain(a, s["act_chain"])
                        a.wait_ge(s["b_ready"], 1)
                        a.activation(th[:], pb[:], ACT.Tanh, scale=0.5).then_inc(s["th_ready"], 1)
                        a.wait_ge(s["mag_ready"], 1)
                        step(a.activation(mag[:], mag[:], ACT.Exp, scale=-1.0))
                        a.activation(mag[:], mag[:], ACT.Ln, bias=1.0).then_inc(s["soft_ready"], 1)

                    @block.tensor
                    def _(pe):
                        pe.wait_ge(s["xs_ready"], 1)
                        for j in range(G):
                            last = pe.matmul(pb[:, j, :], xs[:, j * P:(j + 1) * P], a_b_wT[:, H:2 * H], start=True, stop=True)
                        last.then_inc(s["b_ready"], 1)
                        for j in range(G):
                            pe.matmul(pa[:, j, :], xs[:, j * P:(j + 1) * P], a_b_wT[:, 0:H], start=True, stop=False)
                            last = pe.matmul(pa[:, j, :], c.ones[0:1, :], dt_row, start=False, stop=True)
                        last.then_inc(s["a_ready"], 1)

                    @block.vector
                    def _(v):
                        step = Chain(v, s["chain"])
                        v.wait_ge(s["a_ready"], 1)
                        step(v.tensor_scalar(relu[:], pa[:], 0.0, None, ALU.max))
                        v.scalar_tensor_tensor(out=mag[:], in0=relu[:], scalar=2.0, in1=pa[:], op0=ALU.mult,
                                               op1=ALU.subtract).then_inc(s["mag_ready"], 1)
                        v.wait_ge(s["th_ready"], 1)
                        step(v.tensor_scalar(beta_all[:, ds(i * G, G), :], th[:], 0.5, 0.5, ALU.mult, ALU.add))
                        v.wait_ge(s["soft_ready"], 1)
                        step(v.tensor_tensor(relu[:], relu[:], mag[:], ALU.add))
                        v.tensor_tensor(g_all[:, ds(i * G, G), :], relu[:], rate[:].broadcast_to([P, G, H]),
                                        ALU.mult).then_inc(s["done"], 1)
                        v.wait_ge(s["done"], 1)
                st.end_step()


def l1_attention_stage(nc, X, XNT, c, d):
    H = HEADS1
    xnt4 = XNT[:].rearrange("p (b s) -> p b s", b=BATCH)
    with Stage(nc, "a1") as outer:
        abT = outer.sb("abT", [P, 2 * H])
        load_turned(nc, "a1t", [(abT[:, 0:H], d["L1_attn_a_w"]), (abT[:, H:2 * H], d["L1_attn_b_w"])], c)
        g_all = outer.sb("g_all", [P, TILES, H])
        beta_all = outer.sb("beta_all", [P, TILES, H])
        rows = outer.sb("rows", [1, 2 * H + P])
        norm_w = outer.sb("norm_w", [P, 1, P])
        masks = outer.sb("masks", [P, len(LEVELS), P])
        with Stage(nc, "a1c") as st:
            pn = st.ps("pn", (P, P))
            s = st.sems("loaded row_ready done")
            with nc.Block(no_gpsimd_drain=True) as block:
                @block.sync
                def _(sp):
                    sp.dma_start(rows[:, 0:H], d["L1_attn_dt_bias"].rearrange("(a d) -> a d", a=1)).then_inc(s["loaded"], 16)
                    sp.dma_start(rows[:, H:2 * H], d["L1_attn_A_log"].rearrange("(a d) -> a d", a=1)).then_inc(s["loaded"], 16)
                    sp.dma_start(rows[:, 2 * H:], d["L1_attn_norm_w"].rearrange("(a d) -> a d", a=1)).then_inc(s["loaded"], 16)
                    sp.dma_start(masks[:], d["const_level_masks"]).then_inc(s["loaded"], 16)
                    sp.wait_ge(s["loaded"], 64)

                @block.tensor
                def _(pe):
                    pe.wait_ge(s["loaded"], 64)
                    pe.matmul(pn[:], c.ones[0:1, :], rows[:, 2 * H:], start=True, stop=True).then_inc(s["row_ready"], 1)

                @block.vector
                def _(v):
                    v.wait_ge(s["row_ready"], 1)
                    v.tensor_scalar(norm_w[:, 0, :], pn[:], 0.5, None, ALU.mult).then_inc(s["done"], 1)
                    v.wait_ge(s["done"], 1)
            st.end_step()
        l1_gates_stage(nc, XNT, c, abT, rows[:, 0:H], rows[:, H:2 * H], g_all, beta_all)

        wT = outer.sb("wT", [P, 5, P])
        raw_w = outer.sb("raw_w", [P, 5, P])
        taps = outer.sb("taps", [P, 3, TAPS])
        S = outer.sb("S", [P, G, P])
        hist = outer.sb("hist", [P, 3, G, P + TAPS - 1])
        gh = outer.sb("gh", [P, TILES])
        bh = outer.sb("bh", [P, TILES])
        with nc.Fori(0, H) as h:
            with Stage(nc, "a1h") as st:
                turned = st.ps("turned", (P, 5, 512))
                s = st.sems("loaded turned_ready copied zeroed")
                with nc.Block(no_gpsimd_drain=True) as block:
                    @block.sync
                    def _(sp):
                        for n in range(3):
                            sp.dma_start(raw_w[:, n, :], d["L1_attn_qkv_w"][ds(h * P + n * H * P, P), :]).then_inc(s["loaded"], 16)
                            sp.dma_start(taps[:, n, :], d["L1_attn_conv_w"][ds(h * P + n * H * P, P), :, :]
                                         .rearrange("p a t -> p (a t)")).then_inc(s["loaded"], 16)
                        sp.dma_start(raw_w[:, 3, :], d["L1_attn_z_w"][ds(h * P, P), :]).then_inc(s["loaded"], 16)
                        sp.dma_start(raw_w[:, 4, :], d["L1_attn_out_w"][:, ds(h * P, P)]).then_inc(s["loaded"], 16)
                        sp.wait_ge(s["loaded"], 8 * 16)

                    @block.tensor
                    def _(pe):
                        pe.wait_ge(s["loaded"], 8 * 16)
                        for n in range(5):
                            pe.transpose(turned[:, n, 0:P], raw_w[:, n, :], c.ident).then_inc(s["turned_ready"], 1)

                    @block.vector
                    def _(v):
                        v.memset(S[:], 0.0)
                        v.memset(hist[:, :, :, 0:TAPS - 1], 0.0)
                        v.tensor_copy(gh[:], g_all[:, :, ds(h, 1)].rearrange("p t a -> p (t a)"))
                        v.tensor_copy(bh[:], beta_all[:, :, ds(h, 1)].rearrange("p t a -> p (t a)"))
                        for n in range(5):
                            v.wait_ge(s["turned_ready"], n + 1)
                            v.tensor_copy(wT[:, n, :], turned[:, n, 0:P]).then_inc(s["copied"], 1)
                        v.wait_ge(s["copied"], 5)
                st.end_step()
            with Stage(nc, "a1s") as st:
                delta_chunk_steps(nc, st, X, xnt4, c, wT, taps, S, hist, gh, bh, masks, norm_w)


def delta_chunk_steps(nc, st, X, xnt4, c, wT, taps, S, hist, gh, bh, masks, norm_w):
    four = [P, G, P]
    gcol, bcol, nbeta, msq, std, rstd = (st.sb(n, [P, G]) for n in ("gcol", "bcol", "nbeta", "msq", "std", "rstd"))
    decays = st.sb("decays", [P, 3, G])
    ga, E, Eincl, Estrict = (st.sb(n, four) for n in ("ga", "E", "Eincl", "Estrict"))
    xs, conv, ktok, vtok = st.sb("xs", four), st.sb("conv", [P, 3, G, P]), st.sb("ktok", four), st.sb("vtok", four)
    N, Nlev, AT = st.sb("N", four), st.sb("Nlev", [P, len(LEVELS), G, P]), st.sb("AT", four)
    T, XT, Zt, R, kS, u, uend = (st.sb(n, four) for n in ("T", "XT", "Zt", "R", "kS", "u", "uend"))
    o, osq, gatez, y, yT, newS = (st.sb(n, four) for n in ("o", "osq", "gatez", "y", "yT", "newS"))
    bank = [st.ps(f"bank{n}", (P, G, P)) for n in range(8)]
    s = st.sems("xs_ready cols_ready ga_ready raw_ready raw_copied conv_ready sums_ready dt_ready decays_ready "
                "E_ready masks_ready z_ready gatez_ready ktok_ps vtok_ps ktok_ready vtok_ready gram_ready N_ready "
                "Nlev_ready qk_ready AT_ready kS_ready qS_ready R_ready qS_used zt_ps zt_ready t_ps t_ready x_ps "
                "x_ready u_ps u_ready uend_ready o_ps o_used s_ps s_used msq_ready std_ready y_ready yT_ps yT_ready "
                "out_ps added chain")
    K = len(LEVELS)
    with nc.Fori(0, BLOCKS) as ch:
        with nc.Block(no_gpsimd_drain=True) as block:
            @block.tensor
            def _(pe):
                def four_of(out, lhs, rhs, sem):
                    for b in range(G):
                        last = pe.matmul(out[:, b, :], lhs(b), rhs(b), start=True, stop=True)
                    last.then_inc(sem, 1)

                for n in range(3):
                    pe.matmul(flat(bank[n][:]), wT[:, n, :], xnt4[:, :, ds(ch * P, P)],
                              start=True, stop=True).then_inc(s["raw_ready"], 1)
                pe.wait_ge(s["cols_ready"], 1)
                for n, m in enumerate((c.upto, c.after, c.ones)):
                    last = pe.matmul(bank[4][:, 0, n * G:(n + 1) * G], m, gcol[:], start=True, stop=True)
                last.then_inc(s["sums_ready"], 1)
                pe.wait_ge(s["ga_ready"], 1)
                four_of(bank[3], lambda b: ga[:, b, :], lambda b: c.upto, s["dt_ready"])
                pe.wait_ge(s["xs_ready"], 1)
                four_of(bank[7], lambda b: xs[:, b, :], lambda b: wT[:, 3, :], s["z_ready"])
                pe.wait_ge(s["conv_ready"], 1)
                for b in range(G):
                    last = pe.transpose(bank[5][:, b, :], conv[:, 1, b, :], c.ident)
                last.then_inc(s["ktok_ps"], 1)
                four_of(bank[6], lambda b: conv[:, 1, b, :], lambda b: conv[:, 1, b, :], s["gram_ready"])
                pe.wait_ge(s["conv_ready"], 2)
                pe.wait_ge(s["raw_copied"], 3)
                four_of(bank[0], lambda b: conv[:, 1, b, :], lambda b: conv[:, 0, b, :], s["qk_ready"])
                four_of(bank[2], lambda b: conv[:, 1, b, :], lambda b: S[:, b, :], s["kS_ready"])
                pe.wait_ge(s["E_ready"], 1)
                four_of(bank[3], lambda b: conv[:, 0, b, :], lambda b: S[:, b, :], s["qS_ready"])
                pe.wait_ge(s["conv_ready"], 3)
                for b in range(G):
                    last = pe.transpose(bank[1][:, b, :], conv[:, 2, b, :], c.ident)
                last.then_inc(s["vtok_ps"], 1)
                pe.wait_ge(s["ktok_ready"], 1)
                pe.wait_ge(s["N_ready"], 1)
                pe.wait_ge(s["AT_ready"], 1)
                for k in range(K):
                    pe.wait_ge(s["Nlev_ready"], k + 1)
                    if k >= 1:
                        pe.wait_ge(s["t_ready"], k)
                    four_of(bank[5], lambda b: Nlev[:, k, b, :], lambda b: c.ident if k == 0 else T[:, b, :], s["zt_ps"])
                    if k >= 1:
                        pe.wait_ge(s["zt_ready"], k)
                        pe.wait_ge(s["x_ready"], k)
                        if k < K - 1:
                            four_of(bank[6], lambda b: XT[:, b, :], lambda b: Zt[:, b, :], s["t_ps"])
                        four_of(bank[0], lambda b: Zt[:, b, :], lambda b: XT[:, b, :], s["x_ps"])
                pe.wait_ge(s["x_ready"], K)
                pe.wait_ge(s["R_ready"], 1)
                pe.wait_ge(s["vtok_ready"], 1)
                four_of(bank[1], lambda b: XT[:, b, :], lambda b: R[:, b, :], s["u_ps"])
                pe.wait_ge(s["u_ready"], 1)
                pe.wait_ge(s["decays_ready"], 1)
                four_of(bank[4], lambda b: AT[:, b, :], lambda b: u[:, b, :], s["o_ps"])
                pe.wait_ge(s["uend_ready"], 1)
                four_of(bank[6], lambda b: ktok[:, b, :], lambda b: uend[:, b, :], s["s_ps"])
                pe.wait_ge(s["y_ready"], 1)
                for b in range(G):
                    last = pe.transpose(bank[5][:, b, :], y[:, b, :], c.ident)
                last.then_inc(s["yT_ps"], 1)
                pe.wait_ge(s["yT_ready"], 1)
                four_of(bank[0], lambda b: yT[:, b, :], lambda b: wT[:, 4, :], s["out_ps"])

            @block.scalar
            def _(a):
                for n in (1, 0, 2):
                    a.wait_ge(s["raw_ready"], n + 1)
                    a.activation(hist[:, n, :, TAPS - 1:], bank[n][:], ACT.Copy).then_inc(s["raw_copied"], 1)
                a.wait_ge(s["sums_ready"], 1)
                a.activation(decays[:].rearrange("p n b -> p (n b)"), bank[4][:, 0, 0:3 * G], ACT.Exp).then_inc(s["decays_ready"], 1)
                a.wait_ge(s["dt_ready"], 1)
                a.activation(E[:], bank[3][:], ACT.Exp).then_inc(s["E_ready"], 1)
                a.wait_ge(s["z_ready"], 1)
                a.activation(gatez[:], bank[7][:], ACT.Tanh, scale=0.5).then_inc(s["gatez_ready"], 1)
                a.wait_ge(s["ktok_ps"], 1)
                a.activation(ktok[:], bank[5][:], ACT.Copy).then_inc(s["ktok_ready"], 1)
                a.wait_ge(s["vtok_ps"], 1)
                a.activation(vtok[:], bank[1][:], ACT.Copy).then_inc(s["vtok_ready"], 1)
                for k in range(1, K):
                    a.wait_ge(s["zt_ps"], k + 1)
                    if k >= 2:
                        a.wait_ge(s["x_ps"], k - 1)
                    a.activation(Zt[:], bank[5][:], ACT.Copy).then_inc(s["zt_ready"], 1)
                a.wait_ge(s["msq_ready"], 1)
                a.activation(std[:], msq[:], ACT.Sqrt).then_inc(s["std_ready"], 1)
                a.wait_ge(s["yT_ps"], 1)
                a.activation(yT[:], bank[5][:], ACT.Copy).then_inc(s["yT_ready"], 1)

            @block.gpsimd
            def _(g):
                g.tensor_copy(xs[:], xnt4[:, :, ds(ch * P, P)]).then_inc(s["xs_ready"], 1)
                g.wait_ge(s["E_ready"], 1)
                g.tensor_tensor(Eincl[:], E[:], c.upto.unsqueeze(1).broadcast_to(four), ALU.mult)
                g.tensor_tensor(Estrict[:], E[:], c.strict.unsqueeze(1).broadcast_to(four), ALU.mult).then_inc(s["masks_ready"], 1)
                g.wait_ge(s["N_ready"], 1)
                for k in range(K):
                    g.tensor_tensor(Nlev[:, k], N[:], masks[:, k:k + 1, :].broadcast_to(four), ALU.mult).then_inc(s["Nlev_ready"], 1)

            @block.vector
            def _(v):
                step = Chain(v, s["chain"])
                v.tensor_copy(bcol[:], bh[:].rearrange("p (b t) -> p b t", b=G)[:, :, ds(ch, 1)].rearrange("p b a -> p (b a)"))
                v.tensor_copy(gcol[:], gh[:].rearrange("p (b t) -> p b t", b=G)[:, :, ds(ch, 1)]
                              .rearrange("p b a -> p (b a)")).then_inc(s["cols_ready"], 1)
                v.wait_ge(s["cols_ready"], 1)
                v.tensor_tensor(ga[:], c.after.unsqueeze(1).broadcast_to(four), spread(gcol[:], P), ALU.mult).then_inc(s["ga_ready"], 1)
                step(v.tensor_scalar(nbeta[:], bcol[:], -1.0, None, ALU.mult))
                for at, n in enumerate((1, 0, 2)):
                    v.wait_ge(s["raw_copied"], at + 1)
                    step(v.tensor_scalar(conv[:, n], hist[:, n, :, TAPS - 1:], taps[:, n, TAPS - 1:TAPS], None, ALU.mult))
                    for k in range(TAPS - 1):
                        last = v.scalar_tensor_tensor(out=conv[:, n], in0=hist[:, n, :, k:k + P], scalar=taps[:, n, k:k + 1],
                                                      in1=conv[:, n], op0=ALU.mult, op1=ALU.add)
                        if k < TAPS - 2:
                            step(last)
                    last.then_inc(s["conv_ready"], 1)
                v.wait_ge(s["conv_ready"], 3)
                v.tensor_copy(hist[:, :, :, 0:TAPS - 1], hist[:, :, :, P:P + TAPS - 1])
                v.wait_ge(s["masks_ready"], 1)
                v.wait_ge(s["gram_ready"], 1)
                step(v.tensor_tensor(N[:], bank[6][:], Estrict[:], ALU.mult))
                v.tensor_tensor(N[:], N[:], spread(nbeta[:], P), ALU.mult).then_inc(s["N_ready"], 1)
                v.wait_ge(s["qk_ready"], 1)
                v.tensor_tensor(AT[:], bank[0][:], Eincl[:], ALU.mult).then_inc(s["AT_ready"], 1)
                idn = c.ident.unsqueeze(1).broadcast_to(four)
                v.wait_ge(s["zt_ps"], 1)
                v.tensor_tensor(T[:], bank[5][:], idn, ALU.add).then_inc(s["t_ready"], 1)
                v.wait_ge(s["Nlev_ready"], 1)
                v.tensor_tensor(XT[:], Nlev[:, 0], idn, ALU.add).then_inc(s["x_ready"], 1)
                for k in range(1, K):
                    if k < K - 1:
                        v.wait_ge(s["t_ready"], k)
                        v.wait_ge(s["t_ps"], k)
                        v.tensor_tensor(T[:], bank[6][:], T[:], ALU.add).then_inc(s["t_ready"], 1)
                    v.wait_ge(s["x_ready"], k)
                    v.wait_ge(s["x_ps"], k)
                    v.tensor_tensor(XT[:], bank[0][:], XT[:], ALU.add).then_inc(s["x_ready"], 1)
                    if k == 1:
                        v.wait_ge(s["kS_ready"], 1)
                        v.wait_ge(s["decays_ready"], 1)
                        step(v.tensor_tensor(kS[:], bank[2][:], spread(decays[:, 0, :], P), ALU.mult))
                        v.wait_ge(s["vtok_ready"], 1)
                        v.tensor_tensor(R[:], vtok[:], kS[:], ALU.subtract).then_inc(s["R_ready"], 1)
                    if k == 2:
                        v.wait_ge(s["qS_ready"], 1)
                        step(v.tensor_tensor(o[:], bank[3][:], spread(decays[:, 0, :], P), ALU.mult))
                        step(v.tensor_tensor(newS[:], S[:], spread(decays[:, 2, :], P), ALU.mult))
                    if k == 3:
                        v.wait_ge(s["gatez_ready"], 1)
                        step(v.scalar_tensor_tensor(out=gatez[:], in0=gatez[:], scalar=1.0, in1=bank[7][:],
                                                    op0=ALU.add, op1=ALU.mult))
                        step(v.tensor_tensor(gatez[:], gatez[:], norm_w[:].broadcast_to(four), ALU.mult))
                v.wait_ge(s["u_ps"], 1)
                v.tensor_tensor(u[:], bank[1][:], spread(bcol[:], P), ALU.mult).then_inc(s["u_ready"], 1)
                v.wait_ge(s["u_ready"], 1)
                v.tensor_tensor(uend[:], u[:], spread(decays[:, 1, :], P), ALU.mult).then_inc(s["uend_ready"], 1)
                v.wait_ge(s["o_ps"], 1)
                step(v.tensor_tensor(o[:], bank[4][:], o[:], ALU.add))
                step(v.tensor_tensor(osq[:], o[:], o[:], ALU.mult))
                step(v.tensor_reduce(msq[:], osq[:], AX.X, ALU.add))
                v.tensor_scalar(msq[:], msq[:], 1.0 / P, RMS_EPS, ALU.mult, ALU.add).then_inc(s["msq_ready"], 1)
                v.tensor_tensor(y[:], o[:], gatez[:], ALU.mult)
                v.wait_ge(s["s_ps"], 1)
                v.tensor_tensor(S[:], bank[6][:], newS[:], ALU.add).then_inc(s["s_used"], 1)
                v.wait_ge(s["std_ready"], 1)
                step(v.reciprocal(rstd[:], std[:]))
                v.tensor_tensor(y[:], y[:], spread(rstd[:], P), ALU.mult).then_inc(s["y_ready"], 1)
                v.wait_ge(s["out_ps"], 1)
                mine = X[:].rearrange("p (b t) d -> p b t d", b=G)[:, :, ds(ch, 1), :].rearrange("p b a d -> p b (a d)")
                v.tensor_tensor(mine, bank[0][:], mine, ALU.add).then_inc(s["added"], 1)
                v.wait_ge(s["added"], 1)
        st.end_step()


DEPTH = 6
HEADSW = 16
HDW = 64
INNER = HEADSW * HDW
WINDOW = 32
KEYS = WINDOW + P
HALFW = P // 2
QK_SCALE = 8.0
UNITS = int(P * 4 * 2 / 3)
PIECES = [(0, P), (P, 2 * P), (2 * P, UNITS)]
GH = 4
BANK_HEADS = 3


def l1_ffn_stage(nc, X, Y, c, d):
    with Stage(nc, "w") as outer:
        rope = outer.sb("rope", [P, 4, BLOCKS, HDW])
        scaled = outer.sb("scaled", [P, 4, BLOCKS, HDW])
        band = outer.sb("band", [P, BLOCKS, KEYS])
        shifts = outer.sb("shifts", [P, 2, P])
        wqkv = outer.sb("wqkv", [P, 3 * INNER])
        wo = outer.sb("wo", [P, INNER // P, P])
        w1 = outer.sb("w1", [P, 2 * UNITS])
        w2 = outer.sb("w2", [P, 3, P])
        b1 = outer.sb("b1", [P, 2, 3])
        b2 = outer.sb("b2", [1, P])
        gb = outer.sb("gb", [P, 2])
        qk_rows = outer.sb("qk_rows", [1, 2, HDW])
        with Stage(nc, "wc") as st:
            s = st.sems("loaded")
            with nc.Block(no_gpsimd_drain=True) as block:
                @block.sync
                def _(sp):
                    sp.dma_start(rope[:], d["const_rope"]).then_inc(s["loaded"], 16)
                    sp.dma_start(band[:], d["const_band"]).then_inc(s["loaded"], 16)
                    sp.dma_start(shifts[:], d["const_shifts"]).then_inc(s["loaded"], 16)
                    sp.wait_ge(s["loaded"], 48)
            st.end_step()

        with nc.Fori(0, DEPTH) as l:
            with Stage(nc, "wl") as st:
                qks = st.sb("qks", [P, 2, HDW])
                pr = st.ps("pr", (P, 2, HDW))
                s = st.sems("rows_loaded loaded rows_ps copied")
                with nc.Block(no_gpsimd_drain=True) as block:
                    @block.sync
                    def _(sp):
                        sp.dma_start(qk_rows[:, 0, :], d["L1_ffn_q_scale"][ds(l, 1), :]).then_inc(s["rows_loaded"], 16)
                        sp.dma_start(qk_rows[:, 1, :], d["L1_ffn_k_scale"][ds(l, 1), :]).then_inc(s["rows_loaded"], 16)
                        loads = [(wqkv[:], d["L1_ffn_Wqkv"][ds(l, 1)].rearrange("a p n -> (a p) n")),
                                 (wo[:], d["L1_ffn_Wo"][ds(l, 1)].rearrange("a (k p) n -> (a p) k n", p=P)),
                                 (w1[:], d["L1_ffn_W1"][ds(l, 1)].rearrange("a p n -> (a p) n")),
                                 (b2[:], d["L1_ffn_b2"][ds(l, 1), :]),
                                 (gb[:, 0:1], d["L1_ffn_ln_g"][ds(l, 1), :].rearrange("a p -> p a")),
                                 (gb[:, 1:2], d["L1_ffn_ln_b"][ds(l, 1), :].rearrange("a p -> p a"))]
                        for n, (k0, k1) in enumerate(PIECES):
                            loads.append((w2[0:k1 - k0, n, :], d["L1_ffn_W2"][ds(l, 1), k0:k1, :].rearrange("a p n -> (a p) n")))
                            for half in range(2):
                                loads.append((b1[0:k1 - k0, half, n:n + 1],
                                              d["L1_ffn_b1"][ds(l, 1), half * UNITS + k0:half * UNITS + k1]
                                              .rearrange("a p -> p a")))
                        for dst, src in loads:
                            sp.dma_start(dst, src).then_inc(s["loaded"], 16)
                        sp.wait_ge(s["loaded"], 16 * len(loads))

                    @block.tensor
                    def _(pe):
                        pe.wait_ge(s["rows_loaded"], 32)
                        pe.matmul(flat(pr[:]), c.ones[0:1, :], qk_rows[:].rearrange("a n d -> a (n d)"), start=True,
                                  stop=True).then_inc(s["rows_ps"], 1)

                    @block.vector
                    def _(v):
                        v.wait_ge(s["rows_ps"], 1)
                        v.tensor_copy(qks[:], pr[:]).then_inc(s["copied"], 1)
                        v.wait_ge(s["copied"], 1)
                        for n in range(2):
                            v.tensor_tensor(scaled[:, 2 * n], rope[:, 2 * n],
                                            qks[:, n:n + 1, :].broadcast_to([P, BLOCKS, HDW]), ALU.mult)
                            for k in range(2):
                                o, p = k * 32, 32 - k * 32
                                v.tensor_tensor(scaled[:, 2 * n + 1, :, o:o + 32], rope[:, 2 * n + 1, :, o:o + 32],
                                                qks[:, n:n + 1, p:p + 32].broadcast_to([P, BLOCKS, 32]), ALU.mult)
                st.end_step()
            with Stage(nc, "wa") as st:
                window_attention_steps(nc, st, Y, c, scaled, band, shifts, wqkv, wo)
            with Stage(nc, "wf") as st:
                geglu_steps(nc, st, Y, c, shifts, w1, w2, b1, b2, gb)

        with Stage(nc, "wx") as st:
            s = st.sems("added")
            with nc.Block(no_gpsimd_drain=True) as block:
                @block.vector
                def _(v):
                    v.tensor_tensor(X[:], X[:], Y[:], ALU.add).then_inc(s["added"], 1)
                    v.wait_ge(s["added"], 1)
            st.end_step()


def window_attention_steps(nc, st, Y, c, scaled, band, shifts, wqkv, wo):
    ya, yb, yprev, xsT = (st.sb(n, [P, P]) for n in ("ya", "yb", "yprev", "xsT"))
    v_cur = st.sb("v_cur", [P, HEADSW, HDW])
    v_prev = st.sb("v_prev", [P, HEADSW // GH, GH, HDW])
    sq = st.sb("sq", [P, 2, HEADSW, HDW])
    rot = st.sb("rot", [P, 2, HEADSW, HDW])
    part = st.sb("part", [P, 2, HEADSW, HDW])
    norm, rnorm = (st.sb(n, [P, 2, HEADSW]) for n in ("norm", "rnorm"))
    qT = st.sb("qT", [P, HEADSW // 2, P])
    kT = st.sb("kT", [P, HEADSW // 2, KEYS])
    sc = st.sb("sc", [P, HEADSW, KEYS])
    smax, bias, total, rtotal = (st.sb(n, [P, HEADSW]) for n in ("smax", "bias", "total", "rtotal"))
    pc = st.sb("pc", [P, HEADSW, KEYS])
    pp = st.sb("pp", [P, HEADSW, WINDOW])
    pcT = st.sb("pcT", [P, HEADSW, P])
    ppT = st.sb("ppT", [P, HEADSW // GH, P])
    o = st.sb("o", [P, HEADSW, HDW])
    oT = st.sb("oT", [P, INNER // P, P])
    bank = st.ps("bank", (P, 8, 512))
    scores_at = [0, 2, 6]
    groups = [range(n, min(n + 2 * BANK_HEADS, HEADSW)) for n in range(0, HEADSW, 2 * BANK_HEADS)]
    s = st.sems("y_copied xsT_ps xsT_ready q_ps k_ps v_ps v_ready sq_ready norm_in norm_ready q_rot k_rot qT_ps kT_ps "
                "qT_ready kT_ready scores_ps sc_ready bias_ready probs_ready ppT_ps ppT_ready pcT_ps pcT_ready o_ps "
                "o_ready oT_ps oT_ready out_ps added part_ready rot_ready pp_ready kept chain")
    with nc.Fori(0, BATCH) as b:
        with nc.Block(no_gpsimd_drain=True) as block:
            @block.gpsimd
            def _(g):
                for buffer in (ya, yb, yprev, kT, v_prev):
                    g.memset(buffer[:], 0.0).then_inc(s["kept"], 1)
                g.wait_ge(s["kept"], 5)
        st.end_step()
        with nc.Fori(0, BLOCKS) as t:
            with nc.Block(no_gpsimd_drain=True) as block:
                @block.gpsimd
                def _(g):
                    for n, done in ((0, s["q_rot"]), (1, s["k_rot"])):
                        g.wait_ge(s["part_ready"], n + 1)
                        if n == 0:
                            g.tensor_tensor(rot[:, n], rot[:, n], part[:, n], ALU.add).then_inc(done, 1)
                        else:
                            g.tensor_tensor(part[:, n], rot[:, n], part[:, n], ALU.add).then_inc(s["rot_ready"], 1)
                            g.wait_ge(s["rot_ready"], 1)
                            g.wait_ge(s["norm_ready"], 2)
                            g.tensor_tensor(rot[:, n], part[:, n], spread(rnorm[:, 1, :], HDW), ALU.mult).then_inc(done, 1)
                    g.wait_ge(s["probs_ready"], len(groups))
                    g.tensor_copy(pp[:], pc[:, :, 0:WINDOW]).then_inc(s["pp_ready"], 1)
                    step = Chain(g, s["kept"])
                    g.wait_ge(s["xsT_ps"], 1)
                    g.wait_ge(s["pp_ready"], 1)
                    step(g.tensor_copy(yprev[:], yb[:]))
                    g.wait_ge(s["o_ps"], 1)
                    for j in range(GH):
                        step(g.tensor_copy(v_prev[j * 32:(j + 1) * 32, :, j, :],
                                           v_cur[P - WINDOW:P].rearrange("p (g j) d -> p g j d", j=GH)[:, :, j, :]))
                    step(g.tensor_copy(kT[:, :, 0:WINDOW], kT[:, :, P:KEYS]))

                @block.scalar
                def _(a):
                    mine = tile(Y, b * BLOCKS + t)
                    a.activation(ya[:, 0:HALFW], mine[:, 0:HALFW], ACT.Copy)
                    a.activation(yb[:, HALFW:P], mine[:, HALFW:P], ACT.Copy).then_inc(s["y_copied"], 1)
                    a.wait_ge(s["xsT_ps"], 1)
                    a.activation(xsT[:], bank[:, 7, 0:P], ACT.Copy).then_inc(s["xsT_ready"], 1)
                    for n, ready in enumerate((s["q_ps"], s["k_ps"])):
                        a.wait_ge(ready, 1)
                        a.activation(sq[:, n].rearrange("p h d -> p (h d)"),
                                     bank[:, 2 * n:2 * n + 2, :].rearrange("p k n -> p (k n)"),
                                     ACT.Square).then_inc(s["sq_ready"], 1)
                    a.wait_ge(s["v_ps"], 1)
                    a.activation(v_cur[:].rearrange("p h d -> p (h d)"), bank[:, 4:6, :].rearrange("p k n -> p (k n)"),
                                 ACT.Copy).then_inc(s["v_ready"], 1)
                    a.wait_ge(s["norm_in"], 1)
                    a.activation(norm[:], norm[:], ACT.Sqrt).then_inc(s["norm_ready"], 1)
                    a.wait_ge(s["qT_ps"], 1)
                    a.activation(qT[:].rearrange("p h n -> p (h n)"), bank[:, 6:8, :].rearrange("p k n -> p (k n)"),
                                 ACT.Copy).then_inc(s["qT_ready"], 1)
                    a.wait_ge(s["kT_ps"], 1)
                    a.activation(kT[:, :, WINDOW:KEYS], bank[:, 4:6, :].rearrange("p k (h n) -> p (k h) n", n=P),
                                 ACT.Copy).then_inc(s["kT_ready"], 1)
                    for n, hs in enumerate(groups):
                        a.wait_ge(s["bias_ready"], n + 1)
                        for h in hs:
                            last = a.activation(pc[:, h, :], sc[:, h, :], ACT.Exp, scale=rnorm[:, 0, h:h + 1],
                                                bias=bias[:, h:h + 1], accum_out=total[:, h:h + 1])
                        last.then_inc(s["probs_ready"], 1)
                    for n in (1, 3):
                        a.wait_ge(s["pcT_ps"], n + 1)
                        a.wait_ge(s["pcT_ready"], n)
                        a.activation(flat(pcT[:, n * GH:(n + 1) * GH, :]), bank[:, 5, :], ACT.Copy).then_inc(s["pcT_ready"], 1)
                        if n == 1:
                            a.wait_ge(s["ppT_ps"], 1)
                            a.activation(flat(ppT[:]), bank[:, 6, :], ACT.Copy).then_inc(s["ppT_ready"], 1)
                    a.wait_ge(s["oT_ps"], 1)
                    a.activation(flat(oT[:]), bank[:, 2:4, :].rearrange("p k n -> p (k n)"), ACT.Copy).then_inc(s["oT_ready"], 1)

                @block.tensor
                def _(pe):
                    pe.wait_ge(s["y_copied"], 1)
                    x = bank[:, 7, 0:P]
                    pe.matmul(x, ya[:], c.ident, start=True, stop=False)
                    pe.matmul(x, yb[:], shifts[:, 0, :], start=False, stop=False)
                    pe.matmul(x, yprev[:], shifts[:, 1, :], start=False, stop=True).then_inc(s["xsT_ps"], 1)
                    pe.wait_ge(s["xsT_ready"], 1)
                    for n, done in enumerate((s["q_ps"], s["k_ps"], s["v_ps"])):
                        for k in range(2 * n, 2 * n + 2):
                            last = pe.matmul(bank[:, k, :], xsT[:], wqkv[:, k * 512:(k + 1) * 512], start=True, stop=True)
                        last.then_inc(done, 1)
                    for n, (wait, free, first, done) in enumerate(((s["q_rot"], s["xsT_ready"], 6, s["qT_ps"]),
                                                                   (s["k_rot"], s["v_ready"], 4, s["kT_ps"]))):
                        pe.wait_ge(wait, 1)
                        pe.wait_ge(free, 1)
                        for k in range(HEADSW // 2):
                            last = pe.transpose(bank[:, first + k // 4, (k % 4) * P:(k % 4 + 1) * P],
                                                rot[:, n, 2 * k:2 * k + 2, :].rearrange("p h d -> p (h d)"), c.ident)
                        last.then_inc(done, 1)
                    pe.wait_ge(s["qT_ready"], 1)
                    pe.wait_ge(s["kT_ready"], 1)
                    for n, hs in enumerate(groups):
                        for h in hs:
                            r = slice((h % 2) * HDW, (h % 2) * HDW + HDW)
                            at = (h - hs[0]) // 2 * KEYS
                            last = pe.matmul(bank[:, scores_at[n] + h % 2, at:at + KEYS], qT[r, h // 2, :], kT[r, h // 2, :],
                                             start=True, stop=True)
                            last.then_inc(s["scores_ps"], 1)
                    pe.wait_ge(s["probs_ready"], len(groups))
                    for g in range(HEADSW // GH):
                        if g >= 2:
                            pe.wait_ge(s["pcT_ready"], g - 1)
                        for j in range(GH):
                            last = pe.transpose(bank[:, 4 + g % 2, j * P:(j + 1) * P], pc[:, g * GH + j, WINDOW:KEYS], c.ident)
                        last.then_inc(s["pcT_ps"], 1)
                        if g == 1:
                            pe.wait_ge(s["pp_ready"], 1)
                            for k in range(HEADSW // GH):
                                last = pe.transpose(bank[:, 6, k * P:(k + 1) * P],
                                                    pp[:, k * GH:(k + 1) * GH, :].rearrange("p h k -> p (h k)"), c.ident)
                            last.then_inc(s["ppT_ps"], 1)
                    pe.wait_ge(s["ppT_ready"], 1)
                    pe.wait_ge(s["pcT_ready"], HEADSW // GH)
                    for g in range(HEADSW // GH):
                        out = bank[:, g // 2, (g % 2) * GH * HDW:(g % 2 + 1) * GH * HDW]
                        pe.matmul(out, ppT[:, g, :], v_prev[:, g].rearrange("p j d -> p (j d)"), start=True, stop=False)
                        for j in range(GH):
                            last = pe.matmul(out[:, j * HDW:(j + 1) * HDW], pcT[:, g * GH + j, :], v_cur[:, g * GH + j, :],
                                             start=False, stop=(j == GH - 1))
                    last.then_inc(s["o_ps"], 1)
                    pe.wait_ge(s["o_ready"], 1)
                    for k in range(INNER // P):
                        last = pe.transpose(bank[:, 2 + k // 4, (k % 4) * P:(k % 4 + 1) * P],
                                            o[:, 2 * k:2 * k + 2, :].rearrange("p h d -> p (h d)"), c.ident)
                    last.then_inc(s["oT_ps"], 1)
                    pe.wait_ge(s["oT_ready"], 1)
                    for k in range(INNER // P):
                        last = pe.matmul(bank[:, 4, 0:P], oT[:, k, :], wo[:, k, :], start=(k == 0), stop=(k == INNER // P - 1))
                    last.then_inc(s["out_ps"], 1)

                @block.vector
                def _(v):
                    step = Chain(v, s["chain"])
                    mine = tile(Y, b * BLOCKS + t)
                    for n, ready in enumerate((s["q_ps"], s["k_ps"])):
                        src = bank[:, 2 * n:2 * n + 2, :].rearrange("p k (h d) -> p (k h) d", d=HDW)
                        cos = scaled[:, 2 * n, ds(t, 1), :].broadcast_to([P, HEADSW, HDW])
                        sin = scaled[:, 2 * n + 1, ds(t, 1), :]
                        v.wait_ge(ready, 1)
                        v.wait_ge(s["sq_ready"], n + 1)
                        v.tensor_tensor(rot[:, n], src, cos, ALU.mult)
                        for k in range(2):
                            p0, p1 = k * 32, 32 - k * 32
                            last = v.tensor_tensor(part[:, n, :, p0:p0 + 32], src[:, :, p1:p1 + 32],
                                                   sin[:, :, p0:p0 + 32].broadcast_to([P, HEADSW, 32]), ALU.mult)
                        last.then_inc(s["part_ready"], 1)
                    step(v.tensor_reduce(norm[:].rearrange("p n h -> p (n h)"), sq[:].rearrange("p n h d -> p (n h) d"),
                                         AX.X, ALU.add))
                    v.wait_ge(s["part_ready"], 2)
                    v.tensor_scalar(norm[:], norm[:], 1.0, None, ALU.mult).then_inc(s["norm_in"], 1)
                    v.wait_ge(s["norm_ready"], 1)
                    step(v.tensor_scalar(norm[:], norm[:], 1e-12, None, ALU.max))
                    v.reciprocal(rnorm[:], norm[:]).then_inc(s["norm_ready"], 1)
                    v.wait_ge(s["norm_ready"], 2)
                    step(v.tensor_scalar(rnorm[:, 0, :], rnorm[:, 0, :], QK_SCALE, None, ALU.mult))
                    for n, hs in enumerate(groups):
                        v.wait_ge(s["scores_ps"], hs[-1] + 1)
                        m = len(hs) // 2
                        for par in range(2):
                            view = sc[:, hs[0]:hs[0] + 2 * m, :].rearrange("p (a two) k -> p a two k", two=2)[:, :, par, :]
                            last = v.tensor_tensor(view, bank[:, scores_at[n] + par, 0:m * KEYS]
                                                   .rearrange("p (a k) -> p a k", a=m),
                                                   band[:, ds(t, 1), :].broadcast_to([P, m, KEYS]), ALU.add)
                        step(last)
                        h0, h1 = hs[0], hs[0] + 2 * m
                        step(v.tensor_reduce(smax[:, h0:h1], sc[:, h0:h1, :], AX.X, ALU.max))
                        v.scalar_tensor_tensor(out=bias[:, h0:h1], in0=smax[:, h0:h1], scalar=-1.0, in1=rnorm[:, 0, h0:h1],
                                               op0=ALU.mult, op1=ALU.mult).then_inc(s["bias_ready"], 1)
                    v.wait_ge(s["probs_ready"], len(groups))
                    step(v.reciprocal(rtotal[:], total[:]))
                    for n in (0, 2):
                        v.wait_ge(s["pcT_ps"], n + 1)
                        if n == 2:
                            v.wait_ge(s["pcT_ready"], 2)
                        v.tensor_copy(flat(pcT[:, n * GH:(n + 1) * GH, :]), bank[:, 4, :]).then_inc(s["pcT_ready"], 1)
                    v.wait_ge(s["o_ps"], 1)
                    v.tensor_tensor(o[:], bank[:, 0:2, :].rearrange("p k (h d) -> p (k h) d", d=HDW),
                                    spread(rtotal[:], HDW), ALU.mult).then_inc(s["o_ready"], 1)
                    v.wait_ge(s["out_ps"], 1)
                    v.tensor_tensor(mine, bank[:, 4, 0:P], mine, ALU.add).then_inc(s["added"], 1)
                    v.wait_ge(s["added"], 1)
            st.end_step()


def geglu_steps(nc, st, Y, c, shifts, w1, w2, b1, b2, gb):
    yh = st.sb("yh", [P, G + 1, HALFW])
    xf, xn = st.sb("xf", [P, G, P]), st.sb("xn", [P, G, P])
    stats, mv = st.sb("stats", [P, G, 6]), st.sb("mv", [P, G, 2])
    var, std, rstd = (st.sb(n, [P, G]) for n in ("var", "std", "rstd"))
    xnT = st.sb("xnT", [P, G * P])
    gate, hid = st.sb("gate", [P, 3, G * P]), st.sb("hid", [P, 3, G * P])
    shp = st.ps("shp", (P, G, HALFW))
    xnp = st.ps("xnp", (P, G * P))
    ap_, gp = st.ps("ap", (P, 2, 512)), st.ps("gp", (P, 2, 512))
    outp = st.ps("outp", (P, G, P))
    s = st.sems("y_copied sh_ps xf_ready var_ready std_ready xn_ready xn_ps xnT_ready a_ps g_ps gate_ready hid_ready "
                "out_ps added zeroed chain")
    with nc.Fori(0, BATCH) as b:
        with nc.Block(no_gpsimd_drain=True) as block:
            @block.gpsimd
            def _(g):
                g.memset(yh[:], 0.0).then_inc(s["zeroed"], 1)
                g.wait_ge(s["zeroed"], 1)
        st.end_step()
        with nc.Fori(0, BLOCKS // G) as i:
            with nc.Block(no_gpsimd_drain=True) as block:
                mine = Y[:, ds(b * BLOCKS + i * G, G), :]

                @block.scalar
                def _(a):
                    a.activation(yh[:, 1:G + 1, :], mine[:, :, HALFW:P], ACT.Copy).then_inc(s["y_copied"], 1)
                    a.wait_ge(s["var_ready"], 1)
                    a.activation(std[:], var[:], ACT.Sqrt).then_inc(s["std_ready"], 1)
                    for n, (k0, k1) in enumerate(PIECES):
                        a.wait_ge(s["g_ps"], n + 1)
                        a.activation(gate[0:k1 - k0, n, :], gp[0:k1 - k0, n % 2, :], ACT.Gelu,
                                     bias=b1[0:k1 - k0, 1, n:n + 1]).then_inc(s["gate_ready"], 1)

                @block.tensor
                def _(pe):
                    pe.wait_ge(s["y_copied"], 1)
                    pe.matmul(flat(shp[:]), shifts[:, 0, :], yh[:, 1:G + 1, :].rearrange("p n d -> p (n d)"),
                              start=True, stop=False)
                    pe.matmul(flat(shp[:]), shifts[:, 1, :], yh[:, 0:G, :].rearrange("p n d -> p (n d)"),
                              start=False, stop=True).then_inc(s["sh_ps"], 1)
                    pe.wait_ge(s["xn_ready"], 1)
                    for j in range(G):
                        last = pe.transpose(xnp[:, j * P:(j + 1) * P], xn[:, j, :], c.ident)
                    last.then_inc(s["xn_ps"], 1)
                    pe.wait_ge(s["xnT_ready"], 1)
                    for n, (k0, k1) in enumerate(PIECES):
                        if n >= 2:
                            pe.wait_ge(s["gate_ready"], n - 1)
                            pe.wait_ge(s["hid_ready"], n - 1)
                        pe.matmul(gp[0:k1 - k0, n % 2, :], w1[:, UNITS + k0:UNITS + k1], xnT[:], start=True,
                                  stop=True).then_inc(s["g_ps"], 1)
                        pe.matmul(ap_[0:k1 - k0, n % 2, :], w1[:, k0:k1], xnT[:], start=True, stop=True).then_inc(s["a_ps"], 1)
                    pe.wait_ge(s["hid_ready"], 3)
                    for j in range(G):
                        for n, (k0, k1) in enumerate(PIECES):
                            pe.matmul(outp[:, j, :], hid[0:k1 - k0, n, j * P:(j + 1) * P], w2[0:k1 - k0, n, :],
                                      start=(n == 0), stop=False)
                        last = pe.matmul(outp[:, j, :], c.ones[0:1, :], b2[:], start=False, stop=True)
                    last.then_inc(s["out_ps"], 1)

                @block.vector
                def _(v):
                    step = Chain(v, s["chain"])
                    v.tensor_copy(xf[:, :, 0:HALFW], mine[:, :, 0:HALFW])
                    v.wait_ge(s["sh_ps"], 1)
                    step(v.tensor_copy(xf[:, :, HALFW:P], shp[:]))
                    v.tensor_copy(yh[:, 0, :], yh[:, G, :])
                    for j in range(G):
                        last = v.bn_stats(stats[:, j, :], xf[:, j, :])
                    step(last)
                    for j in range(G):
                        last = v.bn_aggr(mv[:, j, :], stats[:, j, :])
                    step(last)
                    v.tensor_scalar(var[:], mv[:, :, 1], LN_EPS, None, ALU.add).then_inc(s["var_ready"], 1)
                    v.wait_ge(s["std_ready"], 1)
                    step(v.reciprocal(rstd[:], std[:]))
                    for j in range(G):
                        last = v.tensor_scalar(xn[:, j, :], xf[:, j, :], mv[:, j, 0:1], rstd[:, j:j + 1],
                                               ALU.subtract, ALU.mult)
                    last.then_inc(s["xn_ready"], 1)
                    v.wait_ge(s["xn_ps"], 1)
                    v.tensor_scalar(xnT[:], xnp[:], gb[:, 0:1], gb[:, 1:2], ALU.mult, ALU.add).then_inc(s["xnT_ready"], 1)
                    for n, (k0, k1) in enumerate(PIECES):
                        v.wait_ge(s["gate_ready"], n + 1)
                        v.wait_ge(s["a_ps"], n + 1)
                        v.scalar_tensor_tensor(out=hid[0:k1 - k0, n, :], in0=ap_[0:k1 - k0, n % 2, :],
                                               scalar=b1[0:k1 - k0, 0, n:n + 1], in1=gate[0:k1 - k0, n, :],
                                               op0=ALU.add, op1=ALU.mult).then_inc(s["hid_ready"], 1)
                    v.wait_ge(s["out_ps"], 1)
                    v.tensor_tensor(mine, outp[:], mine, ALU.add).then_inc(s["added"], 1)
                    v.wait_ge(s["added"], 1)
            st.end_step()


COS_EPS = 1e-8


def l2_attention_stage(nc, X, XN, XNT, c):
    with Stage(nc, "a2") as st:
        xs = st.sb("xs", [P, SEQ])
        xv = st.sb("xv", [P, BLOCKS, P + 1])
        squares = st.sb("squares", [P, BLOCKS, P])
        norm2, norm, rnorm, rtotal = (st.sb(n, [P, BLOCKS]) for n in ("norm2", "norm", "rnorm", "rtotal"))
        diag = st.sb("diag", [P, BLOCKS, P])
        rrow = st.sb("rrow", [P, SEQ])
        scale = st.sb("scale", [P, 2, SEQ])
        sim = st.sb("sim", [P, 2, SEQ])
        E = st.sb("E", [P, BLOCKS, SEQ])
        mean = st.sb("mean", [P, 2, P])
        wide = st.ps("wide", (P, 2, SEQ))
        out = st.ps("out", (P, 2, 512))
        s = st.sems("xs_ready xv_ready norm2_ready norm_ready diag_ready row_ready rrow_done dots_ready sim_ready "
                    "exps out_ready out_used added ones_set chain")
        with nc.Fori(0, BATCH) as b:
            with nc.Block(no_gpsimd_drain=True) as block:
                @block.scalar
                def _(a):
                    a.activation(xs[:], XNT[:, ds(b * SEQ, SEQ)], ACT.Copy).then_inc(s["xs_ready"], 1)
                    a.wait_ge(s["norm2_ready"], 1)
                    a.activation(norm[:], norm2[:], ACT.Sqrt).then_inc(s["norm_ready"], 1)
                    a.wait_ge(s["row_ready"], 1)
                    a.activation(rrow[:], wide[:, 0, :], ACT.Copy).then_inc(s["rrow_done"], 1)
                    for t in range(BLOCKS):
                        a.wait_ge(s["sim_ready"], t + 1)
                        a.activation(E[:, t, :], sim[:, t % 2, :], ACT.Exp).then_inc(s["exps"], 1)

                @block.gpsimd
                def _(g):
                    g.memset(xv[:, :, P:P + 1], 1.0)
                    g.tensor_copy(xv[:, :, 0:P], XN[:, ds(b * BLOCKS, BLOCKS), :]).then_inc(s["xv_ready"], 1)

                @block.vector
                def _(v):
                    step = Chain(v, s["chain"])
                    v.wait_ge(s["xv_ready"], 1)
                    step(v.tensor_tensor(squares[:], xv[:, :, 0:P], xv[:, :, 0:P], ALU.mult))
                    v.tensor_reduce(norm2[:], squares[:], AX.X, ALU.add).then_inc(s["norm2_ready"], 1)
                    v.wait_ge(s["norm_ready"], 1)
                    step(v.tensor_scalar(norm[:], norm[:], 1e-30, None, ALU.max))
                    step(v.reciprocal(rnorm[:], norm[:]))
                    for t in range(BLOCKS):
                        last = v.tensor_scalar(diag[:, t, :], c.ident, rnorm[:, t:t + 1], None, ALU.mult)
                    last.then_inc(s["diag_ready"], 1)
                    v.wait_ge(s["rrow_done"], 1)
                    for t in range(BLOCKS):
                        step(v.tensor_scalar(scale[:, t % 2, :], rrow[:], rnorm[:, t:t + 1], 1.0 / COS_EPS,
                                             ALU.mult, ALU.min))
                        v.wait_ge(s["dots_ready"], t + 1)
                        if t >= 2:
                            v.wait_ge(s["exps"], t - 1)
                        v.tensor_tensor(sim[:, t % 2, :], wide[:, (t + 1) % 2, :], scale[:, t % 2, :],
                                        ALU.mult).then_inc(s["sim_ready"], 1)
                    for t in range(BLOCKS):
                        v.wait_ge(s["out_ready"], t + 1)
                        step(v.reciprocal(rtotal[:, t:t + 1], out[:, t % 2, P:P + 1]))
                        v.scalar_tensor_tensor(out=mean[:, t % 2, :], in0=out[:, t % 2, 0:P],
                                               scalar=rtotal[:, t:t + 1], in1=xv[:, t, 0:P],
                                               op0=ALU.mult, op1=ALU.add).then_inc(s["out_used"], 1)
                        v.wait_ge(s["out_used"], t + 1)
                        v.tensor_tensor(tile(X, b * BLOCKS + t), mean[:, t % 2, :], tile(X, b * BLOCKS + t),
                                        ALU.add).then_inc(s["added"], 1)
                    v.wait_ge(s["added"], BLOCKS)

                @block.tensor
                def _(pe):
                    pe.wait_ge(s["diag_ready"], 1)
                    for t in range(BLOCKS):
                        last = pe.matmul(wide[:, 0, t * P:(t + 1) * P], c.ones, diag[:, t, :], start=True, stop=True)
                    last.then_inc(s["row_ready"], 1)
                    pe.wait_ge(s["xs_ready"], 1)
                    for t in range(BLOCKS):
                        if t == 1:
                            pe.wait_ge(s["rrow_done"], 1)
                        if t >= 2:
                            pe.wait_ge(s["sim_ready"], t - 1)
                        for k in range(2):
                            last = pe.matmul(wide[:, (t + 1) % 2, k * 512:(k + 1) * 512], xs[:, t * P:(t + 1) * P],
                                             xs[:, k * 512:(k + 1) * 512], start=True, stop=True)
                        last.then_inc(s["dots_ready"], 1)
                    pe.wait_ge(s["exps"], BLOCKS)
                    for t in range(BLOCKS):
                        if t >= 2:
                            pe.wait_ge(s["out_used"], t - 1)
                        for k in range(BLOCKS):
                            last = pe.matmul(out[:, t % 2, 0:P + 1], E[:, k, t * P:(t + 1) * P], xv[:, k, :],
                                             start=(k == 0), stop=(k == BLOCKS - 1))
                        last.then_inc(s["out_ready"], 1)
            st.end_step()


JITTER = 0.01
WIDTH2 = 256


def l2_ffn_stage(nc, X, XNT, c, gate_w, w1, w2, w3):
    with Stage(nc, "f2") as outer:
        gT = outer.sb("gT", [P, EXPERTS])
        w1T = outer.sb("w1T", [P, EXPERTS, WIDTH2])
        w3T = outer.sb("w3T", [P, EXPERTS, WIDTH2])
        w2T = outer.sb("w2T", [P, EXPERTS, 2, P])
        for n, pairs in enumerate((
            [(gT[:], gate_w)] + [(w1T[:, e, k * P:(k + 1) * P], w1[e, k * P:(k + 1) * P, :])
                                 for e in range(EXPERTS) for k in range(2)],
            [(w3T[:, e, k * P:(k + 1) * P], w3[e, k * P:(k + 1) * P, :]) for e in range(EXPERTS) for k in range(2)],
            [(w2T[:, e, k, :], w2[e, :, k * P:(k + 1) * P]) for e in range(EXPERTS) for k in range(2)],
        )):
            load_turned(nc, f"f2w{n}", pairs, c)
        with Stage(nc, "f2s") as st:
            xs = st.sb("xs", [P, G * P])
            lg, size, gap, first, second, rest = (st.sb(n, [P, G, EXPERTS]) for n in
                                                  ("lg", "size", "gap", "first", "second", "rest"))
            ex1, ex2, lim1, lim2 = (st.sb(n, [P, G, EXPERTS]) for n in ("ex1", "ex2", "lim1", "lim2"))
            weight = st.sb("weight", [P, G, EXPERTS])
            top = st.sb("top", [P, G, 8])
            at = st.sb("at", [P, G, 8], U32)
            atf = st.sb("atf", [P, G, 8])
            total, mult = (st.sb(n, [P, 2, G]) for n in ("total", "mult"))
            th = st.sb("th", [P, 2, 512])
            gated = st.sb("gated", [P, 2, 512])
            act = st.sb("act", [P, 2, 2, 512])
            acc = st.sb("acc", [P, G, P])
            logits = st.ps("logits", (P, G, EXPERTS))
            h1 = st.ps("h1", (P, 2, 512))
            h3 = st.ps("h3", (P, 2, 512))
            y = st.ps("y", (P, 2, G, P))
            s = st.sems("xs_ready logits_ready shifted1 exps h1_ready h3_ready th_ready act_ready y_ready y_used "
                        "added chain")
            with nc.Fori(0, TILES // G) as i:
                with nc.Block(no_gpsimd_drain=True) as block:
                    @block.scalar
                    def _(a):
                        a.activation(xs[:], XNT[:, ds(i * G * P, G * P)], ACT.Copy).then_inc(s["xs_ready"], 1)
                        a.wait_ge(s["shifted1"], 1)
                        a.activation(ex1[:], ex1[:], ACT.Exp)
                        a.activation(ex2[:], ex2[:], ACT.Exp).then_inc(s["exps"], 1)
                        for n in range(2 * EXPERTS):
                            a.wait_ge(s["h1_ready"], n + 1)
                            if n >= 2:
                                a.wait_ge(s["act_ready"], n - 1)
                            a.activation(th[:, n % 2, :], h1[:, n % 2, :], ACT.Tanh, scale=0.5).then_inc(s["th_ready"], 1)

                    @block.tensor
                    def _(pe):
                        pe.wait_ge(s["xs_ready"], 1)
                        for j in range(G):
                            last = pe.matmul(logits[:, j, :], xs[:, j * P:(j + 1) * P], gT[:], start=True, stop=True)
                        last.then_inc(s["logits_ready"], 1)

                        def second_product(e):
                            pe.wait_ge(s["act_ready"], 2 * e + 2)
                            if e >= 2:
                                pe.wait_ge(s["y_used"], e - 1)
                            for j in range(G):
                                for k in range(2):
                                    last = pe.matmul(y[:, e % 2, j, :], act[:, e % 2, k, j * P:(j + 1) * P],
                                                     w2T[:, e, k, :], start=(k == 0), stop=(k == 1))
                            last.then_inc(s["y_ready"], 1)

                        for e in range(EXPERTS):
                            for k in range(2):
                                n = 2 * e + k
                                if n >= 2:
                                    pe.wait_ge(s["act_ready"], n - 1)
                                pe.matmul(h1[:, n % 2, :], w1T[:, e, k * P:(k + 1) * P], xs[:],
                                          start=True, stop=True).then_inc(s["h1_ready"], 1)
                                pe.matmul(h3[:, n % 2, :], w3T[:, e, k * P:(k + 1) * P], xs[:],
                                          start=True, stop=True).then_inc(s["h3_ready"], 1)
                            if e >= 1:
                                second_product(e - 1)
                        second_product(EXPERTS - 1)

                    @block.vector
                    def _(v):
                        step = Chain(v, s["chain"])
                        v.wait_ge(s["logits_ready"], 1)
                        step(v.tensor_copy(lg[:], logits[:]))
                        for j in range(G):
                            last = v.max(top[:, j, :], lg[:, j, :])
                        step(last)
                        for j in range(G):
                            last = v.max_index(at[:, j, :], top[:, j, :], lg[:, j, :])
                        step(last)
                        v.tensor_scalar(size[:], lg[:], -1.0, None, ALU.mult)
                        step(v.tensor_copy(atf[:], at[:]))
                        step(v.tensor_tensor(size[:], size[:], lg[:], ALU.max))
                        for j in range(G):
                            v.tensor_scalar(first[:, j, :], c.count8, atf[:, j, 0:1], None, ALU.is_equal)
                            last = v.tensor_scalar(second[:, j, :], c.count8, atf[:, j, 1:2], None, ALU.is_equal)
                        step(last)
                        for ex, lim, k in ((ex1, lim1, 0), (ex2, lim2, 1)):
                            t = top[:, :, k:k + 1].broadcast_to([P, G, EXPERTS])
                            step(v.tensor_tensor(lim[:], size[:], t, ALU.max))
                            step(v.tensor_tensor(gap[:], t, lg[:], ALU.subtract))
                            step(v.scalar_tensor_tensor(out=lim[:], in0=lim[:], scalar=2 * JITTER, in1=gap[:],
                                                        op0=ALU.mult, op1=ALU.is_ge))
                            last = v.tensor_scalar(ex[:], gap[:], -1.0, 0.0, ALU.mult, ALU.min)
                            if k == 0:
                                step(last)
                            else:
                                last.then_inc(s["shifted1"], 1)
                        step(v.tensor_scalar(rest[:], first[:], -1.0, 1.0, ALU.mult, ALU.add))
                        step(v.tensor_tensor(lim2[:], lim2[:], rest[:], ALU.mult))
                        v.wait_ge(s["exps"], 1)
                        v.tensor_tensor(ex1[:], ex1[:], lim1[:], ALU.mult)
                        step(v.tensor_tensor(ex2[:], ex2[:], lim2[:], ALU.mult))
                        v.tensor_reduce(total[:, 0, :], ex1[:], AX.X, ALU.add)
                        step(v.tensor_reduce(total[:, 1, :], ex2[:], AX.X, ALU.add))
                        step(v.reciprocal(mult[:], total[:]))
                        v.tensor_tensor(first[:], first[:], spread(mult[:, 0, :], EXPERTS), ALU.mult)
                        step(v.tensor_tensor(second[:], second[:], spread(mult[:, 1, :], EXPERTS), ALU.mult))
                        step(v.tensor_tensor(weight[:], first[:], second[:], ALU.add))

                        def hidden(n):
                            v.wait_ge(s["th_ready"], n + 1)
                            step(v.scalar_tensor_tensor(out=gated[:, n % 2, :], in0=th[:, n % 2, :], scalar=1.0,
                                                        in1=h1[:, n % 2, :], op0=ALU.add, op1=ALU.mult))
                            v.wait_ge(s["h3_ready"], n + 1)
                            if n >= 4:
                                v.wait_ge(s["y_ready"], (n - 4) // 2 + 1)
                            v.scalar_tensor_tensor(out=act[:, (n // 2) % 2, n % 2, :], in0=h3[:, n % 2, :], scalar=0.5,
                                                   in1=gated[:, n % 2, :], op0=ALU.mult,
                                                   op1=ALU.mult).then_inc(s["act_ready"], 1)

                        def gather(e):
                            v.wait_ge(s["y_ready"], e + 1)
                            for j in range(G):
                                if e == 0:
                                    last = v.tensor_scalar(acc[:, j, :], y[:, 0, j, :], weight[:, j, 0:1], None, ALU.mult)
                                else:
                                    last = v.scalar_tensor_tensor(out=acc[:, j, :], in0=y[:, e % 2, j, :],
                                                                  scalar=weight[:, j, e:e + 1], in1=acc[:, j, :],
                                                                  op0=ALU.mult, op1=ALU.add)
                            last.then_inc(s["y_used"], 1)
                            v.wait_ge(s["y_used"], e + 1)

                        for e in range(EXPERTS):
                            hidden(2 * e)
                            hidden(2 * e + 1)
                            if e >= 1:
                                gather(e - 1)
                        gather(EXPERTS - 1)
                        v.tensor_tensor(X[:, ds(i * G, G), :], acc[:], X[:, ds(i * G, G), :], ALU.add).then_inc(s["added"], 1)
                        v.wait_ge(s["added"], 1)
                st.end_step()


HEADS3 = 4
HD3 = P // HEADS3
LOCAL, MID = 7, 25
PATHS = 4
PAIRS = [(0, 1), (0, 2), (0, 3), (1, 2), (1, 3), (2, 3)]
FEATS = HEADS3 * (2 * PATHS + len(PAIRS))
HIDDEN3 = 2 * (P + FEATS)
FLOOR = 0.01
L2_EPS, MIX_EPS = 1e-12, 1e-5


def l3_attention_stage(nc, X, XNT, c, d):
    with Stage(nc, "a3") as outer:
        outs = outer.sb("outs", [P, TILES, PATHS, P])
        with Stage(nc, "a3x") as st:
            l3_paths_stage(nc, st, XNT, c, d, outs)
        with Stage(nc, "a3y") as st:
            l3_router_stage(nc, st, X, XNT, c, d, outs)


def l3_paths_stage(nc, outer, XNT, c, d, outs):
    proj = outer.sb("proj", [P, 3, P])
    wb = outer.sb("wb", [P, HEADS3])
    taps = outer.sb("taps", [P, 3, TAPS])
    wide_taps = outer.sb("wide_taps", [P, LOCAL + MID])
    masks = outer.sb("masks", [P, len(LEVELS), P])
    raw = outer.sb("raw", [P, 3, TAPS - 1 + SEQ])
    act = outer.sb("act", [P, 3, SEQ])
    th = outer.sb("th", [P, SEQ])
    qk = outer.sb("qk", [P, 2, SEQ])
    vh = outer.sb("vh", [P, MID - 1 + SEQ])
    lm = outer.sb("lm", [P, 2, SEQ])
    S = outer.sb("S", [P, P])
    with Stage(nc, "a3w") as st:
        s = st.sems("loaded")
        with nc.Block(no_gpsimd_drain=True) as block:
            @block.sync
            def _(sp):
                loads = [(proj[:, n, :], d[f"L3_attn_W{w}"]) for n, w in enumerate("qkv")]
                loads += [(taps[:, n, :], d[f"L3_attn_conv_{w}_w"]) for n, w in enumerate("qkv")]
                loads += [(wb[:], d["L3_attn_Wb"]), (wide_taps[:, 0:LOCAL], d["L3_attn_local_w"]),
                          (wide_taps[:, LOCAL:], d["L3_attn_mid_w"]), (masks[:], d["const_level_masks"])]
                for dst, src in loads:
                    sp.dma_start(dst, src).then_inc(s["loaded"], 16)
                sp.wait_ge(s["loaded"], 16 * len(loads))

            @block.vector
            def _(v):
                v.memset(raw[:, :, 0:TAPS - 1], 0.0)
                v.memset(vh[:, 0:MID - 1], 0.0)
                v.wait_ge(s["loaded"], 160)
                v.tensor_scalar(taps[:], taps[:], 0.5, None, ALU.mult)
        st.end_step()

    with nc.Fori(0, BATCH) as b:
        with Stage(nc, "a3p") as st:
            rawp = st.ps("rawp", (P, 3, SEQ))
            s = st.sems("raw_ready raw_copied conv_ready th_ready silu_ready done chain")
            with nc.Block(no_gpsimd_drain=True) as block:
                @block.tensor
                def _(pe):
                    for n in range(3):
                        for k in range(2):
                            last = pe.matmul(rawp[:, n, k * 512:(k + 1) * 512], proj[:, n, :],
                                             XNT[:, ds(b * SEQ + k * 512, 512)], start=True, stop=True)
                        last.then_inc(s["raw_ready"], 1)

                @block.scalar
                def _(a):
                    for n in range(3):
                        a.wait_ge(s["raw_ready"], n + 1)
                        a.activation(raw[:, n, TAPS - 1:], rawp[:, n, :], ACT.Copy).then_inc(s["raw_copied"], 1)
                    for n in range(3):
                        a.wait_ge(s["conv_ready"], n + 1)
                        if n >= 1:
                            a.wait_ge(s["silu_ready"], n)
                        a.activation(th[:], act[:, n, :], ACT.Tanh).then_inc(s["th_ready"], 1)

                @block.vector
                def _(v):
                    step = Chain(v, s["chain"])
                    v.memset(S[:], 0.0)

                    def convolve(out, src, w, taps_n):
                        step(v.tensor_scalar(out, src[:, taps_n - 1:taps_n - 1 + SEQ], w[:, taps_n - 1:taps_n], None, ALU.mult))
                        for k in range(taps_n - 1):
                            last = v.scalar_tensor_tensor(out=out, in0=src[:, k:k + SEQ], scalar=w[:, k:k + 1], in1=out,
                                                          op0=ALU.mult, op1=ALU.add)
                            if k < taps_n - 2:
                                step(last)
                        return last

                    for n in range(3):
                        v.wait_ge(s["raw_copied"], n + 1)
                        convolve(act[:, n, :], raw[:, n, :], taps[:, n, :], TAPS).then_inc(s["conv_ready"], 1)
                    for n, dst in enumerate((qk[:, 0, :], qk[:, 1, :], vh[:, MID - 1:])):
                        v.wait_ge(s["th_ready"], n + 1)
                        v.scalar_tensor_tensor(out=dst, in0=th[:], scalar=1.0, in1=act[:, n, :], op0=ALU.add,
                                               op1=ALU.mult).then_inc(s["silu_ready"], 1)
                    v.wait_ge(s["silu_ready"], 3)
                    convolve(lm[:, 0, :], vh[:, MID - LOCAL:], wide_taps[:, 0:LOCAL], LOCAL).then_inc(s["done"], 1)
                    convolve(lm[:, 1, :], vh[:], wide_taps[:, LOCAL:], MID).then_inc(s["done"], 1)
                    v.wait_ge(s["done"], 2)
            st.end_step()
        with Stage(nc, "a3d") as st:
            l3_chunk_steps(nc, st, XNT, c, b, wb, masks, qk, vh, lm, S, outs)


def l3_chunk_steps(nc, st, XNT, c, b, wb, masks, qk, vh, lm, S, outs):
    four = [P, HEADS3, P]
    heads = [P, HEADS3, HD3]
    K = len(LEVELS)
    xs, q, k0, kn, kn_tok, q2, k2, R, u = (st.sb(n, [P, P]) for n in
                                           ("xs", "q", "k0", "kn", "kn_tok", "q2", "k2", "R", "u"))
    vlm = st.sb("vlm", [P, 3, P])
    norms, rnorms = (st.sb(n, [P, 2, HEADS3]) for n in ("norms", "rnorms"))
    beta, nbeta, tb = (st.sb(n, [P, HEADS3]) for n in ("beta", "nbeta", "tb"))
    N, Nlev, AT = st.sb("N", four), st.sb("Nlev", [P, K, HEADS3, P]), st.sb("AT", four)
    T, XT, Zt = (st.sb(n, four) for n in ("T", "XT", "Zt"))
    small, tok, ups, sps = (st.ps(n, four) for n in ("small", "tok", "ups", "sps"))
    big = st.ps("big", (P, 4, 4, P))
    zt, tps, xps, os_ = (big[:, n] for n in range(4))
    s = st.sems("copied q_ready sq_ready small_ready tanh_ready sqrt_in sqrt_ready tok_ready kn_tok_ready kn_ps "
                "kn_ready gram_ready N_ready Nlev_ready qk_ready AT_ready kS_ready R_ready zt_ps zt_ready t_ps t_ready "
                "x_ps x_ready u_ps u_ready o_ps s_ps done vtok_ready chain")

    def head(h):
        return slice(h * HD3, (h + 1) * HD3)

    with nc.Fori(0, BLOCKS) as ch:
        with nc.Block(no_gpsimd_drain=True) as block:
            @block.gpsimd
            def _(g):
                g.tensor_copy(k0[:], qk[:, 1, ds(ch * P, P)])
                g.tensor_copy(q[:], qk[:, 0, ds(ch * P, P)]).then_inc(s["q_ready"], 1)
                g.tensor_copy(xs[:], XNT[:, ds(b * SEQ + ch * P, P)])
                g.tensor_copy(vlm[:, 0, :], vh[:, ds(ch * P + (MID - 1), P)])
                g.tensor_copy(vlm[:, 1:3, :], lm[:, :, ds(ch * P, P)]).then_inc(s["copied"], 1)
                g.wait_ge(s["N_ready"], 1)
                for k in range(K):
                    g.tensor_tensor(Nlev[:, k], N[:], masks[:, k:k + 1, :].broadcast_to(four), ALU.mult).then_inc(s["Nlev_ready"], 1)

            @block.scalar
            def _(a):
                a.wait_ge(s["q_ready"], 1)
                a.activation(k2[:], k0[:], ACT.Square)
                a.activation(q2[:], q[:], ACT.Square).then_inc(s["sq_ready"], 1)
                a.wait_ge(s["small_ready"], 1)
                a.activation(tb[:], small[:, 0, 2 * HEADS3:3 * HEADS3], ACT.Tanh, scale=0.5).then_inc(s["tanh_ready"], 1)
                a.wait_ge(s["sqrt_in"], 1)
                a.activation(norms[:], norms[:], ACT.Sqrt).then_inc(s["sqrt_ready"], 1)
                a.wait_ge(s["kn_ps"], 1)
                a.activation(kn[:], tok[:, 3, :], ACT.Copy).then_inc(s["kn_ready"], 1)
                for k in range(1, K):
                    a.wait_ge(s["zt_ps"], k + 1)
                    if k >= 2:
                        a.wait_ge(s["x_ps"], k - 1)
                    a.activation(Zt[:], zt, ACT.Copy).then_inc(s["zt_ready"], 1)

            @block.tensor
            def _(pe):
                def heads_of(out, lhs, rhs, sem):
                    for h in range(HEADS3):
                        last = pe.matmul(out[:, h, :], lhs(h), rhs(h), start=True, stop=True)
                    last.then_inc(sem, 1)

                pe.wait_ge(s["copied"], 1)
                pe.transpose(tok[:, 0, :], k0[:], c.ident)
                for n in range(3):
                    last = pe.transpose(ups[:, n, :], vlm[:, n, :], c.ident)
                last.then_inc(s["tok_ready"], 1)
                pe.wait_ge(s["sq_ready"], 1)
                pe.matmul(small[:, 0, 0:HEADS3], q2[:], c.head_blocks[:, 0:P:HD3], start=True, stop=True)
                pe.matmul(small[:, 0, HEADS3:2 * HEADS3], k2[:], c.head_blocks[:, 0:P:HD3], start=True, stop=True)
                pe.matmul(small[:, 0, 2 * HEADS3:3 * HEADS3], xs[:], wb[:], start=True, stop=True).then_inc(s["small_ready"], 1)
                pe.wait_ge(s["kn_tok_ready"], 1)
                pe.transpose(tok[:, 3, :], kn_tok[:], c.ident).then_inc(s["kn_ps"], 1)
                pe.wait_ge(s["kn_ready"], 1)
                heads_of(big[:, :, 0], lambda h: kn[head(h), :], lambda h: kn[head(h), :], s["gram_ready"])
                heads_of(big[:, :, 1], lambda h: kn[head(h), :], lambda h: q[head(h), :], s["qk_ready"])
                pe.matmul(sps[:, 0, :], kn[:], S[:], start=True, stop=True).then_inc(s["kS_ready"], 1)
                pe.wait_ge(s["N_ready"], 1)
                pe.wait_ge(s["AT_ready"], 1)
                for k in range(K):
                    pe.wait_ge(s["Nlev_ready"], k + 1)
                    if k >= 1:
                        pe.wait_ge(s["t_ready"], k)
                    heads_of(zt, lambda h: Nlev[:, k, h, :], lambda h: c.ident if k == 0 else T[:, h, :], s["zt_ps"])
                    if k >= 1:
                        pe.wait_ge(s["zt_ready"], k)
                        pe.wait_ge(s["x_ready"], k)
                        if k < K - 1:
                            heads_of(tps, lambda h: XT[:, h, :], lambda h: Zt[:, h, :], s["t_ps"])
                        heads_of(xps, lambda h: Zt[:, h, :], lambda h: XT[:, h, :], s["x_ps"])
                pe.wait_ge(s["x_ready"], K)
                pe.wait_ge(s["R_ready"], 1)
                pe.wait_ge(s["vtok_ready"], 1)
                for h in range(HEADS3):
                    last = pe.matmul(ups[:, 0, head(h)], XT[:, h, :], R[:, head(h)], start=True, stop=True)
                last.then_inc(s["u_ps"], 1)
                pe.matmul(os_[:, 0, :], q[:], S[:], start=True, stop=False)
                pe.wait_ge(s["u_ready"], 1)
                for h in range(HEADS3):
                    last = pe.matmul(os_[:, 0, head(h)], AT[:, h, :], u[:, head(h)], start=False, stop=(h == HEADS3 - 1))
                last.then_inc(s["o_ps"], 1)
                pe.matmul(sps[:, 0, :], kn_tok[:], u[:], start=True, stop=True).then_inc(s["s_ps"], 1)

            @block.vector
            def _(v):
                step = Chain(v, s["chain"])
                mine = outs[:, ds(b * BLOCKS + ch, 1), :, :].rearrange("p t n d -> p (t n) d")
                v.wait_ge(s["small_ready"], 1)
                v.wait_ge(s["tanh_ready"], 1)
                step(v.tensor_scalar(beta[:], tb[:], 0.5, 0.5, ALU.mult, ALU.add))
                v.tensor_scalar(nbeta[:], beta[:], -1.0, None, ALU.mult)
                v.tensor_scalar(norms[:].rearrange("p a h -> p (a h)"), small[:, 0, 0:2 * HEADS3], L2_EPS, None,
                                ALU.add).then_inc(s["sqrt_in"], 1)
                v.wait_ge(s["tok_ready"], 1)
                v.tensor_copy(mine[:, 3, :], ups[:, 0, :])
                v.tensor_copy(mine[:, 0:2, :], ups[:, 1:3, :]).then_inc(s["vtok_ready"], 1)
                v.wait_ge(s["sqrt_ready"], 1)
                step(v.reciprocal(rnorms[:], norms[:]))
                v.tensor_tensor(kn_tok[:].rearrange("p (h d) -> p h d", h=HEADS3),
                                tok[:, 0, :].rearrange("p (h d) -> p h d", h=HEADS3),
                                spread(rnorms[:, 1, :], HD3), ALU.mult).then_inc(s["kn_tok_ready"], 1)
                v.wait_ge(s["qk_ready"], 1)
                step(v.tensor_tensor(N[:], big[:, :, 0], c.strict.unsqueeze(1).broadcast_to(four), ALU.mult))
                v.tensor_tensor(N[:], N[:], spread(nbeta[:], P), ALU.mult).then_inc(s["N_ready"], 1)
                v.tensor_tensor(AT[:], big[:, :, 1], c.upto.unsqueeze(1).broadcast_to(four), ALU.mult).then_inc(s["AT_ready"], 1)
                v.wait_ge(s["kS_ready"], 1)
                v.wait_ge(s["vtok_ready"], 1)
                v.tensor_tensor(R[:], mine[:, 3, :], sps[:, 0, :], ALU.subtract).then_inc(s["R_ready"], 1)
                idn = c.ident.unsqueeze(1).broadcast_to(four)
                v.wait_ge(s["zt_ps"], 1)
                v.tensor_tensor(T[:], zt, idn, ALU.add).then_inc(s["t_ready"], 1)
                v.wait_ge(s["Nlev_ready"], 1)
                v.tensor_tensor(XT[:], Nlev[:, 0], idn, ALU.add).then_inc(s["x_ready"], 1)
                for k in range(1, K):
                    if k < K - 1:
                        v.wait_ge(s["t_ready"], k)
                        v.wait_ge(s["t_ps"], k)
                        v.tensor_tensor(T[:], tps, T[:], ALU.add).then_inc(s["t_ready"], 1)
                    v.wait_ge(s["x_ready"], k)
                    v.wait_ge(s["x_ps"], k)
                    v.tensor_tensor(XT[:], xps, XT[:], ALU.add).then_inc(s["x_ready"], 1)
                v.wait_ge(s["u_ps"], 1)
                v.tensor_tensor(u[:].rearrange("p (h d) -> p h d", h=HEADS3),
                                ups[:, 0, :].rearrange("p (h d) -> p h d", h=HEADS3),
                                spread(beta[:], HD3), ALU.mult).then_inc(s["u_ready"], 1)
                v.wait_ge(s["o_ps"], 1)
                v.tensor_tensor(mine[:, 2, :].rearrange("p (h d) -> p h d", h=HEADS3),
                                os_[:, 0, :].rearrange("p (h d) -> p h d", h=HEADS3),
                                spread(rnorms[:, 0, :], HD3), ALU.mult)
                v.wait_ge(s["s_ps"], 1)
                step(v.tensor_tensor(R[:], sps[:, 0, :], c.head_blocks, ALU.mult))
                v.tensor_tensor(S[:], S[:], R[:], ALU.add).then_inc(s["done"], 1)
                v.wait_ge(s["done"], 1)
        st.end_step()


def l3_router_stage(nc, outer, X, XNT, c, d, outs):
    HC = [(0, P), (P, 2 * P), (2 * P, HIDDEN3)]
    Q = HEADS3 * PATHS
    rw1a = outer.sb("rw1a", [P, HIDDEN3])
    rw1b = outer.sb("rw1b", [FEATS, HIDDEN3])
    rb1 = outer.sb("rb1", [1, HIDDEN3])
    rw2 = outer.sb("rw2", [P, 3, Q])
    rb2 = outer.sb("rb2", [1, Q])
    wo = outer.sb("wo", [P, P])
    rows = outer.sb("rows", [1, 2, P])
    mixw = outer.sb("mixw", [P, 2, P])
    with Stage(nc, "a3v") as st:
        pr = st.ps("pr", (P, 2, P))
        s = st.sems("loaded rows_ready rows_ps")
        with nc.Block(no_gpsimd_drain=True) as block:
            @block.sync
            def _(sp):
                loads = [(rw1a[:], d["L3_attn_r_w1"][0:P, :]), (rw1b[:], d["L3_attn_r_w1"][P:P + FEATS, :]),
                         (rb1[:], d["L3_attn_r_b1"].rearrange("(a d) -> a d", a=1)),
                         (rb2[:], d["L3_attn_r_b2"].rearrange("(a d) -> a d", a=1)), (wo[:], d["L3_attn_Wo"]),
                         (rows[:, 0, :], d["L3_attn_mix_w"].rearrange("(a h) e -> a (h e)", a=1))]
                loads += [(rw2[0:k1 - k0, n, :], d["L3_attn_r_w2"][k0:k1, :]) for n, (k0, k1) in enumerate(HC)]
                loads += [(rows[:, 1, h * HD3:(h + 1) * HD3], d["L3_attn_onorm_w"].rearrange("(a d) -> a d", a=1))
                          for h in range(HEADS3)]
                for dst, src in loads:
                    sp.dma_start(dst, src).then_inc(s["loaded"], 16)
                assert len(loads) == 13
                sp.wait_ge(s["loaded"], 16 * 13)

            @block.tensor
            def _(pe):
                pe.wait_ge(s["loaded"], 16 * 13)
                pe.matmul(flat(pr[:]), c.ones[0:1, :], rows[:].rearrange("a n d -> a (n d)"), start=True,
                          stop=True).then_inc(s["rows_ps"], 1)

            @block.vector
            def _(v):
                v.wait_ge(s["rows_ps"], 1)
                v.tensor_copy(mixw[:], pr[:])
                for n, (k0, k1) in enumerate(HC):
                    v.tensor_scalar(rw2[0:k1 - k0, n, :], rw2[0:k1 - k0, n, :], 0.5, None, ALU.mult)
        st.end_step()

    with Stage(nc, "a3s") as st:
        NP = len(PAIRS)
        xs = st.sb("xs", [P, G, P])
        o = st.sb("o", [P, G * PATHS, P])
        mean, var = st.sb("mean", [P, G * Q]), st.sb("var", [P, G * Q])
        cent = st.sb("cent", [P, G * Q, HD3])
        prod = st.sb("prod", [P, G, NP, P])
        cross = st.sb("cross", [P, G, NP * HEADS3])
        F = st.sb("F", [P, G, FEATS])
        FT = st.sb("FT", [FEATS, G, P])
        th, hid = st.sb("th", [P, 2, HIDDEN3]), st.sb("hid", [P, 2, HIDDEN3])
        hT = st.sb("hT", [P, 2, 3, P])
        lg, w = (st.sb(n, [P, G * HEADS3, PATHS]) for n in ("lg", "w"))
        hmax, total, ms, rms = (st.sb(n, [P, G * HEADS3]) for n in ("hmax", "total", "ms", "rms"))
        mixed, sq = st.sb("mixed", [P, G * HEADS3, HD3]), st.sb("sq", [P, G * HEADS3, HD3])
        mT = st.sb("mT", [P, G, P])
        FTp = st.ps("FTp", (P, G, P))
        h1 = st.ps("h1", (P, 2, 512))
        hTp = st.ps("hTp", (P, 2, 512))
        lgp = st.ps("lgp", (P, G, Q))
        mTp = st.ps("mTp", (P, G, P))
        outp = st.ps("outp", (P, G, P))
        s = st.sems("xs_ready F_ready FT_ps FT_ready h1_ready th_ready hid_ready hT_ps hT_ready lg_ready shifted exps "
                    "ms_ready rms_ready mixed_ready mT_ps mT_ready out_ps o_ready added chain")
        with nc.Fori(0, TILES // G) as i:
            with nc.Block(no_gpsimd_drain=True) as block:
                @block.gpsimd
                def _(g):
                    g.tensor_copy(o[:], outs[:, ds(i * G, G), :, :].rearrange("p t n d -> p (t n) d")).then_inc(s["o_ready"], 1)

                @block.scalar
                def _(a):
                    a.activation(xs[:].rearrange("p t d -> p (t d)"), XNT[:, ds(i * G * P, G * P)],
                                 ACT.Copy).then_inc(s["xs_ready"], 1)
                    a.wait_ge(s["FT_ps"], 1)
                    a.activation(FT[:], FTp[0:FEATS], ACT.Copy).then_inc(s["FT_ready"], 1)
                    for j in range(G):
                        a.wait_ge(s["h1_ready"], j + 1)
                        if j >= 2:
                            a.wait_ge(s["hid_ready"], j - 1)
                        a.activation(th[:, j % 2, :], h1[:, j % 2, 0:HIDDEN3], ACT.Tanh, scale=0.5).then_inc(s["th_ready"], 1)
                        a.wait_ge(s["hT_ps"], j + 1)
                        a.activation(hT[:, j % 2, 0:2, :].rearrange("p n d -> p (n d)"), hTp[:, j % 2, 0:2 * P], ACT.Copy)
                        last = a.activation(hT[0:HIDDEN3 - 2 * P, j % 2, 2, :], hTp[0:HIDDEN3 - 2 * P, j % 2, 2 * P:3 * P],
                                            ACT.Copy)
                        last.then_inc(s["hT_ready"], 1)
                    a.wait_ge(s["shifted"], 1)
                    a.activation(lg[:], lg[:], ACT.Exp).then_inc(s["exps"], 1)
                    for n in range(2):
                        a.wait_ge(s["ms_ready"], n + 1)
                        a.activation(rms[:], ms[:], ACT.Sqrt).then_inc(s["rms_ready"], 1)
                    a.wait_ge(s["mT_ps"], 1)
                    a.activation(mT[:], mTp[:], ACT.Copy).then_inc(s["mT_ready"], 1)

                @block.tensor
                def _(pe):
                    pe.wait_ge(s["F_ready"], 1)
                    for j in range(G):
                        last = pe.transpose(FTp[0:FEATS, j, :], F[:, j, :], c.ident)
                    last.then_inc(s["FT_ps"], 1)
                    pe.wait_ge(s["xs_ready"], 1)
                    pe.wait_ge(s["FT_ready"], 1)

                    def hidden(j):
                        if j >= 2:
                            pe.wait_ge(s["hid_ready"], j - 1)
                        o1 = h1[:, j % 2, 0:HIDDEN3]
                        pe.matmul(o1, xs[:, j, :], rw1a[:], start=True, stop=False)
                        pe.matmul(o1, FT[:, j, :], rw1b[:], start=False, stop=False)
                        pe.matmul(o1, c.ones[0:1, :], rb1[:], start=False, stop=True).then_inc(s["h1_ready"], 1)

                    hidden(0)
                    for j in range(G):
                        if j + 1 < G:
                            hidden(j + 1)
                        pe.wait_ge(s["hid_ready"], j + 1)
                        if j >= 2:
                            pe.wait_ge(s["hT_ready"], j - 1)
                        for n, (k0, k1) in enumerate(HC):
                            last = pe.transpose(hTp[0:k1 - k0, j % 2, n * P:(n + 1) * P], hid[:, j % 2, k0:k1], c.ident)
                        last.then_inc(s["hT_ps"], 1)
                        pe.wait_ge(s["hT_ready"], j + 1)
                        for n, (k0, k1) in enumerate(HC):
                            pe.matmul(lgp[:, j, :], hT[0:k1 - k0, j % 2, n, :], rw2[0:k1 - k0, n, :], start=(n == 0), stop=False)
                        pe.matmul(lgp[:, j, :], c.ones[0:1, :], rb2[:], start=False, stop=True).then_inc(s["lg_ready"], 1)
                    pe.wait_ge(s["mixed_ready"], 1)
                    for j in range(G):
                        last = pe.transpose(mTp[:, j, :], mixed[:, j * HEADS3:(j + 1) * HEADS3, :]
                                            .rearrange("p h e -> p (h e)"), c.ident)
                    last.then_inc(s["mT_ps"], 1)
                    pe.wait_ge(s["mT_ready"], 1)
                    for j in range(G):
                        last = pe.matmul(outp[:, j, :], mT[:, j, :], wo[:], start=True, stop=True)
                    last.then_inc(s["out_ps"], 1)

                @block.vector
                def _(v):
                    step = Chain(v, s["chain"])
                    v.wait_ge(s["o_ready"], 1)
                    by_head = o[:].rearrange("p n (h e) -> p (n h) e", h=HEADS3)
                    step(v.tensor_reduce(mean[:], by_head, AX.X, ALU.add))
                    step(v.tensor_scalar(mean[:], mean[:], 1.0 / HD3, None, ALU.mult))
                    step(v.tensor_tensor(cent[:], by_head, spread(mean[:], HD3), ALU.subtract))
                    step(v.tensor_tensor(cent[:], cent[:], cent[:], ALU.mult))
                    step(v.tensor_reduce(var[:], cent[:], AX.X, ALU.add))
                    by_tile = o[:].rearrange("p (t n) d -> p t n d", t=G)
                    for n, (x, y) in enumerate(PAIRS):
                        last = v.tensor_tensor(prod[:, :, n, :], by_tile[:, :, x, :], by_tile[:, :, y, :], ALU.mult)
                    step(last)
                    step(v.tensor_reduce(cross[:].rearrange("p t n -> p (t n)"),
                                         prod[:].rearrange("p t n (h e) -> p (t n h) e", h=HEADS3), AX.X, ALU.add))
                    stats = F[:, :, 0:2 * Q].rearrange("p t (n w h) -> p t n w h", n=PATHS, w=2)
                    for j in range(G):
                        v.tensor_copy(stats[:, j, :, 0, :], mean[:, j * Q:(j + 1) * Q].rearrange("p (n h) -> p n h", n=PATHS))
                        v.tensor_scalar(stats[:, j, :, 1, :], var[:, j * Q:(j + 1) * Q].rearrange("p (n h) -> p n h", n=PATHS),
                                        1.0 / (HD3 - 1), None, ALU.mult)
                    v.tensor_scalar(F[:, :, 2 * Q:], cross[:], 1.0 / HD3, None, ALU.mult).then_inc(s["F_ready"], 1)
                    for j in range(G):
                        v.wait_ge(s["th_ready"], j + 1)
                        if j >= 2:
                            v.wait_ge(s["hT_ps"], j - 1)
                        v.scalar_tensor_tensor(out=hid[:, j % 2, :], in0=th[:, j % 2, :], scalar=1.0,
                                               in1=h1[:, j % 2, 0:HIDDEN3], op0=ALU.add, op1=ALU.mult).then_inc(s["hid_ready"], 1)
                    v.wait_ge(s["lg_ready"], G)
                    logit = lgp[:].rearrange("p t (h n) -> p (t h) n", h=HEADS3)
                    step(v.tensor_reduce(hmax[:], logit, AX.X, ALU.max))
                    v.tensor_tensor(lg[:], logit, spread(hmax[:], PATHS), ALU.subtract).then_inc(s["shifted"], 1)
                    v.wait_ge(s["exps"], 1)
                    step(v.tensor_reduce(total[:], lg[:], AX.X, ALU.add))
                    step(v.reciprocal(total[:], total[:]))
                    step(v.tensor_tensor(w[:], lg[:], spread(total[:], PATHS), ALU.mult))
                    step(v.tensor_scalar(w[:], w[:], 1.0 - 4.0 * FLOOR, FLOOR, ALU.mult, ALU.add))
                    for j in range(G):
                        wj = w[:, j * HEADS3:(j + 1) * HEADS3, :].rearrange("p h n -> p n h")
                        last = v.tensor_tensor(cent[:, j * Q:(j + 1) * Q, :].rearrange("p (n h) e -> p n h e", n=PATHS),
                                               by_head[:, j * Q:(j + 1) * Q, :].rearrange("p (n h) e -> p n h e", n=PATHS),
                                               wj.unsqueeze(3).broadcast_to([P, PATHS, HEADS3, HD3]), ALU.mult)
                    step(last)
                    for j in range(G):
                        last = v.tensor_reduce(mixed[:, j * HEADS3:(j + 1) * HEADS3, :].rearrange("p h e -> p (h e)"),
                                               cent[:, j * Q:(j + 1) * Q, :].rearrange("p (n h) e -> p (h e) n", n=PATHS),
                                               AX.X, ALU.add)
                    step(last)
                    for n in range(2):
                        step(v.tensor_tensor(sq[:], mixed[:], mixed[:], ALU.mult))
                        step(v.tensor_reduce(ms[:], sq[:], AX.X, ALU.add))
                        v.tensor_scalar(ms[:], ms[:], 1.0 / HD3, MIX_EPS, ALU.mult, ALU.add).then_inc(s["ms_ready"], 1)
                        v.wait_ge(s["rms_ready"], n + 1)
                        step(v.reciprocal(total[:], rms[:]))
                        step(v.tensor_tensor(mixed[:], mixed[:], spread(total[:], HD3), ALU.mult))
                        last = v.tensor_tensor(mixed[:].rearrange("p (t h) e -> p t (h e)", t=G),
                                               mixed[:].rearrange("p (t h) e -> p t (h e)", t=G),
                                               mixw[:, n:n + 1, :].broadcast_to([P, G, P]), ALU.mult)
                        if n == 0:
                            step(last)
                    last.then_inc(s["mixed_ready"], 1)
                    v.wait_ge(s["out_ps"], 1)
                    v.tensor_tensor(X[:, ds(i * G, G), :], outp[:], X[:, ds(i * G, G), :], ALU.add).then_inc(s["added"], 1)
                    v.wait_ge(s["added"], 1)
            st.end_step()



def l3_ffn_stage(nc, X, XNT, c, router_w, router_b, expert_w, expert_b):
    with Stage(nc, "f3") as outer:
        rwT = outer.sb("rwT", [P, EXPERTS])
        ewT = outer.sb("ewT", [P, EXPERTS, P])
        rb = outer.sb("rb", [1, EXPERTS])
        eb = outer.sb("eb", [1, EXPERTS * P])
        load_turned(nc, "f3t", [(rwT[:], router_w)] + [(ewT[:, e, :], expert_w[e]) for e in range(EXPERTS)], c)
        with Stage(nc, "f3w") as st:
            s = st.sems("loaded")
            with nc.Block(no_gpsimd_drain=True) as block:
                @block.sync
                def _(sp):
                    sp.dma_start(rb[:], router_b.rearrange("(a d) -> a d", a=1)).then_inc(s["loaded"], 16)
                    sp.dma_start(eb[:], expert_b.rearrange("(a e) d -> a (e d)", a=1)).then_inc(s["loaded"], 16)
                    sp.wait_ge(s["loaded"], 32)
            st.end_step()
        with Stage(nc, "f3s") as st:
            xs = st.sb("xs", [P, G * P])
            lg, ex, choice = (st.sb(n, [P, G, EXPERTS]) for n in ("lg", "ex", "choice"))
            top = st.sb("top", [P, G, 8])
            at = st.sb("at", [P, G, 8], U32)
            atf = st.sb("atf", [P, G, 8])
            total, weight = (st.sb(n, [P, G]) for n in ("total", "weight"))
            picked = st.sb("picked", [P, 2, EXPERTS, P])
            summed = st.sb("summed", [P, G, P])
            logits = st.ps("logits", (P, G, EXPERTS))
            y = st.ps("y", (P, 2, EXPERTS, P))
            s = st.sems("xs_ready logits_ready y_ready shifted exps y_used added chain")
            with nc.Fori(0, TILES // G) as i:
                with nc.Block(no_gpsimd_drain=True) as block:
                    @block.scalar
                    def _(a):
                        a.activation(xs[:], XNT[:, ds(i * G * P, G * P)], ACT.Copy).then_inc(s["xs_ready"], 1)
                        a.wait_ge(s["shifted"], 1)
                        a.activation(ex[:], ex[:], ACT.Exp).then_inc(s["exps"], 1)

                    @block.tensor
                    def _(pe):
                        pe.wait_ge(s["xs_ready"], 1)
                        for j in range(G):
                            pe.matmul(logits[:, j, :], xs[:, j * P:(j + 1) * P], rwT[:], start=True, stop=False)
                            last = pe.matmul(logits[:, j, :], c.ones[0:1, :], rb[:], start=False, stop=True)
                        last.then_inc(s["logits_ready"], 1)
                        for j in range(G):
                            if j >= 2:
                                pe.wait_ge(s["y_used"], j - 1)
                            for k in range(0, EXPERTS, 4):
                                o = y[:, j % 2, k:k + 4, :].rearrange("p e d -> p (e d)")
                                pe.matmul(o, xs[:, j * P:(j + 1) * P], ewT[:, k:k + 4, :].rearrange("p e d -> p (e d)"),
                                          start=True, stop=False)
                                last = pe.matmul(o, c.ones[0:1, :], eb[:, k * P:(k + 4) * P], start=False, stop=True)
                            last.then_inc(s["y_ready"], 1)

                    @block.vector
                    def _(v):
                        step = Chain(v, s["chain"])
                        v.wait_ge(s["logits_ready"], 1)
                        step(v.tensor_copy(lg[:], logits[:]))
                        for j in range(G):
                            last = v.max(top[:, j, :], lg[:, j, :])
                        step(last)
                        v.tensor_tensor(ex[:], lg[:], top[:, :, 0:1].broadcast_to([P, G, EXPERTS]),
                                        ALU.subtract).then_inc(s["shifted"], 1)
                        for j in range(G):
                            last = v.max_index(at[:, j, :], top[:, j, :], lg[:, j, :])
                        step(last)
                        step(v.tensor_copy(atf[:], at[:]))
                        v.wait_ge(s["exps"], 1)
                        step(v.tensor_reduce(total[:], ex[:], AX.X, ALU.add))
                        step(v.reciprocal(weight[:], total[:]))
                        for j in range(G):
                            last = v.tensor_scalar(choice[:, j, :], c.count8, atf[:, j, 0:1], weight[:, j:j + 1],
                                                   ALU.is_equal, ALU.mult)
                        step(last)
                        for j in range(G):
                            v.wait_ge(s["y_ready"], j + 1)
                            v.tensor_tensor(picked[:, j % 2], y[:, j % 2], spread(choice[:, j, :], P),
                                            ALU.mult).then_inc(s["y_used"], 1)
                            v.wait_ge(s["y_used"], j + 1)
                            step(v.tensor_reduce(summed[:, j, :], picked[:, j % 2].rearrange("p e d -> p d e"),
                                                 AX.X, ALU.add))
                        v.tensor_tensor(X[:, ds(i * G, G), :], summed[:], X[:, ds(i * G, G), :],
                                        ALU.add).then_inc(s["added"], 1)
                        v.wait_ge(s["added"], 1)
                st.end_step()


def build(nc, d, out, stages):
    with ExitStack() as ctx:
        def sb(name, shape):
            return ctx.enter_context(nc.sbuf_tensor(name, shape, F32))

        X = sb("X", [P, TILES, P])
        consts = sb("consts", [P, len(SQUARES) * P + 8])
        c = Constants(consts)
        load_stage(nc, X, d["L0_attn_x"], d["const_squares"], c)

        for k, stage in enumerate(SUBLAYERS):
            if k in stages:
                with ExitStack() as inner:
                    XN = inner.enter_context(nc.sbuf_tensor(f"XN{k}", [P, TILES, P], F32))
                    XNT = inner.enter_context(nc.sbuf_tensor(f"XNT{k}", [P, TILES * P], F32))
                    layernorm_stage(nc, X, XN, XNT, c)
                    stage(nc, d, X, XN, XNT, c)

        with Stage(nc, "store") as st:
            s = st.sems("stored")
            with nc.Block(no_gpsimd_drain=True) as block:
                @block.sync
                def _(sp):
                    sp.dma_start(out.rearrange("b (t p) d -> p (b t) d", p=P), X[:]).then_inc(s["stored"], 16)
                    sp.wait_ge(s["stored"], 16)
            st.end_step()


def sub0(nc, d, X, XN, XNT, c):
    l0_attention_stage(nc, X, XNT, c, d["L0_attn_W_Q"], d["L0_attn_W_K"], d["L0_attn_W_V"], d["L0_attn_W_O"],
                       d["const_alibi"], d["const_key_pos"])


def sub1(nc, d, X, XN, XNT, c):
    l0_ffn_stage(nc, X, XNT, c, d["L0_ffn_w_gate"], d["L0_ffn_w_expert"], d["L0_ffn_b_expert"])


def sub2(nc, d, X, XN, XNT, c):
    l1_attention_stage(nc, X, XNT, c, d)


def sub3(nc, d, X, XN, XNT, c):
    l1_ffn_stage(nc, X, XN, c, d)


def sub4(nc, d, X, XN, XNT, c):
    l2_attention_stage(nc, X, XN, XNT, c)


def sub5(nc, d, X, XN, XNT, c):
    l2_ffn_stage(nc, X, XNT, c, d["L2_ffn_gate_w"], d["L2_ffn_w1"], d["L2_ffn_w2"], d["L2_ffn_w3"])


def sub6(nc, d, X, XN, XNT, c):
    l3_attention_stage(nc, X, XNT, c, d)


def sub7(nc, d, X, XN, XNT, c):
    l3_ffn_stage(nc, X, XNT, c, d["L3_ffn_router_w"], d["L3_ffn_router_b"], d["L3_ffn_expert_w"],
                 d["L3_ffn_expert_b"])


def more_constants():
    j, i = np.arange(P)[:, None], np.arange(P)[None, :]
    masks = [(j // (2 * n) == i // (2 * n)) & (j // n % 2 == 0) & (i // n % 2 == 1) for n in LEVELS]
    half = np.arange(0, HDW, 2, dtype=np.float32)
    t = np.arange(SEQ, dtype=np.float32)
    freqs = t[:, None] * (np.float32(1.0) / np.float32(10000.0) ** (half / np.float32(HDW)))[None, :]
    power = (t - SEQ // 2) / np.float32(WINDOW // 2)
    scale = ((half + 0.4 * HDW) / (1.4 * HDW)).astype(np.float64)[None, :] ** power[:, None]
    cos, sin = np.cos(freqs.astype(np.float64)), np.sin(freqs.astype(np.float64))
    rope = [np.concatenate([cos * w, cos * w], 1) if n == 0 else np.concatenate([-sin * w, sin * w], 1)
            for w in (scale, 1.0 / scale) for n in range(2)]
    rope = np.stack(rope).reshape(4, BLOCKS, P, HDW).transpose(2, 0, 1, 3)
    query = (np.arange(BLOCKS)[None, :] * P + np.arange(P)[:, None])[:, :, None]
    key = (np.arange(BLOCKS)[:, None] * P - WINDOW + np.arange(KEYS)[None, :])[None]
    seen = (key <= query) & (key >= query - WINDOW) & (key >= 0)
    return {"const_level_masks": np.stack(masks, axis=1), "const_rope": rope,
            "const_band": np.where(seen, 0.0, NEG),
            "const_shifts": np.stack([j == i - 1, (j == P - 1) & (i == 0)], axis=1)}


SUBLAYERS = [sub0, sub1, sub2, sub3, sub4, sub5, sub6, sub7]

SQUARES = ["ident", "ones", "upto", "after", "strict", "neg_upper", "head_blocks"]


def constants():
    i = np.arange(P)
    row, col = i[:, None], i[None, :]
    squares = {
        "ident": row == col,
        "ones": np.ones((P, P)),
        "upto": row <= col,
        "after": row > col,
        "strict": row < col,
        "neg_upper": np.where(col > row, NEG, 0.0),
        "head_blocks": row // 32 == col // 32,
    }
    table = np.concatenate([squares[n].astype(np.float32) for n in SQUARES]
                           + [np.broadcast_to(np.arange(8, dtype=np.float32), (P, 8))], axis=1)
    slopes = 1.0 / np.float32(256.0) ** ((np.arange(HEADS0, dtype=np.float32) + 1) / HEADS0)
    alibi = np.zeros((1, HEADS0 + 1, AUG), np.float32)
    alibi[0, :HEADS0, HD0] = slopes
    alibi[0, HEADS0, HD0] = 1.0
    made = {"const_squares": table, "const_alibi": alibi,
            "const_key_pos": np.arange(SEQ, dtype=np.float32)[None, :] - SEQ // 2}
    made.update(more_constants())
    return {k: np.ascontiguousarray(a, dtype=np.float32) for k, a in made.items()}


_STAGES = range(8)


def kernel(**inputs):
    import concourse.bacc as _bacc
    from concourse.bass_utils import run_bass_kernel_spmd as _run

    nc = _bacc.Bacc("TRN2", target_bir_lowering=False, num_devices=1)
    arrays, d = {}, {}
    for name, a in {**inputs, **constants()}.items():
        a = np.ascontiguousarray(a)
        arrays[f"in_{name}_dram"] = a
        d[name] = nc.dram_tensor(f"in_{name}_dram", a.shape, mybir.dt.from_np(a.dtype), kind="ExternalInput").ap()
    out = nc.dram_tensor("out_0_dram", (BATCH, SEQ, P), F32, kind="ExternalOutput").ap()
    build(nc, d, out, _STAGES)
    r = _run(nc, [arrays], core_ids=[0])
    return r.results[0]["out_0_dram"]
```

```python
from contextlib import ExitStack

import numpy as np

import concourse.bass as bass
from concourse import mybir

F32 = mybir.dt.float32
U32 = mybir.dt.uint32
ACT = mybir.ActivationFunctionType
ALU = mybir.AluOpType
AX = mybir.AxisListType
ds = bass.ds

P = 128
BATCH = 4
BLOCKS = 8
TILES = BATCH * BLOCKS
SEQ = BLOCKS * P
G = 4
LN_EPS = 1e-5
NEG = -1e30


class Stage:

    def __init__(self, nc, name):
        self.nc, self.name, self.ctx = nc, name, ExitStack()

    def __enter__(self):
        self.ctx.__enter__()
        return self

    def __exit__(self, *exc):
        return self.ctx.__exit__(*exc)

    def sb(self, name, shape, dt=F32):
        return self.ctx.enter_context(self.nc.sbuf_tensor(f"{self.name}_{name}", shape, dt))

    def ps(self, name, shape=(P, 512)):
        return self.ctx.enter_context(self.nc.psum_tensor(f"{self.name}_{name}", list(shape), F32))

    def sems(self, names):
        made = {n: self.ctx.enter_context(self.nc.semaphore(f"{self.name}_{n}")) for n in names.split()}
        nums = sorted(sem.num for sem in made.values())
        starts = [n for n in nums if n - 1 not in nums]
        ends = [n + 1 for n in nums if n + 1 not in nums]
        self.ranges = [range(a, b) for a, b in zip(starts, ends)]
        return made

    def end_step(self):
        for r in self.ranges:
            self.nc.gpsimd.sem_clear(r)
        self.nc.all_engine_barrier(sem_only=True)


class Constants:

    def __init__(self, table):
        self.all = table
        (self.ident, self.ones, self.upto, self.after, self.strict, self.neg_upper,
         self.head_blocks) = (table[:, k * P:(k + 1) * P] for k in range(len(SQUARES)))
        self.count8 = table[:, len(SQUARES) * P:]


class Chain:

    def __init__(self, engine, sem):
        self.engine, self.sem, self.n = engine, sem, 0

    def __call__(self, ins):
        self.n += 1
        ins.then_inc(self.sem, 1)
        self.engine.wait_ge(self.sem, self.n)


def tile(X, i):
    return X[:, ds(i, 1), :].rearrange("p a d -> p (a d)")


def flat(ap):
    return ap.rearrange("p a d -> p (a d)")


def spread(ap, n):
    return ap.unsqueeze(2).broadcast_to([ap.shape[0], ap.shape[1], n])


def load_stage(nc, X, x, consts, c):
    with Stage(nc, "load") as st:
        s = st.sems("loaded")
        with nc.Block(no_gpsimd_drain=True) as block:
            @block.sync
            def _(sp):
                sp.dma_start(X[:], x.rearrange("b (t p) d -> p (b t) d", p=P)).then_inc(s["loaded"], 16)
                sp.dma_start(c.all[:], consts).then_inc(s["loaded"], 16)
                sp.wait_ge(s["loaded"], 32)
        st.end_step()


def layernorm_stage(nc, X, XN, XNT, c):
    with Stage(nc, f"ln{nc.next_id()}") as st:
        stats = st.sb("stats", [P, G, 6])
        mv = st.sb("mv", [P, G, 2])
        var = st.sb("var", [P, G])
        std = st.sb("std", [P, G])
        rstd = st.sb("rstd", [P, G])
        xs = st.sb("xs", [P, G, P])
        turned = st.ps("turned")
        s = st.sems("var_ready std_ready xs_ready turned_ready xnt_done xn_done chain")
        with nc.Fori(0, TILES // G) as i:
            with nc.Block(no_gpsimd_drain=True) as block:
                @block.vector
                def _(v):
                    step = Chain(v, s["chain"])
                    for j in range(G):
                        last = v.bn_stats(stats[:, j, :], tile(X, i * G + j))
                    step(last)
                    for j in range(G):
                        last = v.bn_aggr(mv[:, j, :], stats[:, j, :])
                    step(last)
                    v.tensor_scalar(var[:], mv[:, :, 1], LN_EPS, None, ALU.add).then_inc(s["var_ready"], 1)
                    v.wait_ge(s["std_ready"], 1)
                    step(v.reciprocal(rstd[:], std[:]))
                    for j in range(G):
                        last = v.tensor_scalar(xs[:, j, :], tile(X, i * G + j), mv[:, j, 0:1], rstd[:, j:j + 1],
                                               ALU.subtract, ALU.mult)
                    last.then_inc(s["xs_ready"], 1)

                @block.scalar
                def _(a):
                    a.wait_ge(s["var_ready"], 1)
                    a.activation(std[:], var[:], ACT.Sqrt).then_inc(s["std_ready"], 1)
                    a.wait_ge(s["turned_ready"], 1)
                    a.activation(XNT[:, ds(i * G * P, G * P)], turned[:], ACT.Copy).then_inc(s["xnt_done"], 1)
                    a.wait_ge(s["xnt_done"], 1)

                @block.tensor
                def _(pe):
                    pe.wait_ge(s["xs_ready"], 1)
                    for j in range(G):
                        last = pe.transpose(turned[:, j * P:(j + 1) * P], xs[:, j, :], c.ident)
                    last.then_inc(s["turned_ready"], 1)

                @block.gpsimd
                def _(g):
                    g.wait_ge(s["xs_ready"], 1)
                    g.tensor_copy(XN[:, ds(i * G, G), :], xs[:]).then_inc(s["xn_done"], 1)
                    g.wait_ge(s["xn_done"], 1)
            st.end_step()


def load_turned(nc, name, pairs, c):
    with Stage(nc, name) as st:
        raw = st.sb("raw", [P, len(pairs), P])
        turned = st.ps("turned", (P, 4, 512))
        s = st.sems("loaded turned_ready copied")
        with nc.Block(no_gpsimd_drain=True) as block:
            @block.sync
            def _(sp):
                for n, (dst, src) in enumerate(pairs):
                    a, b = src.shape
                    sp.dma_start(raw[0:a, n, 0:b], src).then_inc(s["loaded"], 16)

            @block.tensor
            def _(pe):
                pe.wait_ge(s["loaded"], 16 * len(pairs))
                for n, (dst, src) in enumerate(pairs):
                    a, b = src.shape
                    if n >= 4:
                        pe.wait_ge(s["copied"], n - 3)
                    pe.transpose(turned[0:b, n % 4, 0:a], raw[0:a, n, 0:b], c.ident[0:a, 0:a]).then_inc(s["turned_ready"], 1)

            @block.vector
            def _(v):
                for n, (dst, src) in enumerate(pairs):
                    a, b = src.shape
                    v.wait_ge(s["turned_ready"], n + 1)
                    v.tensor_copy(dst, turned[0:b, n % 4, 0:a]).then_inc(s["copied"], 1)
                v.wait_ge(s["copied"], len(pairs))
        st.end_step()


HEADS0 = 16
HD0 = P // HEADS0
HG = 4
ROWS = P // HG


def l0_attention_stage(nc, X, XNT, c, W_Q, W_K, W_V, W_O, alibi_rows, key_pos):
    with Stage(nc, "a0") as outer:
        WQT, WKT, WVT, WOT = (outer.sb(n, [P, P]) for n in ("WQT", "WKT", "WVT", "WOT"))
        load_turned(nc, "a0w", [(WQT[:], W_Q), (WKT[:], W_K), (WVT[:], W_V), (WOT[:], W_O)], c)
        slope_rows = outer.sb("slope_rows", [1, HEADS0 // HG, P])
        unit_row = outer.sb("unit_row", [1, P])
        pos = outer.sb("pos", [1, SEQ])
        ones = outer.sb("ones", [1, SEQ])
        V = outer.sb("V", [P, BLOCKS, P])
        O = outer.sb("O", [P, BLOCKS, P])
        xs = outer.sb("xs", [P, SEQ])
        wq = outer.sb("wq", [P, HG, ROWS])
        wk = outer.sb("wk", [P, HG, ROWS])
        QA = outer.sb("QA", [P, HG, SEQ])
        with Stage(nc, "a0c") as st:
            s = st.sems("loaded")
            with nc.Block(no_gpsimd_drain=True) as block:
                @block.sync
                def _(sp):
                    sp.dma_start(slope_rows[:], alibi_rows[0:1, 0:HEADS0 // HG, :]).then_inc(s["loaded"], 16)
                    sp.dma_start(unit_row[:], alibi_rows[0:1, HEADS0 // HG, :]).then_inc(s["loaded"], 16)
                    sp.dma_start(pos[:], key_pos).then_inc(s["loaded"], 16)
                    sp.wait_ge(s["loaded"], 48)

                @block.vector
                def _(v):
                    v.memset(ones[:], 1.0)
                    v.memset(wq[:], 0.0)
                    v.memset(wk[:], 0.0)
                    v.memset(QA[:], 0.0)
            st.end_step()

        with nc.Fori(0, BATCH) as b:
            with Stage(nc, "a0v") as st:
                pv = st.ps("pv", (P, 2, 512))
                s = st.sems("xs_ready values copied")
                with nc.Block(no_gpsimd_drain=True) as block:
                    @block.scalar
                    def _(a):
                        a.activation(xs[:], XNT[:, ds(b * SEQ, SEQ)], ACT.Copy).then_inc(s["xs_ready"], 1)

                    @block.tensor
                    def _(pe):
                        pe.wait_ge(s["xs_ready"], 1)
                        for t in range(BLOCKS):
                            last = pe.matmul(pv[:, t // 4, (t % 4) * P:(t % 4 + 1) * P], xs[:, t * P:(t + 1) * P],
                                             WVT[:], start=True, stop=True)
                        last.then_inc(s["values"], 1)

                    @block.vector
                    def _(v):
                        v.wait_ge(s["values"], 1)
                        v.tensor_copy(flat(V[:]), flat(pv[:])).then_inc(s["copied"], 1)
                        v.wait_ge(s["copied"], 1)
                st.end_step()
            with Stage(nc, "a0h") as st:
                causal_head_steps(nc, st, c, WQT, WKT, V, O, xs, wq, wk, QA, slope_rows, unit_row, pos, ones)

            with Stage(nc, "a0o") as st:
                OT = st.sb("OT", [P, SEQ])
                turned = st.ps("turned", (P, 2 * 512))
                out = st.ps("out", (P, BLOCKS, P))
                s = st.sems("turned_ready copied out_ready added")
                with nc.Block(no_gpsimd_drain=True) as block:
                    @block.tensor
                    def _(pe):
                        for t in range(BLOCKS):
                            last = pe.transpose(turned[:, t * P:(t + 1) * P], O[:, t, :], c.ident)
                        last.then_inc(s["turned_ready"], 1)
                        pe.wait_ge(s["copied"], 1)
                        for t in range(BLOCKS):
                            last = pe.matmul(out[:, t, :], OT[:, t * P:(t + 1) * P], WOT[:], start=True, stop=True)
                        last.then_inc(s["out_ready"], 1)

                    @block.scalar
                    def _(a):
                        a.wait_ge(s["turned_ready"], 1)
                        a.activation(OT[:], turned[:], ACT.Copy).then_inc(s["copied"], 1)

                    @block.vector
                    def _(v):
                        v.wait_ge(s["out_ready"], 1)
                        v.tensor_tensor(X[:, ds(b * BLOCKS, BLOCKS), :], out[:], X[:, ds(b * BLOCKS, BLOCKS), :],
                                        ALU.add).then_inc(s["added"], 1)
                        v.wait_ge(s["added"], 1)
                st.end_step()


def causal_head_steps(nc, st, c, WQT, WKT, V, O, xs, wq, wk, QA, slope_rows, unit_row, pos, ones):
    slope = st.sb("slope", [1, P])
    KA = st.sb("KA", [P, SEQ])
    Vh = st.sb("Vh", [P, BLOCKS, HG * HD0])
    probs = st.sb("probs", [P, 2, SEQ])
    probsT = st.sb("probsT", [P, 2, SEQ])
    negmax, total, rtotal = (st.sb(n, [P, HG * BLOCKS]) for n in ("negmax", "total", "rtotal"))
    OT = st.sb("OT", [HD0, HG * BLOCKS, P])
    scores = st.ps("scores", (P, 2, 2 * 512))
    turned = st.ps("turned", (P, 2 * 512))
    outT = st.ps("outT", (P, 2, 512))
    s = st.sems("weights q_proj k_proj q_done k_done scores_ready masked max_ready probs_ready turned_ready probsT_v "
                "probsT_a outT_ready outT_used mix_ready total_ready out_done")
    items = [(j, t) for j in range(HG) for t in range(BLOCKS)]
    second = [sum(t >= 4 for _, t in items[:n + 1]) for n in range(len(items))]
    with nc.Fori(0, HEADS0 // HG) as h:
        with nc.Block(no_gpsimd_drain=True) as block:
            @block.vector
            def _(v):
                v.tensor_copy(slope[:], slope_rows[0:1, ds(h, 1), :].rearrange("p a d -> p (a d)"))
                v.tensor_scalar(wq[:, :, 0:HD0], WQT[:, ds(h * HG * HD0, HG * HD0)].rearrange("p (j d) -> p j d", j=HG),
                                HD0 ** -0.5, None, ALU.mult)
                v.tensor_copy(wk[:, :, 0:HD0], WKT[:, ds(h * HG * HD0, HG * HD0)]
                              .rearrange("p (j d) -> p j d", j=HG)).then_inc(s["weights"], 1)
                v.wait_ge(s["k_proj"], 1)
                v.tensor_copy(KA[:], scores[:, 1, :]).then_inc(s["k_done"], 1)

                def row_max(n):
                    j, t = items[n]
                    diag = scores[:, n % 2, t * P:(t + 1) * P]
                    v.wait_ge(s["scores_ready"], n + 1)
                    v.tensor_tensor(diag, diag, c.neg_upper, ALU.add).then_inc(s["masked"], 1)
                    v.wait_ge(s["masked"], n + 1)
                    v.tensor_reduce(negmax[:, n:n + 1], scores[:, n % 2, 0:(t + 1) * P], AX.X, ALU.max,
                                    negate=True).then_inc(s["max_ready"], 1)

                row_max(0)
                for n, (j, t) in enumerate(items):
                    if n + 1 < len(items):
                        row_max(n + 1)
                    w = min(512, (t + 1) * P)
                    v.wait_ge(s["turned_ready"], n + 1)
                    if n >= 2:
                        v.wait_ge(s["outT_ready"], n - 1)
                    v.tensor_copy(probsT[:, n % 2, 0:w], turned[:, 0:w]).then_inc(s["probsT_v"], 1)
                v.wait_ge(s["probs_ready"], len(items))
                v.reciprocal(rtotal[:], total[:]).then_inc(s["total_ready"], 1)
                v.wait_ge(s["total_ready"], 1)
                v.wait_ge(s["mix_ready"], 1)
                v.tensor_tensor(O[:, :, ds(h * HG * HD0, HG * HD0)].rearrange("p t (j d) -> p j t d", j=HG),
                                scores[:, 0, 0:HG * BLOCKS * HD0].rearrange("p (j t d) -> p j t d", j=HG, t=BLOCKS),
                                rtotal[:].rearrange("p (j t) -> p j t", j=HG).unsqueeze(3)
                                .broadcast_to([P, HG, BLOCKS, HD0]), ALU.mult).then_inc(s["out_done"], 1)
                v.wait_ge(s["out_done"], 1)

            @block.gpsimd
            def _(g):
                g.tensor_copy(Vh[:], V[:, :, ds(h * HG * HD0, HG * HD0)]).then_inc(s["q_done"], 1)

            @block.scalar
            def _(a):
                a.wait_ge(s["q_proj"], 1)
                for j in range(HG):
                    r = slice(j * ROWS, (j + 1) * ROWS)
                    a.activation(QA[r, j, :], scores[r, 0, :], ACT.Copy).then_inc(s["q_done"], 1)

                def exps(n):
                    j, t = items[n]
                    a.wait_ge(s["max_ready"], n + 1)
                    if n >= 2:
                        a.wait_ge(s["turned_ready"], n - 1)
                    a.activation(probs[:, n % 2, 0:(t + 1) * P], scores[:, n % 2, 0:(t + 1) * P], ACT.Exp,
                                 bias=negmax[:, n:n + 1], accum_out=total[:, n:n + 1]).then_inc(s["probs_ready"], 1)

                def copy_out(n):
                    a.wait_ge(s["outT_ready"], n + 1)
                    a.activation(OT[:, n, :], outT[0:HD0, n % 2, 0:P], ACT.Copy).then_inc(s["outT_used"], 1)

                exps(0)
                for n, (j, t) in enumerate(items):
                    if n + 1 < len(items):
                        exps(n + 1)
                    w = (t + 1) * P
                    if w > 512:
                        a.wait_ge(s["turned_ready"], n + 1)
                        a.wait_ge(s["outT_ready"], n - 1)
                        a.activation(probsT[:, n % 2, 512:w], turned[:, 512:w], ACT.Copy).then_inc(s["probsT_a"], 1)
                    if n >= 2:
                        copy_out(n - 2)
                copy_out(len(items) - 2)
                copy_out(len(items) - 1)

            @block.tensor
            def _(pe):
                pe.wait_ge(s["weights"], 1)
                for w, extra, src, half, done in ((wq, unit_row, ones, 0, "q_proj"), (wk, slope, pos, 1, "k_proj")):
                    for k in range(2):
                        o = scores[:, half, k * 512:(k + 1) * 512]
                        pe.matmul(o, w[:].rearrange("p j r -> p (j r)"), xs[:, k * 512:(k + 1) * 512], start=True, stop=False)
                        last = pe.matmul(o, extra[:], src[:, k * 512:(k + 1) * 512], start=False, stop=True)
                    last.then_inc(s[done], 1)

                def score(n):
                    j, t = items[n]
                    if n >= 2:
                        pe.wait_ge(s["probs_ready"], n - 1)
                    w = (t + 1) * P
                    for k0 in range(0, w, 512):
                        k1 = min(w, k0 + 512)
                        last = pe.matmul(scores[:, n % 2, k0:k1], QA[:, j, t * P:(t + 1) * P], KA[:, k0:k1],
                                         start=True, stop=True)
                    last.then_inc(s["scores_ready"], 1)

                def turn(n):
                    j, t = items[n]
                    pe.wait_ge(s["probs_ready"], n + 1)
                    if n >= 1:
                        pe.wait_ge(s["probsT_v"], n)
                        if second[n - 1]:
                            pe.wait_ge(s["probsT_a"], second[n - 1])
                    for k in range(t + 1):
                        last = pe.transpose(turned[:, k * P:(k + 1) * P], probs[:, n % 2, k * P:(k + 1) * P], c.ident)
                    last.then_inc(s["turned_ready"], 1)

                def weigh(n):
                    j, t = items[n]
                    pe.wait_ge(s["probsT_v"], n + 1)
                    if t >= 4:
                        pe.wait_ge(s["probsT_a"], second[n])
                    if n >= 2:
                        pe.wait_ge(s["outT_used"], n - 1)
                    for k in range(t + 1):
                        last = pe.matmul(outT[0:HD0, n % 2, 0:P], Vh[:, k, j * HD0:(j + 1) * HD0],
                                         probsT[:, n % 2, k * P:(k + 1) * P], start=(k == 0), stop=(k == t))
                    last.then_inc(s["outT_ready"], 1)

                pe.wait_ge(s["q_done"], HG + 1)
                pe.wait_ge(s["k_done"], 1)
                score(0)
                for n in range(len(items)):
                    if n + 1 < len(items):
                        score(n + 1)
                    turn(n)
                    if n >= 1:
                        weigh(n - 1)
                weigh(len(items) - 1)
                pe.wait_ge(s["outT_used"], len(items))
                for n in range(len(items)):
                    last = pe.transpose(scores[:, 0, n * HD0:(n + 1) * HD0], OT[:, n, :], c.ident[0:HD0, 0:HD0])
                last.then_inc(s["mix_ready"], 1)
        st.end_step()


EXPERTS = 8
CAPACITY = 100


def l0_ffn_stage(nc, X, XNT, c, w_gate, w_expert, b_expert):
    with Stage(nc, "f0") as outer:
        wg = outer.sb("wg", [P, EXPERTS])
        we = outer.sb("we", [P, P])
        bias = outer.sb("bias", [1, P])
        seen = outer.sb("seen", [P, EXPERTS])
        with Stage(nc, "f0w") as st:
            s = st.sems("loaded")
            with nc.Block(no_gpsimd_drain=True) as block:
                @block.sync
                def _(sp):
                    sp.dma_start(wg[:], w_gate).then_inc(s["loaded"], 16)
                    sp.dma_start(we[:], w_expert).then_inc(s["loaded"], 16)
                    sp.dma_start(bias[:], b_expert.rearrange("(a d) -> a d", a=1)).then_inc(s["loaded"], 16)
                    sp.wait_ge(s["loaded"], 48)

                @block.vector
                def _(v):
                    v.memset(seen[:], 0.0)
            st.end_step()
        with Stage(nc, "f0s") as st:
            xs = st.sb("xs", [P, G * P])
            lg = st.sb("lg", [P, G, EXPERTS])
            top = st.sb("top", [P, G, 8])
            at = st.sb("at", [P, G, 8], U32)
            atf = st.sb("atf", [P, G, 8])
            choice = st.sb("choice", [P, G, EXPERTS])
            ex = st.sb("ex", [P, G, EXPERTS])
            kept = st.sb("kept", [P, G, EXPERTS])
            total, gate, keep = (st.sb(n, [P, G]) for n in ("total", "gate", "keep"))
            add = st.sb("add", [P, EXPERTS])
            logits = st.ps("logits", (P, G, EXPERTS))
            place = st.ps("place", (P, G, EXPERTS))
            y = st.ps("y", (P, G, P))
            s = st.sems("xs_ready logits_ready y_ready chosen shifted exps place_ready added chain")
            with nc.Fori(0, TILES // G) as i:
                with nc.Block(no_gpsimd_drain=True) as block:
                    @block.scalar
                    def _(a):
                        a.activation(xs[:], XNT[:, ds(i * G * P, G * P)], ACT.Copy).then_inc(s["xs_ready"], 1)
                        a.wait_ge(s["shifted"], 1)
                        a.activation(ex[:], ex[:], ACT.Exp).then_inc(s["exps"], 1)

                    @block.tensor
                    def _(pe):
                        pe.wait_ge(s["xs_ready"], 1)
                        for j in range(G):
                            last = pe.matmul(logits[:, j, :], xs[:, j * P:(j + 1) * P], wg[:], start=True, stop=True)
                        last.then_inc(s["logits_ready"], 1)
                        for j in range(G):
                            pe.matmul(y[:, j, :], xs[:, j * P:(j + 1) * P], we[:], start=True, stop=False)
                            last = pe.matmul(y[:, j, :], c.ones[0:1, :], bias[:], start=False, stop=True)
                        last.then_inc(s["y_ready"], 1)
                        pe.wait_ge(s["chosen"], 1)
                        for j in range(G):
                            pe.matmul(place[:, j, :], c.upto, choice[:, j, :], start=True, stop=False)
                            for k in range(j):
                                pe.matmul(place[:, j, :], c.ones, choice[:, k, :], start=False, stop=False)
                            last = pe.matmul(place[:, j, :], c.ones, seen[:], start=False, stop=True)
                        last.then_inc(s["place_ready"], 1)

                    @block.vector
                    def _(v):
                        step = Chain(v, s["chain"])
                        v.wait_ge(s["logits_ready"], 1)
                        step(v.tensor_copy(lg[:], logits[:]))
                        for j in range(G):
                            last = v.max(top[:, j, :], lg[:, j, :])
                        step(last)
                        v.tensor_tensor(ex[:], lg[:], top[:, :, 0:1].broadcast_to([P, G, EXPERTS]),
                                        ALU.subtract).then_inc(s["shifted"], 1)
                        for j in range(G):
                            last = v.max_index(at[:, j, :], top[:, j, :], lg[:, j, :])
                        step(last)
                        step(v.tensor_copy(atf[:], at[:]))
                        for j in range(G):
                            last = v.tensor_scalar(choice[:, j, :], c.count8, atf[:, j, 0:1], None, ALU.is_equal)
                        last.then_inc(s["chosen"], 1)
                        v.wait_ge(s["exps"], 1)
                        step(v.tensor_reduce(total[:], ex[:], AX.X, ALU.add))
                        step(v.reciprocal(gate[:], total[:]))
                        v.wait_ge(s["place_ready"], 1)
                        step(v.scalar_tensor_tensor(out=kept[:], in0=place[:], scalar=float(CAPACITY), in1=choice[:],
                                                    op0=ALU.is_le, op1=ALU.mult))
                        v.tensor_reduce(keep[:], kept[:], AX.X, ALU.add)
                        step(v.tensor_reduce(add[:], choice[:].rearrange("p j e -> p e j"), AX.X, ALU.add))
                        v.tensor_tensor(seen[:], seen[:], add[:], ALU.add)
                        step(v.tensor_tensor(gate[:], gate[:], keep[:], ALU.mult))
                        v.wait_ge(s["y_ready"], 1)
                        for j in range(G):
                            last = v.scalar_tensor_tensor(out=tile(X, i * G + j), in0=y[:, j, :],
                                                          scalar=gate[:, j:j + 1], in1=tile(X, i * G + j),
                                                          op0=ALU.mult, op1=ALU.add)
                        last.then_inc(s["added"], 1)
                        v.wait_ge(s["added"], 1)
                st.end_step()


HEADS1 = 8
TAPS = 4
RMS_EPS = 1e-6
LEVELS = [1, 2, 4, 8, 16, 32, 64]


def l1_gates_stage(nc, XNT, c, a_b_wT, dt_row, alog_row, g_all, beta_all):
    H = HEADS1
    with Stage(nc, "g1") as outer:
        rate = outer.sb("rate", [P, 1, H])
        with Stage(nc, "g1r") as st:
            pr = st.ps("pr", (P, H))
            s = st.sems("row_ready exp_ready done")
            with nc.Block(no_gpsimd_drain=True) as block:
                @block.tensor
                def _(pe):
                    pe.matmul(pr[:], c.ones[0:1, :], alog_row, start=True, stop=True).then_inc(s["row_ready"], 1)

                @block.scalar
                def _(a):
                    a.wait_ge(s["row_ready"], 1)
                    a.activation(rate[:, 0, :], pr[:], ACT.Exp).then_inc(s["exp_ready"], 1)

                @block.vector
                def _(v):
                    v.wait_ge(s["exp_ready"], 1)
                    v.tensor_scalar(rate[:], rate[:], -1.0, None, ALU.mult).then_inc(s["done"], 1)
                    v.wait_ge(s["done"], 1)
            st.end_step()
        with Stage(nc, "g1s") as st:
            xs = st.sb("xs", [P, G * P])
            th, mag, relu = (st.sb(n, [P, G, H]) for n in ("th", "mag", "relu"))
            pa = st.ps("pa", (P, G, H))
            pb = st.ps("pb", (P, G, H))
            s = st.sems("xs_ready a_ready b_ready th_ready mag_ready soft_ready done chain act_chain")
            with nc.Fori(0, TILES // G) as i:
                with nc.Block(no_gpsimd_drain=True) as block:
                    @block.scalar
                    def _(a):
                        a.activation(xs[:], XNT[:, ds(i * G * P, G * P)], ACT.Copy).then_inc(s["xs_ready"], 1)
                        step = Chain(a, s["act_chain"])
                        a.wait_ge(s["b_ready"], 1)
                        a.activation(th[:], pb[:], ACT.Tanh, scale=0.5).then_inc(s["th_ready"], 1)
                        a.wait_ge(s["mag_ready"], 1)
                        step(a.activation(mag[:], mag[:], ACT.Exp, scale=-1.0))
                        a.activation(mag[:], mag[:], ACT.Ln, bias=1.0).then_inc(s["soft_ready"], 1)

                    @block.tensor
                    def _(pe):
                        pe.wait_ge(s["xs_ready"], 1)
                        for j in range(G):
                            last = pe.matmul(pb[:, j, :], xs[:, j * P:(j + 1) * P], a_b_wT[:, H:2 * H], start=True, stop=True)
                        last.then_inc(s["b_ready"], 1)
                        for j in range(G):
                            pe.matmul(pa[:, j, :], xs[:, j * P:(j + 1) * P], a_b_wT[:, 0:H], start=True, stop=False)
                            last = pe.matmul(pa[:, j, :], c.ones[0:1, :], dt_row, start=False, stop=True)
                        last.then_inc(s["a_ready"], 1)

                    @block.vector
                    def _(v):
                        step = Chain(v, s["chain"])
                        v.wait_ge(s["a_ready"], 1)
                        step(v.tensor_scalar(relu[:], pa[:], 0.0, None, ALU.max))
                        v.scalar_tensor_tensor(out=mag[:], in0=relu[:], scalar=2.0, in1=pa[:], op0=ALU.mult,
                                               op1=ALU.subtract).then_inc(s["mag_ready"], 1)
                        v.wait_ge(s["th_ready"], 1)
                        step(v.tensor_scalar(beta_all[:, ds(i * G, G), :], th[:], 0.5, 0.5, ALU.mult, ALU.add))
                        v.wait_ge(s["soft_ready"], 1)
                        step(v.tensor_tensor(relu[:], relu[:], mag[:], ALU.add))
                        v.tensor_tensor(g_all[:, ds(i * G, G), :], relu[:], rate[:].broadcast_to([P, G, H]),
                                        ALU.mult).then_inc(s["done"], 1)
                        v.wait_ge(s["done"], 1)
                st.end_step()


def l1_attention_stage(nc, X, XNT, c, d):
    H = HEADS1
    xnt4 = XNT[:].rearrange("p (b s) -> p b s", b=BATCH)
    with Stage(nc, "a1") as outer:
        abT = outer.sb("abT", [P, 2 * H])
        load_turned(nc, "a1t", [(abT[:, 0:H], d["L1_attn_a_w"]), (abT[:, H:2 * H], d["L1_attn_b_w"])], c)
        g_all = outer.sb("g_all", [P, TILES, H])
        beta_all = outer.sb("beta_all", [P, TILES, H])
        rows = outer.sb("rows", [1, 2 * H + P])
        norm_w = outer.sb("norm_w", [P, 1, P])
        masks = outer.sb("masks", [P, len(LEVELS), P])
        with Stage(nc, "a1c") as st:
            pn = st.ps("pn", (P, P))
            s = st.sems("loaded row_ready done")
            with nc.Block(no_gpsimd_drain=True) as block:
                @block.sync
                def _(sp):
                    sp.dma_start(rows[:, 0:H], d["L1_attn_dt_bias"].rearrange("(a d) -> a d", a=1)).then_inc(s["loaded"], 16)
                    sp.dma_start(rows[:, H:2 * H], d["L1_attn_A_log"].rearrange("(a d) -> a d", a=1)).then_inc(s["loaded"], 16)
                    sp.dma_start(rows[:, 2 * H:], d["L1_attn_norm_w"].rearrange("(a d) -> a d", a=1)).then_inc(s["loaded"], 16)
                    sp.dma_start(masks[:], d["const_level_masks"]).then_inc(s["loaded"], 16)
                    sp.wait_ge(s["loaded"], 64)

                @block.tensor
                def _(pe):
                    pe.wait_ge(s["loaded"], 64)
                    pe.matmul(pn[:], c.ones[0:1, :], rows[:, 2 * H:], start=True, stop=True).then_inc(s["row_ready"], 1)

                @block.vector
                def _(v):
                    v.wait_ge(s["row_ready"], 1)
                    v.tensor_scalar(norm_w[:, 0, :], pn[:], 0.5, None, ALU.mult).then_inc(s["done"], 1)
                    v.wait_ge(s["done"], 1)
            st.end_step()
        l1_gates_stage(nc, XNT, c, abT, rows[:, 0:H], rows[:, H:2 * H], g_all, beta_all)

        wT = outer.sb("wT", [P, 5, P])
        raw_w = outer.sb("raw_w", [P, 5, P])
        taps = outer.sb("taps", [P, 3, TAPS])
        S = outer.sb("S", [P, G, P])
        hist = outer.sb("hist", [P, 3, G, P + TAPS - 1])
        gh = outer.sb("gh", [P, TILES])
        bh = outer.sb("bh", [P, TILES])
        with nc.Fori(0, H) as h:
            with Stage(nc, "a1h") as st:
                turned = st.ps("turned", (P, 5, 512))
                s = st.sems("loaded turned_ready copied zeroed")
                with nc.Block(no_gpsimd_drain=True) as block:
                    @block.sync
                    def _(sp):
                        for n in range(3):
                            sp.dma_start(raw_w[:, n, :], d["L1_attn_qkv_w"][ds(h * P + n * H * P, P), :]).then_inc(s["loaded"], 16)
                            sp.dma_start(taps[:, n, :], d["L1_attn_conv_w"][ds(h * P + n * H * P, P), :, :]
                                         .rearrange("p a t -> p (a t)")).then_inc(s["loaded"], 16)
                        sp.dma_start(raw_w[:, 3, :], d["L1_attn_z_w"][ds(h * P, P), :]).then_inc(s["loaded"], 16)
                        sp.dma_start(raw_w[:, 4, :], d["L1_attn_out_w"][:, ds(h * P, P)]).then_inc(s["loaded"], 16)
                        sp.wait_ge(s["loaded"], 8 * 16)

                    @block.tensor
                    def _(pe):
                        pe.wait_ge(s["loaded"], 8 * 16)
                        for n in range(5):
                            pe.transpose(turned[:, n, 0:P], raw_w[:, n, :], c.ident).then_inc(s["turned_ready"], 1)

                    @block.vector
                    def _(v):
                        v.memset(S[:], 0.0)
                        v.memset(hist[:, :, :, 0:TAPS - 1], 0.0)
                        v.tensor_copy(gh[:], g_all[:, :, ds(h, 1)].rearrange("p t a -> p (t a)"))
                        v.tensor_copy(bh[:], beta_all[:, :, ds(h, 1)].rearrange("p t a -> p (t a)"))
                        for n in range(5):
                            v.wait_ge(s["turned_ready"], n + 1)
                            v.tensor_copy(wT[:, n, :], turned[:, n, 0:P]).then_inc(s["copied"], 1)
                        v.wait_ge(s["copied"], 5)
                st.end_step()
            with Stage(nc, "a1s") as st:
                delta_chunk_steps(nc, st, X, xnt4, c, wT, taps, S, hist, gh, bh, masks, norm_w)


def delta_chunk_steps(nc, st, X, xnt4, c, wT, taps, S, hist, gh, bh, masks, norm_w):
    four = [P, G, P]
    gcol, bcol, nbeta, msq, std, rstd = (st.sb(n, [P, G]) for n in ("gcol", "bcol", "nbeta", "msq", "std", "rstd"))
    decays = st.sb("decays", [P, 3, G])
    ga, E, Eincl, Estrict = (st.sb(n, four) for n in ("ga", "E", "Eincl", "Estrict"))
    xs, conv, ktok, vtok = st.sb("xs", four), st.sb("conv", [P, 3, G, P]), st.sb("ktok", four), st.sb("vtok", four)
    N, Nlev, AT = st.sb("N", four), st.sb("Nlev", [P, len(LEVELS), G, P]), st.sb("AT", four)
    T, XT, Zt, R, kS, u, uend = (st.sb(n, four) for n in ("T", "XT", "Zt", "R", "kS", "u", "uend"))
    o, osq, gatez, y, yT, newS = (st.sb(n, four) for n in ("o", "osq", "gatez", "y", "yT", "newS"))
    bank = [st.ps(f"bank{n}", (P, G, P)) for n in range(8)]
    s = st.sems("xs_ready cols_ready ga_ready raw_ready raw_copied conv_ready sums_ready dt_ready decays_ready "
                "E_ready masks_ready z_ready gatez_ready ktok_ps vtok_ps ktok_ready vtok_ready gram_ready N_ready "
                "Nlev_ready qk_ready AT_ready kS_ready qS_ready R_ready qS_used zt_ps zt_ready t_ps t_ready x_ps "
                "x_ready u_ps u_ready uend_ready o_ps o_used s_ps s_used msq_ready std_ready y_ready yT_ps yT_ready "
                "out_ps added chain")
    K = len(LEVELS)
    with nc.Fori(0, BLOCKS) as ch:
        with nc.Block(no_gpsimd_drain=True) as block:
            @block.tensor
            def _(pe):
                def four_of(out, lhs, rhs, sem):
                    for b in range(G):
                        last = pe.matmul(out[:, b, :], lhs(b), rhs(b), start=True, stop=True)
                    last.then_inc(sem, 1)

                for n in range(3):
                    pe.matmul(flat(bank[n][:]), wT[:, n, :], xnt4[:, :, ds(ch * P, P)],
                              start=True, stop=True).then_inc(s["raw_ready"], 1)
                pe.wait_ge(s["cols_ready"], 1)
                for n, m in enumerate((c.upto, c.after, c.ones)):
                    last = pe.matmul(bank[4][:, 0, n * G:(n + 1) * G], m, gcol[:], start=True, stop=True)
                last.then_inc(s["sums_ready"], 1)
                pe.wait_ge(s["ga_ready"], 1)
                four_of(bank[3], lambda b: ga[:, b, :], lambda b: c.upto, s["dt_ready"])
                pe.wait_ge(s["xs_ready"], 1)
                four_of(bank[7], lambda b: xs[:, b, :], lambda b: wT[:, 3, :], s["z_ready"])
                pe.wait_ge(s["conv_ready"], 1)
                for b in range(G):
                    last = pe.transpose(bank[5][:, b, :], conv[:, 1, b, :], c.ident)
                last.then_inc(s["ktok_ps"], 1)
                four_of(bank[6], lambda b: conv[:, 1, b, :], lambda b: conv[:, 1, b, :], s["gram_ready"])
                pe.wait_ge(s["conv_ready"], 2)
                pe.wait_ge(s["raw_copied"], 3)
                four_of(bank[0], lambda b: conv[:, 1, b, :], lambda b: conv[:, 0, b, :], s["qk_ready"])
                four_of(bank[2], lambda b: conv[:, 1, b, :], lambda b: S[:, b, :], s["kS_ready"])
                pe.wait_ge(s["E_ready"], 1)
                four_of(bank[3], lambda b: conv[:, 0, b, :], lambda b: S[:, b, :], s["qS_ready"])
                pe.wait_ge(s["conv_ready"], 3)
                for b in range(G):
                    last = pe.transpose(bank[1][:, b, :], conv[:, 2, b, :], c.ident)
                last.then_inc(s["vtok_ps"], 1)
                pe.wait_ge(s["ktok_ready"], 1)
                pe.wait_ge(s["N_ready"], 1)
                pe.wait_ge(s["AT_ready"], 1)
                for k in range(K):
                    pe.wait_ge(s["Nlev_ready"], k + 1)
                    if k >= 1:
                        pe.wait_ge(s["t_ready"], k)
                    four_of(bank[5], lambda b: Nlev[:, k, b, :], lambda b: c.ident if k == 0 else T[:, b, :], s["zt_ps"])
                    if k >= 1:
                        pe.wait_ge(s["zt_ready"], k)
                        pe.wait_ge(s["x_ready"], k)
                        if k < K - 1:
                            four_of(bank[6], lambda b: XT[:, b, :], lambda b: Zt[:, b, :], s["t_ps"])
                        four_of(bank[0], lambda b: Zt[:, b, :], lambda b: XT[:, b, :], s["x_ps"])
                pe.wait_ge(s["x_ready"], K)
                pe.wait_ge(s["R_ready"], 1)
                pe.wait_ge(s["vtok_ready"], 1)
                four_of(bank[1], lambda b: XT[:, b, :], lambda b: R[:, b, :], s["u_ps"])
                pe.wait_ge(s["u_ready"], 1)
                pe.wait_ge(s["decays_ready"], 1)
                four_of(bank[4], lambda b: AT[:, b, :], lambda b: u[:, b, :], s["o_ps"])
                pe.wait_ge(s["uend_ready"], 1)
                four_of(bank[6], lambda b: ktok[:, b, :], lambda b: uend[:, b, :], s["s_ps"])
                pe.wait_ge(s["y_ready"], 1)
                for b in range(G):
                    last = pe.transpose(bank[5][:, b, :], y[:, b, :], c.ident)
                last.then_inc(s["yT_ps"], 1)
                pe.wait_ge(s["yT_ready"], 1)
                four_of(bank[0], lambda b: yT[:, b, :], lambda b: wT[:, 4, :], s["out_ps"])

            @block.scalar
            def _(a):
                for n in (1, 0, 2):
                    a.wait_ge(s["raw_ready"], n + 1)
                    a.activation(hist[:, n, :, TAPS - 1:], bank[n][:], ACT.Copy).then_inc(s["raw_copied"], 1)
                a.wait_ge(s["sums_ready"], 1)
                a.activation(decays[:].rearrange("p n b -> p (n b)"), bank[4][:, 0, 0:3 * G], ACT.Exp).then_inc(s["decays_ready"], 1)
                a.wait_ge(s["dt_ready"], 1)
                a.activation(E[:], bank[3][:], ACT.Exp).then_inc(s["E_ready"], 1)
                a.wait_ge(s["z_ready"], 1)
                a.activation(gatez[:], bank[7][:], ACT.Tanh, scale=0.5).then_inc(s["gatez_ready"], 1)
                a.wait_ge(s["ktok_ps"], 1)
                a.activation(ktok[:], bank[5][:], ACT.Copy).then_inc(s["ktok_ready"], 1)
                a.wait_ge(s["vtok_ps"], 1)
                a.activation(vtok[:], bank[1][:], ACT.Copy).then_inc(s["vtok_ready"], 1)
                for k in range(1, K):
                    a.wait_ge(s["zt_ps"], k + 1)
                    if k >= 2:
                        a.wait_ge(s["x_ps"], k - 1)
                    a.activation(Zt[:], bank[5][:], ACT.Copy).then_inc(s["zt_ready"], 1)
                a.wait_ge(s["msq_ready"], 1)
                a.activation(std[:], msq[:], ACT.Sqrt).then_inc(s["std_ready"], 1)
                a.wait_ge(s["yT_ps"], 1)
                a.activation(yT[:], bank[5][:], ACT.Copy).then_inc(s["yT_ready"], 1)

            @block.gpsimd
            def _(g):
                g.tensor_copy(xs[:], xnt4[:, :, ds(ch * P, P)]).then_inc(s["xs_ready"], 1)
                g.wait_ge(s["E_ready"], 1)
                g.tensor_tensor(Eincl[:], E[:], c.upto.unsqueeze(1).broadcast_to(four), ALU.mult)
                g.tensor_tensor(Estrict[:], E[:], c.strict.unsqueeze(1).broadcast_to(four), ALU.mult).then_inc(s["masks_ready"], 1)
                g.wait_ge(s["N_ready"], 1)
                for k in range(K):
                    g.tensor_tensor(Nlev[:, k], N[:], masks[:, k:k + 1, :].broadcast_to(four), ALU.mult).then_inc(s["Nlev_ready"], 1)

            @block.vector
            def _(v):
                step = Chain(v, s["chain"])
                v.tensor_copy(bcol[:], bh[:].rearrange("p (b t) -> p b t", b=G)[:, :, ds(ch, 1)].rearrange("p b a -> p (b a)"))
                v.tensor_copy(gcol[:], gh[:].rearrange("p (b t) -> p b t", b=G)[:, :, ds(ch, 1)]
                              .rearrange("p b a -> p (b a)")).then_inc(s["cols_ready"], 1)
                v.wait_ge(s["cols_ready"], 1)
                v.tensor_tensor(ga[:], c.after.unsqueeze(1).broadcast_to(four), spread(gcol[:], P), ALU.mult).then_inc(s["ga_ready"], 1)
                step(v.tensor_scalar(nbeta[:], bcol[:], -1.0, None, ALU.mult))
                for at, n in enumerate((1, 0, 2)):
                    v.wait_ge(s["raw_copied"], at + 1)
                    step(v.tensor_scalar(conv[:, n], hist[:, n, :, TAPS - 1:], taps[:, n, TAPS - 1:TAPS], None, ALU.mult))
                    for k in range(TAPS - 1):
                        last = v.scalar_tensor_tensor(out=conv[:, n], in0=hist[:, n, :, k:k + P], scalar=taps[:, n, k:k + 1],
                                                      in1=conv[:, n], op0=ALU.mult, op1=ALU.add)
                        if k < TAPS - 2:
                            step(last)
                    last.then_inc(s["conv_ready"], 1)
                v.wait_ge(s["conv_ready"], 3)
                v.tensor_copy(hist[:, :, :, 0:TAPS - 1], hist[:, :, :, P:P + TAPS - 1])
                v.wait_ge(s["masks_ready"], 1)
                v.wait_ge(s["gram_ready"], 1)
                step(v.tensor_tensor(N[:], bank[6][:], Estrict[:], ALU.mult))
                v.tensor_tensor(N[:], N[:], spread(nbeta[:], P), ALU.mult).then_inc(s["N_ready"], 1)
                v.wait_ge(s["qk_ready"], 1)
                v.tensor_tensor(AT[:], bank[0][:], Eincl[:], ALU.mult).then_inc(s["AT_ready"], 1)
                idn = c.ident.unsqueeze(1).broadcast_to(four)
                v.wait_ge(s["zt_ps"], 1)
                v.tensor_tensor(T[:], bank[5][:], idn, ALU.add).then_inc(s["t_ready"], 1)
                v.wait_ge(s["Nlev_ready"], 1)
                v.tensor_tensor(XT[:], Nlev[:, 0], idn, ALU.add).then_inc(s["x_ready"], 1)
                for k in range(1, K):
                    if k < K - 1:
                        v.wait_ge(s["t_ready"], k)
                        v.wait_ge(s["t_ps"], k)
                        v.tensor_tensor(T[:], bank[6][:], T[:], ALU.add).then_inc(s["t_ready"], 1)
                    v.wait_ge(s["x_ready"], k)
                    v.wait_ge(s["x_ps"], k)
                    v.tensor_tensor(XT[:], bank[0][:], XT[:], ALU.add).then_inc(s["x_ready"], 1)
                    if k == 1:
                        v.wait_ge(s["kS_ready"], 1)
                        v.wait_ge(s["decays_ready"], 1)
                        step(v.tensor_tensor(kS[:], bank[2][:], spread(decays[:, 0, :], P), ALU.mult))
                        v.wait_ge(s["vtok_ready"], 1)
                        v.tensor_tensor(R[:], vtok[:], kS[:], ALU.subtract).then_inc(s["R_ready"], 1)
                    if k == 2:
                        v.wait_ge(s["qS_ready"], 1)
                        step(v.tensor_tensor(o[:], bank[3][:], spread(decays[:, 0, :], P), ALU.mult))
                        step(v.tensor_tensor(newS[:], S[:], spread(decays[:, 2, :], P), ALU.mult))
                    if k == 3:
                        v.wait_ge(s["gatez_ready"], 1)
                        step(v.scalar_tensor_tensor(out=gatez[:], in0=gatez[:], scalar=1.0, in1=bank[7][:],
                                                    op0=ALU.add, op1=ALU.mult))
                        step(v.tensor_tensor(gatez[:], gatez[:], norm_w[:].broadcast_to(four), ALU.mult))
                v.wait_ge(s["u_ps"], 1)
                v.tensor_tensor(u[:], bank[1][:], spread(bcol[:], P), ALU.mult).then_inc(s["u_ready"], 1)
                v.wait_ge(s["u_ready"], 1)
                v.tensor_tensor(uend[:], u[:], spread(decays[:, 1, :], P), ALU.mult).then_inc(s["uend_ready"], 1)
                v.wait_ge(s["o_ps"], 1)
                step(v.tensor_tensor(o[:], bank[4][:], o[:], ALU.add))
                step(v.tensor_tensor(osq[:], o[:], o[:], ALU.mult))
                step(v.tensor_reduce(msq[:], osq[:], AX.X, ALU.add))
                v.tensor_scalar(msq[:], msq[:], 1.0 / P, RMS_EPS, ALU.mult, ALU.add).then_inc(s["msq_ready"], 1)
                v.tensor_tensor(y[:], o[:], gatez[:], ALU.mult)
                v.wait_ge(s["s_ps"], 1)
                v.tensor_tensor(S[:], bank[6][:], newS[:], ALU.add).then_inc(s["s_used"], 1)
                v.wait_ge(s["std_ready"], 1)
                step(v.reciprocal(rstd[:], std[:]))
                v.tensor_tensor(y[:], y[:], spread(rstd[:], P), ALU.mult).then_inc(s["y_ready"], 1)
                v.wait_ge(s["out_ps"], 1)
                mine = X[:].rearrange("p (b t) d -> p b t d", b=G)[:, :, ds(ch, 1), :].rearrange("p b a d -> p b (a d)")
                v.tensor_tensor(mine, bank[0][:], mine, ALU.add).then_inc(s["added"], 1)
                v.wait_ge(s["added"], 1)
        st.end_step()


DEPTH = 6
HEADSW = 16
HDW = 64
INNER = HEADSW * HDW
WINDOW = 32
KEYS = WINDOW + P
HALFW = P // 2
QK_SCALE = 8.0
UNITS = int(P * 4 * 2 / 3)
PIECES = [(0, P), (P, 2 * P), (2 * P, UNITS)]
GH = 4
BANK_HEADS = 3


def l1_ffn_stage(nc, X, Y, c, d):
    with Stage(nc, "w") as outer:
        rope = outer.sb("rope", [P, 4, BLOCKS + 1, HDW])
        scaled = outer.sb("scaled", [P, 4, BLOCKS + 1, HDW])
        band = outer.sb("band", [P, BLOCKS, KEYS])
        shifts = outer.sb("shifts", [P, 2, P])
        has_prev = outer.sb("has_prev", [P, 2, BLOCKS + 1])
        wqkv = outer.sb("wqkv", [P, 3 * INNER])
        wo = outer.sb("wo", [P, INNER // P, P])
        w1 = outer.sb("w1", [P, 2 * UNITS])
        w2 = outer.sb("w2", [P, 3, P])
        b1 = outer.sb("b1", [P, 2, 3])
        b2 = outer.sb("b2", [1, P])
        gb = outer.sb("gb", [P, 2])
        qk_rows = outer.sb("qk_rows", [1, 2, HDW])
        with Stage(nc, "wc") as st:
            s = st.sems("loaded")
            with nc.Block(no_gpsimd_drain=True) as block:
                @block.sync
                def _(sp):
                    sp.dma_start(rope[:], d["const_rope"]).then_inc(s["loaded"], 16)
                    sp.dma_start(band[:], d["const_band"]).then_inc(s["loaded"], 16)
                    sp.dma_start(shifts[:], d["const_shifts"]).then_inc(s["loaded"], 16)
                    sp.dma_start(has_prev[:], d["const_has_prev"]).then_inc(s["loaded"], 16)
                    sp.wait_ge(s["loaded"], 64)
            st.end_step()

        with nc.Fori(0, DEPTH) as l:
            with Stage(nc, "wl") as st:
                qks = st.sb("qks", [P, 2, HDW])
                pr = st.ps("pr", (P, 2, HDW))
                s = st.sems("rows_loaded loaded rows_ps copied")
                with nc.Block(no_gpsimd_drain=True) as block:
                    @block.sync
                    def _(sp):
                        sp.dma_start(qk_rows[:, 0, :], d["L1_ffn_q_scale"][ds(l, 1), :]).then_inc(s["rows_loaded"], 16)
                        sp.dma_start(qk_rows[:, 1, :], d["L1_ffn_k_scale"][ds(l, 1), :]).then_inc(s["rows_loaded"], 16)
                        loads = [(wqkv[:], d["L1_ffn_Wqkv"][ds(l, 1)].rearrange("a p n -> (a p) n")),
                                 (wo[:], d["L1_ffn_Wo"][ds(l, 1)].rearrange("a (k p) n -> (a p) k n", p=P)),
                                 (w1[:], d["L1_ffn_W1"][ds(l, 1)].rearrange("a p n -> (a p) n")),
                                 (b2[:], d["L1_ffn_b2"][ds(l, 1), :]),
                                 (gb[:, 0:1], d["L1_ffn_ln_g"][ds(l, 1), :].rearrange("a p -> p a")),
                                 (gb[:, 1:2], d["L1_ffn_ln_b"][ds(l, 1), :].rearrange("a p -> p a"))]
                        for n, (k0, k1) in enumerate(PIECES):
                            loads.append((w2[0:k1 - k0, n, :], d["L1_ffn_W2"][ds(l, 1), k0:k1, :].rearrange("a p n -> (a p) n")))
                            for half in range(2):
                                loads.append((b1[0:k1 - k0, half, n:n + 1],
                                              d["L1_ffn_b1"][ds(l, 1), half * UNITS + k0:half * UNITS + k1]
                                              .rearrange("a p -> p a")))
                        for dst, src in loads:
                            sp.dma_start(dst, src).then_inc(s["loaded"], 16)
                        sp.wait_ge(s["loaded"], 16 * len(loads))

                    @block.tensor
                    def _(pe):
                        pe.wait_ge(s["rows_loaded"], 32)
                        pe.matmul(flat(pr[:]), c.ones[0:1, :], qk_rows[:].rearrange("a n d -> a (n d)"), start=True,
                                  stop=True).then_inc(s["rows_ps"], 1)

                    @block.vector
                    def _(v):
                        v.wait_ge(s["rows_ps"], 1)
                        v.tensor_copy(qks[:], pr[:]).then_inc(s["copied"], 1)
                        v.wait_ge(s["copied"], 1)
                        for n in range(2):
                            v.tensor_tensor(scaled[:, 2 * n], rope[:, 2 * n],
                                            qks[:, n:n + 1, :].broadcast_to([P, BLOCKS + 1, HDW]), ALU.mult)
                            for k in range(2):
                                o, p = k * 32, 32 - k * 32
                                v.tensor_tensor(scaled[:, 2 * n + 1, :, o:o + 32], rope[:, 2 * n + 1, :, o:o + 32],
                                                qks[:, n:n + 1, p:p + 32].broadcast_to([P, BLOCKS + 1, 32]), ALU.mult)
                st.end_step()
            with Stage(nc, "wa") as st:
                window_attention_steps(nc, st, Y, c, scaled, band, shifts, has_prev, wqkv, wo)
            with Stage(nc, "wf") as st:
                geglu_steps(nc, st, Y, c, shifts, w1, w2, b1, b2, gb)

        with Stage(nc, "wx") as st:
            s = st.sems("added")
            with nc.Block(no_gpsimd_drain=True) as block:
                @block.vector
                def _(v):
                    v.tensor_tensor(X[:], X[:], Y[:, 0:TILES, :], ALU.add).then_inc(s["added"], 1)
                    v.wait_ge(s["added"], 1)
            st.end_step()


def window_attention_steps(nc, st, Y, c, scaled, band, shifts, has_prev, wqkv, wo):
    ya = st.sb("ya", [P, P])
    yb = st.sb("yb", [P, 2, P])
    xsT = st.sb("xsT", [P, P])
    v_all = st.sb("v_all", [P, 2, HEADSW, HDW])
    v_prev = st.sb("v_prev", [P, 2, HEADSW // GH, GH, HDW])
    sq = st.sb("sq", [P, 2, HEADSW, HDW])
    rot = st.sb("rot", [P, 2, HEADSW, HDW])
    part = st.sb("part", [P, 2, HEADSW, HDW])
    norm = st.sb("norm", [P, 2, HEADSW])
    rnorm = st.sb("rnorm", [P, 2, 2, HEADSW])
    qT = st.sb("qT", [P, 2, HEADSW, P])
    kT = st.sb("kT", [P, 2, HEADSW // 2, KEYS])
    sc = st.sb("sc", [P, HEADSW, KEYS])
    smax, bias, total, rtotal = (st.sb(n, [P, HEADSW]) for n in ("smax", "bias", "total", "rtotal"))
    pc = st.sb("pc", [P, HEADSW, KEYS])
    pp = st.sb("pp", [P, HEADSW, WINDOW])
    pcT = st.sb("pcT", [P, HEADSW, P])
    ppT = st.sb("ppT", [P, HEADSW // GH, P])
    o = st.sb("o", [P, HEADSW, HDW])
    oT = st.sb("oT", [P, INNER // P, P])
    front = st.ps("front", (P, 4, 512))
    back = st.ps("back", (P, 4, 512))
    scores_at = [0, 2, 0]
    groups = [range(n, min(n + 2 * BANK_HEADS, HEADSW)) for n in range(0, HEADSW, 2 * BANK_HEADS)]
    s = st.sems("y_copied xsT_ps xsT_ready q_ps k_ps v_ps v_ready sq_ready norm_ready rnorm_ready q_rot k_sum k_rot "
                "qT_ps kT_ps qT_even qT_odd kT_ready kT_kept v_kept scores_ps sc_ready bias_ready probs_ready ppT_ps "
                "ppT_ready pcT_ps pcT_v pcT_a o_ps o_ready oT_ps oT_ready out_ps added part_ready norm_in pp_ready "
                "zeroed chain kept total_ready")

    def two_banks(ps, k):
        return ps[:, k:k + 2, :].rearrange("p k n -> p (k n)")

    def half_step(block, k, u, tile_a, in_row_a, tile_b, in_row_b):
        w = 1 - u

        @block.gpsimd
        def _(g):
            step = Chain(g, s["kept"])
            step.n = k * (GH + 1)
            if tile_b is not None:
                if k >= 1:
                    g.wait_ge(s["kT_ready"], k)
                    g.wait_ge(s["v_ready"], k)
                    g.wait_ge(s["pp_ready"], k)
                    g.wait_ge(s["o_ps"], k)
                for j in range(GH):
                    step(g.tensor_copy(v_prev[j * 32:(j + 1) * 32, w, :, j, :],
                                       v_all[P - WINDOW:P, u].rearrange("p (g j) d -> p g j d", j=GH)[:, :, j, :]))
                step(g.tensor_tensor(kT[:, w, :, 0:WINDOW], kT[:, u, :, P:KEYS],
                                     has_prev[:, 1, ds(in_row_a, 1)].unsqueeze(2).broadcast_to([P, HEADSW // 2, WINDOW]),
                                     ALU.mult))
            if tile_a is not None:
                for n, done in enumerate(("q_rot", "k_sum")):
                    g.wait_ge(s["part_ready"], 2 * k + n + 1)
                    g.tensor_tensor(rot[:, n], rot[:, n], part[:, n], ALU.add).then_inc(s[done], 1)
            if tile_b is not None:
                g.wait_ge(s["probs_ready"], len(groups) * (k + 1))
                if k >= 1:
                    g.wait_ge(s["ppT_ps"], k)
                g.tensor_copy(pp[:], pc[:, :, 0:WINDOW]).then_inc(s["pp_ready"], 1)
            g.wait_ge(s["q_rot"], k + 1)
            g.wait_ge(s["k_sum"], k + 1)

        @block.scalar
        def _(a):
            def exps(n):
                a.wait_ge(s["bias_ready"], len(groups) * k + n + 1)
                for h in groups[n]:
                    last = a.activation(pc[:, h, :], sc[:, h, :], ACT.Exp, scale=rnorm[:, u, 0, h:h + 1],
                                        bias=bias[:, h:h + 1], accum_out=total[:, h:h + 1])
                last.then_inc(s["probs_ready"], 1)

            def square(n, ready):
                a.wait_ge(s[ready], k + 1)
                a.activation(sq[:, n].rearrange("p h d -> p (h d)"), two_banks(front, 2 * n),
                             ACT.Square).then_inc(s["sq_ready"], 1)

            if tile_a is not None:
                mine = tile(Y, tile_a)
                if k >= 1:
                    a.wait_ge(s["xsT_ps"], k)
                a.activation(ya[:, 0:HALFW], mine[:, 0:HALFW], ACT.Copy)
                a.activation(yb[:, w, HALFW:P], mine[:, HALFW:P], ACT.Copy).then_inc(s["y_copied"], 1)
                a.wait_ge(s["xsT_ps"], k + 1)
                a.activation(xsT[:], front[:, 3, 0:P], ACT.Copy).then_inc(s["xsT_ready"], 1)
                if k >= 1:
                    a.wait_ge(s["norm_in"], k)
                square(0, "q_ps")
            if tile_b is not None:
                exps(0)
            if tile_a is not None:
                square(1, "k_ps")
            if tile_b is not None:
                exps(1)
            if tile_a is not None:
                a.wait_ge(s["v_ps"], k + 1)
                if k >= 1:
                    a.wait_ge(s["o_ps"], k)
                a.activation(v_all[:, w].rearrange("p h d -> p (h d)"), two_banks(front, 0),
                             ACT.Copy).then_inc(s["v_ready"], 1)
                a.wait_ge(s["norm_in"], k + 1)
                a.activation(norm[:], norm[:], ACT.Sqrt).then_inc(s["norm_ready"], 1)
            if tile_b is not None:
                exps(2)
            if tile_a is not None:
                a.wait_ge(s["qT_ps"], k + 1)
                a.activation(qT[0:HDW, w, 0:HEADSW:2, :], front[0:HDW, 2:4, :].rearrange("p k (h n) -> p (k h) n", n=P),
                             ACT.Copy).then_inc(s["qT_even"], 1)
                a.wait_ge(s["kT_ps"], k + 1)
                a.activation(kT[:, w, :, WINDOW:KEYS], front[:, 0:2, :].rearrange("p k (h n) -> p (k h) n", n=P),
                             ACT.Copy).then_inc(s["kT_ready"], 1)
            if tile_b is not None:
                for n in (1, 3):
                    a.wait_ge(s["pcT_ps"], 4 * k + n + 1)
                    a.activation(flat(pcT[:, n * GH:(n + 1) * GH, :]), back[:, 3, :], ACT.Copy).then_inc(s["pcT_a"], 1)
                    if n == 1:
                        a.wait_ge(s["ppT_ps"], k + 1)
                        a.activation(flat(ppT[:]), back[:, 0, :], ACT.Copy).then_inc(s["ppT_ready"], 1)
                a.wait_ge(s["oT_ps"], k + 1)
                a.activation(flat(oT[:]), two_banks(back, 2), ACT.Copy).then_inc(s["oT_ready"], 1)

        @block.tensor
        def _(pe):
            def score(n):
                hs = groups[n]
                m = len(hs) // 2
                if n == 2:
                    pe.wait_ge(s["sc_ready"], len(groups) * k + 1)
                for h in hs:
                    bank, at = (h - hs[0]) // m, (h - hs[0]) % m * KEYS
                    last = pe.matmul(back[:, scores_at[n] + bank, at:at + KEYS], qT[:, u, h, :], kT[:, u, h // 2, :],
                                     start=True, stop=True)
                last.then_inc(s["scores_ps"], 1)

            def project(n, done):
                for i in range(2):
                    last = pe.matmul(front[:, 2 * n % 4 + i, :], xsT[:], wqkv[:, (2 * n + i) * 512:(2 * n + i + 1) * 512],
                                     start=True, stop=True)
                last.then_inc(s[done], 1)

            def turn(n, first, done):
                for i in range(HEADSW // 2):
                    last = pe.transpose(front[:, first + i // 4, (i % 4) * P:(i % 4 + 1) * P],
                                        rot[:, n, 2 * i:2 * i + 2, :].rearrange("p h d -> p (h d)"), c.ident)
                last.then_inc(s[done], 1)

            def turn_probs(g):
                if g < 2:
                    pe.wait_ge(s["sc_ready"], len(groups) * k + 2)
                else:
                    pe.wait_ge(s["pcT_v"] if g == 2 else s["pcT_a"], 2 * k + 1)
                for j in range(GH):
                    last = pe.transpose(back[:, 2 + g % 2, j * P:(j + 1) * P], pc[:, g * GH + j, WINDOW:KEYS], c.ident)
                last.then_inc(s["pcT_ps"], 1)

            if tile_a is not None:
                pe.wait_ge(s["y_copied"], k + 1)
                if k >= 1:
                    pe.wait_ge(s["qT_even"], k)
                    pe.wait_ge(s["qT_odd"], k)
                x = front[:, 3, 0:P]
                pe.matmul(x, ya[:], c.ident, start=True, stop=False)
                pe.matmul(x, yb[:, w], shifts[:, 0, :], start=False, stop=False)
                pe.matmul(x[:, 0:1], yb[:, u], has_prev[:, 0, ds(in_row_a, 1)], start=False, stop=True).then_inc(s["xsT_ps"], 1)
            if tile_b is not None:
                if k >= 1:
                    pe.wait_ge(s["qT_odd"], k)
                    pe.wait_ge(s["kT_ready"], k)
                    pe.wait_ge(s["kept"], k * (GH + 1))
                    pe.wait_ge(s["oT_ready"], k)
                    pe.wait_ge(s["added"], k)
                score(0)
            if tile_a is not None:
                pe.wait_ge(s["xsT_ready"], k + 1)
                if k >= 1:
                    pe.wait_ge(s["kT_ready"], k)
                project(0, "q_ps")
                project(1, "k_ps")
            if tile_b is not None:
                score(1)
            if tile_a is not None:
                pe.wait_ge(s["sq_ready"], 2 * k + 1)
                pe.wait_ge(s["part_ready"], 2 * k + 1)
                project(2, "v_ps")
            if tile_b is not None:
                score(2)
            if tile_a is not None:
                pe.wait_ge(s["sq_ready"], 2 * k + 2)
                pe.wait_ge(s["part_ready"], 2 * k + 2)
                pe.wait_ge(s["q_rot"], k + 1)
                turn(0, 2, "qT_ps")
            if tile_b is not None:
                pe.wait_ge(s["probs_ready"], len(groups) * k + 2)
                turn_probs(0)
                turn_probs(1)
            if tile_a is not None:
                pe.wait_ge(s["k_rot"], k + 1)
                pe.wait_ge(s["v_ready"], k + 1)
                turn(1, 0, "kT_ps")
            if tile_b is not None:
                pe.wait_ge(s["probs_ready"], len(groups) * (k + 1))
                turn_probs(2)
                turn_probs(3)
                pe.wait_ge(s["sc_ready"], len(groups) * (k + 1))
                pe.wait_ge(s["pp_ready"], k + 1)
                for g in range(HEADSW // GH):
                    last = pe.transpose(back[:, 0, g * P:(g + 1) * P],
                                        pp[:, g * GH:(g + 1) * GH, :].rearrange("p h k -> p (h k)"), c.ident)
                last.then_inc(s["ppT_ps"], 1)
                pe.wait_ge(s["ppT_ready"], k + 1)
                pe.wait_ge(s["pcT_v"], 2 * k + 2)
                pe.wait_ge(s["pcT_a"], 2 * k + 2)
                for g in range(HEADSW // GH):
                    out = back[:, g // 2, (g % 2) * GH * HDW:(g % 2 + 1) * GH * HDW]
                    pe.matmul(out, ppT[:, g, :], v_prev[:, u, g].rearrange("p j d -> p (j d)"), start=True, stop=False)
                    for j in range(GH):
                        last = pe.matmul(out[:, j * HDW:(j + 1) * HDW], pcT[:, g * GH + j, :], v_all[:, u, g * GH + j, :],
                                         start=False, stop=(j == GH - 1))
                last.then_inc(s["o_ps"], 1)
                pe.wait_ge(s["o_ready"], k + 1)
                for i in range(INNER // P):
                    last = pe.transpose(back[:, 2 + i // 4, (i % 4) * P:(i % 4 + 1) * P],
                                        o[:, 2 * i:2 * i + 2, :].rearrange("p h d -> p (h d)"), c.ident)
                last.then_inc(s["oT_ps"], 1)
                pe.wait_ge(s["oT_ready"], k + 1)
                for i in range(INNER // P):
                    last = pe.matmul(back[:, 0, 0:P], oT[:, i, :], wo[:, i, :], start=(i == 0), stop=(i == INNER // P - 1))
                last.then_inc(s["out_ps"], 1)

        @block.vector
        def _(v):
            def masked_max(n):
                hs = groups[n]
                m = len(hs) // 2
                v.wait_ge(s["scores_ps"], len(groups) * k + n + 1)
                if k >= 1 and n == 0:
                    v.wait_ge(s["probs_ready"], len(groups) * k)
                at = hs[0]
                v.tensor_tensor(sc[:, at:at + 2 * m, :].rearrange("p (k a) x -> p k a x", k=2),
                                back[:, scores_at[n]:scores_at[n] + 2, 0:m * KEYS].rearrange("p k (a x) -> p k a x", a=m),
                                band[:, ds(in_row_b, 1), :].unsqueeze(2).broadcast_to([P, 2, m, KEYS]),
                                ALU.add).then_inc(s["sc_ready"], 1)
                v.wait_ge(s["sc_ready"], len(groups) * k + n + 1)
                v.tensor_reduce(smax[:, at:at + 2 * m], sc[:, at:at + 2 * m, :], AX.X, ALU.max).then_inc(s["chain"], 1)
                v.wait_ge(s["chain"], len(groups) * k + n + 1)
                v.scalar_tensor_tensor(out=bias[:, at:at + 2 * m], in0=smax[:, at:at + 2 * m], scalar=-1.0,
                                       in1=rnorm[:, u, 0, at:at + 2 * m], op0=ALU.mult, op1=ALU.mult).then_inc(s["bias_ready"], 1)

            def rotate(n, ready):
                src = front[:, 2 * n:2 * n + 2, :].rearrange("p k (h d) -> p (k h) d", d=HDW)
                cos = scaled[:, 2 * n, ds(in_row_a, 1), :].broadcast_to([P, HEADSW, HDW])
                sin = scaled[:, 2 * n + 1, ds(in_row_a, 1), :]
                v.wait_ge(s[ready], k + 1)
                v.wait_ge(s["sq_ready"], 2 * k + n + 1)
                if k >= 1:
                    v.wait_ge(s["qT_ps"] if n == 0 else s["kT_ps"], k)
                v.tensor_tensor(rot[:, n], src, cos, ALU.mult)
                for i in range(2):
                    p0, p1 = i * 32, 32 - i * 32
                    last = v.tensor_tensor(part[:, n, :, p0:p0 + 32], src[:, :, p1:p1 + 32],
                                           sin[:, :, p0:p0 + 32].broadcast_to([P, HEADSW, 32]), ALU.mult)
                last.then_inc(s["part_ready"], 1)

            if tile_b is not None:
                masked_max(0)
            if tile_a is not None:
                rotate(0, "q_ps")
            if tile_b is not None:
                masked_max(1)
            if tile_a is not None:
                rotate(1, "k_ps")
                if k >= 1:
                    v.wait_ge(s["rnorm_ready"], 3 * k)
                v.tensor_reduce(norm[:].rearrange("p n h -> p (n h)"), sq[:].rearrange("p n h d -> p (n h) d"),
                                AX.X, ALU.add).then_inc(s["norm_in"], 1)
            if tile_b is not None:
                masked_max(2)
            if tile_a is not None:
                v.wait_ge(s["norm_ready"], k + 1)
                v.tensor_scalar(norm[:], norm[:], 1e-12, None, ALU.max).then_inc(s["rnorm_ready"], 1)
                v.wait_ge(s["rnorm_ready"], 3 * k + 1)
                v.reciprocal(rnorm[:, w], norm[:]).then_inc(s["rnorm_ready"], 1)
                v.wait_ge(s["rnorm_ready"], 3 * k + 2)
                v.tensor_scalar(rnorm[:, w, 0, :], rnorm[:, w, 0, :], QK_SCALE, None, ALU.mult).then_inc(s["rnorm_ready"], 1)
                v.wait_ge(s["k_sum"], k + 1)
                v.tensor_tensor(rot[:, 1], rot[:, 1], spread(rnorm[:, w, 1, :], HDW), ALU.mult).then_inc(s["k_rot"], 1)
                v.wait_ge(s["qT_ps"], k + 1)
                if k >= 1:
                    v.wait_ge(s["scores_ps"], len(groups) * k)
                v.tensor_copy(qT[HDW:P, w, 1:HEADSW:2, :],
                              front[HDW:P, 2:4, :].rearrange("p k (h n) -> p (k h) n", n=P)).then_inc(s["qT_odd"], 1)
            if tile_b is not None:
                for n in (0, 2):
                    v.wait_ge(s["pcT_ps"], 4 * k + n + 1)
                    v.tensor_copy(flat(pcT[:, n * GH:(n + 1) * GH, :]), back[:, 2, :]).then_inc(s["pcT_v"], 1)
                v.wait_ge(s["probs_ready"], len(groups) * (k + 1))
                v.reciprocal(rtotal[:], total[:]).then_inc(s["total_ready"], 1)
                v.wait_ge(s["total_ready"], k + 1)
                v.wait_ge(s["o_ps"], k + 1)
                v.tensor_tensor(o[:], back[:, 0:2, :].rearrange("p k (h d) -> p (k h) d", d=HDW),
                                spread(rtotal[:], HDW), ALU.mult).then_inc(s["o_ready"], 1)
                v.wait_ge(s["out_ps"], k + 1)
                v.tensor_tensor(tile(Y, tile_b), back[:, 0, 0:P], tile(Y, tile_b), ALU.add).then_inc(s["added"], 1)
                v.wait_ge(s["added"], k + 1)

    with nc.Block(no_gpsimd_drain=True) as block:
        @block.gpsimd
        def _(g):
            for buffer in (ya, yb, kT, v_prev):
                g.memset(buffer[:], 0.0).then_inc(s["zeroed"], 1)
            g.wait_ge(s["zeroed"], 4)

        @block.vector
        def _(v):
            v.memset(qT[:], 0.0)
            v.memset(Y[:, TILES:TILES + 1, :], 0.0)
    st.end_step()
    with nc.Block(no_gpsimd_drain=True) as block:
        half_step(block, 0, 1, 0, 0, None, None)
    st.end_step()
    with nc.Fori(0, BATCH) as b:
        with nc.Fori(0, BLOCKS // 2) as i:
            with nc.Block(no_gpsimd_drain=True) as block:
                for u in range(2):
                    at = b * BLOCKS + i * 2 + u
                    half_step(block, u, u, at + 1, i * 2 + u + 1, at, i * 2 + u)
            st.end_step()


def geglu_steps(nc, st, Y, c, shifts, w1, w2, b1, b2, gb):
    yh = st.sb("yh", [P, G + 1, HALFW])
    xf, xn = st.sb("xf", [P, G, P]), st.sb("xn", [P, G, P])
    stats, mv = st.sb("stats", [P, G, 6]), st.sb("mv", [P, G, 2])
    var, std, rstd = (st.sb(n, [P, G]) for n in ("var", "std", "rstd"))
    xnT = st.sb("xnT", [P, G * P])
    gate, hid = st.sb("gate", [P, 3, G * P]), st.sb("hid", [P, 3, G * P])
    shp = st.ps("shp", (P, G, HALFW))
    xnp = st.ps("xnp", (P, G * P))
    ap_, gp = st.ps("ap", (P, 2, 512)), st.ps("gp", (P, 2, 512))
    outp = st.ps("outp", (P, G, P))
    s = st.sems("y_copied sh_ps xf_ready var_ready std_ready xn_ready xn_ps xnT_ready a_ps g_ps gate_ready hid_ready "
                "out_ps added zeroed chain")
    with nc.Fori(0, BATCH) as b:
        with nc.Block(no_gpsimd_drain=True) as block:
            @block.gpsimd
            def _(g):
                g.memset(yh[:], 0.0).then_inc(s["zeroed"], 1)
                g.wait_ge(s["zeroed"], 1)
        st.end_step()
        with nc.Fori(0, BLOCKS // G) as i:
            with nc.Block(no_gpsimd_drain=True) as block:
                mine = Y[:, ds(b * BLOCKS + i * G, G), :]

                @block.scalar
                def _(a):
                    a.activation(yh[:, 1:G + 1, :], mine[:, :, HALFW:P], ACT.Copy).then_inc(s["y_copied"], 1)
                    a.wait_ge(s["var_ready"], 1)
                    a.activation(std[:], var[:], ACT.Sqrt).then_inc(s["std_ready"], 1)
                    for n, (k0, k1) in enumerate(PIECES):
                        a.wait_ge(s["g_ps"], n + 1)
                        a.activation(gate[0:k1 - k0, n, :], gp[0:k1 - k0, n % 2, :], ACT.Gelu,
                                     bias=b1[0:k1 - k0, 1, n:n + 1]).then_inc(s["gate_ready"], 1)

                @block.tensor
                def _(pe):
                    pe.wait_ge(s["y_copied"], 1)
                    pe.matmul(flat(shp[:]), shifts[:, 0, :], yh[:, 1:G + 1, :].rearrange("p n d -> p (n d)"),
                              start=True, stop=False)
                    pe.matmul(flat(shp[:]), shifts[:, 1, :], yh[:, 0:G, :].rearrange("p n d -> p (n d)"),
                              start=False, stop=True).then_inc(s["sh_ps"], 1)
                    pe.wait_ge(s["xn_ready"], 1)
                    for j in range(G):
                        last = pe.transpose(xnp[:, j * P:(j + 1) * P], xn[:, j, :], c.ident)
                    last.then_inc(s["xn_ps"], 1)
                    pe.wait_ge(s["xnT_ready"], 1)
                    for n, (k0, k1) in enumerate(PIECES):
                        if n >= 2:
                            pe.wait_ge(s["gate_ready"], n - 1)
                            pe.wait_ge(s["hid_ready"], n - 1)
                        pe.matmul(gp[0:k1 - k0, n % 2, :], w1[:, UNITS + k0:UNITS + k1], xnT[:], start=True,
                                  stop=True).then_inc(s["g_ps"], 1)
                        pe.matmul(ap_[0:k1 - k0, n % 2, :], w1[:, k0:k1], xnT[:], start=True, stop=True).then_inc(s["a_ps"], 1)
                    pe.wait_ge(s["hid_ready"], 3)
                    for j in range(G):
                        for n, (k0, k1) in enumerate(PIECES):
                            pe.matmul(outp[:, j, :], hid[0:k1 - k0, n, j * P:(j + 1) * P], w2[0:k1 - k0, n, :],
                                      start=(n == 0), stop=False)
                        last = pe.matmul(outp[:, j, :], c.ones[0:1, :], b2[:], start=False, stop=True)
                    last.then_inc(s["out_ps"], 1)

                @block.vector
                def _(v):
                    step = Chain(v, s["chain"])
                    v.tensor_copy(xf[:, :, 0:HALFW], mine[:, :, 0:HALFW])
                    v.wait_ge(s["sh_ps"], 1)
                    step(v.tensor_copy(xf[:, :, HALFW:P], shp[:]))
                    v.tensor_copy(yh[:, 0, :], yh[:, G, :])
                    for j in range(G):
                        last = v.bn_stats(stats[:, j, :], xf[:, j, :])
                    step(last)
                    for j in range(G):
                        last = v.bn_aggr(mv[:, j, :], stats[:, j, :])
                    step(last)
                    v.tensor_scalar(var[:], mv[:, :, 1], LN_EPS, None, ALU.add).then_inc(s["var_ready"], 1)
                    v.wait_ge(s["std_ready"], 1)
                    step(v.reciprocal(rstd[:], std[:]))
                    for j in range(G):
                        last = v.tensor_scalar(xn[:, j, :], xf[:, j, :], mv[:, j, 0:1], rstd[:, j:j + 1],
                                               ALU.subtract, ALU.mult)
                    last.then_inc(s["xn_ready"], 1)
                    v.wait_ge(s["xn_ps"], 1)
                    v.tensor_scalar(xnT[:], xnp[:], gb[:, 0:1], gb[:, 1:2], ALU.mult, ALU.add).then_inc(s["xnT_ready"], 1)
                    for n, (k0, k1) in enumerate(PIECES):
                        v.wait_ge(s["gate_ready"], n + 1)
                        v.wait_ge(s["a_ps"], n + 1)
                        v.scalar_tensor_tensor(out=hid[0:k1 - k0, n, :], in0=ap_[0:k1 - k0, n % 2, :],
                                               scalar=b1[0:k1 - k0, 0, n:n + 1], in1=gate[0:k1 - k0, n, :],
                                               op0=ALU.add, op1=ALU.mult).then_inc(s["hid_ready"], 1)
                    v.wait_ge(s["out_ps"], 1)
                    v.tensor_tensor(mine, outp[:], mine, ALU.add).then_inc(s["added"], 1)
                    v.wait_ge(s["added"], 1)
            st.end_step()


COS_EPS = 1e-8


def l2_attention_stage(nc, X, XN, XNT, c):
    with Stage(nc, "a2") as st:
        xs = st.sb("xs", [P, SEQ])
        xv = st.sb("xv", [P, BLOCKS, P + 1])
        squares = st.sb("squares", [P, BLOCKS, P])
        norm2, norm, rnorm, rtotal = (st.sb(n, [P, BLOCKS]) for n in ("norm2", "norm", "rnorm", "rtotal"))
        diag = st.sb("diag", [P, BLOCKS, P])
        rrow = st.sb("rrow", [P, SEQ])
        scale = st.sb("scale", [P, 2, SEQ])
        sim = st.sb("sim", [P, 2, SEQ])
        E = st.sb("E", [P, BLOCKS, SEQ])
        mean = st.sb("mean", [P, 2, P])
        wide = st.ps("wide", (P, 2, SEQ))
        out = st.ps("out", (P, 2, 512))
        s = st.sems("xs_ready xv_ready norm2_ready norm_ready diag_ready row_ready rrow_done dots_ready sim_ready "
                    "exps out_ready out_used added ones_set chain")
        with nc.Fori(0, BATCH) as b:
            with nc.Block(no_gpsimd_drain=True) as block:
                @block.scalar
                def _(a):
                    a.activation(xs[:], XNT[:, ds(b * SEQ, SEQ)], ACT.Copy).then_inc(s["xs_ready"], 1)
                    a.wait_ge(s["norm2_ready"], 1)
                    a.activation(norm[:], norm2[:], ACT.Sqrt).then_inc(s["norm_ready"], 1)
                    a.wait_ge(s["row_ready"], 1)
                    a.activation(rrow[:], wide[:, 0, :], ACT.Copy).then_inc(s["rrow_done"], 1)
                    for t in range(BLOCKS):
                        a.wait_ge(s["sim_ready"], t + 1)
                        a.activation(E[:, t, :], sim[:, t % 2, :], ACT.Exp).then_inc(s["exps"], 1)

                @block.gpsimd
                def _(g):
                    g.memset(xv[:, :, P:P + 1], 1.0)
                    g.tensor_copy(xv[:, :, 0:P], XN[:, ds(b * BLOCKS, BLOCKS), :]).then_inc(s["xv_ready"], 1)

                @block.vector
                def _(v):
                    step = Chain(v, s["chain"])
                    v.wait_ge(s["xv_ready"], 1)
                    step(v.tensor_tensor(squares[:], xv[:, :, 0:P], xv[:, :, 0:P], ALU.mult))
                    v.tensor_reduce(norm2[:], squares[:], AX.X, ALU.add).then_inc(s["norm2_ready"], 1)
                    v.wait_ge(s["norm_ready"], 1)
                    step(v.tensor_scalar(norm[:], norm[:], 1e-30, None, ALU.max))
                    step(v.reciprocal(rnorm[:], norm[:]))
                    for t in range(BLOCKS):
                        last = v.tensor_scalar(diag[:, t, :], c.ident, rnorm[:, t:t + 1], None, ALU.mult)
                    last.then_inc(s["diag_ready"], 1)
                    v.wait_ge(s["rrow_done"], 1)
                    for t in range(BLOCKS):
                        step(v.tensor_scalar(scale[:, t % 2, :], rrow[:], rnorm[:, t:t + 1], 1.0 / COS_EPS,
                                             ALU.mult, ALU.min))
                        v.wait_ge(s["dots_ready"], t + 1)
                        if t >= 2:
                            v.wait_ge(s["exps"], t - 1)
                        v.tensor_tensor(sim[:, t % 2, :], wide[:, (t + 1) % 2, :], scale[:, t % 2, :],
                                        ALU.mult).then_inc(s["sim_ready"], 1)
                    for t in range(BLOCKS):
                        v.wait_ge(s["out_ready"], t + 1)
                        step(v.reciprocal(rtotal[:, t:t + 1], out[:, t % 2, P:P + 1]))
                        v.scalar_tensor_tensor(out=mean[:, t % 2, :], in0=out[:, t % 2, 0:P],
                                               scalar=rtotal[:, t:t + 1], in1=xv[:, t, 0:P],
                                               op0=ALU.mult, op1=ALU.add).then_inc(s["out_used"], 1)
                        v.wait_ge(s["out_used"], t + 1)
                        v.tensor_tensor(tile(X, b * BLOCKS + t), mean[:, t % 2, :], tile(X, b * BLOCKS + t),
                                        ALU.add).then_inc(s["added"], 1)
                    v.wait_ge(s["added"], BLOCKS)

                @block.tensor
                def _(pe):
                    pe.wait_ge(s["diag_ready"], 1)
                    for t in range(BLOCKS):
                        last = pe.matmul(wide[:, 0, t * P:(t + 1) * P], c.ones, diag[:, t, :], start=True, stop=True)
                    last.then_inc(s["row_ready"], 1)
                    pe.wait_ge(s["xs_ready"], 1)
                    for t in range(BLOCKS):
                        if t == 1:
                            pe.wait_ge(s["rrow_done"], 1)
                        if t >= 2:
                            pe.wait_ge(s["sim_ready"], t - 1)
                        for k in range(2):
                            last = pe.matmul(wide[:, (t + 1) % 2, k * 512:(k + 1) * 512], xs[:, t * P:(t + 1) * P],
                                             xs[:, k * 512:(k + 1) * 512], start=True, stop=True)
                        last.then_inc(s["dots_ready"], 1)
                    pe.wait_ge(s["exps"], BLOCKS)
                    for t in range(BLOCKS):
                        if t >= 2:
                            pe.wait_ge(s["out_used"], t - 1)
                        for k in range(BLOCKS):
                            last = pe.matmul(out[:, t % 2, 0:P + 1], E[:, k, t * P:(t + 1) * P], xv[:, k, :],
                                             start=(k == 0), stop=(k == BLOCKS - 1))
                        last.then_inc(s["out_ready"], 1)
            st.end_step()


JITTER = 0.01
WIDTH2 = 256


def l2_ffn_stage(nc, X, XNT, c, gate_w, w1, w2, w3):
    with Stage(nc, "f2") as outer:
        gT = outer.sb("gT", [P, EXPERTS])
        w1T = outer.sb("w1T", [P, EXPERTS, WIDTH2])
        w3T = outer.sb("w3T", [P, EXPERTS, WIDTH2])
        w2T = outer.sb("w2T", [P, EXPERTS, 2, P])
        for n, pairs in enumerate((
            [(gT[:], gate_w)] + [(w1T[:, e, k * P:(k + 1) * P], w1[e, k * P:(k + 1) * P, :])
                                 for e in range(EXPERTS) for k in range(2)],
            [(w3T[:, e, k * P:(k + 1) * P], w3[e, k * P:(k + 1) * P, :]) for e in range(EXPERTS) for k in range(2)],
            [(w2T[:, e, k, :], w2[e, :, k * P:(k + 1) * P]) for e in range(EXPERTS) for k in range(2)],
        )):
            load_turned(nc, f"f2w{n}", pairs, c)
        with Stage(nc, "f2s") as st:
            xs = st.sb("xs", [P, G * P])
            lg, size, gap, first, second, rest = (st.sb(n, [P, G, EXPERTS]) for n in
                                                  ("lg", "size", "gap", "first", "second", "rest"))
            ex1, ex2, lim1, lim2 = (st.sb(n, [P, G, EXPERTS]) for n in ("ex1", "ex2", "lim1", "lim2"))
            weight = st.sb("weight", [P, G, EXPERTS])
            top = st.sb("top", [P, G, 8])
            at = st.sb("at", [P, G, 8], U32)
            atf = st.sb("atf", [P, G, 8])
            total, mult = (st.sb(n, [P, 2, G]) for n in ("total", "mult"))
            th = st.sb("th", [P, 2, 512])
            gated = st.sb("gated", [P, 2, 512])
            act = st.sb("act", [P, 2, 2, 512])
            acc = st.sb("acc", [P, G, P])
            logits = st.ps("logits", (P, G, EXPERTS))
            h1 = st.ps("h1", (P, 2, 512))
            h3 = st.ps("h3", (P, 2, 512))
            y = st.ps("y", (P, 2, G, P))
            s = st.sems("xs_ready logits_ready shifted1 exps h1_ready h3_ready th_ready act_ready y_ready y_used "
                        "added chain")
            with nc.Fori(0, TILES // G) as i:
                with nc.Block(no_gpsimd_drain=True) as block:
                    @block.scalar
                    def _(a):
                        a.activation(xs[:], XNT[:, ds(i * G * P, G * P)], ACT.Copy).then_inc(s["xs_ready"], 1)
                        a.wait_ge(s["shifted1"], 1)
                        a.activation(ex1[:], ex1[:], ACT.Exp)
                        a.activation(ex2[:], ex2[:], ACT.Exp).then_inc(s["exps"], 1)
                        for n in range(2 * EXPERTS):
                            a.wait_ge(s["h1_ready"], n + 1)
                            if n >= 2:
                                a.wait_ge(s["act_ready"], n - 1)
                            a.activation(th[:, n % 2, :], h1[:, n % 2, :], ACT.Tanh, scale=0.5).then_inc(s["th_ready"], 1)

                    @block.tensor
                    def _(pe):
                        pe.wait_ge(s["xs_ready"], 1)
                        for j in range(G):
                            last = pe.matmul(logits[:, j, :], xs[:, j * P:(j + 1) * P], gT[:], start=True, stop=True)
                        last.then_inc(s["logits_ready"], 1)

                        def second_product(e):
                            pe.wait_ge(s["act_ready"], 2 * e + 2)
                            if e >= 2:
                                pe.wait_ge(s["y_used"], e - 1)
                            for j in range(G):
                                for k in range(2):
                                    last = pe.matmul(y[:, e % 2, j, :], act[:, e % 2, k, j * P:(j + 1) * P],
                                                     w2T[:, e, k, :], start=(k == 0), stop=(k == 1))
                            last.then_inc(s["y_ready"], 1)

                        for e in range(EXPERTS):
                            for k in range(2):
                                n = 2 * e + k
                                if n >= 2:
                                    pe.wait_ge(s["act_ready"], n - 1)
                                pe.matmul(h1[:, n % 2, :], w1T[:, e, k * P:(k + 1) * P], xs[:],
                                          start=True, stop=True).then_inc(s["h1_ready"], 1)
                                pe.matmul(h3[:, n % 2, :], w3T[:, e, k * P:(k + 1) * P], xs[:],
                                          start=True, stop=True).then_inc(s["h3_ready"], 1)
                            if e >= 1:
                                second_product(e - 1)
                        second_product(EXPERTS - 1)

                    @block.vector
                    def _(v):
                        step = Chain(v, s["chain"])
                        v.wait_ge(s["logits_ready"], 1)
                        step(v.tensor_copy(lg[:], logits[:]))
                        for j in range(G):
                            last = v.max(top[:, j, :], lg[:, j, :])
                        step(last)
                        for j in range(G):
                            last = v.max_index(at[:, j, :], top[:, j, :], lg[:, j, :])
                        step(last)
                        v.tensor_scalar(size[:], lg[:], -1.0, None, ALU.mult)
                        step(v.tensor_copy(atf[:], at[:]))
                        step(v.tensor_tensor(size[:], size[:], lg[:], ALU.max))
                        for j in range(G):
                            v.tensor_scalar(first[:, j, :], c.count8, atf[:, j, 0:1], None, ALU.is_equal)
                            last = v.tensor_scalar(second[:, j, :], c.count8, atf[:, j, 1:2], None, ALU.is_equal)
                        step(last)
                        for ex, lim, k in ((ex1, lim1, 0), (ex2, lim2, 1)):
                            t = top[:, :, k:k + 1].broadcast_to([P, G, EXPERTS])
                            step(v.tensor_tensor(lim[:], size[:], t, ALU.max))
                            step(v.tensor_tensor(gap[:], t, lg[:], ALU.subtract))
                            step(v.scalar_tensor_tensor(out=lim[:], in0=lim[:], scalar=2 * JITTER, in1=gap[:],
                                                        op0=ALU.mult, op1=ALU.is_ge))
                            last = v.tensor_scalar(ex[:], gap[:], -1.0, 0.0, ALU.mult, ALU.min)
                            if k == 0:
                                step(last)
                            else:
                                last.then_inc(s["shifted1"], 1)
                        step(v.tensor_scalar(rest[:], first[:], -1.0, 1.0, ALU.mult, ALU.add))
                        step(v.tensor_tensor(lim2[:], lim2[:], rest[:], ALU.mult))
                        v.wait_ge(s["exps"], 1)
                        v.tensor_tensor(ex1[:], ex1[:], lim1[:], ALU.mult)
                        step(v.tensor_tensor(ex2[:], ex2[:], lim2[:], ALU.mult))
                        v.tensor_reduce(total[:, 0, :], ex1[:], AX.X, ALU.add)
                        step(v.tensor_reduce(total[:, 1, :], ex2[:], AX.X, ALU.add))
                        step(v.reciprocal(mult[:], total[:]))
                        v.tensor_tensor(first[:], first[:], spread(mult[:, 0, :], EXPERTS), ALU.mult)
                        step(v.tensor_tensor(second[:], second[:], spread(mult[:, 1, :], EXPERTS), ALU.mult))
                        step(v.tensor_tensor(weight[:], first[:], second[:], ALU.add))

                        def hidden(n):
                            v.wait_ge(s["th_ready"], n + 1)
                            step(v.scalar_tensor_tensor(out=gated[:, n % 2, :], in0=th[:, n % 2, :], scalar=1.0,
                                                        in1=h1[:, n % 2, :], op0=ALU.add, op1=ALU.mult))
                            v.wait_ge(s["h3_ready"], n + 1)
                            if n >= 4:
                                v.wait_ge(s["y_ready"], (n - 4) // 2 + 1)
                            v.scalar_tensor_tensor(out=act[:, (n // 2) % 2, n % 2, :], in0=h3[:, n % 2, :], scalar=0.5,
                                                   in1=gated[:, n % 2, :], op0=ALU.mult,
                                                   op1=ALU.mult).then_inc(s["act_ready"], 1)

                        def gather(e):
                            v.wait_ge(s["y_ready"], e + 1)
                            for j in range(G):
                                if e == 0:
                                    last = v.tensor_scalar(acc[:, j, :], y[:, 0, j, :], weight[:, j, 0:1], None, ALU.mult)
                                else:
                                    last = v.scalar_tensor_tensor(out=acc[:, j, :], in0=y[:, e % 2, j, :],
                                                                  scalar=weight[:, j, e:e + 1], in1=acc[:, j, :],
                                                                  op0=ALU.mult, op1=ALU.add)
                            last.then_inc(s["y_used"], 1)
                            v.wait_ge(s["y_used"], e + 1)

                        for e in range(EXPERTS):
                            hidden(2 * e)
                            hidden(2 * e + 1)
                            if e >= 1:
                                gather(e - 1)
                        gather(EXPERTS - 1)
                        v.tensor_tensor(X[:, ds(i * G, G), :], acc[:], X[:, ds(i * G, G), :], ALU.add).then_inc(s["added"], 1)
                        v.wait_ge(s["added"], 1)
                st.end_step()


HEADS3 = 4
HD3 = P // HEADS3
LOCAL, MID = 7, 25
PATHS = 4
PAIRS = [(0, 1), (0, 2), (0, 3), (1, 2), (1, 3), (2, 3)]
FEATS = HEADS3 * (2 * PATHS + len(PAIRS))
HIDDEN3 = 2 * (P + FEATS)
FLOOR = 0.01
L2_EPS, MIX_EPS = 1e-12, 1e-5


def l3_attention_stage(nc, X, XNT, c, d):
    with Stage(nc, "a3") as outer:
        outs = outer.sb("outs", [P, TILES, PATHS, P])
        with Stage(nc, "a3x") as st:
            l3_paths_stage(nc, st, XNT, c, d, outs)
        with Stage(nc, "a3y") as st:
            l3_router_stage(nc, st, X, XNT, c, d, outs)


def l3_paths_stage(nc, outer, XNT, c, d, outs):
    proj = outer.sb("proj", [P, 3, P])
    wb = outer.sb("wb", [P, HEADS3])
    taps = outer.sb("taps", [P, 3, TAPS])
    wide_taps = outer.sb("wide_taps", [P, LOCAL + MID])
    masks = outer.sb("masks", [P, len(LEVELS), P])
    raw = outer.sb("raw", [P, 3, TAPS - 1 + SEQ])
    act = outer.sb("act", [P, 3, SEQ])
    th = outer.sb("th", [P, SEQ])
    qk = outer.sb("qk", [P, 2, SEQ])
    vh = outer.sb("vh", [P, MID - 1 + SEQ])
    lm = outer.sb("lm", [P, 2, SEQ])
    S = outer.sb("S", [P, P])
    with Stage(nc, "a3w") as st:
        s = st.sems("loaded")
        with nc.Block(no_gpsimd_drain=True) as block:
            @block.sync
            def _(sp):
                loads = [(proj[:, n, :], d[f"L3_attn_W{w}"]) for n, w in enumerate("qkv")]
                loads += [(taps[:, n, :], d[f"L3_attn_conv_{w}_w"]) for n, w in enumerate("qkv")]
                loads += [(wb[:], d["L3_attn_Wb"]), (wide_taps[:, 0:LOCAL], d["L3_attn_local_w"]),
                          (wide_taps[:, LOCAL:], d["L3_attn_mid_w"]), (masks[:], d["const_level_masks"])]
                for dst, src in loads:
                    sp.dma_start(dst, src).then_inc(s["loaded"], 16)
                sp.wait_ge(s["loaded"], 16 * len(loads))

            @block.vector
            def _(v):
                v.memset(raw[:, :, 0:TAPS - 1], 0.0)
                v.memset(vh[:, 0:MID - 1], 0.0)
                v.wait_ge(s["loaded"], 160)
                v.tensor_scalar(taps[:], taps[:], 0.5, None, ALU.mult)
        st.end_step()

    with nc.Fori(0, BATCH) as b:
        with Stage(nc, "a3p") as st:
            rawp = st.ps("rawp", (P, 3, SEQ))
            s = st.sems("raw_ready raw_copied conv_ready th_ready silu_ready done chain")
            with nc.Block(no_gpsimd_drain=True) as block:
                @block.tensor
                def _(pe):
                    for n in range(3):
                        for k in range(2):
                            last = pe.matmul(rawp[:, n, k * 512:(k + 1) * 512], proj[:, n, :],
                                             XNT[:, ds(b * SEQ + k * 512, 512)], start=True, stop=True)
                        last.then_inc(s["raw_ready"], 1)

                @block.scalar
                def _(a):
                    for n in range(3):
                        a.wait_ge(s["raw_ready"], n + 1)
                        a.activation(raw[:, n, TAPS - 1:], rawp[:, n, :], ACT.Copy).then_inc(s["raw_copied"], 1)
                    for n in range(3):
                        a.wait_ge(s["conv_ready"], n + 1)
                        if n >= 1:
                            a.wait_ge(s["silu_ready"], n)
                        a.activation(th[:], act[:, n, :], ACT.Tanh).then_inc(s["th_ready"], 1)

                @block.vector
                def _(v):
                    step = Chain(v, s["chain"])
                    v.memset(S[:], 0.0)

                    def convolve(out, src, w, taps_n):
                        step(v.tensor_scalar(out, src[:, taps_n - 1:taps_n - 1 + SEQ], w[:, taps_n - 1:taps_n], None, ALU.mult))
                        for k in range(taps_n - 1):
                            last = v.scalar_tensor_tensor(out=out, in0=src[:, k:k + SEQ], scalar=w[:, k:k + 1], in1=out,
                                                          op0=ALU.mult, op1=ALU.add)
                            if k < taps_n - 2:
                                step(last)
                        return last

                    for n in range(3):
                        v.wait_ge(s["raw_copied"], n + 1)
                        convolve(act[:, n, :], raw[:, n, :], taps[:, n, :], TAPS).then_inc(s["conv_ready"], 1)
                    for n, dst in enumerate((qk[:, 0, :], qk[:, 1, :], vh[:, MID - 1:])):
                        v.wait_ge(s["th_ready"], n + 1)
                        v.scalar_tensor_tensor(out=dst, in0=th[:], scalar=1.0, in1=act[:, n, :], op0=ALU.add,
                                               op1=ALU.mult).then_inc(s["silu_ready"], 1)
                    v.wait_ge(s["silu_ready"], 3)
                    convolve(lm[:, 0, :], vh[:, MID - LOCAL:], wide_taps[:, 0:LOCAL], LOCAL).then_inc(s["done"], 1)
                    convolve(lm[:, 1, :], vh[:], wide_taps[:, LOCAL:], MID).then_inc(s["done"], 1)
                    v.wait_ge(s["done"], 2)
            st.end_step()
        with Stage(nc, "a3d") as st:
            l3_chunk_steps(nc, st, XNT, c, b, wb, masks, qk, vh, lm, S, outs)


def l3_chunk_steps(nc, st, XNT, c, b, wb, masks, qk, vh, lm, S, outs):
    four = [P, HEADS3, P]
    heads = [P, HEADS3, HD3]
    K = len(LEVELS)
    xs, q, k0, kn, kn_tok, q2, k2, R, u = (st.sb(n, [P, P]) for n in
                                           ("xs", "q", "k0", "kn", "kn_tok", "q2", "k2", "R", "u"))
    vlm = st.sb("vlm", [P, 3, P])
    norms, rnorms = (st.sb(n, [P, 2, HEADS3]) for n in ("norms", "rnorms"))
    beta, nbeta, tb = (st.sb(n, [P, HEADS3]) for n in ("beta", "nbeta", "tb"))
    N, Nlev, AT = st.sb("N", four), st.sb("Nlev", [P, K, HEADS3, P]), st.sb("AT", four)
    T, XT, Zt = (st.sb(n, four) for n in ("T", "XT", "Zt"))
    small, tok, ups, sps = (st.ps(n, four) for n in ("small", "tok", "ups", "sps"))
    big = st.ps("big", (P, 4, 4, P))
    zt, tps, xps, os_ = (big[:, n] for n in range(4))
    s = st.sems("copied q_ready sq_ready small_ready tanh_ready sqrt_in sqrt_ready tok_ready kn_tok_ready kn_ps "
                "kn_ready gram_ready N_ready Nlev_ready qk_ready AT_ready kS_ready R_ready zt_ps zt_ready t_ps t_ready "
                "x_ps x_ready u_ps u_ready o_ps s_ps done vtok_ready chain")

    def head(h):
        return slice(h * HD3, (h + 1) * HD3)

    with nc.Fori(0, BLOCKS) as ch:
        with nc.Block(no_gpsimd_drain=True) as block:
            @block.gpsimd
            def _(g):
                g.tensor_copy(k0[:], qk[:, 1, ds(ch * P, P)])
                g.tensor_copy(q[:], qk[:, 0, ds(ch * P, P)]).then_inc(s["q_ready"], 1)
                g.tensor_copy(xs[:], XNT[:, ds(b * SEQ + ch * P, P)])
                g.tensor_copy(vlm[:, 0, :], vh[:, ds(ch * P + (MID - 1), P)])
                g.tensor_copy(vlm[:, 1:3, :], lm[:, :, ds(ch * P, P)]).then_inc(s["copied"], 1)
                g.wait_ge(s["N_ready"], 1)
                for k in range(K):
                    g.tensor_tensor(Nlev[:, k], N[:], masks[:, k:k + 1, :].broadcast_to(four), ALU.mult).then_inc(s["Nlev_ready"], 1)

            @block.scalar
            def _(a):
                a.wait_ge(s["q_ready"], 1)
                a.activation(k2[:], k0[:], ACT.Square)
                a.activation(q2[:], q[:], ACT.Square).then_inc(s["sq_ready"], 1)
                a.wait_ge(s["small_ready"], 1)
                a.activation(tb[:], small[:, 0, 2 * HEADS3:3 * HEADS3], ACT.Tanh, scale=0.5).then_inc(s["tanh_ready"], 1)
                a.wait_ge(s["sqrt_in"], 1)
                a.activation(norms[:], norms[:], ACT.Sqrt).then_inc(s["sqrt_ready"], 1)
                a.wait_ge(s["kn_ps"], 1)
                a.activation(kn[:], tok[:, 3, :], ACT.Copy).then_inc(s["kn_ready"], 1)
                for k in range(1, K):
                    a.wait_ge(s["zt_ps"], k + 1)
                    if k >= 2:
                        a.wait_ge(s["x_ps"], k - 1)
                    a.activation(Zt[:], zt, ACT.Copy).then_inc(s["zt_ready"], 1)

            @block.tensor
            def _(pe):
                def heads_of(out, lhs, rhs, sem):
                    for h in range(HEADS3):
                        last = pe.matmul(out[:, h, :], lhs(h), rhs(h), start=True, stop=True)
                    last.then_inc(sem, 1)

                pe.wait_ge(s["copied"], 1)
                pe.transpose(tok[:, 0, :], k0[:], c.ident)
                for n in range(3):
                    last = pe.transpose(ups[:, n, :], vlm[:, n, :], c.ident)
                last.then_inc(s["tok_ready"], 1)
                pe.wait_ge(s["sq_ready"], 1)
                pe.matmul(small[:, 0, 0:HEADS3], q2[:], c.head_blocks[:, 0:P:HD3], start=True, stop=True)
                pe.matmul(small[:, 0, HEADS3:2 * HEADS3], k2[:], c.head_blocks[:, 0:P:HD3], start=True, stop=True)
                pe.matmul(small[:, 0, 2 * HEADS3:3 * HEADS3], xs[:], wb[:], start=True, stop=True).then_inc(s["small_ready"], 1)
                pe.wait_ge(s["kn_tok_ready"], 1)
                pe.transpose(tok[:, 3, :], kn_tok[:], c.ident).then_inc(s["kn_ps"], 1)
                pe.wait_ge(s["kn_ready"], 1)
                heads_of(big[:, :, 0], lambda h: kn[head(h), :], lambda h: kn[head(h), :], s["gram_ready"])
                heads_of(big[:, :, 1], lambda h: kn[head(h), :], lambda h: q[head(h), :], s["qk_ready"])
                pe.matmul(sps[:, 0, :], kn[:], S[:], start=True, stop=True).then_inc(s["kS_ready"], 1)
                pe.wait_ge(s["N_ready"], 1)
                pe.wait_ge(s["AT_ready"], 1)
                for k in range(K):
                    pe.wait_ge(s["Nlev_ready"], k + 1)
                    if k >= 1:
                        pe.wait_ge(s["t_ready"], k)
                    heads_of(zt, lambda h: Nlev[:, k, h, :], lambda h: c.ident if k == 0 else T[:, h, :], s["zt_ps"])
                    if k >= 1:
                        pe.wait_ge(s["zt_ready"], k)
                        pe.wait_ge(s["x_ready"], k)
                        if k < K - 1:
                            heads_of(tps, lambda h: XT[:, h, :], lambda h: Zt[:, h, :], s["t_ps"])
                        heads_of(xps, lambda h: Zt[:, h, :], lambda h: XT[:, h, :], s["x_ps"])
                pe.wait_ge(s["x_ready"], K)
                pe.wait_ge(s["R_ready"], 1)
                pe.wait_ge(s["vtok_ready"], 1)
                for h in range(HEADS3):
                    last = pe.matmul(ups[:, 0, head(h)], XT[:, h, :], R[:, head(h)], start=True, stop=True)
                last.then_inc(s["u_ps"], 1)
                pe.matmul(os_[:, 0, :], q[:], S[:], start=True, stop=False)
                pe.wait_ge(s["u_ready"], 1)
                for h in range(HEADS3):
                    last = pe.matmul(os_[:, 0, head(h)], AT[:, h, :], u[:, head(h)], start=False, stop=(h == HEADS3 - 1))
                last.then_inc(s["o_ps"], 1)
                pe.matmul(sps[:, 0, :], kn_tok[:], u[:], start=True, stop=True).then_inc(s["s_ps"], 1)

            @block.vector
            def _(v):
                step = Chain(v, s["chain"])
                mine = outs[:, ds(b * BLOCKS + ch, 1), :, :].rearrange("p t n d -> p (t n) d")
                v.wait_ge(s["small_ready"], 1)
                v.wait_ge(s["tanh_ready"], 1)
                step(v.tensor_scalar(beta[:], tb[:], 0.5, 0.5, ALU.mult, ALU.add))
                v.tensor_scalar(nbeta[:], beta[:], -1.0, None, ALU.mult)
                v.tensor_scalar(norms[:].rearrange("p a h -> p (a h)"), small[:, 0, 0:2 * HEADS3], L2_EPS, None,
                                ALU.add).then_inc(s["sqrt_in"], 1)
                v.wait_ge(s["tok_ready"], 1)
                v.tensor_copy(mine[:, 3, :], ups[:, 0, :])
                v.tensor_copy(mine[:, 0:2, :], ups[:, 1:3, :]).then_inc(s["vtok_ready"], 1)
                v.wait_ge(s["sqrt_ready"], 1)
                step(v.reciprocal(rnorms[:], norms[:]))
                v.tensor_tensor(kn_tok[:].rearrange("p (h d) -> p h d", h=HEADS3),
                                tok[:, 0, :].rearrange("p (h d) -> p h d", h=HEADS3),
                                spread(rnorms[:, 1, :], HD3), ALU.mult).then_inc(s["kn_tok_ready"], 1)
                v.wait_ge(s["qk_ready"], 1)
                step(v.tensor_tensor(N[:], big[:, :, 0], c.strict.unsqueeze(1).broadcast_to(four), ALU.mult))
                v.tensor_tensor(N[:], N[:], spread(nbeta[:], P), ALU.mult).then_inc(s["N_ready"], 1)
                v.tensor_tensor(AT[:], big[:, :, 1], c.upto.unsqueeze(1).broadcast_to(four), ALU.mult).then_inc(s["AT_ready"], 1)
                v.wait_ge(s["kS_ready"], 1)
                v.wait_ge(s["vtok_ready"], 1)
                v.tensor_tensor(R[:], mine[:, 3, :], sps[:, 0, :], ALU.subtract).then_inc(s["R_ready"], 1)
                idn = c.ident.unsqueeze(1).broadcast_to(four)
                v.wait_ge(s["zt_ps"], 1)
                v.tensor_tensor(T[:], zt, idn, ALU.add).then_inc(s["t_ready"], 1)
                v.wait_ge(s["Nlev_ready"], 1)
                v.tensor_tensor(XT[:], Nlev[:, 0], idn, ALU.add).then_inc(s["x_ready"], 1)
                for k in range(1, K):
                    if k < K - 1:
                        v.wait_ge(s["t_ready"], k)
                        v.wait_ge(s["t_ps"], k)
                        v.tensor_tensor(T[:], tps, T[:], ALU.add).then_inc(s["t_ready"], 1)
                    v.wait_ge(s["x_ready"], k)
                    v.wait_ge(s["x_ps"], k)
                    v.tensor_tensor(XT[:], xps, XT[:], ALU.add).then_inc(s["x_ready"], 1)
                v.wait_ge(s["u_ps"], 1)
                v.tensor_tensor(u[:].rearrange("p (h d) -> p h d", h=HEADS3),
                                ups[:, 0, :].rearrange("p (h d) -> p h d", h=HEADS3),
                                spread(beta[:], HD3), ALU.mult).then_inc(s["u_ready"], 1)
                v.wait_ge(s["o_ps"], 1)
                v.tensor_tensor(mine[:, 2, :].rearrange("p (h d) -> p h d", h=HEADS3),
                                os_[:, 0, :].rearrange("p (h d) -> p h d", h=HEADS3),
                                spread(rnorms[:, 0, :], HD3), ALU.mult)
                v.wait_ge(s["s_ps"], 1)
                step(v.tensor_tensor(R[:], sps[:, 0, :], c.head_blocks, ALU.mult))
                v.tensor_tensor(S[:], S[:], R[:], ALU.add).then_inc(s["done"], 1)
                v.wait_ge(s["done"], 1)
        st.end_step()


def l3_router_stage(nc, outer, X, XNT, c, d, outs):
    HC = [(0, P), (P, 2 * P), (2 * P, HIDDEN3)]
    Q = HEADS3 * PATHS
    rw1a = outer.sb("rw1a", [P, HIDDEN3])
    rw1b = outer.sb("rw1b", [FEATS, HIDDEN3])
    rb1 = outer.sb("rb1", [1, HIDDEN3])
    rw2 = outer.sb("rw2", [P, 3, Q])
    rb2 = outer.sb("rb2", [1, Q])
    wo = outer.sb("wo", [P, P])
    rows = outer.sb("rows", [1, 2, P])
    mixw = outer.sb("mixw", [P, 2, P])
    with Stage(nc, "a3v") as st:
        pr = st.ps("pr", (P, 2, P))
        s = st.sems("loaded rows_ready rows_ps")
        with nc.Block(no_gpsimd_drain=True) as block:
            @block.sync
            def _(sp):
                loads = [(rw1a[:], d["L3_attn_r_w1"][0:P, :]), (rw1b[:], d["L3_attn_r_w1"][P:P + FEATS, :]),
                         (rb1[:], d["L3_attn_r_b1"].rearrange("(a d) -> a d", a=1)),
                         (rb2[:], d["L3_attn_r_b2"].rearrange("(a d) -> a d", a=1)), (wo[:], d["L3_attn_Wo"]),
                         (rows[:, 0, :], d["L3_attn_mix_w"].rearrange("(a h) e -> a (h e)", a=1))]
                loads += [(rw2[0:k1 - k0, n, :], d["L3_attn_r_w2"][k0:k1, :]) for n, (k0, k1) in enumerate(HC)]
                loads += [(rows[:, 1, h * HD3:(h + 1) * HD3], d["L3_attn_onorm_w"].rearrange("(a d) -> a d", a=1))
                          for h in range(HEADS3)]
                for dst, src in loads:
                    sp.dma_start(dst, src).then_inc(s["loaded"], 16)
                assert len(loads) == 13
                sp.wait_ge(s["loaded"], 16 * 13)

            @block.tensor
            def _(pe):
                pe.wait_ge(s["loaded"], 16 * 13)
                pe.matmul(flat(pr[:]), c.ones[0:1, :], rows[:].rearrange("a n d -> a (n d)"), start=True,
                          stop=True).then_inc(s["rows_ps"], 1)

            @block.vector
            def _(v):
                v.wait_ge(s["rows_ps"], 1)
                v.tensor_copy(mixw[:], pr[:])
                for n, (k0, k1) in enumerate(HC):
                    v.tensor_scalar(rw2[0:k1 - k0, n, :], rw2[0:k1 - k0, n, :], 0.5, None, ALU.mult)
        st.end_step()

    with Stage(nc, "a3s") as st:
        NP = len(PAIRS)
        xs = st.sb("xs", [P, G, P])
        o = st.sb("o", [P, G * PATHS, P])
        mean, var = st.sb("mean", [P, G * Q]), st.sb("var", [P, G * Q])
        cent = st.sb("cent", [P, G * Q, HD3])
        prod = st.sb("prod", [P, G, NP, P])
        cross = st.sb("cross", [P, G, NP * HEADS3])
        F = st.sb("F", [P, G, FEATS])
        FT = st.sb("FT", [FEATS, G, P])
        th, hid = st.sb("th", [P, 2, HIDDEN3]), st.sb("hid", [P, 2, HIDDEN3])
        hT = st.sb("hT", [P, 2, 3, P])
        lg, w = (st.sb(n, [P, G * HEADS3, PATHS]) for n in ("lg", "w"))
        hmax, total, ms, rms = (st.sb(n, [P, G * HEADS3]) for n in ("hmax", "total", "ms", "rms"))
        mixed, sq = st.sb("mixed", [P, G * HEADS3, HD3]), st.sb("sq", [P, G * HEADS3, HD3])
        mT = st.sb("mT", [P, G, P])
        FTp = st.ps("FTp", (P, G, P))
        h1 = st.ps("h1", (P, 2, 512))
        hTp = st.ps("hTp", (P, 2, 512))
        lgp = st.ps("lgp", (P, G, Q))
        mTp = st.ps("mTp", (P, G, P))
        outp = st.ps("outp", (P, G, P))
        s = st.sems("xs_ready F_ready FT_ps FT_ready h1_ready th_ready hid_ready hT_ps hT_ready lg_ready shifted exps "
                    "ms_ready rms_ready mixed_ready mT_ps mT_ready out_ps o_ready added chain")
        with nc.Fori(0, TILES // G) as i:
            with nc.Block(no_gpsimd_drain=True) as block:
                @block.gpsimd
                def _(g):
                    g.tensor_copy(o[:], outs[:, ds(i * G, G), :, :].rearrange("p t n d -> p (t n) d")).then_inc(s["o_ready"], 1)

                @block.scalar
                def _(a):
                    a.activation(xs[:].rearrange("p t d -> p (t d)"), XNT[:, ds(i * G * P, G * P)],
                                 ACT.Copy).then_inc(s["xs_ready"], 1)
                    a.wait_ge(s["FT_ps"], 1)
                    a.activation(FT[:], FTp[0:FEATS], ACT.Copy).then_inc(s["FT_ready"], 1)
                    for j in range(G):
                        a.wait_ge(s["h1_ready"], j + 1)
                        if j >= 2:
                            a.wait_ge(s["hid_ready"], j - 1)
                        a.activation(th[:, j % 2, :], h1[:, j % 2, 0:HIDDEN3], ACT.Tanh, scale=0.5).then_inc(s["th_ready"], 1)
                        a.wait_ge(s["hT_ps"], j + 1)
                        a.activation(hT[:, j % 2, 0:2, :].rearrange("p n d -> p (n d)"), hTp[:, j % 2, 0:2 * P], ACT.Copy)
                        last = a.activation(hT[0:HIDDEN3 - 2 * P, j % 2, 2, :], hTp[0:HIDDEN3 - 2 * P, j % 2, 2 * P:3 * P],
                                            ACT.Copy)
                        last.then_inc(s["hT_ready"], 1)
                    a.wait_ge(s["shifted"], 1)
                    a.activation(lg[:], lg[:], ACT.Exp).then_inc(s["exps"], 1)
                    for n in range(2):
                        a.wait_ge(s["ms_ready"], n + 1)
                        a.activation(rms[:], ms[:], ACT.Sqrt).then_inc(s["rms_ready"], 1)
                    a.wait_ge(s["mT_ps"], 1)
                    a.activation(mT[:], mTp[:], ACT.Copy).then_inc(s["mT_ready"], 1)

                @block.tensor
                def _(pe):
                    pe.wait_ge(s["F_ready"], 1)
                    for j in range(G):
                        last = pe.transpose(FTp[0:FEATS, j, :], F[:, j, :], c.ident)
                    last.then_inc(s["FT_ps"], 1)
                    pe.wait_ge(s["xs_ready"], 1)
                    pe.wait_ge(s["FT_ready"], 1)

                    def hidden(j):
                        if j >= 2:
                            pe.wait_ge(s["hid_ready"], j - 1)
                        o1 = h1[:, j % 2, 0:HIDDEN3]
                        pe.matmul(o1, xs[:, j, :], rw1a[:], start=True, stop=False)
                        pe.matmul(o1, FT[:, j, :], rw1b[:], start=False, stop=False)
                        pe.matmul(o1, c.ones[0:1, :], rb1[:], start=False, stop=True).then_inc(s["h1_ready"], 1)

                    hidden(0)
                    for j in range(G):
                        if j + 1 < G:
                            hidden(j + 1)
                        pe.wait_ge(s["hid_ready"], j + 1)
                        if j >= 2:
                            pe.wait_ge(s["hT_ready"], j - 1)
                        for n, (k0, k1) in enumerate(HC):
                            last = pe.transpose(hTp[0:k1 - k0, j % 2, n * P:(n + 1) * P], hid[:, j % 2, k0:k1], c.ident)
                        last.then_inc(s["hT_ps"], 1)
                        pe.wait_ge(s["hT_ready"], j + 1)
                        for n, (k0, k1) in enumerate(HC):
                            pe.matmul(lgp[:, j, :], hT[0:k1 - k0, j % 2, n, :], rw2[0:k1 - k0, n, :], start=(n == 0), stop=False)
                        pe.matmul(lgp[:, j, :], c.ones[0:1, :], rb2[:], start=False, stop=True).then_inc(s["lg_ready"], 1)
                    pe.wait_ge(s["mixed_ready"], 1)
                    for j in range(G):
                        last = pe.transpose(mTp[:, j, :], mixed[:, j * HEADS3:(j + 1) * HEADS3, :]
                                            .rearrange("p h e -> p (h e)"), c.ident)
                    last.then_inc(s["mT_ps"], 1)
                    pe.wait_ge(s["mT_ready"], 1)
                    for j in range(G):
                        last = pe.matmul(outp[:, j, :], mT[:, j, :], wo[:], start=True, stop=True)
                    last.then_inc(s["out_ps"], 1)

                @block.vector
                def _(v):
                    step = Chain(v, s["chain"])
                    v.wait_ge(s["o_ready"], 1)
                    by_head = o[:].rearrange("p n (h e) -> p (n h) e", h=HEADS3)
                    step(v.tensor_reduce(mean[:], by_head, AX.X, ALU.add))
                    step(v.tensor_scalar(mean[:], mean[:], 1.0 / HD3, None, ALU.mult))
                    step(v.tensor_tensor(cent[:], by_head, spread(mean[:], HD3), ALU.subtract))
                    step(v.tensor_tensor(cent[:], cent[:], cent[:], ALU.mult))
                    step(v.tensor_reduce(var[:], cent[:], AX.X, ALU.add))
                    by_tile = o[:].rearrange("p (t n) d -> p t n d", t=G)
                    for n, (x, y) in enumerate(PAIRS):
                        last = v.tensor_tensor(prod[:, :, n, :], by_tile[:, :, x, :], by_tile[:, :, y, :], ALU.mult)
                    step(last)
                    step(v.tensor_reduce(cross[:].rearrange("p t n -> p (t n)"),
                                         prod[:].rearrange("p t n (h e) -> p (t n h) e", h=HEADS3), AX.X, ALU.add))
                    stats = F[:, :, 0:2 * Q].rearrange("p t (n w h) -> p t n w h", n=PATHS, w=2)
                    for j in range(G):
                        v.tensor_copy(stats[:, j, :, 0, :], mean[:, j * Q:(j + 1) * Q].rearrange("p (n h) -> p n h", n=PATHS))
                        v.tensor_scalar(stats[:, j, :, 1, :], var[:, j * Q:(j + 1) * Q].rearrange("p (n h) -> p n h", n=PATHS),
                                        1.0 / (HD3 - 1), None, ALU.mult)
                    v.tensor_scalar(F[:, :, 2 * Q:], cross[:], 1.0 / HD3, None, ALU.mult).then_inc(s["F_ready"], 1)
                    for j in range(G):
                        v.wait_ge(s["th_ready"], j + 1)
                        if j >= 2:
                            v.wait_ge(s["hT_ps"], j - 1)
                        v.scalar_tensor_tensor(out=hid[:, j % 2, :], in0=th[:, j % 2, :], scalar=1.0,
                                               in1=h1[:, j % 2, 0:HIDDEN3], op0=ALU.add, op1=ALU.mult).then_inc(s["hid_ready"], 1)
                    v.wait_ge(s["lg_ready"], G)
                    logit = lgp[:].rearrange("p t (h n) -> p (t h) n", h=HEADS3)
                    step(v.tensor_reduce(hmax[:], logit, AX.X, ALU.max))
                    v.tensor_tensor(lg[:], logit, spread(hmax[:], PATHS), ALU.subtract).then_inc(s["shifted"], 1)
                    v.wait_ge(s["exps"], 1)
                    step(v.tensor_reduce(total[:], lg[:], AX.X, ALU.add))
                    step(v.reciprocal(total[:], total[:]))
                    step(v.tensor_tensor(w[:], lg[:], spread(total[:], PATHS), ALU.mult))
                    step(v.tensor_scalar(w[:], w[:], 1.0 - 4.0 * FLOOR, FLOOR, ALU.mult, ALU.add))
                    for j in range(G):
                        wj = w[:, j * HEADS3:(j + 1) * HEADS3, :].rearrange("p h n -> p n h")
                        last = v.tensor_tensor(cent[:, j * Q:(j + 1) * Q, :].rearrange("p (n h) e -> p n h e", n=PATHS),
                                               by_head[:, j * Q:(j + 1) * Q, :].rearrange("p (n h) e -> p n h e", n=PATHS),
                                               wj.unsqueeze(3).broadcast_to([P, PATHS, HEADS3, HD3]), ALU.mult)
                    step(last)
                    for j in range(G):
                        last = v.tensor_reduce(mixed[:, j * HEADS3:(j + 1) * HEADS3, :].rearrange("p h e -> p (h e)"),
                                               cent[:, j * Q:(j + 1) * Q, :].rearrange("p (n h) e -> p (h e) n", n=PATHS),
                                               AX.X, ALU.add)
                    step(last)
                    for n in range(2):
                        step(v.tensor_tensor(sq[:], mixed[:], mixed[:], ALU.mult))
                        step(v.tensor_reduce(ms[:], sq[:], AX.X, ALU.add))
                        v.tensor_scalar(ms[:], ms[:], 1.0 / HD3, MIX_EPS, ALU.mult, ALU.add).then_inc(s["ms_ready"], 1)
                        v.wait_ge(s["rms_ready"], n + 1)
                        step(v.reciprocal(total[:], rms[:]))
                        step(v.tensor_tensor(mixed[:], mixed[:], spread(total[:], HD3), ALU.mult))
                        last = v.tensor_tensor(mixed[:].rearrange("p (t h) e -> p t (h e)", t=G),
                                               mixed[:].rearrange("p (t h) e -> p t (h e)", t=G),
                                               mixw[:, n:n + 1, :].broadcast_to([P, G, P]), ALU.mult)
                        if n == 0:
                            step(last)
                    last.then_inc(s["mixed_ready"], 1)
                    v.wait_ge(s["out_ps"], 1)
                    v.tensor_tensor(X[:, ds(i * G, G), :], outp[:], X[:, ds(i * G, G), :], ALU.add).then_inc(s["added"], 1)
                    v.wait_ge(s["added"], 1)
            st.end_step()



def l3_ffn_stage(nc, X, XNT, c, router_w, router_b, expert_w, expert_b):
    with Stage(nc, "f3") as outer:
        rwT = outer.sb("rwT", [P, EXPERTS])
        ewT = outer.sb("ewT", [P, EXPERTS, P])
        rb = outer.sb("rb", [1, EXPERTS])
        eb = outer.sb("eb", [1, EXPERTS * P])
        load_turned(nc, "f3t", [(rwT[:], router_w)] + [(ewT[:, e, :], expert_w[e]) for e in range(EXPERTS)], c)
        with Stage(nc, "f3w") as st:
            s = st.sems("loaded")
            with nc.Block(no_gpsimd_drain=True) as block:
                @block.sync
                def _(sp):
                    sp.dma_start(rb[:], router_b.rearrange("(a d) -> a d", a=1)).then_inc(s["loaded"], 16)
                    sp.dma_start(eb[:], expert_b.rearrange("(a e) d -> a (e d)", a=1)).then_inc(s["loaded"], 16)
                    sp.wait_ge(s["loaded"], 32)
            st.end_step()
        with Stage(nc, "f3s") as st:
            xs = st.sb("xs", [P, G * P])
            lg, ex, choice = (st.sb(n, [P, G, EXPERTS]) for n in ("lg", "ex", "choice"))
            top = st.sb("top", [P, G, 8])
            at = st.sb("at", [P, G, 8], U32)
            atf = st.sb("atf", [P, G, 8])
            total, weight = (st.sb(n, [P, G]) for n in ("total", "weight"))
            picked = st.sb("picked", [P, 2, EXPERTS, P])
            summed = st.sb("summed", [P, G, P])
            logits = st.ps("logits", (P, G, EXPERTS))
            y = st.ps("y", (P, 2, EXPERTS, P))
            s = st.sems("xs_ready logits_ready y_ready shifted exps y_used added chain")
            with nc.Fori(0, TILES // G) as i:
                with nc.Block(no_gpsimd_drain=True) as block:
                    @block.scalar
                    def _(a):
                        a.activation(xs[:], XNT[:, ds(i * G * P, G * P)], ACT.Copy).then_inc(s["xs_ready"], 1)
                        a.wait_ge(s["shifted"], 1)
                        a.activation(ex[:], ex[:], ACT.Exp).then_inc(s["exps"], 1)

                    @block.tensor
                    def _(pe):
                        pe.wait_ge(s["xs_ready"], 1)
                        for j in range(G):
                            pe.matmul(logits[:, j, :], xs[:, j * P:(j + 1) * P], rwT[:], start=True, stop=False)
                            last = pe.matmul(logits[:, j, :], c.ones[0:1, :], rb[:], start=False, stop=True)
                        last.then_inc(s["logits_ready"], 1)
                        for j in range(G):
                            if j >= 2:
                                pe.wait_ge(s["y_used"], j - 1)
                            for k in range(0, EXPERTS, 4):
                                o = y[:, j % 2, k:k + 4, :].rearrange("p e d -> p (e d)")
                                pe.matmul(o, xs[:, j * P:(j + 1) * P], ewT[:, k:k + 4, :].rearrange("p e d -> p (e d)"),
                                          start=True, stop=False)
                                last = pe.matmul(o, c.ones[0:1, :], eb[:, k * P:(k + 4) * P], start=False, stop=True)
                            last.then_inc(s["y_ready"], 1)

                    @block.vector
                    def _(v):
                        step = Chain(v, s["chain"])
                        v.wait_ge(s["logits_ready"], 1)
                        step(v.tensor_copy(lg[:], logits[:]))
                        for j in range(G):
                            last = v.max(top[:, j, :], lg[:, j, :])
                        step(last)
                        v.tensor_tensor(ex[:], lg[:], top[:, :, 0:1].broadcast_to([P, G, EXPERTS]),
                                        ALU.subtract).then_inc(s["shifted"], 1)
                        for j in range(G):
                            last = v.max_index(at[:, j, :], top[:, j, :], lg[:, j, :])
                        step(last)
                        step(v.tensor_copy(atf[:], at[:]))
                        v.wait_ge(s["exps"], 1)
                        step(v.tensor_reduce(total[:], ex[:], AX.X, ALU.add))
                        step(v.reciprocal(weight[:], total[:]))
                        for j in range(G):
                            last = v.tensor_scalar(choice[:, j, :], c.count8, atf[:, j, 0:1], weight[:, j:j + 1],
                                                   ALU.is_equal, ALU.mult)
                        step(last)
                        for j in range(G):
                            v.wait_ge(s["y_ready"], j + 1)
                            v.tensor_tensor(picked[:, j % 2], y[:, j % 2], spread(choice[:, j, :], P),
                                            ALU.mult).then_inc(s["y_used"], 1)
                            v.wait_ge(s["y_used"], j + 1)
                            step(v.tensor_reduce(summed[:, j, :], picked[:, j % 2].rearrange("p e d -> p d e"),
                                                 AX.X, ALU.add))
                        v.tensor_tensor(X[:, ds(i * G, G), :], summed[:], X[:, ds(i * G, G), :],
                                        ALU.add).then_inc(s["added"], 1)
                        v.wait_ge(s["added"], 1)
                st.end_step()


def build(nc, d, out, stages):
    with ExitStack() as ctx:
        def sb(name, shape):
            return ctx.enter_context(nc.sbuf_tensor(name, shape, F32))

        X = sb("X", [P, TILES, P])
        consts = sb("consts", [P, len(SQUARES) * P + 8])
        c = Constants(consts)
        load_stage(nc, X, d["L0_attn_x"], d["const_squares"], c)

        for k, stage in enumerate(SUBLAYERS):
            if k in stages:
                with ExitStack() as inner:
                    XN = inner.enter_context(nc.sbuf_tensor(f"XN{k}", [P, TILES + 1, P], F32))
                    XNT = inner.enter_context(nc.sbuf_tensor(f"XNT{k}", [P, TILES * P], F32))
                    layernorm_stage(nc, X, XN, XNT, c)
                    stage(nc, d, X, XN, XNT, c)

        with Stage(nc, "store") as st:
            s = st.sems("stored")
            with nc.Block(no_gpsimd_drain=True) as block:
                @block.sync
                def _(sp):
                    sp.dma_start(out.rearrange("b (t p) d -> p (b t) d", p=P), X[:]).then_inc(s["stored"], 16)
                    sp.wait_ge(s["stored"], 16)
            st.end_step()


def sub0(nc, d, X, XN, XNT, c):
    l0_attention_stage(nc, X, XNT, c, d["L0_attn_W_Q"], d["L0_attn_W_K"], d["L0_attn_W_V"], d["L0_attn_W_O"],
                       d["const_alibi"], d["const_key_pos"])


def sub1(nc, d, X, XN, XNT, c):
    l0_ffn_stage(nc, X, XNT, c, d["L0_ffn_w_gate"], d["L0_ffn_w_expert"], d["L0_ffn_b_expert"])


def sub2(nc, d, X, XN, XNT, c):
    l1_attention_stage(nc, X, XNT, c, d)


def sub3(nc, d, X, XN, XNT, c):
    l1_ffn_stage(nc, X, XN, c, d)


def sub4(nc, d, X, XN, XNT, c):
    l2_attention_stage(nc, X, XN, XNT, c)


def sub5(nc, d, X, XN, XNT, c):
    l2_ffn_stage(nc, X, XNT, c, d["L2_ffn_gate_w"], d["L2_ffn_w1"], d["L2_ffn_w2"], d["L2_ffn_w3"])


def sub6(nc, d, X, XN, XNT, c):
    l3_attention_stage(nc, X, XNT, c, d)


def sub7(nc, d, X, XN, XNT, c):
    l3_ffn_stage(nc, X, XNT, c, d["L3_ffn_router_w"], d["L3_ffn_router_b"], d["L3_ffn_expert_w"],
                 d["L3_ffn_expert_b"])


def more_constants():
    j, i = np.arange(P)[:, None], np.arange(P)[None, :]
    masks = [(j // (2 * n) == i // (2 * n)) & (j // n % 2 == 0) & (i // n % 2 == 1) for n in LEVELS]
    half = np.arange(0, HDW, 2, dtype=np.float32)
    t = np.arange(SEQ, dtype=np.float32)
    freqs = t[:, None] * (np.float32(1.0) / np.float32(10000.0) ** (half / np.float32(HDW)))[None, :]
    power = (t - SEQ // 2) / np.float32(WINDOW // 2)
    scale = ((half + 0.4 * HDW) / (1.4 * HDW)).astype(np.float64)[None, :] ** power[:, None]
    cos, sin = np.cos(freqs.astype(np.float64)), np.sin(freqs.astype(np.float64))
    rope = [np.concatenate([cos * w, cos * w], 1) if n == 0 else np.concatenate([-sin * w, sin * w], 1)
            for w in (scale, 1.0 / scale) for n in range(2)]
    rope = np.stack(rope).reshape(4, BLOCKS, P, HDW).transpose(2, 0, 1, 3)
    rope = np.concatenate([rope, rope[:, :, 0:1]], axis=2)
    has_prev = np.zeros((P, 2, BLOCKS + 1))
    has_prev[P - 1, 0, 1:BLOCKS] = 1.0
    has_prev[:, 1, 1:BLOCKS] = 1.0
    query = (np.arange(BLOCKS)[None, :] * P + np.arange(P)[:, None])[:, :, None]
    key = (np.arange(BLOCKS)[:, None] * P - WINDOW + np.arange(KEYS)[None, :])[None]
    seen = (key <= query) & (key >= query - WINDOW) & (key >= 0)
    return {"const_level_masks": np.stack(masks, axis=1), "const_rope": rope, "const_has_prev": has_prev,
            "const_band": np.where(seen, 0.0, NEG),
            "const_shifts": np.stack([j == i - 1, (j == P - 1) & (i == 0)], axis=1)}


SUBLAYERS = [sub0, sub1, sub2, sub3, sub4, sub5, sub6, sub7]

SQUARES = ["ident", "ones", "upto", "after", "strict", "neg_upper", "head_blocks"]


def constants():
    i = np.arange(P)
    row, col = i[:, None], i[None, :]
    squares = {
        "ident": row == col,
        "ones": np.ones((P, P)),
        "upto": row <= col,
        "after": row > col,
        "strict": row < col,
        "neg_upper": np.where(col > row, NEG, 0.0),
        "head_blocks": row // 32 == col // 32,
    }
    table = np.concatenate([squares[n].astype(np.float32) for n in SQUARES]
                           + [np.broadcast_to(np.arange(8, dtype=np.float32), (P, 8))], axis=1)
    slopes = 1.0 / np.float32(256.0) ** ((np.arange(HEADS0, dtype=np.float32) + 1) / HEADS0)
    alibi = np.zeros((1, HEADS0 // HG + 1, HG, ROWS), np.float32)
    alibi[0, :-1, :, HD0] = slopes.reshape(-1, HG)
    alibi[0, -1, :, HD0] = 1.0
    alibi = alibi.reshape(1, HEADS0 // HG + 1, P)
    made = {"const_squares": table, "const_alibi": alibi,
            "const_key_pos": np.arange(SEQ, dtype=np.float32)[None, :] - SEQ // 2}
    made.update(more_constants())
    return {k: np.ascontiguousarray(a, dtype=np.float32) for k, a in made.items()}


_STAGES = range(8)


def kernel(**inputs):
    import concourse.bacc as _bacc
    from concourse.bass_utils import run_bass_kernel_spmd as _run

    nc = _bacc.Bacc("TRN2", target_bir_lowering=False, num_devices=1)
    arrays, d = {}, {}
    for name, a in {**inputs, **constants()}.items():
        a = np.ascontiguousarray(a)
        arrays[f"in_{name}_dram"] = a
        d[name] = nc.dram_tensor(f"in_{name}_dram", a.shape, mybir.dt.from_np(a.dtype), kind="ExternalInput").ap()
    out = nc.dram_tensor("out_0_dram", (BATCH, SEQ, P), F32, kind="ExternalOutput").ap()
    build(nc, d, out, _STAGES)
    r = _run(nc, [arrays], core_ids=[0])
    return r.results[0]["out_0_dram"]
```

```python
from contextlib import ExitStack

import numpy as np

import concourse.bass as bass
from concourse import mybir

F32 = mybir.dt.float32
U32 = mybir.dt.uint32
ACT = mybir.ActivationFunctionType
ALU = mybir.AluOpType
AX = mybir.AxisListType
ds = bass.ds

P = 128
BATCH = 4
BLOCKS = 8
TILES = BATCH * BLOCKS
SEQ = BLOCKS * P
G = 4
LN_EPS = 1e-5
NEG = -1e30


class Stage:

    def __init__(self, nc, name):
        self.nc, self.name, self.ctx = nc, name, ExitStack()

    def __enter__(self):
        self.ctx.__enter__()
        return self

    def __exit__(self, *exc):
        return self.ctx.__exit__(*exc)

    def sb(self, name, shape, dt=F32):
        return self.ctx.enter_context(self.nc.sbuf_tensor(f"{self.name}_{name}", shape, dt))

    def ps(self, name, shape=(P, 512)):
        return self.ctx.enter_context(self.nc.psum_tensor(f"{self.name}_{name}", list(shape), F32))

    def sems(self, names):
        made = {n: self.ctx.enter_context(self.nc.semaphore(f"{self.name}_{n}")) for n in names.split()}
        nums = sorted(sem.num for sem in made.values())
        starts = [n for n in nums if n - 1 not in nums]
        ends = [n + 1 for n in nums if n + 1 not in nums]
        self.ranges = [range(a, b) for a, b in zip(starts, ends)]
        return made

    def end_step(self):
        for r in self.ranges:
            self.nc.gpsimd.sem_clear(r)
        self.nc.all_engine_barrier(sem_only=True)


class Constants:

    def __init__(self, table):
        self.all = table
        (self.ident, self.ones, self.upto, self.after, self.strict, self.neg_upper,
         self.head_blocks) = (table[:, k * P:(k + 1) * P] for k in range(len(SQUARES)))
        self.count8 = table[:, len(SQUARES) * P:]


class Chain:

    def __init__(self, engine, sem):
        self.engine, self.sem, self.n = engine, sem, 0

    def __call__(self, ins):
        self.n += 1
        ins.then_inc(self.sem, 1)
        self.engine.wait_ge(self.sem, self.n)


def tile(X, i):
    return X[:, ds(i, 1), :].rearrange("p a d -> p (a d)")


def flat(ap):
    return ap.rearrange("p a d -> p (a d)")


def spread(ap, n):
    return ap.unsqueeze(2).broadcast_to([ap.shape[0], ap.shape[1], n])


def load_stage(nc, X, x, consts, c):
    with Stage(nc, "load") as st:
        s = st.sems("loaded")
        with nc.Block(no_gpsimd_drain=True) as block:
            @block.sync
            def _(sp):
                sp.dma_start(X[:], x.rearrange("b (t p) d -> p (b t) d", p=P)).then_inc(s["loaded"], 16)
                sp.dma_start(c.all[:], consts).then_inc(s["loaded"], 16)
                sp.wait_ge(s["loaded"], 32)
        st.end_step()


def layernorm_stage(nc, X, XN, XNT, c):
    with Stage(nc, f"ln{nc.next_id()}") as st:
        stats = st.sb("stats", [P, G, 6])
        mv = st.sb("mv", [P, G, 2])
        var = st.sb("var", [P, G])
        std = st.sb("std", [P, G])
        rstd = st.sb("rstd", [P, G])
        xs = st.sb("xs", [P, G, P])
        turned = st.ps("turned")
        s = st.sems("var_ready std_ready xs_ready turned_ready xnt_done xn_done chain")
        with nc.Fori(0, TILES // G) as i:
            with nc.Block(no_gpsimd_drain=True) as block:
                @block.vector
                def _(v):
                    step = Chain(v, s["chain"])
                    for j in range(G):
                        last = v.bn_stats(stats[:, j, :], tile(X, i * G + j))
                    step(last)
                    for j in range(G):
                        last = v.bn_aggr(mv[:, j, :], stats[:, j, :])
                    step(last)
                    v.tensor_scalar(var[:], mv[:, :, 1], LN_EPS, None, ALU.add).then_inc(s["var_ready"], 1)
                    v.wait_ge(s["std_ready"], 1)
                    step(v.reciprocal(rstd[:], std[:]))
                    for j in range(G):
                        last = v.tensor_scalar(xs[:, j, :], tile(X, i * G + j), mv[:, j, 0:1], rstd[:, j:j + 1],
                                               ALU.subtract, ALU.mult)
                    last.then_inc(s["xs_ready"], 1)

                @block.scalar
                def _(a):
                    a.wait_ge(s["var_ready"], 1)
                    a.activation(std[:], var[:], ACT.Sqrt).then_inc(s["std_ready"], 1)
                    a.wait_ge(s["turned_ready"], 1)
                    a.activation(XNT[:, ds(i * G * P, G * P)], turned[:], ACT.Copy).then_inc(s["xnt_done"], 1)
                    a.wait_ge(s["xnt_done"], 1)

                @block.tensor
                def _(pe):
                    pe.wait_ge(s["xs_ready"], 1)
                    for j in range(G):
                        last = pe.transpose(turned[:, j * P:(j + 1) * P], xs[:, j, :], c.ident)
                    last.then_inc(s["turned_ready"], 1)

                @block.gpsimd
                def _(g):
                    g.wait_ge(s["xs_ready"], 1)
                    g.tensor_copy(XN[:, ds(i * G, G), :], xs[:]).then_inc(s["xn_done"], 1)
                    g.wait_ge(s["xn_done"], 1)
            st.end_step()


def load_turned(nc, name, pairs, c):
    with Stage(nc, name) as st:
        raw = st.sb("raw", [P, len(pairs), P])
        turned = st.ps("turned", (P, 4, 512))
        s = st.sems("loaded turned_ready copied")
        with nc.Block(no_gpsimd_drain=True) as block:
            @block.sync
            def _(sp):
                for n, (dst, src) in enumerate(pairs):
                    a, b = src.shape
                    sp.dma_start(raw[0:a, n, 0:b], src).then_inc(s["loaded"], 16)

            @block.tensor
            def _(pe):
                pe.wait_ge(s["loaded"], 16 * len(pairs))
                for n, (dst, src) in enumerate(pairs):
                    a, b = src.shape
                    if n >= 4:
                        pe.wait_ge(s["copied"], n - 3)
                    pe.transpose(turned[0:b, n % 4, 0:a], raw[0:a, n, 0:b], c.ident[0:a, 0:a]).then_inc(s["turned_ready"], 1)

            @block.vector
            def _(v):
                for n, (dst, src) in enumerate(pairs):
                    a, b = src.shape
                    v.wait_ge(s["turned_ready"], n + 1)
                    v.tensor_copy(dst, turned[0:b, n % 4, 0:a]).then_inc(s["copied"], 1)
                v.wait_ge(s["copied"], len(pairs))
        st.end_step()


HEADS0 = 16
HD0 = P // HEADS0
HG = 4
ROWS = P // HG


def l0_attention_stage(nc, X, XNT, c, W_Q, W_K, W_V, W_O, alibi_rows, key_pos):
    with Stage(nc, "a0") as outer:
        WQT, WKT, WVT, WOT = (outer.sb(n, [P, P]) for n in ("WQT", "WKT", "WVT", "WOT"))
        load_turned(nc, "a0w", [(WQT[:], W_Q), (WKT[:], W_K), (WVT[:], W_V), (WOT[:], W_O)], c)
        slope_rows = outer.sb("slope_rows", [1, HEADS0 // HG, P])
        unit_row = outer.sb("unit_row", [1, P])
        pos = outer.sb("pos", [1, SEQ])
        ones = outer.sb("ones", [1, SEQ])
        V = outer.sb("V", [P, BLOCKS, P])
        O = outer.sb("O", [P, BLOCKS, P])
        xs = outer.sb("xs", [P, SEQ])
        wq = outer.sb("wq", [P, HG, ROWS])
        wk = outer.sb("wk", [P, HG, ROWS])
        QA = outer.sb("QA", [P, HG, SEQ])
        with Stage(nc, "a0c") as st:
            s = st.sems("loaded")
            with nc.Block(no_gpsimd_drain=True) as block:
                @block.sync
                def _(sp):
                    sp.dma_start(slope_rows[:], alibi_rows[0:1, 0:HEADS0 // HG, :]).then_inc(s["loaded"], 16)
                    sp.dma_start(unit_row[:], alibi_rows[0:1, HEADS0 // HG, :]).then_inc(s["loaded"], 16)
                    sp.dma_start(pos[:], key_pos).then_inc(s["loaded"], 16)
                    sp.wait_ge(s["loaded"], 48)

                @block.vector
                def _(v):
                    v.memset(ones[:], 1.0)
                    v.memset(wq[:], 0.0)
                    v.memset(wk[:], 0.0)
                    v.memset(QA[:], 0.0)
            st.end_step()

        with nc.Fori(0, BATCH) as b:
            with Stage(nc, "a0v") as st:
                pv = st.ps("pv", (P, 2, 512))
                s = st.sems("xs_ready values copied")
                with nc.Block(no_gpsimd_drain=True) as block:
                    @block.scalar
                    def _(a):
                        a.activation(xs[:], XNT[:, ds(b * SEQ, SEQ)], ACT.Copy).then_inc(s["xs_ready"], 1)

                    @block.tensor
                    def _(pe):
                        pe.wait_ge(s["xs_ready"], 1)
                        for t in range(BLOCKS):
                            last = pe.matmul(pv[:, t // 4, (t % 4) * P:(t % 4 + 1) * P], xs[:, t * P:(t + 1) * P],
                                             WVT[:], start=True, stop=True)
                        last.then_inc(s["values"], 1)

                    @block.vector
                    def _(v):
                        v.wait_ge(s["values"], 1)
                        v.tensor_copy(flat(V[:]), flat(pv[:])).then_inc(s["copied"], 1)
                        v.wait_ge(s["copied"], 1)
                st.end_step()
            with Stage(nc, "a0h") as st:
                causal_head_steps(nc, st, c, WQT, WKT, V, O, xs, wq, wk, QA, slope_rows, unit_row, pos, ones)

            with Stage(nc, "a0o") as st:
                OT = st.sb("OT", [P, SEQ])
                turned = st.ps("turned", (P, 2 * 512))
                out = st.ps("out", (P, BLOCKS, P))
                s = st.sems("turned_ready copied out_ready added")
                with nc.Block(no_gpsimd_drain=True) as block:
                    @block.tensor
                    def _(pe):
                        for t in range(BLOCKS):
                            last = pe.transpose(turned[:, t * P:(t + 1) * P], O[:, t, :], c.ident)
                        last.then_inc(s["turned_ready"], 1)
                        pe.wait_ge(s["copied"], 1)
                        for t in range(BLOCKS):
                            last = pe.matmul(out[:, t, :], OT[:, t * P:(t + 1) * P], WOT[:], start=True, stop=True)
                        last.then_inc(s["out_ready"], 1)

                    @block.scalar
                    def _(a):
                        a.wait_ge(s["turned_ready"], 1)
                        a.activation(OT[:], turned[:], ACT.Copy).then_inc(s["copied"], 1)

                    @block.vector
                    def _(v):
                        v.wait_ge(s["out_ready"], 1)
                        v.tensor_tensor(X[:, ds(b * BLOCKS, BLOCKS), :], out[:], X[:, ds(b * BLOCKS, BLOCKS), :],
                                        ALU.add).then_inc(s["added"], 1)
                        v.wait_ge(s["added"], 1)
                st.end_step()


def causal_head_steps(nc, st, c, WQT, WKT, V, O, xs, wq, wk, QA, slope_rows, unit_row, pos, ones):
    slope = st.sb("slope", [1, P])
    KA = st.sb("KA", [P, SEQ])
    Vh = st.sb("Vh", [P, BLOCKS, HG * HD0])
    probs = st.sb("probs", [P, 2, SEQ])
    probsT = st.sb("probsT", [P, 2, SEQ])
    negmax, total, rtotal = (st.sb(n, [P, HG * BLOCKS]) for n in ("negmax", "total", "rtotal"))
    OT = st.sb("OT", [HD0, HG * BLOCKS, P])
    scores = st.ps("scores", (P, 2, 2 * 512))
    turned = st.ps("turned", (P, 2 * 512))
    outT = st.ps("outT", (P, 2, 512))
    s = st.sems("weights q_proj k_proj q_done k_done scores_ready masked max_ready probs_ready turned_ready probsT_v "
                "probsT_a outT_ready outT_used mix_ready total_ready out_done")
    items = [(j, t) for j in range(HG) for t in range(BLOCKS)]
    second = [sum(t >= 4 for _, t in items[:n + 1]) for n in range(len(items))]
    with nc.Fori(0, HEADS0 // HG) as h:
        with nc.Block(no_gpsimd_drain=True) as block:
            @block.vector
            def _(v):
                v.tensor_copy(slope[:], slope_rows[0:1, ds(h, 1), :].rearrange("p a d -> p (a d)"))
                v.tensor_scalar(wq[:, :, 0:HD0], WQT[:, ds(h * HG * HD0, HG * HD0)].rearrange("p (j d) -> p j d", j=HG),
                                HD0 ** -0.5, None, ALU.mult)
                v.tensor_copy(wk[:, :, 0:HD0], WKT[:, ds(h * HG * HD0, HG * HD0)]
                              .rearrange("p (j d) -> p j d", j=HG)).then_inc(s["weights"], 1)
                v.wait_ge(s["k_proj"], 1)
                v.tensor_copy(KA[:], scores[:, 1, :]).then_inc(s["k_done"], 1)

                def row_max(n):
                    j, t = items[n]
                    diag = scores[:, n % 2, t * P:(t + 1) * P]
                    v.wait_ge(s["scores_ready"], n + 1)
                    v.tensor_tensor(diag, diag, c.neg_upper, ALU.add).then_inc(s["masked"], 1)
                    v.wait_ge(s["masked"], n + 1)
                    v.tensor_reduce(negmax[:, n:n + 1], scores[:, n % 2, 0:(t + 1) * P], AX.X, ALU.max,
                                    negate=True).then_inc(s["max_ready"], 1)

                row_max(0)
                for n, (j, t) in enumerate(items):
                    if n + 1 < len(items):
                        row_max(n + 1)
                    w = min(512, (t + 1) * P)
                    v.wait_ge(s["turned_ready"], n + 1)
                    if n >= 2:
                        v.wait_ge(s["outT_ready"], n - 1)
                    v.tensor_copy(probsT[:, n % 2, 0:w], turned[:, 0:w]).then_inc(s["probsT_v"], 1)
                v.wait_ge(s["probs_ready"], len(items))
                v.reciprocal(rtotal[:], total[:]).then_inc(s["total_ready"], 1)
                v.wait_ge(s["total_ready"], 1)
                v.wait_ge(s["mix_ready"], 1)
                v.tensor_tensor(O[:, :, ds(h * HG * HD0, HG * HD0)].rearrange("p t (j d) -> p j t d", j=HG),
                                scores[:, 0, 0:HG * BLOCKS * HD0].rearrange("p (j t d) -> p j t d", j=HG, t=BLOCKS),
                                rtotal[:].rearrange("p (j t) -> p j t", j=HG).unsqueeze(3)
                                .broadcast_to([P, HG, BLOCKS, HD0]), ALU.mult).then_inc(s["out_done"], 1)
                v.wait_ge(s["out_done"], 1)

            @block.gpsimd
            def _(g):
                g.tensor_copy(Vh[:], V[:, :, ds(h * HG * HD0, HG * HD0)]).then_inc(s["q_done"], 1)

            @block.scalar
            def _(a):
                a.wait_ge(s["q_proj"], 1)
                for j in range(HG):
                    r = slice(j * ROWS, (j + 1) * ROWS)
                    a.activation(QA[r, j, :], scores[r, 0, :], ACT.Copy).then_inc(s["q_done"], 1)

                def exps(n):
                    j, t = items[n]
                    a.wait_ge(s["max_ready"], n + 1)
                    if n >= 2:
                        a.wait_ge(s["turned_ready"], n - 1)
                    a.activation(probs[:, n % 2, 0:(t + 1) * P], scores[:, n % 2, 0:(t + 1) * P], ACT.Exp,
                                 bias=negmax[:, n:n + 1], accum_out=total[:, n:n + 1]).then_inc(s["probs_ready"], 1)

                def copy_out(n):
                    a.wait_ge(s["outT_ready"], n + 1)
                    a.activation(OT[:, n, :], outT[0:HD0, n % 2, 0:P], ACT.Copy).then_inc(s["outT_used"], 1)

                exps(0)
                for n, (j, t) in enumerate(items):
                    if n + 1 < len(items):
                        exps(n + 1)
                    w = (t + 1) * P
                    if w > 512:
                        a.wait_ge(s["turned_ready"], n + 1)
                        a.wait_ge(s["outT_ready"], n - 1)
                        a.activation(probsT[:, n % 2, 512:w], turned[:, 512:w], ACT.Copy).then_inc(s["probsT_a"], 1)
                    if n >= 2:
                        copy_out(n - 2)
                copy_out(len(items) - 2)
                copy_out(len(items) - 1)

            @block.tensor
            def _(pe):
                pe.wait_ge(s["weights"], 1)
                for w, extra, src, half, done in ((wq, unit_row, ones, 0, "q_proj"), (wk, slope, pos, 1, "k_proj")):
                    for k in range(2):
                        o = scores[:, half, k * 512:(k + 1) * 512]
                        pe.matmul(o, w[:].rearrange("p j r -> p (j r)"), xs[:, k * 512:(k + 1) * 512], start=True, stop=False)
                        last = pe.matmul(o, extra[:], src[:, k * 512:(k + 1) * 512], start=False, stop=True)
                    last.then_inc(s[done], 1)

                def score(n):
                    j, t = items[n]
                    if n >= 2:
                        pe.wait_ge(s["probs_ready"], n - 1)
                    w = (t + 1) * P
                    for k0 in range(0, w, 512):
                        k1 = min(w, k0 + 512)
                        last = pe.matmul(scores[:, n % 2, k0:k1], QA[:, j, t * P:(t + 1) * P], KA[:, k0:k1],
                                         start=True, stop=True)
                    last.then_inc(s["scores_ready"], 1)

                def turn(n):
                    j, t = items[n]
                    pe.wait_ge(s["probs_ready"], n + 1)
                    if n >= 1:
                        pe.wait_ge(s["probsT_v"], n)
                        if second[n - 1]:
                            pe.wait_ge(s["probsT_a"], second[n - 1])
                    for k in range(t + 1):
                        last = pe.transpose(turned[:, k * P:(k + 1) * P], probs[:, n % 2, k * P:(k + 1) * P], c.ident)
                    last.then_inc(s["turned_ready"], 1)

                def weigh(n):
                    j, t = items[n]
                    pe.wait_ge(s["probsT_v"], n + 1)
                    if t >= 4:
                        pe.wait_ge(s["probsT_a"], second[n])
                    if n >= 2:
                        pe.wait_ge(s["outT_used"], n - 1)
                    for k in range(t + 1):
                        last = pe.matmul(outT[0:HD0, n % 2, 0:P], Vh[:, k, j * HD0:(j + 1) * HD0],
                                         probsT[:, n % 2, k * P:(k + 1) * P], start=(k == 0), stop=(k == t))
                    last.then_inc(s["outT_ready"], 1)

                pe.wait_ge(s["q_done"], HG + 1)
                pe.wait_ge(s["k_done"], 1)
                score(0)
                for n in range(len(items)):
                    if n + 1 < len(items):
                        score(n + 1)
                    turn(n)
                    if n >= 1:
                        weigh(n - 1)
                weigh(len(items) - 1)
                pe.wait_ge(s["outT_used"], len(items))
                for n in range(len(items)):
                    last = pe.transpose(scores[:, 0, n * HD0:(n + 1) * HD0], OT[:, n, :], c.ident[0:HD0, 0:HD0])
                last.then_inc(s["mix_ready"], 1)
        st.end_step()


EXPERTS = 8
CAPACITY = 100


def l0_ffn_stage(nc, X, XNT, c, w_gate, w_expert, b_expert):
    with Stage(nc, "f0") as outer:
        wg = outer.sb("wg", [P, EXPERTS])
        we = outer.sb("we", [P, P])
        bias = outer.sb("bias", [1, P])
        seen = outer.sb("seen", [P, EXPERTS])
        with Stage(nc, "f0w") as st:
            s = st.sems("loaded")
            with nc.Block(no_gpsimd_drain=True) as block:
                @block.sync
                def _(sp):
                    sp.dma_start(wg[:], w_gate).then_inc(s["loaded"], 16)
                    sp.dma_start(we[:], w_expert).then_inc(s["loaded"], 16)
                    sp.dma_start(bias[:], b_expert.rearrange("(a d) -> a d", a=1)).then_inc(s["loaded"], 16)
                    sp.wait_ge(s["loaded"], 48)

                @block.vector
                def _(v):
                    v.memset(seen[:], 0.0)
            st.end_step()
        with Stage(nc, "f0s") as st:
            xs = st.sb("xs", [P, G * P])
            lg = st.sb("lg", [P, G, EXPERTS])
            top = st.sb("top", [P, G, 8])
            at = st.sb("at", [P, G, 8], U32)
            atf = st.sb("atf", [P, G, 8])
            choice = st.sb("choice", [P, G, EXPERTS])
            ex = st.sb("ex", [P, G, EXPERTS])
            kept = st.sb("kept", [P, G, EXPERTS])
            total, gate, keep = (st.sb(n, [P, G]) for n in ("total", "gate", "keep"))
            add = st.sb("add", [P, EXPERTS])
            logits = st.ps("logits", (P, G, EXPERTS))
            place = st.ps("place", (P, G, EXPERTS))
            y = st.ps("y", (P, G, P))
            s = st.sems("xs_ready logits_ready y_ready chosen shifted exps place_ready added chain")
            with nc.Fori(0, TILES // G) as i:
                with nc.Block(no_gpsimd_drain=True) as block:
                    @block.scalar
                    def _(a):
                        a.activation(xs[:], XNT[:, ds(i * G * P, G * P)], ACT.Copy).then_inc(s["xs_ready"], 1)
                        a.wait_ge(s["shifted"], 1)
                        a.activation(ex[:], ex[:], ACT.Exp).then_inc(s["exps"], 1)

                    @block.tensor
                    def _(pe):
                        pe.wait_ge(s["xs_ready"], 1)
                        for j in range(G):
                            last = pe.matmul(logits[:, j, :], xs[:, j * P:(j + 1) * P], wg[:], start=True, stop=True)
                        last.then_inc(s["logits_ready"], 1)
                        for j in range(G):
                            pe.matmul(y[:, j, :], xs[:, j * P:(j + 1) * P], we[:], start=True, stop=False)
                            last = pe.matmul(y[:, j, :], c.ones[0:1, :], bias[:], start=False, stop=True)
                        last.then_inc(s["y_ready"], 1)
                        pe.wait_ge(s["chosen"], 1)
                        for j in range(G):
                            pe.matmul(place[:, j, :], c.upto, choice[:, j, :], start=True, stop=False)
                            for k in range(j):
                                pe.matmul(place[:, j, :], c.ones, choice[:, k, :], start=False, stop=False)
                            last = pe.matmul(place[:, j, :], c.ones, seen[:], start=False, stop=True)
                        last.then_inc(s["place_ready"], 1)

                    @block.vector
                    def _(v):
                        step = Chain(v, s["chain"])
                        v.wait_ge(s["logits_ready"], 1)
                        step(v.tensor_copy(lg[:], logits[:]))
                        for j in range(G):
                            last = v.max(top[:, j, :], lg[:, j, :])
                        step(last)
                        v.tensor_tensor(ex[:], lg[:], top[:, :, 0:1].broadcast_to([P, G, EXPERTS]),
                                        ALU.subtract).then_inc(s["shifted"], 1)
                        for j in range(G):
                            last = v.max_index(at[:, j, :], top[:, j, :], lg[:, j, :])
                        step(last)
                        step(v.tensor_copy(atf[:], at[:]))
                        for j in range(G):
                            last = v.tensor_scalar(choice[:, j, :], c.count8, atf[:, j, 0:1], None, ALU.is_equal)
                        last.then_inc(s["chosen"], 1)
                        v.wait_ge(s["exps"], 1)
                        step(v.tensor_reduce(total[:], ex[:], AX.X, ALU.add))
                        step(v.reciprocal(gate[:], total[:]))
                        v.wait_ge(s["place_ready"], 1)
                        step(v.scalar_tensor_tensor(out=kept[:], in0=place[:], scalar=float(CAPACITY), in1=choice[:],
                                                    op0=ALU.is_le, op1=ALU.mult))
                        v.tensor_reduce(keep[:], kept[:], AX.X, ALU.add)
                        step(v.tensor_reduce(add[:], choice[:].rearrange("p j e -> p e j"), AX.X, ALU.add))
                        v.tensor_tensor(seen[:], seen[:], add[:], ALU.add)
                        step(v.tensor_tensor(gate[:], gate[:], keep[:], ALU.mult))
                        v.wait_ge(s["y_ready"], 1)
                        for j in range(G):
                            last = v.scalar_tensor_tensor(out=tile(X, i * G + j), in0=y[:, j, :],
                                                          scalar=gate[:, j:j + 1], in1=tile(X, i * G + j),
                                                          op0=ALU.mult, op1=ALU.add)
                        last.then_inc(s["added"], 1)
                        v.wait_ge(s["added"], 1)
                st.end_step()


HEADS1 = 8
TAPS = 4
RMS_EPS = 1e-6
LEVELS = [1, 2, 4, 8, 16, 32, 64]


def l1_gates_stage(nc, XNT, c, a_b_wT, dt_row, alog_row, g_all, beta_all):
    H = HEADS1
    with Stage(nc, "g1") as outer:
        rate = outer.sb("rate", [P, 1, H])
        with Stage(nc, "g1r") as st:
            pr = st.ps("pr", (P, H))
            s = st.sems("row_ready exp_ready done")
            with nc.Block(no_gpsimd_drain=True) as block:
                @block.tensor
                def _(pe):
                    pe.matmul(pr[:], c.ones[0:1, :], alog_row, start=True, stop=True).then_inc(s["row_ready"], 1)

                @block.scalar
                def _(a):
                    a.wait_ge(s["row_ready"], 1)
                    a.activation(rate[:, 0, :], pr[:], ACT.Exp).then_inc(s["exp_ready"], 1)

                @block.vector
                def _(v):
                    v.wait_ge(s["exp_ready"], 1)
                    v.tensor_scalar(rate[:], rate[:], -1.0, None, ALU.mult).then_inc(s["done"], 1)
                    v.wait_ge(s["done"], 1)
            st.end_step()
        with Stage(nc, "g1s") as st:
            xs = st.sb("xs", [P, G * P])
            th, mag, relu = (st.sb(n, [P, G, H]) for n in ("th", "mag", "relu"))
            pa = st.ps("pa", (P, G, H))
            pb = st.ps("pb", (P, G, H))
            s = st.sems("xs_ready a_ready b_ready th_ready mag_ready soft_ready done chain act_chain")
            with nc.Fori(0, TILES // G) as i:
                with nc.Block(no_gpsimd_drain=True) as block:
                    @block.scalar
                    def _(a):
                        a.activation(xs[:], XNT[:, ds(i * G * P, G * P)], ACT.Copy).then_inc(s["xs_ready"], 1)
                        step = Chain(a, s["act_chain"])
                        a.wait_ge(s["b_ready"], 1)
                        a.activation(th[:], pb[:], ACT.Tanh, scale=0.5).then_inc(s["th_ready"], 1)
                        a.wait_ge(s["mag_ready"], 1)
                        step(a.activation(mag[:], mag[:], ACT.Exp, scale=-1.0))
                        a.activation(mag[:], mag[:], ACT.Ln, bias=1.0).then_inc(s["soft_ready"], 1)

                    @block.tensor
                    def _(pe):
                        pe.wait_ge(s["xs_ready"], 1)
                        for j in range(G):
                            last = pe.matmul(pb[:, j, :], xs[:, j * P:(j + 1) * P], a_b_wT[:, H:2 * H], start=True, stop=True)
                        last.then_inc(s["b_ready"], 1)
                        for j in range(G):
                            pe.matmul(pa[:, j, :], xs[:, j * P:(j + 1) * P], a_b_wT[:, 0:H], start=True, stop=False)
                            last = pe.matmul(pa[:, j, :], c.ones[0:1, :], dt_row, start=False, stop=True)
                        last.then_inc(s["a_ready"], 1)

                    @block.vector
                    def _(v):
                        step = Chain(v, s["chain"])
                        v.wait_ge(s["a_ready"], 1)
                        step(v.tensor_scalar(relu[:], pa[:], 0.0, None, ALU.max))
                        v.scalar_tensor_tensor(out=mag[:], in0=relu[:], scalar=2.0, in1=pa[:], op0=ALU.mult,
                                               op1=ALU.subtract).then_inc(s["mag_ready"], 1)
                        v.wait_ge(s["th_ready"], 1)
                        step(v.tensor_scalar(beta_all[:, ds(i * G, G), :], th[:], 0.5, 0.5, ALU.mult, ALU.add))
                        v.wait_ge(s["soft_ready"], 1)
                        step(v.tensor_tensor(relu[:], relu[:], mag[:], ALU.add))
                        v.tensor_tensor(g_all[:, ds(i * G, G), :], relu[:], rate[:].broadcast_to([P, G, H]),
                                        ALU.mult).then_inc(s["done"], 1)
                        v.wait_ge(s["done"], 1)
                st.end_step()


def l1_attention_stage(nc, X, XNT, c, d):
    H = HEADS1
    xnt4 = XNT[:].rearrange("p (b s) -> p b s", b=BATCH)
    with Stage(nc, "a1") as outer:
        abT = outer.sb("abT", [P, 2 * H])
        load_turned(nc, "a1t", [(abT[:, 0:H], d["L1_attn_a_w"]), (abT[:, H:2 * H], d["L1_attn_b_w"])], c)
        g_all = outer.sb("g_all", [P, TILES, H])
        beta_all = outer.sb("beta_all", [P, TILES, H])
        rows = outer.sb("rows", [1, 2 * H + P])
        norm_w = outer.sb("norm_w", [P, 1, P])
        masks = outer.sb("masks", [P, len(LEVELS), P])
        with Stage(nc, "a1c") as st:
            pn = st.ps("pn", (P, P))
            s = st.sems("loaded row_ready done")
            with nc.Block(no_gpsimd_drain=True) as block:
                @block.sync
                def _(sp):
                    sp.dma_start(rows[:, 0:H], d["L1_attn_dt_bias"].rearrange("(a d) -> a d", a=1)).then_inc(s["loaded"], 16)
                    sp.dma_start(rows[:, H:2 * H], d["L1_attn_A_log"].rearrange("(a d) -> a d", a=1)).then_inc(s["loaded"], 16)
                    sp.dma_start(rows[:, 2 * H:], d["L1_attn_norm_w"].rearrange("(a d) -> a d", a=1)).then_inc(s["loaded"], 16)
                    sp.dma_start(masks[:], d["const_level_masks"]).then_inc(s["loaded"], 16)
                    sp.wait_ge(s["loaded"], 64)

                @block.tensor
                def _(pe):
                    pe.wait_ge(s["loaded"], 64)
                    pe.matmul(pn[:], c.ones[0:1, :], rows[:, 2 * H:], start=True, stop=True).then_inc(s["row_ready"], 1)

                @block.vector
                def _(v):
                    v.wait_ge(s["row_ready"], 1)
                    v.tensor_scalar(norm_w[:, 0, :], pn[:], 0.5, None, ALU.mult).then_inc(s["done"], 1)
                    v.wait_ge(s["done"], 1)
            st.end_step()
        l1_gates_stage(nc, XNT, c, abT, rows[:, 0:H], rows[:, H:2 * H], g_all, beta_all)

        wT = outer.sb("wT", [P, 5, P])
        raw_w = outer.sb("raw_w", [P, 5, P])
        taps = outer.sb("taps", [P, 3, TAPS])
        S = outer.sb("S", [P, G, P])
        hist = outer.sb("hist", [P, 3, G, P + TAPS - 1])
        gh = outer.sb("gh", [P, TILES])
        bh = outer.sb("bh", [P, TILES])
        with nc.Fori(0, H) as h:
            with Stage(nc, "a1h") as st:
                turned = st.ps("turned", (P, 5, 512))
                s = st.sems("loaded turned_ready copied zeroed")
                with nc.Block(no_gpsimd_drain=True) as block:
                    @block.sync
                    def _(sp):
                        for n in range(3):
                            sp.dma_start(raw_w[:, n, :], d["L1_attn_qkv_w"][ds(h * P + n * H * P, P), :]).then_inc(s["loaded"], 16)
                            sp.dma_start(taps[:, n, :], d["L1_attn_conv_w"][ds(h * P + n * H * P, P), :, :]
                                         .rearrange("p a t -> p (a t)")).then_inc(s["loaded"], 16)
                        sp.dma_start(raw_w[:, 3, :], d["L1_attn_z_w"][ds(h * P, P), :]).then_inc(s["loaded"], 16)
                        sp.dma_start(raw_w[:, 4, :], d["L1_attn_out_w"][:, ds(h * P, P)]).then_inc(s["loaded"], 16)
                        sp.wait_ge(s["loaded"], 8 * 16)

                    @block.tensor
                    def _(pe):
                        pe.wait_ge(s["loaded"], 8 * 16)
                        for n in range(5):
                            pe.transpose(turned[:, n, 0:P], raw_w[:, n, :], c.ident).then_inc(s["turned_ready"], 1)

                    @block.vector
                    def _(v):
                        v.memset(S[:], 0.0)
                        v.memset(hist[:, :, :, 0:TAPS - 1], 0.0)
                        v.tensor_copy(gh[:], g_all[:, :, ds(h, 1)].rearrange("p t a -> p (t a)"))
                        v.tensor_copy(bh[:], beta_all[:, :, ds(h, 1)].rearrange("p t a -> p (t a)"))
                        for n in range(5):
                            v.wait_ge(s["turned_ready"], n + 1)
                            v.tensor_copy(wT[:, n, :], turned[:, n, 0:P]).then_inc(s["copied"], 1)
                        v.wait_ge(s["copied"], 5)
                st.end_step()
            with Stage(nc, "a1s") as st:
                delta_chunk_steps(nc, st, X, xnt4, c, wT, taps, S, hist, gh, bh, masks, norm_w)


def delta_chunk_steps(nc, st, X, xnt4, c, wT, taps, S, hist, gh, bh, masks, norm_w):
    four, pair = [P, G, P], [P, 2, G, P]
    gcol, nbeta, msq, std, rstd = (st.sb(n, [P, G]) for n in ("gcol", "nbeta", "msq", "std", "rstd"))
    bcol = st.sb("bcol", [P, 2, G])
    decays = st.sb("decays", [P, 2, 3, G])
    ga, E, Eincl, Estrict = (st.sb(n, four) for n in ("ga", "E", "Eincl", "Estrict"))
    xs, conv = st.sb("xs", four), st.sb("conv", [P, 2, 3, G, P])
    ktok, vtok, AT, XT, gatez = (st.sb(n, pair) for n in ("ktok", "vtok", "AT", "XT", "gatez"))
    N, Nlev = st.sb("N", four), st.sb("Nlev", [P, len(LEVELS), G, P])
    T, Zt, R, kS, u, uend = (st.sb(n, four) for n in ("T", "Zt", "R", "kS", "u", "uend"))
    o, osq, y, yT, newS = (st.sb(n, four) for n in ("o", "osq", "y", "yT", "newS"))
    bank = [st.ps(f"bank{n}", (P, G, P)) for n in range(8)]
    s = st.sems("xs_ready cols_ready ga_ready raw_ready raw_copied conv_ready hist_kept sums_ready dt_ready "
                "decays_ready E_ready strict_ready incl_ready z_ready tanh_ready gatez_ready ktok_ps vtok_ps ktok_ready "
                "vtok_ready gram_ready N_ready Nlev_ready qk_ready AT_ready kS_ready qS_ready R_ready qS_used zt_ps "
                "zt_ready t_ps t_ready x_ps x_ready u_ps u_ready uend_ready o_ps s_ps s_used msq_ready std_ready "
                "y_ready yT_ps yT_ready out_ps added newS_ready chain")
    K = len(LEVELS)

    def pipeline_step(block, k, chained, prepare=None, recur=None):
        @block.tensor
        def _(pe):
            def four_of(out, lhs, rhs, sem):
                for b in range(G):
                    last = pe.matmul(out[:, b, :], lhs(b), rhs(b), start=True, stop=True)
                last.then_inc(sem, 1)

            def turn_four(out, src, sem):
                for b in range(G):
                    last = pe.transpose(out[:, b, :], src[:, b, :], c.ident)
                last.then_inc(sem, 1)

            if prepare is not None:
                ch, w = prepare
                if k >= 1:
                    pe.wait_ge(s["AT_ready"], k)
                    pe.wait_ge(s["zt_ready"], (K - 1) * k)
                    pe.wait_ge(s["t_ready"], (K - 1) * k)
                for n in range(3):
                    pe.matmul(flat(bank[n][:]), wT[:, n, :], xnt4[:, :, ds(ch * P, P)],
                              start=True, stop=True).then_inc(s["raw_ready"], 1)
            if recur is not None:
                r = recur[1]
                if k >= 1:
                    pe.wait_ge(s["conv_ready"], 3 * k)
                    pe.wait_ge(s["added"], k)
                    pe.wait_ge(s["s_used"], k)
                four_of(bank[5], lambda b: conv[:, r, 1, b, :], lambda b: S[:, b, :], s["kS_ready"])
                four_of(bank[6], lambda b: conv[:, r, 0, b, :], lambda b: S[:, b, :], s["qS_ready"])
            if prepare is not None:
                pe.wait_ge(s["cols_ready"], k + 1)
                if k >= 1:
                    pe.wait_ge(s["vtok_ready"], k)
                for n, m in enumerate((c.upto, c.after, c.ones)):
                    last = pe.matmul(bank[3][:, 0, n * G:(n + 1) * G], m, gcol[:], start=True, stop=True)
                last.then_inc(s["sums_ready"], 1)
                pe.wait_ge(s["ga_ready"], k + 1)
                if k >= 1:
                    pe.wait_ge(s["x_ready"], K * k)
                four_of(bank[4], lambda b: ga[:, b, :], lambda b: c.upto, s["dt_ready"])
                pe.wait_ge(s["xs_ready"], k + 1)
                pe.wait_ge(s["raw_copied"], 3 * k + 3)
                four_of(bank[0], lambda b: xs[:, b, :], lambda b: wT[:, 3, :], s["z_ready"])
            if recur is not None:
                pe.wait_ge(s["R_ready"], k + 1)
                if k >= 1:
                    pe.wait_ge(s["x_ready"], K * k)
                    pe.wait_ge(s["yT_ready"], k)
                four_of(bank[7], lambda b: XT[:, r, b, :], lambda b: R[:, b, :], s["u_ps"])
            if prepare is not None:
                pe.wait_ge(s["conv_ready"], 3 * k + 1)
                turn_four(bank[1], conv[:, w, 1], s["ktok_ps"])
                four_of(bank[2], lambda b: conv[:, w, 1, b, :], lambda b: conv[:, w, 1, b, :], s["gram_ready"])
            if recur is not None:
                pe.wait_ge(s["u_ready"], k + 1)
                if k >= 1:
                    pe.wait_ge(s["AT_ready"], k)
                    pe.wait_ge(s["ktok_ready"], k)
                four_of(bank[5], lambda b: AT[:, r, b, :], lambda b: u[:, b, :], s["o_ps"])
                pe.wait_ge(s["uend_ready"], k + 1)
                pe.wait_ge(s["qS_used"], k + 1)
                four_of(bank[6], lambda b: ktok[:, r, b, :], lambda b: uend[:, b, :], s["s_ps"])

            def turn_out():
                if recur is not None:
                    pe.wait_ge(s["y_ready"], k + 1)
                    turn_four(bank[7], y, s["yT_ps"])

            def project_out():
                if recur is not None:
                    pe.wait_ge(s["yT_ready"], k + 1)
                    four_of(bank[5], lambda b: yT[:, b, :], lambda b: wT[:, 4, :], s["out_ps"])

            if prepare is not None:
                pe.wait_ge(s["ktok_ready"], k + 1)
                pe.wait_ge(s["N_ready"], k + 1)
                pe.wait_ge(s["E_ready"], k + 1)
                for n in range(K):
                    pe.wait_ge(s["Nlev_ready"], K * k + n + 1)
                    if n >= 1:
                        pe.wait_ge(s["t_ready"], (K - 1) * k + n)
                    four_of(bank[1], lambda b: Nlev[:, n, b, :], lambda b: c.ident if n == 0 else T[:, b, :], s["zt_ps"])
                    if n >= 1:
                        pe.wait_ge(s["zt_ready"], (K - 1) * k + n)
                        pe.wait_ge(s["x_ready"], K * k + n)
                        if n < K - 1:
                            four_of(bank[2], lambda b: XT[:, w, b, :], lambda b: Zt[:, b, :], s["t_ps"])
                        four_of(bank[4], lambda b: Zt[:, b, :], lambda b: XT[:, w, b, :], s["x_ps"])
                    if n == 2:
                        turn_out()
                    if n == 3:
                        project_out()
                        pe.wait_ge(s["conv_ready"], 3 * k + 2)
                        pe.wait_ge(s["gatez_ready"], k + 1)
                        four_of(bank[0], lambda b: conv[:, w, 1, b, :], lambda b: conv[:, w, 0, b, :], s["qk_ready"])
                    if n == 4:
                        pe.wait_ge(s["conv_ready"], 3 * k + 3)
                        pe.wait_ge(s["decays_ready"], k + 1)
                        turn_four(bank[3], conv[:, w, 2], s["vtok_ps"])
            else:
                turn_out()
                project_out()

        @block.scalar
        def _(a):
            def root():
                if recur is not None:
                    a.wait_ge(s["msq_ready"], k + 1)
                    a.activation(std[:], msq[:], ACT.Sqrt).then_inc(s["std_ready"], 1)

            def copy_turned():
                if recur is not None:
                    a.wait_ge(s["yT_ps"], k + 1)
                    a.activation(yT[:], bank[7][:], ACT.Copy).then_inc(s["yT_ready"], 1)

            if prepare is not None:
                w = prepare[1]
                if k >= 1:
                    a.wait_ge(s["hist_kept"], k)
                for at, n in enumerate((1, 0, 2)):
                    a.wait_ge(s["raw_ready"], 3 * k + n + 1)
                    a.activation(hist[:, n, :, TAPS - 1:], bank[n][:], ACT.Copy).then_inc(s["raw_copied"], 1)
                a.wait_ge(s["sums_ready"], k + 1)
                a.activation(decays[:, w].rearrange("p n b -> p (n b)"), bank[3][:, 0, 0:3 * G],
                             ACT.Exp).then_inc(s["decays_ready"], 1)
                a.wait_ge(s["dt_ready"], k + 1)
                if k >= 1:
                    a.wait_ge(s["incl_ready"], k)
                a.activation(E[:], bank[4][:], ACT.Exp).then_inc(s["E_ready"], 1)
                a.wait_ge(s["z_ready"], k + 1)
                a.activation(gatez[:, w], bank[0][:], ACT.Tanh, scale=0.5).then_inc(s["tanh_ready"], 1)
                a.wait_ge(s["ktok_ps"], k + 1)
                a.activation(ktok[:, w], bank[1][:], ACT.Copy).then_inc(s["ktok_ready"], 1)
            root()
            if prepare is not None:
                for n in range(1, K):
                    a.wait_ge(s["zt_ps"], K * k + n + 1)
                    if (K - 1) * k + n >= 2:
                        a.wait_ge(s["x_ps"], (K - 1) * k + n - 1)
                    a.activation(Zt[:], bank[1][:], ACT.Copy).then_inc(s["zt_ready"], 1)
                    if n == 2:
                        copy_turned()
                    if n == 4:
                        a.wait_ge(s["vtok_ps"], k + 1)
                        a.activation(vtok[:, w], bank[3][:], ACT.Copy).then_inc(s["vtok_ready"], 1)
            else:
                copy_turned()

        @block.gpsimd
        def _(g):
            if recur is not None:
                if k >= 1:
                    g.wait_ge(s["s_used"], k)
                    g.wait_ge(s["decays_ready"], k)
                g.tensor_tensor(newS[:], S[:], spread(decays[:, recur[1], 2, :], P), ALU.mult).then_inc(s["newS_ready"], 1)
            if prepare is not None:
                if k >= 1:
                    g.wait_ge(s["z_ready"], k)
                    g.wait_ge(s["AT_ready"], k)
                    g.wait_ge(s["N_ready"], k)
                g.tensor_copy(xs[:], xnt4[:, :, ds(prepare[0] * P, P)]).then_inc(s["xs_ready"], 1)
                g.wait_ge(s["E_ready"], k + 1)
                g.tensor_tensor(Estrict[:], E[:], c.strict.unsqueeze(1).broadcast_to(four), ALU.mult).then_inc(s["strict_ready"], 1)
                g.wait_ge(s["N_ready"], k + 1)
                for n in range(K):
                    g.tensor_tensor(Nlev[:, n], N[:], masks[:, n:n + 1, :].broadcast_to(four), ALU.mult).then_inc(s["Nlev_ready"], 1)
                    if n == 2:
                        g.tensor_tensor(Eincl[:], E[:], c.upto.unsqueeze(1).broadcast_to(four), ALU.mult).then_inc(s["incl_ready"], 1)
                g.wait_ge(s["Nlev_ready"], K * (k + 1))
            if recur is not None:
                g.wait_ge(s["newS_ready"], k + 1)

        @block.vector
        def _(v):
            step = Chain(v, s["chain"])
            step.n = chained[0]

            def convolve(at, n):
                v.wait_ge(s["raw_copied"], 3 * k + at + 1)
                step(v.tensor_scalar(conv[:, w, n], hist[:, n, :, TAPS - 1:], taps[:, n, TAPS - 1:TAPS], None, ALU.mult))
                for j in range(TAPS - 1):
                    last = v.scalar_tensor_tensor(out=conv[:, w, n], in0=hist[:, n, :, j:j + P], scalar=taps[:, n, j:j + 1],
                                                  in1=conv[:, w, n], op0=ALU.mult, op1=ALU.add)
                    if j < TAPS - 2:
                        step(last)
                last.then_inc(s["conv_ready"], 1)

            if prepare is not None:
                ch, w = prepare
                if k >= 1:
                    v.wait_ge(s["sums_ready"], k)
                    v.wait_ge(s["dt_ready"], k)
                v.tensor_copy(bcol[:, w], bh[:].rearrange("p (b t) -> p b t", b=G)[:, :, ds(ch, 1)].rearrange("p b a -> p (b a)"))
                v.tensor_copy(gcol[:], gh[:].rearrange("p (b t) -> p b t", b=G)[:, :, ds(ch, 1)]
                              .rearrange("p b a -> p (b a)")).then_inc(s["cols_ready"], 1)
                v.wait_ge(s["cols_ready"], k + 1)
                v.tensor_tensor(ga[:], c.after.unsqueeze(1).broadcast_to(four), spread(gcol[:], P), ALU.mult).then_inc(s["ga_ready"], 1)
                step(v.tensor_scalar(nbeta[:], bcol[:, w], -1.0, None, ALU.mult))
            if recur is not None:
                r = recur[1]
                v.wait_ge(s["kS_ready"], k + 1)
                if k >= 1:
                    v.wait_ge(s["decays_ready"], k)
                    v.wait_ge(s["vtok_ready"], k)
                step(v.tensor_tensor(kS[:], bank[5][:], spread(decays[:, r, 0, :], P), ALU.mult))
                v.tensor_tensor(R[:], vtok[:, r], kS[:], ALU.subtract).then_inc(s["R_ready"], 1)
            if prepare is not None:
                convolve(0, 1)
            if recur is not None:
                v.wait_ge(s["u_ps"], k + 1)
                v.tensor_tensor(u[:], bank[7][:], spread(bcol[:, r], P), ALU.mult).then_inc(s["u_ready"], 1)
                v.wait_ge(s["u_ready"], k + 1)
                v.tensor_tensor(uend[:], u[:], spread(decays[:, r, 1, :], P), ALU.mult).then_inc(s["uend_ready"], 1)
                v.wait_ge(s["qS_ready"], k + 1)
                v.tensor_tensor(o[:], bank[6][:], spread(decays[:, r, 0, :], P), ALU.mult).then_inc(s["qS_used"], 1)
                v.wait_ge(s["qS_used"], k + 1)
            if prepare is not None:
                v.wait_ge(s["strict_ready"], k + 1)
                v.wait_ge(s["gram_ready"], k + 1)
                step(v.tensor_tensor(N[:], bank[2][:], Estrict[:], ALU.mult))
                v.tensor_tensor(N[:], N[:], spread(nbeta[:], P), ALU.mult).then_inc(s["N_ready"], 1)
            if recur is not None:
                v.wait_ge(s["o_ps"], k + 1)
                step(v.tensor_tensor(o[:], bank[5][:], o[:], ALU.add))
                step(v.tensor_tensor(osq[:], o[:], o[:], ALU.mult))
                step(v.tensor_reduce(msq[:], osq[:], AX.X, ALU.add))
                v.tensor_scalar(msq[:], msq[:], 1.0 / P, RMS_EPS, ALU.mult, ALU.add).then_inc(s["msq_ready"], 1)

            def update_state():
                if recur is not None:
                    if k >= 1:
                        v.wait_ge(s["gatez_ready"], k)
                    v.tensor_tensor(y[:], o[:], gatez[:, r], ALU.mult)
                    v.wait_ge(s["s_ps"], k + 1)
                    v.wait_ge(s["newS_ready"], k + 1)
                    v.tensor_tensor(S[:], bank[6][:], newS[:], ALU.add).then_inc(s["s_used"], 1)

            def normalise():
                if recur is not None:
                    v.wait_ge(s["std_ready"], k + 1)
                    step(v.reciprocal(rstd[:], std[:]))
                    v.tensor_tensor(y[:], y[:], spread(rstd[:], P), ALU.mult).then_inc(s["y_ready"], 1)

            def add_out():
                if recur is not None:
                    v.wait_ge(s["out_ps"], k + 1)
                    mine = X[:].rearrange("p (b t) d -> p b t d", b=G)[:, :, ds(recur[0], 1), :].rearrange("p b a d -> p b (a d)")
                    v.tensor_tensor(mine, bank[5][:], mine, ALU.add).then_inc(s["added"], 1)
                    v.wait_ge(s["added"], k + 1)

            if prepare is not None:
                idn = c.ident.unsqueeze(1).broadcast_to(four)
                v.wait_ge(s["zt_ps"], K * k + 1)
                v.tensor_tensor(T[:], bank[1][:], idn, ALU.add).then_inc(s["t_ready"], 1)
                v.wait_ge(s["Nlev_ready"], K * k + 1)
                v.tensor_tensor(XT[:, w], Nlev[:, 0], idn, ALU.add).then_inc(s["x_ready"], 1)
                update_state()
                for n in range(1, K):
                    if n < K - 1:
                        v.wait_ge(s["t_ready"], (K - 1) * k + n)
                        v.wait_ge(s["t_ps"], (K - 2) * k + n)
                        v.tensor_tensor(T[:], bank[2][:], T[:], ALU.add).then_inc(s["t_ready"], 1)
                    v.wait_ge(s["x_ready"], K * k + n)
                    v.wait_ge(s["x_ps"], (K - 1) * k + n)
                    v.tensor_tensor(XT[:, w], bank[4][:], XT[:, w], ALU.add).then_inc(s["x_ready"], 1)
                    if n == 1:
                        convolve(1, 0)
                    if n == 2:
                        normalise()
                        v.wait_ge(s["tanh_ready"], k + 1)
                        step(v.scalar_tensor_tensor(out=gatez[:, w], in0=gatez[:, w], scalar=1.0, in1=bank[0][:],
                                                    op0=ALU.add, op1=ALU.mult))
                        v.tensor_tensor(gatez[:, w], gatez[:, w], norm_w[:].broadcast_to(four),
                                        ALU.mult).then_inc(s["gatez_ready"], 1)
                    if n == 3:
                        convolve(2, 2)
                        v.wait_ge(s["conv_ready"], 3 * k + 3)
                        v.tensor_copy(hist[:, :, :, 0:TAPS - 1], hist[:, :, :, P:P + TAPS - 1]).then_inc(s["hist_kept"], 1)
                    if n == 4:
                        v.wait_ge(s["qk_ready"], k + 1)
                        v.wait_ge(s["incl_ready"], k + 1)
                        v.tensor_tensor(AT[:, w], bank[0][:], Eincl[:], ALU.mult).then_inc(s["AT_ready"], 1)
                    if n == 5:
                        add_out()
            else:
                update_state()
                normalise()
                add_out()
            chained[0] = step.n

    with nc.Block(no_gpsimd_drain=True) as block:
        pipeline_step(block, 0, [0], prepare=(0, 0))
    st.end_step()
    with nc.Fori(0, (BLOCKS - 2) // 2) as i:
        with nc.Block(no_gpsimd_drain=True) as block:
            chained = [0]
            for k in range(2):
                pipeline_step(block, k, chained, prepare=(i * 2 + k + 1, 1 - k), recur=(i * 2 + k, k))
        st.end_step()
    with nc.Block(no_gpsimd_drain=True) as block:
        chained = [0]
        pipeline_step(block, 0, chained, prepare=(BLOCKS - 1, 1), recur=(BLOCKS - 2, 0))
        pipeline_step(block, 1, chained, recur=(BLOCKS - 1, 1))
    st.end_step()


DEPTH = 6
HEADSW = 16
HDW = 64
INNER = HEADSW * HDW
WINDOW = 32
KEYS = WINDOW + P
HALFW = P // 2
QK_SCALE = 8.0
UNITS = int(P * 4 * 2 / 3)
PIECES = [(0, P), (P, 2 * P), (2 * P, UNITS)]
GH = 4
BANK_HEADS = 3
STEPS = 8


def l1_ffn_stage(nc, X, padded, XNT, c, d):
    Y = padded[:, 1:TILES + 1, :]
    with Stage(nc, "w") as outer:
        rope = outer.sb("rope", [P, 4, BLOCKS + 1, HDW])
        scaled = outer.sb("scaled", [P, 4, BLOCKS + 1, HDW])
        band = outer.sb("band", [P, BLOCKS, KEYS])
        shifts = outer.sb("shifts", [P, 2, P])
        has_prev = outer.sb("has_prev", [P, 2, BLOCKS + 1])
        wqkv = outer.sb("wqkv", [P, 3 * INNER])
        wo = outer.sb("wo", [P, INNER // P, P])
        w1 = outer.sb("w1", [P, 2 * UNITS])
        w2 = outer.sb("w2", [P, 3, P])
        b1 = outer.sb("b1", [P, 2, 3])
        b2 = outer.sb("b2", [1, P])
        gb = outer.sb("gb", [P, 2])
        qk_rows = outer.sb("qk_rows", [1, 2, HDW])
        with Stage(nc, "wc") as st:
            s = st.sems("loaded")
            with nc.Block(no_gpsimd_drain=True) as block:
                @block.sync
                def _(sp):
                    sp.dma_start(rope[:], d["const_rope"]).then_inc(s["loaded"], 16)
                    sp.dma_start(band[:], d["const_band"]).then_inc(s["loaded"], 16)
                    sp.dma_start(shifts[:], d["const_shifts"]).then_inc(s["loaded"], 16)
                    sp.dma_start(has_prev[:], d["const_has_prev"]).then_inc(s["loaded"], 16)
                    sp.wait_ge(s["loaded"], 64)
            st.end_step()

        with nc.Fori(0, DEPTH) as l:
            with Stage(nc, "wl") as st:
                qks = st.sb("qks", [P, 2, HDW])
                pr = st.ps("pr", (P, 2, HDW))
                s = st.sems("rows_loaded loaded rows_ps copied")
                with nc.Block(no_gpsimd_drain=True) as block:
                    @block.sync
                    def _(sp):
                        sp.dma_start(qk_rows[:, 0, :], d["L1_ffn_q_scale"][ds(l, 1), :]).then_inc(s["rows_loaded"], 16)
                        sp.dma_start(qk_rows[:, 1, :], d["L1_ffn_k_scale"][ds(l, 1), :]).then_inc(s["rows_loaded"], 16)
                        loads = [(wqkv[:], d["L1_ffn_Wqkv"][ds(l, 1)].rearrange("a p n -> (a p) n")),
                                 (wo[:], d["L1_ffn_Wo"][ds(l, 1)].rearrange("a (k p) n -> (a p) k n", p=P)),
                                 (w1[:], d["L1_ffn_W1"][ds(l, 1)].rearrange("a p n -> (a p) n")),
                                 (b2[:], d["L1_ffn_b2"][ds(l, 1), :]),
                                 (gb[:, 0:1], d["L1_ffn_ln_g"][ds(l, 1), :].rearrange("a p -> p a")),
                                 (gb[:, 1:2], d["L1_ffn_ln_b"][ds(l, 1), :].rearrange("a p -> p a"))]
                        for n, (k0, k1) in enumerate(PIECES):
                            loads.append((w2[0:k1 - k0, n, :], d["L1_ffn_W2"][ds(l, 1), k0:k1, :].rearrange("a p n -> (a p) n")))
                            for half in range(2):
                                loads.append((b1[0:k1 - k0, half, n:n + 1],
                                              d["L1_ffn_b1"][ds(l, 1), half * UNITS + k0:half * UNITS + k1]
                                              .rearrange("a p -> p a")))
                        for dst, src in loads:
                            sp.dma_start(dst, src).then_inc(s["loaded"], 16)
                        sp.wait_ge(s["loaded"], 16 * len(loads))

                    @block.tensor
                    def _(pe):
                        pe.wait_ge(s["rows_loaded"], 32)
                        pe.matmul(flat(pr[:]), c.ones[0:1, :], qk_rows[:].rearrange("a n d -> a (n d)"), start=True,
                                  stop=True).then_inc(s["rows_ps"], 1)

                    @block.vector
                    def _(v):
                        v.wait_ge(s["rows_ps"], 1)
                        v.tensor_copy(qks[:], pr[:]).then_inc(s["copied"], 1)
                        v.wait_ge(s["copied"], 1)
                        for n in range(2):
                            v.tensor_tensor(scaled[:, 2 * n], rope[:, 2 * n],
                                            qks[:, n:n + 1, :].broadcast_to([P, BLOCKS + 1, HDW]), ALU.mult)
                            for k in range(2):
                                o, p = k * 32, 32 - k * 32
                                v.tensor_tensor(scaled[:, 2 * n + 1, :, o:o + 32], rope[:, 2 * n + 1, :, o:o + 32],
                                                qks[:, n:n + 1, p:p + 32].broadcast_to([P, BLOCKS + 1, 32]), ALU.mult)
                st.end_step()
            with Stage(nc, "wa") as st:
                window_attention_steps(nc, st, padded, XNT, c, scaled, band, has_prev, shifts, wqkv, wo)
            with Stage(nc, "wf") as st:
                geglu_steps(nc, st, Y, c, shifts, w1, w2, b1, b2, gb)

        with Stage(nc, "wx") as st:
            s = st.sems("added")
            with nc.Block(no_gpsimd_drain=True) as block:
                @block.vector
                def _(v):
                    v.tensor_tensor(X[:], X[:], Y, ALU.add).then_inc(s["added"], 1)
                    v.wait_ge(s["added"], 1)
            st.end_step()


def window_attention_steps(nc, st, Y, XNT, c, scaled, band, has_prev, shifts, wqkv, wo):
    H = HEADSW
    ya = st.sb("ya", [P, P])
    yb = st.sb("yb", [P, 2, P])
    xsT = st.sb("xsT", [P, P])
    v_all = st.sb("v_all", [P, 2, H, HDW])
    v_prev = st.sb("v_prev", [P, 2, H // GH, GH, HDW])
    sq = st.sb("sq", [P, 2, H, HDW])
    rot, part = (XNT[:, n * 2 * INNER:(n + 1) * 2 * INNER].rearrange("p (n h d) -> p n h d", n=2, d=HDW)
                 for n in range(2))
    norm = st.sb("norm", [P, 2, H])
    rnorm = st.sb("rnorm", [P, 2, 2, H])
    qT = st.sb("qT", [P, 2, H, P])
    kT = st.sb("kT", [P, 2, H // 2, KEYS])
    sc = st.sb("sc", [P, H, KEYS])
    smax, bias, rtotal = (st.sb(n, [P, H]) for n in ("smax", "bias", "rtotal"))
    total = st.sb("total", [P, 2, H])
    pc = st.sb("pc", [P, 2, H, KEYS])
    pp = st.sb("pp", [P, H, WINDOW])
    pcT = st.sb("pcT", [P, H, P])
    ppT = st.sb("ppT", [P, H // GH, P])
    o = st.sb("o", [P, H, HDW])
    oT = st.sb("oT", [P, INNER // P, P])
    front = st.ps("front", (P, 4, 512))
    scored = st.ps("scored", (P, 2, 512))
    back = st.ps("back", (P, 2, 512))
    groups = [range(n, min(n + 2 * BANK_HEADS, H)) for n in range(0, H, 2 * BANK_HEADS)]
    NG = len(groups)
    s = st.sems("y_copied xsT_ps xsT_ready q_ps k_ps v_ps v_ready sq_ready norm_ready rnorm_ready q_rot k_sum k_rot "
                "qT_ps kT_ps qT_even qT_odd kT_ready kT_kept v_kept scores_ps sc_ready max_ready bias_ready "
                "probs_ready ppT_ps ppT_ready pcT_ps pcT_v pcT_a o_ps o_ready oT_ps oT_ready out_ps added part_ready "
                "norm_in pp_ready zeroed total_ready")

    def two_banks(ps, k):
        return ps[:, k:k + 2, :].rearrange("p k n -> p (k n)")

    def pipeline_step(block, k, u, project=None, score=None, attend=None):
        w = 1 - u

        @block.gpsimd
        def _(g):
            if attend is not None:
                if k >= 1:
                    g.wait_ge(s["probs_ready"], NG * k)
                    g.wait_ge(s["ppT_ps"], k)
                    g.wait_ge(s["v_kept"], GH * k)
                g.tensor_copy(pp[:], pc[:, w, :, 0:WINDOW]).then_inc(s["pp_ready"], 1)
            if score is not None:
                if k >= 1:
                    g.wait_ge(s["kT_ready"], k)
                    g.wait_ge(s["scores_ps"], NG * k)
                g.tensor_tensor(kT[:, w, :, 0:WINDOW], kT[:, u, :, P:KEYS],
                                has_prev[:, 1, ds(project[1], 1)].unsqueeze(2).broadcast_to([P, H // 2, WINDOW]),
                                ALU.mult).then_inc(s["kT_kept"], 1)
            if project is not None:
                for n, done in enumerate(("q_rot", "k_sum")):
                    g.wait_ge(s["part_ready"], 2 * k + n + 1)
                    g.tensor_tensor(rot[:, n], rot[:, n], part[:, n], ALU.add).then_inc(s[done], 1)
            if score is not None:
                g.wait_ge(s["o_ps"], k + 1)
                g.wait_ge(s["pp_ready"], k + 1)
                g.wait_ge(s["kT_kept"], k + 1)
                g.wait_ge(s["q_rot"], k + 1)
                g.wait_ge(s["k_sum"], k + 1)
                if k >= 1:
                    g.wait_ge(s["v_ready"], k)
                for j in range(GH):
                    g.tensor_copy(v_prev[j * 32:(j + 1) * 32, w, :, j, :],
                                  v_all[P - WINDOW:P, u].rearrange("p (g j) d -> p g j d", j=GH)[:, :, j, :]
                                  ).then_inc(s["v_kept"], 1)
                    g.wait_ge(s["v_kept"], GH * k + j + 1)
            elif project is not None:
                g.wait_ge(s["q_rot"], k + 1)
                g.wait_ge(s["k_sum"], k + 1)
            else:
                g.wait_ge(s["pp_ready"], k + 1)

        @block.scalar
        def _(a):
            def exps(n):
                if n == 0 and k >= 1:
                    a.wait_ge(s["total_ready"], k)
                a.wait_ge(s["bias_ready"], NG * k + n + 1)
                for h in groups[n]:
                    last = a.activation(pc[:, u, h, :], sc[:, h, :], ACT.Exp, scale=rnorm[:, u, 0, h:h + 1],
                                        bias=bias[:, h:h + 1], accum_out=total[:, u, h:h + 1])
                last.then_inc(s["probs_ready"], 1)

            def square(n, ready):
                a.wait_ge(s[ready], k + 1)
                a.activation(sq[:, n].rearrange("p h d -> p (h d)"), two_banks(front, 2 * n),
                             ACT.Square).then_inc(s["sq_ready"], 1)

            def copy_probs(n):
                a.wait_ge(s["pcT_ps"], 4 * k + n + 1)
                a.activation(flat(pcT[:, n * GH:(n + 1) * GH, :]), back[:, 1, :], ACT.Copy).then_inc(s["pcT_a"], 1)

            if project is not None:
                mine = Y[:, ds(project[0] + 1, 1), :].rearrange("p a d -> p (a d)")
                if k >= 1:
                    a.wait_ge(s["xsT_ps"], k)
                a.activation(ya[:, 0:HALFW], mine[:, 0:HALFW], ACT.Copy)
                a.activation(yb[:, w, HALFW:P], mine[:, HALFW:P], ACT.Copy).then_inc(s["y_copied"], 1)
                a.wait_ge(s["xsT_ps"], k + 1)
                a.activation(xsT[:], front[:, 3, 0:P], ACT.Copy).then_inc(s["xsT_ready"], 1)
            if attend is not None:
                copy_probs(1)
            if project is not None:
                if k >= 1:
                    a.wait_ge(s["norm_in"], k)
                square(0, "q_ps")
                square(1, "k_ps")
            if attend is not None:
                copy_probs(3)
                a.wait_ge(s["ppT_ps"], k + 1)
                a.activation(flat(ppT[:]), back[:, 0, :], ACT.Copy).then_inc(s["ppT_ready"], 1)
            if score is not None:
                exps(0)
            if project is not None:
                a.wait_ge(s["norm_in"], k + 1)
                a.activation(norm[:], norm[:], ACT.Sqrt).then_inc(s["norm_ready"], 1)
            if score is not None:
                exps(1)
            if project is not None:
                a.wait_ge(s["v_ps"], k + 1)
                if attend is not None:
                    a.wait_ge(s["o_ps"], k + 1)
                if k >= 1:
                    a.wait_ge(s["v_kept"], GH * k)
                a.activation(v_all[:, w].rearrange("p h d -> p (h d)"), two_banks(front, 0),
                             ACT.Copy).then_inc(s["v_ready"], 1)
                a.wait_ge(s["qT_ps"], k + 1)
                a.activation(qT[0:HDW, w, 0:H:2, :], front[0:HDW, 2:4, :].rearrange("p k (h n) -> p (k h) n", n=P),
                             ACT.Copy).then_inc(s["qT_even"], 1)
            if score is not None:
                exps(2)
            if attend is not None:
                a.wait_ge(s["oT_ps"], k + 1)
                a.activation(flat(oT[:]), two_banks(back, 0), ACT.Copy).then_inc(s["oT_ready"], 1)
            if project is not None:
                a.wait_ge(s["kT_ps"], k + 1)
                a.activation(kT[:, w, :, WINDOW:KEYS], front[:, 0:2, :].rearrange("p k (h n) -> p (k h) n", n=P),
                             ACT.Copy).then_inc(s["kT_ready"], 1)

        @block.tensor
        def _(pe):
            def scores(n):
                hs = groups[n]
                m = len(hs) // 2
                if k >= 1 or n >= 1:
                    pe.wait_ge(s["sc_ready"], NG * k + n)
                for h in hs:
                    bank, at = (h - hs[0]) // m, (h - hs[0]) % m * KEYS
                    last = pe.matmul(scored[:, bank, at:at + KEYS], qT[:, u, h, :], kT[:, u, h // 2, :],
                                     start=True, stop=True)
                last.then_inc(s["scores_ps"], 1)

            def product(n, done):
                for i in range(2):
                    last = pe.matmul(front[:, 2 * n % 4 + i, :], xsT[:], wqkv[:, (2 * n + i) * 512:(2 * n + i + 1) * 512],
                                     start=True, stop=True)
                last.then_inc(s[done], 1)

            def turn(n, first, done):
                for i in range(H // 2):
                    last = pe.transpose(front[:, first + i // 4, (i % 4) * P:(i % 4 + 1) * P],
                                        rot[:, n, 2 * i:2 * i + 2, :].rearrange("p h d -> p (h d)"), c.ident)
                last.then_inc(s[done], 1)

            def turn_probs(g):
                for j in range(GH):
                    last = pe.transpose(back[:, g % 2, j * P:(j + 1) * P], pc[:, w, g * GH + j, WINDOW:KEYS], c.ident)
                last.then_inc(s["pcT_ps"], 1)

            if project is not None:
                pe.wait_ge(s["y_copied"], k + 1)
                if k >= 1:
                    pe.wait_ge(s["qT_even"], k)
                    pe.wait_ge(s["qT_odd"], k)
                x = front[:, 3, 0:P]
                pe.matmul(x, ya[:], c.ident, start=True, stop=False)
                pe.matmul(x, yb[:, w], shifts[:, 0, :], start=False, stop=False)
                pe.matmul(x[:, 0:1], yb[:, u], has_prev[:, 0, ds(project[1], 1)], start=False,
                          stop=True).then_inc(s["xsT_ps"], 1)
            if score is not None:
                if k >= 1:
                    pe.wait_ge(s["qT_odd"], k)
                    pe.wait_ge(s["kT_ready"], k)
                    pe.wait_ge(s["kT_kept"], k)
                scores(0)
            if attend is not None:
                if k >= 1:
                    pe.wait_ge(s["probs_ready"], NG * k)
                    pe.wait_ge(s["added"], k)
                    pe.wait_ge(s["oT_ready"], k)
                turn_probs(0)
                turn_probs(1)
            if project is not None:
                pe.wait_ge(s["xsT_ready"], k + 1)
                if k >= 1:
                    pe.wait_ge(s["kT_ready"], k)
                product(0, "q_ps")
                product(1, "k_ps")
            if score is not None:
                scores(1)
            if attend is not None:
                pe.wait_ge(s["pcT_v"], 2 * k + 1)
                turn_probs(2)
                pe.wait_ge(s["pcT_a"], 2 * k + 1)
                turn_probs(3)
                pe.wait_ge(s["pcT_v"], 2 * k + 2)
                pe.wait_ge(s["pp_ready"], k + 1)
                for g in range(H // GH):
                    last = pe.transpose(back[:, 0, g * P:(g + 1) * P],
                                        pp[:, g * GH:(g + 1) * GH, :].rearrange("p h k -> p (h k)"), c.ident)
                last.then_inc(s["ppT_ps"], 1)
                pe.wait_ge(s["ppT_ready"], k + 1)
                pe.wait_ge(s["pcT_a"], 2 * k + 2)
                if k >= 2:
                    pe.wait_ge(s["v_kept"], GH * (k - 1))
                for g in range(H // GH):
                    out = back[:, g // 2, (g % 2) * GH * HDW:(g % 2 + 1) * GH * HDW]
                    pe.matmul(out, ppT[:, g, :], v_prev[:, w, g].rearrange("p j d -> p (j d)"), start=True, stop=False)
                    for j in range(GH):
                        last = pe.matmul(out[:, j * HDW:(j + 1) * HDW], pcT[:, g * GH + j, :], v_all[:, w, g * GH + j, :],
                                         start=False, stop=(j == GH - 1))
                last.then_inc(s["o_ps"], 1)
            if project is not None:
                pe.wait_ge(s["sq_ready"], 2 * k + 1)
                pe.wait_ge(s["part_ready"], 2 * k + 1)
                product(2, "v_ps")
            if score is not None:
                scores(2)
            if project is not None:
                pe.wait_ge(s["sq_ready"], 2 * k + 2)
                pe.wait_ge(s["part_ready"], 2 * k + 2)
                pe.wait_ge(s["q_rot"], k + 1)
                turn(0, 2, "qT_ps")
            if attend is not None:
                pe.wait_ge(s["o_ready"], k + 1)
                for i in range(INNER // P):
                    last = pe.transpose(back[:, i // 4, (i % 4) * P:(i % 4 + 1) * P],
                                        o[:, 2 * i:2 * i + 2, :].rearrange("p h d -> p (h d)"), c.ident)
                last.then_inc(s["oT_ps"], 1)
            if project is not None:
                pe.wait_ge(s["k_rot"], k + 1)
                pe.wait_ge(s["v_ready"], k + 1)
                turn(1, 0, "kT_ps")
            if attend is not None:
                pe.wait_ge(s["oT_ready"], k + 1)
                for i in range(INNER // P):
                    last = pe.matmul(back[:, 0, 0:P], oT[:, i, :], wo[:, i, :], start=(i == 0), stop=(i == INNER // P - 1))
                last.then_inc(s["out_ps"], 1)

        @block.vector
        def _(v):
            def masked_max(n):
                hs = groups[n]
                m = len(hs) // 2
                v.wait_ge(s["scores_ps"], NG * k + n + 1)
                if k >= 1 and n == 0:
                    v.wait_ge(s["probs_ready"], NG * k)
                at = hs[0]
                v.tensor_tensor(sc[:, at:at + 2 * m, :].rearrange("p (k a) x -> p k a x", k=2),
                                scored[:, :, 0:m * KEYS].rearrange("p k (a x) -> p k a x", a=m),
                                band[:, ds(score[1], 1), :].unsqueeze(2).broadcast_to([P, 2, m, KEYS]),
                                ALU.add).then_inc(s["sc_ready"], 1)
                v.wait_ge(s["sc_ready"], NG * k + n + 1)
                v.tensor_reduce(smax[:, at:at + 2 * m], sc[:, at:at + 2 * m, :], AX.X, ALU.max).then_inc(s["max_ready"], 1)
                v.wait_ge(s["max_ready"], NG * k + n + 1)
                v.scalar_tensor_tensor(out=bias[:, at:at + 2 * m], in0=smax[:, at:at + 2 * m], scalar=-1.0,
                                       in1=rnorm[:, u, 0, at:at + 2 * m], op0=ALU.mult, op1=ALU.mult).then_inc(s["bias_ready"], 1)

            def rotate(n, ready):
                src = front[:, 2 * n:2 * n + 2, :].rearrange("p k (h d) -> p (k h) d", d=HDW)
                cos = scaled[:, 2 * n, ds(project[1], 1), :].broadcast_to([P, H, HDW])
                sin = scaled[:, 2 * n + 1, ds(project[1], 1), :]
                v.wait_ge(s[ready], k + 1)
                v.wait_ge(s["sq_ready"], 2 * k + n + 1)
                if k >= 1:
                    v.wait_ge(s["qT_ps"] if n == 0 else s["kT_ps"], k)
                v.tensor_tensor(rot[:, n], src, cos, ALU.mult)
                for i in range(2):
                    p0, p1 = i * 32, 32 - i * 32
                    last = v.tensor_tensor(part[:, n, :, p0:p0 + 32], src[:, :, p1:p1 + 32],
                                           sin[:, :, p0:p0 + 32].broadcast_to([P, H, 32]), ALU.mult)
                last.then_inc(s["part_ready"], 1)

            def copy_probs(n):
                v.wait_ge(s["pcT_ps"], 4 * k + n + 1)
                v.tensor_copy(flat(pcT[:, n * GH:(n + 1) * GH, :]), back[:, 0, :]).then_inc(s["pcT_v"], 1)

            if score is not None:
                masked_max(0)
            if attend is not None:
                copy_probs(0)
            if project is not None:
                rotate(0, "q_ps")
            if attend is not None:
                copy_probs(2)
            if project is not None:
                rotate(1, "k_ps")
            if project is not None:
                if k >= 1:
                    v.wait_ge(s["rnorm_ready"], 3 * k)
                v.tensor_reduce(norm[:].rearrange("p n h -> p (n h)"), sq[:].rearrange("p n h d -> p (n h) d"),
                                AX.X, ALU.add).then_inc(s["norm_in"], 1)
            if score is not None:
                masked_max(1)
            if attend is not None:
                v.reciprocal(rtotal[:], total[:, w]).then_inc(s["total_ready"], 1)
                v.wait_ge(s["total_ready"], k + 1)
                v.wait_ge(s["o_ps"], k + 1)
                v.tensor_tensor(o[:], back[:].rearrange("p k (h d) -> p (k h) d", d=HDW),
                                spread(rtotal[:], HDW), ALU.mult).then_inc(s["o_ready"], 1)
            if project is not None:
                v.wait_ge(s["norm_ready"], k + 1)
                v.tensor_scalar(norm[:], norm[:], 1e-12, None, ALU.max).then_inc(s["rnorm_ready"], 1)
                v.wait_ge(s["rnorm_ready"], 3 * k + 1)
                v.reciprocal(rnorm[:, w], norm[:]).then_inc(s["rnorm_ready"], 1)
                v.wait_ge(s["rnorm_ready"], 3 * k + 2)
                v.tensor_scalar(rnorm[:, w, 0, :], rnorm[:, w, 0, :], QK_SCALE, None, ALU.mult).then_inc(s["rnorm_ready"], 1)
                v.wait_ge(s["k_sum"], k + 1)
                v.tensor_tensor(rot[:, 1], rot[:, 1], spread(rnorm[:, w, 1, :], HDW), ALU.mult).then_inc(s["k_rot"], 1)
            if score is not None:
                masked_max(2)
            if project is not None:
                v.wait_ge(s["qT_ps"], k + 1)
                v.tensor_copy(qT[HDW:P, w, 1:H:2, :],
                              front[HDW:P, 2:4, :].rearrange("p k (h n) -> p (k h) n", n=P)).then_inc(s["qT_odd"], 1)
            if attend is not None:
                v.wait_ge(s["out_ps"], k + 1)
                mine = Y[:, ds(attend + 1, 1), :].rearrange("p a d -> p (a d)")
                v.tensor_tensor(mine, back[:, 0, 0:P], mine, ALU.add).then_inc(s["added"], 1)
                v.wait_ge(s["added"], k + 1)

    with nc.Block(no_gpsimd_drain=True) as block:
        @block.gpsimd
        def _(g):
            for buffer in (ya[:], yb[:], kT[:], v_prev[:]):
                g.memset(buffer, 0.0).then_inc(s["zeroed"], 1)
            g.wait_ge(s["zeroed"], 4)

        @block.vector
        def _(v):
            v.memset(qT[:], 0.0)
            v.memset(pc[:, 1], 0.0)
            v.memset(v_all[:, 1], 0.0)
            v.memset(total[:, 1], 1.0)
            v.memset(Y[:, 0:1, :], 0.0)
            v.memset(Y[:, TILES + 1:TILES + 2, :], 0.0)
    st.end_step()
    with nc.Block(no_gpsimd_drain=True) as block:
        pipeline_step(block, 0, 1, project=(0, 0))
    st.end_step()
    with nc.Fori(0, BATCH) as b:
        with nc.Fori(0, BLOCKS // STEPS) as i:
            with nc.Block(no_gpsimd_drain=True) as block:
                for k in range(STEPS):
                    place = i * STEPS + k
                    at = b * BLOCKS + place
                    pipeline_step(block, k, k % 2, project=(at + 1, place + 1), score=(at, place), attend=at - 1)
            st.end_step()
    with nc.Block(no_gpsimd_drain=True) as block:
        pipeline_step(block, 0, 0, attend=TILES - 1)
    st.end_step()


def geglu_steps(nc, st, Y, c, shifts, w1, w2, b1, b2, gb):
    yh = st.sb("yh", [P, G + 1, HALFW])
    xf, xn = st.sb("xf", [P, G, P]), st.sb("xn", [P, G, P])
    stats, mv = st.sb("stats", [P, G, 6]), st.sb("mv", [P, G, 2])
    var, std, rstd = (st.sb(n, [P, G]) for n in ("var", "std", "rstd"))
    xnT = st.sb("xnT", [P, G * P])
    gate, hid = st.sb("gate", [P, 3, G * P]), st.sb("hid", [P, 3, G * P])
    shp = st.ps("shp", (P, G, HALFW))
    xnp = st.ps("xnp", (P, G * P))
    ap_, gp = st.ps("ap", (P, 2, 512)), st.ps("gp", (P, 2, 512))
    outp = st.ps("outp", (P, G, P))
    s = st.sems("y_copied sh_ps xf_ready var_ready std_ready xn_ready xn_ps xnT_ready a_ps g_ps gate_ready hid_ready "
                "out_ps added zeroed chain")
    with nc.Fori(0, BATCH) as b:
        with nc.Block(no_gpsimd_drain=True) as block:
            @block.gpsimd
            def _(g):
                g.memset(yh[:], 0.0).then_inc(s["zeroed"], 1)
                g.wait_ge(s["zeroed"], 1)
        st.end_step()
        with nc.Fori(0, BLOCKS // G) as i:
            with nc.Block(no_gpsimd_drain=True) as block:
                mine = Y[:, ds(b * BLOCKS + i * G, G), :]

                @block.scalar
                def _(a):
                    a.activation(yh[:, 1:G + 1, :], mine[:, :, HALFW:P], ACT.Copy).then_inc(s["y_copied"], 1)
                    a.wait_ge(s["var_ready"], 1)
                    a.activation(std[:], var[:], ACT.Sqrt).then_inc(s["std_ready"], 1)
                    for n, (k0, k1) in enumerate(PIECES):
                        a.wait_ge(s["g_ps"], n + 1)
                        a.activation(gate[0:k1 - k0, n, :], gp[0:k1 - k0, n % 2, :], ACT.Gelu,
                                     bias=b1[0:k1 - k0, 1, n:n + 1]).then_inc(s["gate_ready"], 1)

                @block.tensor
                def _(pe):
                    pe.wait_ge(s["y_copied"], 1)
                    pe.matmul(flat(shp[:]), shifts[:, 0, :], yh[:, 1:G + 1, :].rearrange("p n d -> p (n d)"),
                              start=True, stop=False)
                    pe.matmul(flat(shp[:]), shifts[:, 1, :], yh[:, 0:G, :].rearrange("p n d -> p (n d)"),
                              start=False, stop=True).then_inc(s["sh_ps"], 1)
                    pe.wait_ge(s["xn_ready"], 1)
                    for j in range(G):
                        last = pe.transpose(xnp[:, j * P:(j + 1) * P], xn[:, j, :], c.ident)
                    last.then_inc(s["xn_ps"], 1)
                    pe.wait_ge(s["xnT_ready"], 1)
                    for n, (k0, k1) in enumerate(PIECES):
                        if n >= 2:
                            pe.wait_ge(s["gate_ready"], n - 1)
                            pe.wait_ge(s["hid_ready"], n - 1)
                        pe.matmul(gp[0:k1 - k0, n % 2, :], w1[:, UNITS + k0:UNITS + k1], xnT[:], start=True,
                                  stop=True).then_inc(s["g_ps"], 1)
                        pe.matmul(ap_[0:k1 - k0, n % 2, :], w1[:, k0:k1], xnT[:], start=True, stop=True).then_inc(s["a_ps"], 1)
                    pe.wait_ge(s["hid_ready"], 3)
                    for j in range(G):
                        for n, (k0, k1) in enumerate(PIECES):
                            pe.matmul(outp[:, j, :], hid[0:k1 - k0, n, j * P:(j + 1) * P], w2[0:k1 - k0, n, :],
                                      start=(n == 0), stop=False)
                        last = pe.matmul(outp[:, j, :], c.ones[0:1, :], b2[:], start=False, stop=True)
                    last.then_inc(s["out_ps"], 1)

                @block.vector
                def _(v):
                    step = Chain(v, s["chain"])
                    v.tensor_copy(xf[:, :, 0:HALFW], mine[:, :, 0:HALFW])
                    v.wait_ge(s["sh_ps"], 1)
                    step(v.tensor_copy(xf[:, :, HALFW:P], shp[:]))
                    v.tensor_copy(yh[:, 0, :], yh[:, G, :])
                    for j in range(G):
                        last = v.bn_stats(stats[:, j, :], xf[:, j, :])
                    step(last)
                    for j in range(G):
                        last = v.bn_aggr(mv[:, j, :], stats[:, j, :])
                    step(last)
                    v.tensor_scalar(var[:], mv[:, :, 1], LN_EPS, None, ALU.add).then_inc(s["var_ready"], 1)
                    v.wait_ge(s["std_ready"], 1)
                    step(v.reciprocal(rstd[:], std[:]))
                    for j in range(G):
                        last = v.tensor_scalar(xn[:, j, :], xf[:, j, :], mv[:, j, 0:1], rstd[:, j:j + 1],
                                               ALU.subtract, ALU.mult)
                    last.then_inc(s["xn_ready"], 1)
                    v.wait_ge(s["xn_ps"], 1)
                    v.tensor_scalar(xnT[:], xnp[:], gb[:, 0:1], gb[:, 1:2], ALU.mult, ALU.add).then_inc(s["xnT_ready"], 1)
                    for n, (k0, k1) in enumerate(PIECES):
                        v.wait_ge(s["gate_ready"], n + 1)
                        v.wait_ge(s["a_ps"], n + 1)
                        v.scalar_tensor_tensor(out=hid[0:k1 - k0, n, :], in0=ap_[0:k1 - k0, n % 2, :],
                                               scalar=b1[0:k1 - k0, 0, n:n + 1], in1=gate[0:k1 - k0, n, :],
                                               op0=ALU.add, op1=ALU.mult).then_inc(s["hid_ready"], 1)
                    v.wait_ge(s["out_ps"], 1)
                    v.tensor_tensor(mine, outp[:], mine, ALU.add).then_inc(s["added"], 1)
                    v.wait_ge(s["added"], 1)
            st.end_step()


COS_EPS = 1e-8


def l2_attention_stage(nc, X, XN, XNT, c):
    with Stage(nc, "a2") as st:
        xs = st.sb("xs", [P, SEQ])
        xv = st.sb("xv", [P, BLOCKS, P + 1])
        squares = st.sb("squares", [P, BLOCKS, P])
        norm2, norm, rnorm, rtotal = (st.sb(n, [P, BLOCKS]) for n in ("norm2", "norm", "rnorm", "rtotal"))
        diag = st.sb("diag", [P, BLOCKS, P])
        rrow = st.sb("rrow", [P, SEQ])
        scale = st.sb("scale", [P, 2, SEQ])
        sim = st.sb("sim", [P, 2, SEQ])
        E = st.sb("E", [P, BLOCKS, SEQ])
        mean = st.sb("mean", [P, 2, P])
        wide = st.ps("wide", (P, 2, SEQ))
        out = st.ps("out", (P, 2, 512))
        s = st.sems("xs_ready xv_ready norm2_ready norm_ready diag_ready row_ready rrow_done dots_ready sim_ready "
                    "exps out_ready out_used added ones_set chain")
        with nc.Fori(0, BATCH) as b:
            with nc.Block(no_gpsimd_drain=True) as block:
                @block.scalar
                def _(a):
                    a.activation(xs[:], XNT[:, ds(b * SEQ, SEQ)], ACT.Copy).then_inc(s["xs_ready"], 1)
                    a.wait_ge(s["norm2_ready"], 1)
                    a.activation(norm[:], norm2[:], ACT.Sqrt).then_inc(s["norm_ready"], 1)
                    a.wait_ge(s["row_ready"], 1)
                    a.activation(rrow[:], wide[:, 0, :], ACT.Copy).then_inc(s["rrow_done"], 1)
                    for t in range(BLOCKS):
                        a.wait_ge(s["sim_ready"], t + 1)
                        a.activation(E[:, t, :], sim[:, t % 2, :], ACT.Exp).then_inc(s["exps"], 1)

                @block.gpsimd
                def _(g):
                    g.memset(xv[:, :, P:P + 1], 1.0)
                    g.tensor_copy(xv[:, :, 0:P], XN[:, ds(b * BLOCKS, BLOCKS), :]).then_inc(s["xv_ready"], 1)

                @block.vector
                def _(v):
                    step = Chain(v, s["chain"])
                    v.wait_ge(s["xv_ready"], 1)
                    step(v.tensor_tensor(squares[:], xv[:, :, 0:P], xv[:, :, 0:P], ALU.mult))
                    v.tensor_reduce(norm2[:], squares[:], AX.X, ALU.add).then_inc(s["norm2_ready"], 1)
                    v.wait_ge(s["norm_ready"], 1)
                    step(v.tensor_scalar(norm[:], norm[:], 1e-30, None, ALU.max))
                    step(v.reciprocal(rnorm[:], norm[:]))
                    for t in range(BLOCKS):
                        last = v.tensor_scalar(diag[:, t, :], c.ident, rnorm[:, t:t + 1], None, ALU.mult)
                    last.then_inc(s["diag_ready"], 1)
                    v.wait_ge(s["rrow_done"], 1)
                    for t in range(BLOCKS):
                        step(v.tensor_scalar(scale[:, t % 2, :], rrow[:], rnorm[:, t:t + 1], 1.0 / COS_EPS,
                                             ALU.mult, ALU.min))
                        v.wait_ge(s["dots_ready"], t + 1)
                        if t >= 2:
                            v.wait_ge(s["exps"], t - 1)
                        v.tensor_tensor(sim[:, t % 2, :], wide[:, (t + 1) % 2, :], scale[:, t % 2, :],
                                        ALU.mult).then_inc(s["sim_ready"], 1)
                    for t in range(BLOCKS):
                        v.wait_ge(s["out_ready"], t + 1)
                        step(v.reciprocal(rtotal[:, t:t + 1], out[:, t % 2, P:P + 1]))
                        v.scalar_tensor_tensor(out=mean[:, t % 2, :], in0=out[:, t % 2, 0:P],
                                               scalar=rtotal[:, t:t + 1], in1=xv[:, t, 0:P],
                                               op0=ALU.mult, op1=ALU.add).then_inc(s["out_used"], 1)
                        v.wait_ge(s["out_used"], t + 1)
                        v.tensor_tensor(tile(X, b * BLOCKS + t), mean[:, t % 2, :], tile(X, b * BLOCKS + t),
                                        ALU.add).then_inc(s["added"], 1)
                    v.wait_ge(s["added"], BLOCKS)

                @block.tensor
                def _(pe):
                    pe.wait_ge(s["diag_ready"], 1)
                    for t in range(BLOCKS):
                        last = pe.matmul(wide[:, 0, t * P:(t + 1) * P], c.ones, diag[:, t, :], start=True, stop=True)
                    last.then_inc(s["row_ready"], 1)
                    pe.wait_ge(s["xs_ready"], 1)
                    for t in range(BLOCKS):
                        if t == 1:
                            pe.wait_ge(s["rrow_done"], 1)
                        if t >= 2:
                            pe.wait_ge(s["sim_ready"], t - 1)
                        for k in range(2):
                            last = pe.matmul(wide[:, (t + 1) % 2, k * 512:(k + 1) * 512], xs[:, t * P:(t + 1) * P],
                                             xs[:, k * 512:(k + 1) * 512], start=True, stop=True)
                        last.then_inc(s["dots_ready"], 1)
                    pe.wait_ge(s["exps"], BLOCKS)
                    for t in range(BLOCKS):
                        if t >= 2:
                            pe.wait_ge(s["out_used"], t - 1)
                        for k in range(BLOCKS):
                            last = pe.matmul(out[:, t % 2, 0:P + 1], E[:, k, t * P:(t + 1) * P], xv[:, k, :],
                                             start=(k == 0), stop=(k == BLOCKS - 1))
                        last.then_inc(s["out_ready"], 1)
            st.end_step()


JITTER = 0.01
WIDTH2 = 256


def l2_ffn_stage(nc, X, XNT, c, gate_w, w1, w2, w3):
    with Stage(nc, "f2") as outer:
        gT = outer.sb("gT", [P, EXPERTS])
        w1T = outer.sb("w1T", [P, EXPERTS, WIDTH2])
        w3T = outer.sb("w3T", [P, EXPERTS, WIDTH2])
        w2T = outer.sb("w2T", [P, EXPERTS, 2, P])
        for n, pairs in enumerate((
            [(gT[:], gate_w)] + [(w1T[:, e, k * P:(k + 1) * P], w1[e, k * P:(k + 1) * P, :])
                                 for e in range(EXPERTS) for k in range(2)],
            [(w3T[:, e, k * P:(k + 1) * P], w3[e, k * P:(k + 1) * P, :]) for e in range(EXPERTS) for k in range(2)],
            [(w2T[:, e, k, :], w2[e, :, k * P:(k + 1) * P]) for e in range(EXPERTS) for k in range(2)],
        )):
            load_turned(nc, f"f2w{n}", pairs, c)
        with Stage(nc, "f2s") as st:
            xs = st.sb("xs", [P, G * P])
            lg, size, gap, first, second, rest = (st.sb(n, [P, G, EXPERTS]) for n in
                                                  ("lg", "size", "gap", "first", "second", "rest"))
            ex1, ex2, lim1, lim2 = (st.sb(n, [P, G, EXPERTS]) for n in ("ex1", "ex2", "lim1", "lim2"))
            weight = st.sb("weight", [P, G, EXPERTS])
            top = st.sb("top", [P, G, 8])
            at = st.sb("at", [P, G, 8], U32)
            atf = st.sb("atf", [P, G, 8])
            total, mult = (st.sb(n, [P, 2, G]) for n in ("total", "mult"))
            th = st.sb("th", [P, 2, 512])
            gated = st.sb("gated", [P, 2, 512])
            act = st.sb("act", [P, 2, 2, 512])
            acc = st.sb("acc", [P, G, P])
            logits = st.ps("logits", (P, G, EXPERTS))
            h1 = st.ps("h1", (P, 2, 512))
            h3 = st.ps("h3", (P, 2, 512))
            y = st.ps("y", (P, 2, G, P))
            s = st.sems("xs_ready logits_ready shifted1 exps h1_ready h3_ready th_ready act_ready y_ready y_used "
                        "added chain")
            with nc.Fori(0, TILES // G) as i:
                with nc.Block(no_gpsimd_drain=True) as block:
                    @block.scalar
                    def _(a):
                        a.activation(xs[:], XNT[:, ds(i * G * P, G * P)], ACT.Copy).then_inc(s["xs_ready"], 1)
                        a.wait_ge(s["shifted1"], 1)
                        a.activation(ex1[:], ex1[:], ACT.Exp)
                        a.activation(ex2[:], ex2[:], ACT.Exp).then_inc(s["exps"], 1)
                        for n in range(2 * EXPERTS):
                            a.wait_ge(s["h1_ready"], n + 1)
                            if n >= 2:
                                a.wait_ge(s["act_ready"], n - 1)
                            a.activation(th[:, n % 2, :], h1[:, n % 2, :], ACT.Tanh, scale=0.5).then_inc(s["th_ready"], 1)

                    @block.tensor
                    def _(pe):
                        pe.wait_ge(s["xs_ready"], 1)
                        for j in range(G):
                            last = pe.matmul(logits[:, j, :], xs[:, j * P:(j + 1) * P], gT[:], start=True, stop=True)
                        last.then_inc(s["logits_ready"], 1)

                        def second_product(e):
                            pe.wait_ge(s["act_ready"], 2 * e + 2)
                            if e >= 2:
                                pe.wait_ge(s["y_used"], e - 1)
                            for j in range(G):
                                for k in range(2):
                                    last = pe.matmul(y[:, e % 2, j, :], act[:, e % 2, k, j * P:(j + 1) * P],
                                                     w2T[:, e, k, :], start=(k == 0), stop=(k == 1))
                            last.then_inc(s["y_ready"], 1)

                        for e in range(EXPERTS):
                            for k in range(2):
                                n = 2 * e + k
                                if n >= 2:
                                    pe.wait_ge(s["act_ready"], n - 1)
                                pe.matmul(h1[:, n % 2, :], w1T[:, e, k * P:(k + 1) * P], xs[:],
                                          start=True, stop=True).then_inc(s["h1_ready"], 1)
                                pe.matmul(h3[:, n % 2, :], w3T[:, e, k * P:(k + 1) * P], xs[:],
                                          start=True, stop=True).then_inc(s["h3_ready"], 1)
                            if e >= 1:
                                second_product(e - 1)
                        second_product(EXPERTS - 1)

                    @block.vector
                    def _(v):
                        step = Chain(v, s["chain"])
                        v.wait_ge(s["logits_ready"], 1)
                        step(v.tensor_copy(lg[:], logits[:]))
                        for j in range(G):
                            last = v.max(top[:, j, :], lg[:, j, :])
                        step(last)
                        for j in range(G):
                            last = v.max_index(at[:, j, :], top[:, j, :], lg[:, j, :])
                        step(last)
                        v.tensor_scalar(size[:], lg[:], -1.0, None, ALU.mult)
                        step(v.tensor_copy(atf[:], at[:]))
                        step(v.tensor_tensor(size[:], size[:], lg[:], ALU.max))
                        for j in range(G):
                            v.tensor_scalar(first[:, j, :], c.count8, atf[:, j, 0:1], None, ALU.is_equal)
                            last = v.tensor_scalar(second[:, j, :], c.count8, atf[:, j, 1:2], None, ALU.is_equal)
                        step(last)
                        for ex, lim, k in ((ex1, lim1, 0), (ex2, lim2, 1)):
                            t = top[:, :, k:k + 1].broadcast_to([P, G, EXPERTS])
                            step(v.tensor_tensor(lim[:], size[:], t, ALU.max))
                            step(v.tensor_tensor(gap[:], t, lg[:], ALU.subtract))
                            step(v.scalar_tensor_tensor(out=lim[:], in0=lim[:], scalar=2 * JITTER, in1=gap[:],
                                                        op0=ALU.mult, op1=ALU.is_ge))
                            last = v.tensor_scalar(ex[:], gap[:], -1.0, 0.0, ALU.mult, ALU.min)
                            if k == 0:
                                step(last)
                            else:
                                last.then_inc(s["shifted1"], 1)
                        step(v.tensor_scalar(rest[:], first[:], -1.0, 1.0, ALU.mult, ALU.add))
                        step(v.tensor_tensor(lim2[:], lim2[:], rest[:], ALU.mult))
                        v.wait_ge(s["exps"], 1)
                        v.tensor_tensor(ex1[:], ex1[:], lim1[:], ALU.mult)
                        step(v.tensor_tensor(ex2[:], ex2[:], lim2[:], ALU.mult))
                        v.tensor_reduce(total[:, 0, :], ex1[:], AX.X, ALU.add)
                        step(v.tensor_reduce(total[:, 1, :], ex2[:], AX.X, ALU.add))
                        step(v.reciprocal(mult[:], total[:]))
                        v.tensor_tensor(first[:], first[:], spread(mult[:, 0, :], EXPERTS), ALU.mult)
                        step(v.tensor_tensor(second[:], second[:], spread(mult[:, 1, :], EXPERTS), ALU.mult))
                        step(v.tensor_tensor(weight[:], first[:], second[:], ALU.add))

                        def hidden(n):
                            v.wait_ge(s["th_ready"], n + 1)
                            step(v.scalar_tensor_tensor(out=gated[:, n % 2, :], in0=th[:, n % 2, :], scalar=1.0,
                                                        in1=h1[:, n % 2, :], op0=ALU.add, op1=ALU.mult))
                            v.wait_ge(s["h3_ready"], n + 1)
                            if n >= 4:
                                v.wait_ge(s["y_ready"], (n - 4) // 2 + 1)
                            v.scalar_tensor_tensor(out=act[:, (n // 2) % 2, n % 2, :], in0=h3[:, n % 2, :], scalar=0.5,
                                                   in1=gated[:, n % 2, :], op0=ALU.mult,
                                                   op1=ALU.mult).then_inc(s["act_ready"], 1)

                        def gather(e):
                            v.wait_ge(s["y_ready"], e + 1)
                            for j in range(G):
                                if e == 0:
                                    last = v.tensor_scalar(acc[:, j, :], y[:, 0, j, :], weight[:, j, 0:1], None, ALU.mult)
                                else:
                                    last = v.scalar_tensor_tensor(out=acc[:, j, :], in0=y[:, e % 2, j, :],
                                                                  scalar=weight[:, j, e:e + 1], in1=acc[:, j, :],
                                                                  op0=ALU.mult, op1=ALU.add)
                            last.then_inc(s["y_used"], 1)
                            v.wait_ge(s["y_used"], e + 1)

                        for e in range(EXPERTS):
                            hidden(2 * e)
                            hidden(2 * e + 1)
                            if e >= 1:
                                gather(e - 1)
                        gather(EXPERTS - 1)
                        v.tensor_tensor(X[:, ds(i * G, G), :], acc[:], X[:, ds(i * G, G), :], ALU.add).then_inc(s["added"], 1)
                        v.wait_ge(s["added"], 1)
                st.end_step()


HEADS3 = 4
HD3 = P // HEADS3
LOCAL, MID = 7, 25
PATHS = 4
PAIRS = [(0, 1), (0, 2), (0, 3), (1, 2), (1, 3), (2, 3)]
FEATS = HEADS3 * (2 * PATHS + len(PAIRS))
HIDDEN3 = 2 * (P + FEATS)
FLOOR = 0.01
L2_EPS, MIX_EPS = 1e-12, 1e-5


def l3_attention_stage(nc, X, XNT, c, d):
    with Stage(nc, "a3") as outer:
        outs = outer.sb("outs", [P, TILES, PATHS, P])
        with Stage(nc, "a3x") as st:
            l3_paths_stage(nc, st, XNT, c, d, outs)
        with Stage(nc, "a3y") as st:
            l3_router_stage(nc, st, X, XNT, c, d, outs)


def l3_paths_stage(nc, outer, XNT, c, d, outs):
    proj = outer.sb("proj", [P, 3, P])
    wb = outer.sb("wb", [P, HEADS3])
    taps = outer.sb("taps", [P, 3, TAPS])
    wide_taps = outer.sb("wide_taps", [P, LOCAL + MID])
    masks = outer.sb("masks", [P, len(LEVELS), P])
    raw = outer.sb("raw", [P, 3, TAPS - 1 + SEQ])
    act = outer.sb("act", [P, 3, SEQ])
    th = outer.sb("th", [P, SEQ])
    qk = outer.sb("qk", [P, 2, SEQ])
    vh = outer.sb("vh", [P, MID - 1 + SEQ])
    lm = outer.sb("lm", [P, 2, SEQ])
    S = outer.sb("S", [P, P])
    with Stage(nc, "a3w") as st:
        s = st.sems("loaded")
        with nc.Block(no_gpsimd_drain=True) as block:
            @block.sync
            def _(sp):
                loads = [(proj[:, n, :], d[f"L3_attn_W{w}"]) for n, w in enumerate("qkv")]
                loads += [(taps[:, n, :], d[f"L3_attn_conv_{w}_w"]) for n, w in enumerate("qkv")]
                loads += [(wb[:], d["L3_attn_Wb"]), (wide_taps[:, 0:LOCAL], d["L3_attn_local_w"]),
                          (wide_taps[:, LOCAL:], d["L3_attn_mid_w"]), (masks[:], d["const_level_masks"])]
                for dst, src in loads:
                    sp.dma_start(dst, src).then_inc(s["loaded"], 16)
                sp.wait_ge(s["loaded"], 16 * len(loads))

            @block.vector
            def _(v):
                v.memset(raw[:, :, 0:TAPS - 1], 0.0)
                v.memset(vh[:, 0:MID - 1], 0.0)
                v.wait_ge(s["loaded"], 160)
                v.tensor_scalar(taps[:], taps[:], 0.5, None, ALU.mult)
        st.end_step()

    with nc.Fori(0, BATCH) as b:
        with Stage(nc, "a3p") as st:
            rawp = st.ps("rawp", (P, 3, SEQ))
            s = st.sems("raw_ready raw_copied conv_ready th_ready silu_ready done chain")
            with nc.Block(no_gpsimd_drain=True) as block:
                @block.tensor
                def _(pe):
                    for n in range(3):
                        for k in range(2):
                            last = pe.matmul(rawp[:, n, k * 512:(k + 1) * 512], proj[:, n, :],
                                             XNT[:, ds(b * SEQ + k * 512, 512)], start=True, stop=True)
                        last.then_inc(s["raw_ready"], 1)

                @block.scalar
                def _(a):
                    for n in range(3):
                        a.wait_ge(s["raw_ready"], n + 1)
                        a.activation(raw[:, n, TAPS - 1:], rawp[:, n, :], ACT.Copy).then_inc(s["raw_copied"], 1)
                    for n in range(3):
                        a.wait_ge(s["conv_ready"], n + 1)
                        if n >= 1:
                            a.wait_ge(s["silu_ready"], n)
                        a.activation(th[:], act[:, n, :], ACT.Tanh).then_inc(s["th_ready"], 1)

                @block.vector
                def _(v):
                    step = Chain(v, s["chain"])
                    v.memset(S[:], 0.0)

                    def convolve(out, src, w, taps_n):
                        step(v.tensor_scalar(out, src[:, taps_n - 1:taps_n - 1 + SEQ], w[:, taps_n - 1:taps_n], None, ALU.mult))
                        for k in range(taps_n - 1):
                            last = v.scalar_tensor_tensor(out=out, in0=src[:, k:k + SEQ], scalar=w[:, k:k + 1], in1=out,
                                                          op0=ALU.mult, op1=ALU.add)
                            if k < taps_n - 2:
                                step(last)
                        return last

                    for n in range(3):
                        v.wait_ge(s["raw_copied"], n + 1)
                        convolve(act[:, n, :], raw[:, n, :], taps[:, n, :], TAPS).then_inc(s["conv_ready"], 1)
                    for n, dst in enumerate((qk[:, 0, :], qk[:, 1, :], vh[:, MID - 1:])):
                        v.wait_ge(s["th_ready"], n + 1)
                        v.scalar_tensor_tensor(out=dst, in0=th[:], scalar=1.0, in1=act[:, n, :], op0=ALU.add,
                                               op1=ALU.mult).then_inc(s["silu_ready"], 1)
                    v.wait_ge(s["silu_ready"], 3)
                    convolve(lm[:, 0, :], vh[:, MID - LOCAL:], wide_taps[:, 0:LOCAL], LOCAL).then_inc(s["done"], 1)
                    convolve(lm[:, 1, :], vh[:], wide_taps[:, LOCAL:], MID).then_inc(s["done"], 1)
                    v.wait_ge(s["done"], 2)
            st.end_step()
        with Stage(nc, "a3d") as st:
            l3_chunk_steps(nc, st, XNT, c, b, wb, masks, qk, vh, lm, S, outs)


def l3_chunk_steps(nc, st, XNT, c, b, wb, masks, qk, vh, lm, S, outs):
    four = [P, HEADS3, P]
    heads = [P, HEADS3, HD3]
    K = len(LEVELS)
    xs, q, k0, kn, kn_tok, q2, k2, R, u = (st.sb(n, [P, P]) for n in
                                           ("xs", "q", "k0", "kn", "kn_tok", "q2", "k2", "R", "u"))
    vlm = st.sb("vlm", [P, 3, P])
    norms, rnorms = (st.sb(n, [P, 2, HEADS3]) for n in ("norms", "rnorms"))
    beta, nbeta, tb = (st.sb(n, [P, HEADS3]) for n in ("beta", "nbeta", "tb"))
    N, Nlev, AT = st.sb("N", four), st.sb("Nlev", [P, K, HEADS3, P]), st.sb("AT", four)
    T, XT, Zt = (st.sb(n, four) for n in ("T", "XT", "Zt"))
    small, tok, ups, sps = (st.ps(n, four) for n in ("small", "tok", "ups", "sps"))
    big = st.ps("big", (P, 4, 4, P))
    zt, tps, xps, os_ = (big[:, n] for n in range(4))
    s = st.sems("copied q_ready sq_ready small_ready tanh_ready sqrt_in sqrt_ready tok_ready kn_tok_ready kn_ps "
                "kn_ready gram_ready N_ready Nlev_ready qk_ready AT_ready kS_ready R_ready zt_ps zt_ready t_ps t_ready "
                "x_ps x_ready u_ps u_ready o_ps s_ps done vtok_ready chain")

    def head(h):
        return slice(h * HD3, (h + 1) * HD3)

    with nc.Fori(0, BLOCKS) as ch:
        with nc.Block(no_gpsimd_drain=True) as block:
            @block.gpsimd
            def _(g):
                g.tensor_copy(k0[:], qk[:, 1, ds(ch * P, P)])
                g.tensor_copy(q[:], qk[:, 0, ds(ch * P, P)]).then_inc(s["q_ready"], 1)
                g.tensor_copy(xs[:], XNT[:, ds(b * SEQ + ch * P, P)])
                g.tensor_copy(vlm[:, 0, :], vh[:, ds(ch * P + (MID - 1), P)])
                g.tensor_copy(vlm[:, 1:3, :], lm[:, :, ds(ch * P, P)]).then_inc(s["copied"], 1)
                g.wait_ge(s["N_ready"], 1)
                for k in range(K):
                    g.tensor_tensor(Nlev[:, k], N[:], masks[:, k:k + 1, :].broadcast_to(four), ALU.mult).then_inc(s["Nlev_ready"], 1)

            @block.scalar
            def _(a):
                a.wait_ge(s["q_ready"], 1)
                a.activation(k2[:], k0[:], ACT.Square)
                a.activation(q2[:], q[:], ACT.Square).then_inc(s["sq_ready"], 1)
                a.wait_ge(s["small_ready"], 1)
                a.activation(tb[:], small[:, 0, 2 * HEADS3:3 * HEADS3], ACT.Tanh, scale=0.5).then_inc(s["tanh_ready"], 1)
                a.wait_ge(s["sqrt_in"], 1)
                a.activation(norms[:], norms[:], ACT.Sqrt).then_inc(s["sqrt_ready"], 1)
                a.wait_ge(s["kn_ps"], 1)
                a.activation(kn[:], tok[:, 3, :], ACT.Copy).then_inc(s["kn_ready"], 1)
                for k in range(1, K):
                    a.wait_ge(s["zt_ps"], k + 1)
                    if k >= 2:
                        a.wait_ge(s["x_ps"], k - 1)
                    a.activation(Zt[:], zt, ACT.Copy).then_inc(s["zt_ready"], 1)

            @block.tensor
            def _(pe):
                def heads_of(out, lhs, rhs, sem):
                    for h in range(HEADS3):
                        last = pe.matmul(out[:, h, :], lhs(h), rhs(h), start=True, stop=True)
                    last.then_inc(sem, 1)

                pe.wait_ge(s["copied"], 1)
                pe.transpose(tok[:, 0, :], k0[:], c.ident)
                for n in range(3):
                    last = pe.transpose(ups[:, n, :], vlm[:, n, :], c.ident)
                last.then_inc(s["tok_ready"], 1)
                pe.wait_ge(s["sq_ready"], 1)
                pe.matmul(small[:, 0, 0:HEADS3], q2[:], c.head_blocks[:, 0:P:HD3], start=True, stop=True)
                pe.matmul(small[:, 0, HEADS3:2 * HEADS3], k2[:], c.head_blocks[:, 0:P:HD3], start=True, stop=True)
                pe.matmul(small[:, 0, 2 * HEADS3:3 * HEADS3], xs[:], wb[:], start=True, stop=True).then_inc(s["small_ready"], 1)
                pe.wait_ge(s["kn_tok_ready"], 1)
                pe.transpose(tok[:, 3, :], kn_tok[:], c.ident).then_inc(s["kn_ps"], 1)
                pe.wait_ge(s["kn_ready"], 1)
                heads_of(big[:, :, 0], lambda h: kn[head(h), :], lambda h: kn[head(h), :], s["gram_ready"])
                heads_of(big[:, :, 1], lambda h: kn[head(h), :], lambda h: q[head(h), :], s["qk_ready"])
                pe.matmul(sps[:, 0, :], kn[:], S[:], start=True, stop=True).then_inc(s["kS_ready"], 1)
                pe.wait_ge(s["N_ready"], 1)
                pe.wait_ge(s["AT_ready"], 1)
                for k in range(K):
                    pe.wait_ge(s["Nlev_ready"], k + 1)
                    if k >= 1:
                        pe.wait_ge(s["t_ready"], k)
                    heads_of(zt, lambda h: Nlev[:, k, h, :], lambda h: c.ident if k == 0 else T[:, h, :], s["zt_ps"])
                    if k >= 1:
                        pe.wait_ge(s["zt_ready"], k)
                        pe.wait_ge(s["x_ready"], k)
                        if k < K - 1:
                            heads_of(tps, lambda h: XT[:, h, :], lambda h: Zt[:, h, :], s["t_ps"])
                        heads_of(xps, lambda h: Zt[:, h, :], lambda h: XT[:, h, :], s["x_ps"])
                pe.wait_ge(s["x_ready"], K)
                pe.wait_ge(s["R_ready"], 1)
                pe.wait_ge(s["vtok_ready"], 1)
                for h in range(HEADS3):
                    last = pe.matmul(ups[:, 0, head(h)], XT[:, h, :], R[:, head(h)], start=True, stop=True)
                last.then_inc(s["u_ps"], 1)
                pe.matmul(os_[:, 0, :], q[:], S[:], start=True, stop=False)
                pe.wait_ge(s["u_ready"], 1)
                for h in range(HEADS3):
                    last = pe.matmul(os_[:, 0, head(h)], AT[:, h, :], u[:, head(h)], start=False, stop=(h == HEADS3 - 1))
                last.then_inc(s["o_ps"], 1)
                pe.matmul(sps[:, 0, :], kn_tok[:], u[:], start=True, stop=True).then_inc(s["s_ps"], 1)

            @block.vector
            def _(v):
                step = Chain(v, s["chain"])
                mine = outs[:, ds(b * BLOCKS + ch, 1), :, :].rearrange("p t n d -> p (t n) d")
                v.wait_ge(s["small_ready"], 1)
                v.wait_ge(s["tanh_ready"], 1)
                step(v.tensor_scalar(beta[:], tb[:], 0.5, 0.5, ALU.mult, ALU.add))
                v.tensor_scalar(nbeta[:], beta[:], -1.0, None, ALU.mult)
                v.tensor_scalar(norms[:].rearrange("p a h -> p (a h)"), small[:, 0, 0:2 * HEADS3], L2_EPS, None,
                                ALU.add).then_inc(s["sqrt_in"], 1)
                v.wait_ge(s["tok_ready"], 1)
                v.tensor_copy(mine[:, 3, :], ups[:, 0, :])
                v.tensor_copy(mine[:, 0:2, :], ups[:, 1:3, :]).then_inc(s["vtok_ready"], 1)
                v.wait_ge(s["sqrt_ready"], 1)
                step(v.reciprocal(rnorms[:], norms[:]))
                v.tensor_tensor(kn_tok[:].rearrange("p (h d) -> p h d", h=HEADS3),
                                tok[:, 0, :].rearrange("p (h d) -> p h d", h=HEADS3),
                                spread(rnorms[:, 1, :], HD3), ALU.mult).then_inc(s["kn_tok_ready"], 1)
                v.wait_ge(s["qk_ready"], 1)
                step(v.tensor_tensor(N[:], big[:, :, 0], c.strict.unsqueeze(1).broadcast_to(four), ALU.mult))
                v.tensor_tensor(N[:], N[:], spread(nbeta[:], P), ALU.mult).then_inc(s["N_ready"], 1)
                v.tensor_tensor(AT[:], big[:, :, 1], c.upto.unsqueeze(1).broadcast_to(four), ALU.mult).then_inc(s["AT_ready"], 1)
                v.wait_ge(s["kS_ready"], 1)
                v.wait_ge(s["vtok_ready"], 1)
                v.tensor_tensor(R[:], mine[:, 3, :], sps[:, 0, :], ALU.subtract).then_inc(s["R_ready"], 1)
                idn = c.ident.unsqueeze(1).broadcast_to(four)
                v.wait_ge(s["zt_ps"], 1)
                v.tensor_tensor(T[:], zt, idn, ALU.add).then_inc(s["t_ready"], 1)
                v.wait_ge(s["Nlev_ready"], 1)
                v.tensor_tensor(XT[:], Nlev[:, 0], idn, ALU.add).then_inc(s["x_ready"], 1)
                for k in range(1, K):
                    if k < K - 1:
                        v.wait_ge(s["t_ready"], k)
                        v.wait_ge(s["t_ps"], k)
                        v.tensor_tensor(T[:], tps, T[:], ALU.add).then_inc(s["t_ready"], 1)
                    v.wait_ge(s["x_ready"], k)
                    v.wait_ge(s["x_ps"], k)
                    v.tensor_tensor(XT[:], xps, XT[:], ALU.add).then_inc(s["x_ready"], 1)
                v.wait_ge(s["u_ps"], 1)
                v.tensor_tensor(u[:].rearrange("p (h d) -> p h d", h=HEADS3),
                                ups[:, 0, :].rearrange("p (h d) -> p h d", h=HEADS3),
                                spread(beta[:], HD3), ALU.mult).then_inc(s["u_ready"], 1)
                v.wait_ge(s["o_ps"], 1)
                v.tensor_tensor(mine[:, 2, :].rearrange("p (h d) -> p h d", h=HEADS3),
                                os_[:, 0, :].rearrange("p (h d) -> p h d", h=HEADS3),
                                spread(rnorms[:, 0, :], HD3), ALU.mult)
                v.wait_ge(s["s_ps"], 1)
                step(v.tensor_tensor(R[:], sps[:, 0, :], c.head_blocks, ALU.mult))
                v.tensor_tensor(S[:], S[:], R[:], ALU.add).then_inc(s["done"], 1)
                v.wait_ge(s["done"], 1)
        st.end_step()


def l3_router_stage(nc, outer, X, XNT, c, d, outs):
    HC = [(0, P), (P, 2 * P), (2 * P, HIDDEN3)]
    Q = HEADS3 * PATHS
    rw1a = outer.sb("rw1a", [P, HIDDEN3])
    rw1b = outer.sb("rw1b", [FEATS, HIDDEN3])
    rb1 = outer.sb("rb1", [1, HIDDEN3])
    rw2 = outer.sb("rw2", [P, 3, Q])
    rb2 = outer.sb("rb2", [1, Q])
    wo = outer.sb("wo", [P, P])
    rows = outer.sb("rows", [1, 2, P])
    mixw = outer.sb("mixw", [P, 2, P])
    with Stage(nc, "a3v") as st:
        pr = st.ps("pr", (P, 2, P))
        s = st.sems("loaded rows_ready rows_ps")
        with nc.Block(no_gpsimd_drain=True) as block:
            @block.sync
            def _(sp):
                loads = [(rw1a[:], d["L3_attn_r_w1"][0:P, :]), (rw1b[:], d["L3_attn_r_w1"][P:P + FEATS, :]),
                         (rb1[:], d["L3_attn_r_b1"].rearrange("(a d) -> a d", a=1)),
                         (rb2[:], d["L3_attn_r_b2"].rearrange("(a d) -> a d", a=1)), (wo[:], d["L3_attn_Wo"]),
                         (rows[:, 0, :], d["L3_attn_mix_w"].rearrange("(a h) e -> a (h e)", a=1))]
                loads += [(rw2[0:k1 - k0, n, :], d["L3_attn_r_w2"][k0:k1, :]) for n, (k0, k1) in enumerate(HC)]
                loads += [(rows[:, 1, h * HD3:(h + 1) * HD3], d["L3_attn_onorm_w"].rearrange("(a d) -> a d", a=1))
                          for h in range(HEADS3)]
                for dst, src in loads:
                    sp.dma_start(dst, src).then_inc(s["loaded"], 16)
                assert len(loads) == 13
                sp.wait_ge(s["loaded"], 16 * 13)

            @block.tensor
            def _(pe):
                pe.wait_ge(s["loaded"], 16 * 13)
                pe.matmul(flat(pr[:]), c.ones[0:1, :], rows[:].rearrange("a n d -> a (n d)"), start=True,
                          stop=True).then_inc(s["rows_ps"], 1)

            @block.vector
            def _(v):
                v.wait_ge(s["rows_ps"], 1)
                v.tensor_copy(mixw[:], pr[:])
                for n, (k0, k1) in enumerate(HC):
                    v.tensor_scalar(rw2[0:k1 - k0, n, :], rw2[0:k1 - k0, n, :], 0.5, None, ALU.mult)
        st.end_step()

    with Stage(nc, "a3s") as st:
        NP = len(PAIRS)
        xs = st.sb("xs", [P, G, P])
        o = st.sb("o", [P, G * PATHS, P])
        mean, var = st.sb("mean", [P, G * Q]), st.sb("var", [P, G * Q])
        cent = st.sb("cent", [P, G * Q, HD3])
        prod = st.sb("prod", [P, G, NP, P])
        cross = st.sb("cross", [P, G, NP * HEADS3])
        F = st.sb("F", [P, G, FEATS])
        FT = st.sb("FT", [FEATS, G, P])
        th, hid = st.sb("th", [P, 2, HIDDEN3]), st.sb("hid", [P, 2, HIDDEN3])
        hT = st.sb("hT", [P, 2, 3, P])
        lg, w = (st.sb(n, [P, G * HEADS3, PATHS]) for n in ("lg", "w"))
        hmax, total, ms, rms = (st.sb(n, [P, G * HEADS3]) for n in ("hmax", "total", "ms", "rms"))
        mixed, sq = st.sb("mixed", [P, G * HEADS3, HD3]), st.sb("sq", [P, G * HEADS3, HD3])
        mT = st.sb("mT", [P, G, P])
        FTp = st.ps("FTp", (P, G, P))
        h1 = st.ps("h1", (P, 2, 512))
        hTp = st.ps("hTp", (P, 2, 512))
        lgp = st.ps("lgp", (P, G, Q))
        mTp = st.ps("mTp", (P, G, P))
        outp = st.ps("outp", (P, G, P))
        s = st.sems("xs_ready F_ready FT_ps FT_ready h1_ready th_ready hid_ready hT_ps hT_ready lg_ready shifted exps "
                    "ms_ready rms_ready mixed_ready mT_ps mT_ready out_ps o_ready added chain")
        with nc.Fori(0, TILES // G) as i:
            with nc.Block(no_gpsimd_drain=True) as block:
                @block.gpsimd
                def _(g):
                    g.tensor_copy(o[:], outs[:, ds(i * G, G), :, :].rearrange("p t n d -> p (t n) d")).then_inc(s["o_ready"], 1)

                @block.scalar
                def _(a):
                    a.activation(xs[:].rearrange("p t d -> p (t d)"), XNT[:, ds(i * G * P, G * P)],
                                 ACT.Copy).then_inc(s["xs_ready"], 1)
                    a.wait_ge(s["FT_ps"], 1)
                    a.activation(FT[:], FTp[0:FEATS], ACT.Copy).then_inc(s["FT_ready"], 1)
                    for j in range(G):
                        a.wait_ge(s["h1_ready"], j + 1)
                        if j >= 2:
                            a.wait_ge(s["hid_ready"], j - 1)
                        a.activation(th[:, j % 2, :], h1[:, j % 2, 0:HIDDEN3], ACT.Tanh, scale=0.5).then_inc(s["th_ready"], 1)
                        a.wait_ge(s["hT_ps"], j + 1)
                        a.activation(hT[:, j % 2, 0:2, :].rearrange("p n d -> p (n d)"), hTp[:, j % 2, 0:2 * P], ACT.Copy)
                        last = a.activation(hT[0:HIDDEN3 - 2 * P, j % 2, 2, :], hTp[0:HIDDEN3 - 2 * P, j % 2, 2 * P:3 * P],
                                            ACT.Copy)
                        last.then_inc(s["hT_ready"], 1)
                    a.wait_ge(s["shifted"], 1)
                    a.activation(lg[:], lg[:], ACT.Exp).then_inc(s["exps"], 1)
                    for n in range(2):
                        a.wait_ge(s["ms_ready"], n + 1)
                        a.activation(rms[:], ms[:], ACT.Sqrt).then_inc(s["rms_ready"], 1)
                    a.wait_ge(s["mT_ps"], 1)
                    a.activation(mT[:], mTp[:], ACT.Copy).then_inc(s["mT_ready"], 1)

                @block.tensor
                def _(pe):
                    pe.wait_ge(s["F_ready"], 1)
                    for j in range(G):
                        last = pe.transpose(FTp[0:FEATS, j, :], F[:, j, :], c.ident)
                    last.then_inc(s["FT_ps"], 1)
                    pe.wait_ge(s["xs_ready"], 1)
                    pe.wait_ge(s["FT_ready"], 1)

                    def hidden(j):
                        if j >= 2:
                            pe.wait_ge(s["hid_ready"], j - 1)
                        o1 = h1[:, j % 2, 0:HIDDEN3]
                        pe.matmul(o1, xs[:, j, :], rw1a[:], start=True, stop=False)
                        pe.matmul(o1, FT[:, j, :], rw1b[:], start=False, stop=False)
                        pe.matmul(o1, c.ones[0:1, :], rb1[:], start=False, stop=True).then_inc(s["h1_ready"], 1)

                    hidden(0)
                    for j in range(G):
                        if j + 1 < G:
                            hidden(j + 1)
                        pe.wait_ge(s["hid_ready"], j + 1)
                        if j >= 2:
                            pe.wait_ge(s["hT_ready"], j - 1)
                        for n, (k0, k1) in enumerate(HC):
                            last = pe.transpose(hTp[0:k1 - k0, j % 2, n * P:(n + 1) * P], hid[:, j % 2, k0:k1], c.ident)
                        last.then_inc(s["hT_ps"], 1)
                        pe.wait_ge(s["hT_ready"], j + 1)
                        for n, (k0, k1) in enumerate(HC):
                            pe.matmul(lgp[:, j, :], hT[0:k1 - k0, j % 2, n, :], rw2[0:k1 - k0, n, :], start=(n == 0), stop=False)
                        pe.matmul(lgp[:, j, :], c.ones[0:1, :], rb2[:], start=False, stop=True).then_inc(s["lg_ready"], 1)
                    pe.wait_ge(s["mixed_ready"], 1)
                    for j in range(G):
                        last = pe.transpose(mTp[:, j, :], mixed[:, j * HEADS3:(j + 1) * HEADS3, :]
                                            .rearrange("p h e -> p (h e)"), c.ident)
                    last.then_inc(s["mT_ps"], 1)
                    pe.wait_ge(s["mT_ready"], 1)
                    for j in range(G):
                        last = pe.matmul(outp[:, j, :], mT[:, j, :], wo[:], start=True, stop=True)
                    last.then_inc(s["out_ps"], 1)

                @block.vector
                def _(v):
                    step = Chain(v, s["chain"])
                    v.wait_ge(s["o_ready"], 1)
                    by_head = o[:].rearrange("p n (h e) -> p (n h) e", h=HEADS3)
                    step(v.tensor_reduce(mean[:], by_head, AX.X, ALU.add))
                    step(v.tensor_scalar(mean[:], mean[:], 1.0 / HD3, None, ALU.mult))
                    step(v.tensor_tensor(cent[:], by_head, spread(mean[:], HD3), ALU.subtract))
                    step(v.tensor_tensor(cent[:], cent[:], cent[:], ALU.mult))
                    step(v.tensor_reduce(var[:], cent[:], AX.X, ALU.add))
                    by_tile = o[:].rearrange("p (t n) d -> p t n d", t=G)
                    for n, (x, y) in enumerate(PAIRS):
                        last = v.tensor_tensor(prod[:, :, n, :], by_tile[:, :, x, :], by_tile[:, :, y, :], ALU.mult)
                    step(last)
                    step(v.tensor_reduce(cross[:].rearrange("p t n -> p (t n)"),
                                         prod[:].rearrange("p t n (h e) -> p (t n h) e", h=HEADS3), AX.X, ALU.add))
                    stats = F[:, :, 0:2 * Q].rearrange("p t (n w h) -> p t n w h", n=PATHS, w=2)
                    for j in range(G):
                        v.tensor_copy(stats[:, j, :, 0, :], mean[:, j * Q:(j + 1) * Q].rearrange("p (n h) -> p n h", n=PATHS))
                        v.tensor_scalar(stats[:, j, :, 1, :], var[:, j * Q:(j + 1) * Q].rearrange("p (n h) -> p n h", n=PATHS),
                                        1.0 / (HD3 - 1), None, ALU.mult)
                    v.tensor_scalar(F[:, :, 2 * Q:], cross[:], 1.0 / HD3, None, ALU.mult).then_inc(s["F_ready"], 1)
                    for j in range(G):
                        v.wait_ge(s["th_ready"], j + 1)
                        if j >= 2:
                            v.wait_ge(s["hT_ps"], j - 1)
                        v.scalar_tensor_tensor(out=hid[:, j % 2, :], in0=th[:, j % 2, :], scalar=1.0,
                                               in1=h1[:, j % 2, 0:HIDDEN3], op0=ALU.add, op1=ALU.mult).then_inc(s["hid_ready"], 1)
                    v.wait_ge(s["lg_ready"], G)
                    logit = lgp[:].rearrange("p t (h n) -> p (t h) n", h=HEADS3)
                    step(v.tensor_reduce(hmax[:], logit, AX.X, ALU.max))
                    v.tensor_tensor(lg[:], logit, spread(hmax[:], PATHS), ALU.subtract).then_inc(s["shifted"], 1)
                    v.wait_ge(s["exps"], 1)
                    step(v.tensor_reduce(total[:], lg[:], AX.X, ALU.add))
                    step(v.reciprocal(total[:], total[:]))
                    step(v.tensor_tensor(w[:], lg[:], spread(total[:], PATHS), ALU.mult))
                    step(v.tensor_scalar(w[:], w[:], 1.0 - 4.0 * FLOOR, FLOOR, ALU.mult, ALU.add))
                    for j in range(G):
                        wj = w[:, j * HEADS3:(j + 1) * HEADS3, :].rearrange("p h n -> p n h")
                        last = v.tensor_tensor(cent[:, j * Q:(j + 1) * Q, :].rearrange("p (n h) e -> p n h e", n=PATHS),
                                               by_head[:, j * Q:(j + 1) * Q, :].rearrange("p (n h) e -> p n h e", n=PATHS),
                                               wj.unsqueeze(3).broadcast_to([P, PATHS, HEADS3, HD3]), ALU.mult)
                    step(last)
                    for j in range(G):
                        last = v.tensor_reduce(mixed[:, j * HEADS3:(j + 1) * HEADS3, :].rearrange("p h e -> p (h e)"),
                                               cent[:, j * Q:(j + 1) * Q, :].rearrange("p (n h) e -> p (h e) n", n=PATHS),
                                               AX.X, ALU.add)
                    step(last)
                    for n in range(2):
                        step(v.tensor_tensor(sq[:], mixed[:], mixed[:], ALU.mult))
                        step(v.tensor_reduce(ms[:], sq[:], AX.X, ALU.add))
                        v.tensor_scalar(ms[:], ms[:], 1.0 / HD3, MIX_EPS, ALU.mult, ALU.add).then_inc(s["ms_ready"], 1)
                        v.wait_ge(s["rms_ready"], n + 1)
                        step(v.reciprocal(total[:], rms[:]))
                        step(v.tensor_tensor(mixed[:], mixed[:], spread(total[:], HD3), ALU.mult))
                        last = v.tensor_tensor(mixed[:].rearrange("p (t h) e -> p t (h e)", t=G),
                                               mixed[:].rearrange("p (t h) e -> p t (h e)", t=G),
                                               mixw[:, n:n + 1, :].broadcast_to([P, G, P]), ALU.mult)
                        if n == 0:
                            step(last)
                    last.then_inc(s["mixed_ready"], 1)
                    v.wait_ge(s["out_ps"], 1)
                    v.tensor_tensor(X[:, ds(i * G, G), :], outp[:], X[:, ds(i * G, G), :], ALU.add).then_inc(s["added"], 1)
                    v.wait_ge(s["added"], 1)
            st.end_step()



def l3_ffn_stage(nc, X, XNT, c, router_w, router_b, expert_w, expert_b):
    with Stage(nc, "f3") as outer:
        rwT = outer.sb("rwT", [P, EXPERTS])
        ewT = outer.sb("ewT", [P, EXPERTS, P])
        rb = outer.sb("rb", [1, EXPERTS])
        eb = outer.sb("eb", [1, EXPERTS * P])
        load_turned(nc, "f3t", [(rwT[:], router_w)] + [(ewT[:, e, :], expert_w[e]) for e in range(EXPERTS)], c)
        with Stage(nc, "f3w") as st:
            s = st.sems("loaded")
            with nc.Block(no_gpsimd_drain=True) as block:
                @block.sync
                def _(sp):
                    sp.dma_start(rb[:], router_b.rearrange("(a d) -> a d", a=1)).then_inc(s["loaded"], 16)
                    sp.dma_start(eb[:], expert_b.rearrange("(a e) d -> a (e d)", a=1)).then_inc(s["loaded"], 16)
                    sp.wait_ge(s["loaded"], 32)
            st.end_step()
        with Stage(nc, "f3s") as st:
            xs = st.sb("xs", [P, G * P])
            lg, ex, choice = (st.sb(n, [P, G, EXPERTS]) for n in ("lg", "ex", "choice"))
            top = st.sb("top", [P, G, 8])
            at = st.sb("at", [P, G, 8], U32)
            atf = st.sb("atf", [P, G, 8])
            total, weight = (st.sb(n, [P, G]) for n in ("total", "weight"))
            picked = st.sb("picked", [P, 2, EXPERTS, P])
            summed = st.sb("summed", [P, G, P])
            logits = st.ps("logits", (P, G, EXPERTS))
            y = st.ps("y", (P, 2, EXPERTS, P))
            s = st.sems("xs_ready logits_ready y_ready shifted exps y_used added chain")
            with nc.Fori(0, TILES // G) as i:
                with nc.Block(no_gpsimd_drain=True) as block:
                    @block.scalar
                    def _(a):
                        a.activation(xs[:], XNT[:, ds(i * G * P, G * P)], ACT.Copy).then_inc(s["xs_ready"], 1)
                        a.wait_ge(s["shifted"], 1)
                        a.activation(ex[:], ex[:], ACT.Exp).then_inc(s["exps"], 1)

                    @block.tensor
                    def _(pe):
                        pe.wait_ge(s["xs_ready"], 1)
                        for j in range(G):
                            pe.matmul(logits[:, j, :], xs[:, j * P:(j + 1) * P], rwT[:], start=True, stop=False)
                            last = pe.matmul(logits[:, j, :], c.ones[0:1, :], rb[:], start=False, stop=True)
                        last.then_inc(s["logits_ready"], 1)
                        for j in range(G):
                            if j >= 2:
                                pe.wait_ge(s["y_used"], j - 1)
                            for k in range(0, EXPERTS, 4):
                                o = y[:, j % 2, k:k + 4, :].rearrange("p e d -> p (e d)")
                                pe.matmul(o, xs[:, j * P:(j + 1) * P], ewT[:, k:k + 4, :].rearrange("p e d -> p (e d)"),
                                          start=True, stop=False)
                                last = pe.matmul(o, c.ones[0:1, :], eb[:, k * P:(k + 4) * P], start=False, stop=True)
                            last.then_inc(s["y_ready"], 1)

                    @block.vector
                    def _(v):
                        step = Chain(v, s["chain"])
                        v.wait_ge(s["logits_ready"], 1)
                        step(v.tensor_copy(lg[:], logits[:]))
                        for j in range(G):
                            last = v.max(top[:, j, :], lg[:, j, :])
                        step(last)
                        v.tensor_tensor(ex[:], lg[:], top[:, :, 0:1].broadcast_to([P, G, EXPERTS]),
                                        ALU.subtract).then_inc(s["shifted"], 1)
                        for j in range(G):
                            last = v.max_index(at[:, j, :], top[:, j, :], lg[:, j, :])
                        step(last)
                        step(v.tensor_copy(atf[:], at[:]))
                        v.wait_ge(s["exps"], 1)
                        step(v.tensor_reduce(total[:], ex[:], AX.X, ALU.add))
                        step(v.reciprocal(weight[:], total[:]))
                        for j in range(G):
                            last = v.tensor_scalar(choice[:, j, :], c.count8, atf[:, j, 0:1], weight[:, j:j + 1],
                                                   ALU.is_equal, ALU.mult)
                        step(last)
                        for j in range(G):
                            v.wait_ge(s["y_ready"], j + 1)
                            v.tensor_tensor(picked[:, j % 2], y[:, j % 2], spread(choice[:, j, :], P),
                                            ALU.mult).then_inc(s["y_used"], 1)
                            v.wait_ge(s["y_used"], j + 1)
                            step(v.tensor_reduce(summed[:, j, :], picked[:, j % 2].rearrange("p e d -> p d e"),
                                                 AX.X, ALU.add))
                        v.tensor_tensor(X[:, ds(i * G, G), :], summed[:], X[:, ds(i * G, G), :],
                                        ALU.add).then_inc(s["added"], 1)
                        v.wait_ge(s["added"], 1)
                st.end_step()


def build(nc, d, out, stages):
    with ExitStack() as ctx:
        def sb(name, shape):
            return ctx.enter_context(nc.sbuf_tensor(name, shape, F32))

        X = sb("X", [P, TILES, P])
        consts = sb("consts", [P, len(SQUARES) * P + 8])
        c = Constants(consts)
        load_stage(nc, X, d["L0_attn_x"], d["const_squares"], c)

        for k, stage in enumerate(SUBLAYERS):
            if k in stages:
                with ExitStack() as inner:
                    padded = inner.enter_context(nc.sbuf_tensor(f"XN{k}", [P, TILES + 2, P], F32))
                    XN = padded[:, 1:TILES + 1, :]
                    XNT = inner.enter_context(nc.sbuf_tensor(f"XNT{k}", [P, TILES * P], F32))
                    layernorm_stage(nc, X, XN, XNT, c)
                    stage(nc, d, X, padded if stage is sub3 else XN, XNT, c)

        with Stage(nc, "store") as st:
            s = st.sems("stored")
            with nc.Block(no_gpsimd_drain=True) as block:
                @block.sync
                def _(sp):
                    sp.dma_start(out.rearrange("b (t p) d -> p (b t) d", p=P), X[:]).then_inc(s["stored"], 16)
                    sp.wait_ge(s["stored"], 16)
            st.end_step()


def sub0(nc, d, X, XN, XNT, c):
    l0_attention_stage(nc, X, XNT, c, d["L0_attn_W_Q"], d["L0_attn_W_K"], d["L0_attn_W_V"], d["L0_attn_W_O"],
                       d["const_alibi"], d["const_key_pos"])


def sub1(nc, d, X, XN, XNT, c):
    l0_ffn_stage(nc, X, XNT, c, d["L0_ffn_w_gate"], d["L0_ffn_w_expert"], d["L0_ffn_b_expert"])


def sub2(nc, d, X, XN, XNT, c):
    l1_attention_stage(nc, X, XNT, c, d)


def sub3(nc, d, X, padded, XNT, c):
    l1_ffn_stage(nc, X, padded, XNT, c, d)


def sub4(nc, d, X, XN, XNT, c):
    l2_attention_stage(nc, X, XN, XNT, c)


def sub5(nc, d, X, XN, XNT, c):
    l2_ffn_stage(nc, X, XNT, c, d["L2_ffn_gate_w"], d["L2_ffn_w1"], d["L2_ffn_w2"], d["L2_ffn_w3"])


def sub6(nc, d, X, XN, XNT, c):
    l3_attention_stage(nc, X, XNT, c, d)


def sub7(nc, d, X, XN, XNT, c):
    l3_ffn_stage(nc, X, XNT, c, d["L3_ffn_router_w"], d["L3_ffn_router_b"], d["L3_ffn_expert_w"],
                 d["L3_ffn_expert_b"])


def more_constants():
    j, i = np.arange(P)[:, None], np.arange(P)[None, :]
    masks = [(j // (2 * n) == i // (2 * n)) & (j // n % 2 == 0) & (i // n % 2 == 1) for n in LEVELS]
    half = np.arange(0, HDW, 2, dtype=np.float32)
    t = np.arange(SEQ, dtype=np.float32)
    freqs = t[:, None] * (np.float32(1.0) / np.float32(10000.0) ** (half / np.float32(HDW)))[None, :]
    power = (t - SEQ // 2) / np.float32(WINDOW // 2)
    scale = ((half + 0.4 * HDW) / (1.4 * HDW)).astype(np.float64)[None, :] ** power[:, None]
    cos, sin = np.cos(freqs.astype(np.float64)), np.sin(freqs.astype(np.float64))
    rope = [np.concatenate([cos * w, cos * w], 1) if n == 0 else np.concatenate([-sin * w, sin * w], 1)
            for w in (scale, 1.0 / scale) for n in range(2)]
    rope = np.stack(rope).reshape(4, BLOCKS, P, HDW).transpose(2, 0, 1, 3)
    rope = np.concatenate([rope, rope[:, :, 0:1]], axis=2)
    has_prev = np.zeros((P, 2, BLOCKS + 1))
    has_prev[P - 1, 0, 1:BLOCKS] = 1.0
    has_prev[:, 1, 1:BLOCKS] = 1.0
    query = (np.arange(BLOCKS)[None, :] * P + np.arange(P)[:, None])[:, :, None]
    key = (np.arange(BLOCKS)[:, None] * P - WINDOW + np.arange(KEYS)[None, :])[None]
    seen = (key <= query) & (key >= query - WINDOW) & (key >= 0)
    return {"const_level_masks": np.stack(masks, axis=1), "const_rope": rope, "const_has_prev": has_prev,
            "const_band": np.where(seen, 0.0, NEG),
            "const_shifts": np.stack([j == i - 1, (j == P - 1) & (i == 0)], axis=1)}


SUBLAYERS = [sub0, sub1, sub2, sub3, sub4, sub5, sub6, sub7]

SQUARES = ["ident", "ones", "upto", "after", "strict", "neg_upper", "head_blocks"]


def constants():
    i = np.arange(P)
    row, col = i[:, None], i[None, :]
    squares = {
        "ident": row == col,
        "ones": np.ones((P, P)),
        "upto": row <= col,
        "after": row > col,
        "strict": row < col,
        "neg_upper": np.where(col > row, NEG, 0.0),
        "head_blocks": row // 32 == col // 32,
    }
    table = np.concatenate([squares[n].astype(np.float32) for n in SQUARES]
                           + [np.broadcast_to(np.arange(8, dtype=np.float32), (P, 8))], axis=1)
    slopes = 1.0 / np.float32(256.0) ** ((np.arange(HEADS0, dtype=np.float32) + 1) / HEADS0)
    alibi = np.zeros((1, HEADS0 // HG + 1, HG, ROWS), np.float32)
    alibi[0, :-1, :, HD0] = slopes.reshape(-1, HG)
    alibi[0, -1, :, HD0] = 1.0
    alibi = alibi.reshape(1, HEADS0 // HG + 1, P)
    made = {"const_squares": table, "const_alibi": alibi,
            "const_key_pos": np.arange(SEQ, dtype=np.float32)[None, :] - SEQ // 2}
    made.update(more_constants())
    return {k: np.ascontiguousarray(a, dtype=np.float32) for k, a in made.items()}


_STAGES = range(8)


def kernel(**inputs):
    import concourse.bacc as _bacc
    from concourse.bass_utils import run_bass_kernel_spmd as _run

    nc = _bacc.Bacc("TRN2", target_bir_lowering=False, num_devices=1)
    arrays, d = {}, {}
    for name, a in {**inputs, **constants()}.items():
        a = np.ascontiguousarray(a)
        arrays[f"in_{name}_dram"] = a
        d[name] = nc.dram_tensor(f"in_{name}_dram", a.shape, mybir.dt.from_np(a.dtype), kind="ExternalInput").ap()
    out = nc.dram_tensor("out_0_dram", (BATCH, SEQ, P), F32, kind="ExternalOutput").ap()
    build(nc, d, out, _STAGES)
    r = _run(nc, [arrays], core_ids=[0])
    return r.results[0]["out_0_dram"]
```
